# Optimizing a Trainium2 kernel written in Bass

```python
import numpy as np
import jax
import jax.numpy as jnp

def _softmax(x, axis=-1):
    return jax.nn.softmax(x, axis=axis)

def _gelu(x):
    return jax.nn.gelu(x, approximate=True)

def _silu(x):
    return jax.nn.silu(x)

def _sigmoid(x):
    return jax.nn.sigmoid(x)

def _layernorm(x, axis=-1, eps=1e-05):
    m = jnp.mean(x, axis=axis, keepdims=True)
    v = jnp.var(x, axis=axis, keepdims=True)
    return (x - m) / jnp.sqrt(v + eps)

def _scatter_add(tgt, idx, src, axis=0):
    return tgt.at[idx].add(src)

def _segment_sum(src, seg, n):
    return jax.ops.segment_sum(src, seg, n)
kernel_name = 'mk_adj_ffn_d4_adj_r2_85db36'

def setup_inputs(seed: int=0):
    np.random.seed(seed)
    _w = jnp.asarray

    def _rec_inputs():
        import jax
        import jax.numpy as jnp
        _gk = jax.random.key(seed)
        x = -0.0002928 + 1 * jax.random.normal(jax.random.fold_in(_gk, 1), (32, 256, 128), jnp.float32)
        _w = (1.0 + jnp.arange(256, dtype=jnp.float32)) ** (-0.5)
        _w = _w / _w.mean()
        _pij = jnp.clip(0.0625 * _w[:, None] * _w[None, :], 0.0, 1.0)
        _a = jax.random.uniform(jax.random.fold_in(_gk, 2), (32, 256, 256)) < _pij
        _a = jnp.logical_or(_a, jnp.swapaxes(_a, -1, -2))
        _a = jnp.logical_or(_a, jnp.eye(256, dtype=bool))
        _af = _a.astype(jnp.float32)
        _af = _af * jax.random.uniform(jax.random.fold_in(_gk, 3), (32, 256, 256), jnp.float32, 0.05, 1)
        adj = _af
        return (x, adj)
    x, adj = _rec_inputs()

    def _L0_gnn_setup():
        import jax, jax.numpy as jnp
        import numpy as np
        K = 4
        EPS = 1e-09
        LEAKY_SLOPE = 0.2
        key = jax.random.key(seed)
        k1, k2, k3, k4, k5 = jax.random.split(key, 5)
        B, N, IN, OUT = (8, 1024, 128, 128)
        h = jax.random.normal(k1, (B, N, IN), dtype=jnp.float32)
        adj = jax.random.uniform(k2, (B, N, N), dtype=jnp.float32)
        W = jax.random.normal(k3, (OUT, IN), dtype=jnp.float32) * 0.05
        conv_w = jax.random.normal(k4, (K,), dtype=jnp.float32)
        conv_b = jax.random.normal(k5, (1,), dtype=jnp.float32)
        return {'h': h, 'adj': adj, 'W': W, 'conv_w': conv_w, 'conv_b': conv_b}
    _L0_gnn_all = _L0_gnn_setup()
    _L0_gnn_in = {k: v for k, v in _L0_gnn_all.items() if k in ('W', 'conv_w', 'conv_b')}
    del _L0_gnn_all

    def _L0_ffn_setup():
        import jax, jax.numpy as jnp
        import numpy as np
        D_MODEL = 128
        N_EXPERTS = 16
        HIDDEN = 256
        SCALE = 0.02
        key = jax.random.key(seed)
        ks = jax.random.split(key, 5)
        x = jax.random.normal(ks[0], (4, 4096, D_MODEL), dtype=jnp.float32)
        gate_w = jax.random.normal(ks[1], (D_MODEL, N_EXPERTS), dtype=jnp.float32) * SCALE
        gate_b = jnp.zeros((N_EXPERTS,), dtype=jnp.float32)
        w1 = jax.random.normal(ks[2], (N_EXPERTS, D_MODEL, HIDDEN), dtype=jnp.float32) * SCALE
        w2 = jax.random.normal(ks[3], (N_EXPERTS, D_MODEL, HIDDEN), dtype=jnp.float32) * SCALE
        w3 = jax.random.normal(ks[4], (N_EXPERTS, HIDDEN, D_MODEL), dtype=jnp.float32) * SCALE
        return {'x': x, 'gate_w': gate_w, 'gate_b': gate_b, 'w1': w1, 'w2': w2, 'w3': w3}
    _L0_ffn_all = _L0_ffn_setup()
    _L0_ffn_in = {k: v for k, v in _L0_ffn_all.items() if k in ('gate_w', 'gate_b', 'w1', 'w2', 'w3')}
    del _L0_ffn_all

    def _L1_gnn_setup():
        import jax, jax.numpy as jnp
        import numpy as np
        GROUPS = [list(range(25)), [0, 1, 2, 3, 4, 5, 6, 7, 8], [0, 9, 10, 11, 12, 13, 14], [6, 7, 8, 12, 13, 14], [3, 4, 5, 9, 10, 11]]
        B, N, D_IN, D_HID = (4096, 25, 128, 256)

        def _graph_conv(x, adj, W, b):
            n = adj.shape[-1]
            A = adj + jnp.eye(n, dtype=adj.dtype)
            deg = jnp.sum(A, axis=-1)
            deg_safe = jnp.where(deg == 0, 1.0, deg)
            dinv = jnp.where(deg == 0, 0.0, deg_safe ** (-0.5))
            norm_adj = dinv[:, :, None] * A * dinv[:, None, :]
            support = jnp.einsum('bnd,de->bne', x, W)
            out = jnp.einsum('bnm,bme->bne', norm_adj, support) + b
            return jax.nn.relu(out)
        key = jax.random.key(seed)
        ks = jax.random.split(key, 7)
        s1 = float(np.sqrt(6.0 / (D_IN + D_HID)))
        s2 = float(np.sqrt(6.0 / (D_HID + D_IN)))
        return {'x': jax.random.normal(ks[0], (B, N, D_IN), dtype=jnp.float32), 'adj': jax.random.uniform(ks[1], (B, N, N), dtype=jnp.float32), 'W1': jax.random.uniform(ks[2], (5, D_IN, D_HID), jnp.float32, -s1, s1), 'b1': jnp.zeros((5, D_HID), dtype=jnp.float32), 'W2': jax.random.uniform(ks[3], (5, D_HID, D_IN), jnp.float32, -s2, s2), 'b2': jnp.zeros((5, D_IN), dtype=jnp.float32), 'fusion_w': jnp.ones((5,), dtype=jnp.float32)}
    _L1_gnn_all = _L1_gnn_setup()
    _L1_gnn_in = {k: v for k, v in _L1_gnn_all.items() if k in ('W1', 'b1', 'W2', 'b2', 'fusion_w')}
    del _L1_gnn_all

    def _L1_ffn_setup():
        import math
        import jax, jax.numpy as jnp
        import numpy as np
        CAPACITY_FACTOR = 1.25
        key = jax.random.key(seed)
        ks = jax.random.split(key, 5)
        B, L, D, F, E = (8, 4096, 128, 512, 8)
        h = jax.random.normal(ks[0], (B, L, D), dtype=jnp.float32)
        gate_w = jax.random.normal(ks[1], (D, E), dtype=jnp.float32) * 0.02
        gate_b = jnp.zeros((E,), dtype=jnp.float32)
        w1 = jax.random.normal(ks[2], (E, D, F), dtype=jnp.float32) * (1.0 / math.sqrt(D))
        b1 = jnp.zeros((E, F), dtype=jnp.float32)
        w2 = jax.random.normal(ks[3], (E, F, D), dtype=jnp.float32) * (1.0 / math.sqrt(F))
        b2 = jnp.zeros((E, D), dtype=jnp.float32)
        return {'h': h, 'gate_w': gate_w, 'gate_b': gate_b, 'w1': w1, 'b1': b1, 'w2': w2, 'b2': b2}
    _L1_ffn_all = _L1_ffn_setup()
    _L1_ffn_in = {k: v for k, v in _L1_ffn_all.items() if k in ('gate_w', 'gate_b', 'w1', 'b1', 'w2', 'b2')}
    del _L1_ffn_all

    def _L2_gnn_setup():
        import jax, jax.numpy as jnp
        import numpy as np
        B, N, D = (8, 256, 128)
        key = jax.random.key(seed)
        ks = jax.random.split(key, 10)
        s = 1.0 / np.sqrt(D)
        u = lambda k, shape: jax.random.uniform(k, shape, jnp.float32, -s, s)
        return {'h_e': jax.random.normal(ks[0], (B, N, D), jnp.float32), 'adj': jax.random.uniform(ks[1], (B, N, N), jnp.float32), 'W_ioux': u(ks[2], (2 * D, D)), 'b_ioux': u(ks[3], (2 * D,)), 'W_iouh': u(ks[4], (2 * D, D)), 'b_iouh': u(ks[5], (2 * D,)), 'W_coux': u(ks[6], (D, D)), 'b_coux': u(ks[7], (D,)), 'W_couh': u(ks[8], (D, D)), 'b_couh': u(ks[9], (D,))}
    _L2_gnn_all = _L2_gnn_setup()
    _L2_gnn_in = {k: v for k, v in _L2_gnn_all.items() if k in ('W_ioux', 'b_ioux', 'W_iouh', 'b_iouh', 'W_coux', 'b_coux', 'W_couh', 'b_couh')}
    del _L2_gnn_all

    def _L2_ffn_setup():
        import jax, jax.numpy as jnp
        import numpy as np
        B, S, D, H, E, K = (8, 4096, 128, 512, 8, 2)
        key = jax.random.key(seed)
        ks = jax.random.split(key, 7)
        s_in = 1.0 / np.sqrt(D)
        s_hid = 1.0 / np.sqrt(H)
        return {'x': jax.random.normal(ks[0], (B, S, D), dtype=jnp.float32), 'Wg': jax.random.uniform(ks[1], (E, D), jnp.float32, -s_in, s_in), 'bg': jax.random.uniform(ks[2], (E,), jnp.float32, -s_in, s_in), 'W1': jax.random.uniform(ks[3], (E, H, D), jnp.float32, -s_in, s_in), 'b1': jax.random.uniform(ks[4], (E, H), jnp.float32, -s_in, s_in), 'W2': jax.random.uniform(ks[5], (E, D, H), jnp.float32, -s_hid, s_hid), 'b2': jax.random.uniform(ks[6], (E, D), jnp.float32, -s_hid, s_hid)}
    _L2_ffn_all = _L2_ffn_setup()
    _L2_ffn_in = {k: v for k, v in _L2_ffn_all.items() if k in ('Wg', 'bg', 'W1', 'b1', 'W2', 'b2')}
    del _L2_ffn_all

    def _L3_gnn_setup():
        import jax, jax.numpy as jnp
        import numpy as np
        ALPHA = 0.2
        EPS = 1e-05
        NEG = -9000000000000000.0
        key = jax.random.key(seed)
        k1, k2, k3, k4 = jax.random.split(key, 4)
        B, N, F_in, F_out = (8, 1024, 128, 128)
        h = jax.random.normal(k1, (B, N, F_in), dtype=jnp.float32)
        adj = jax.random.randint(k2, (B, N, N), 0, 2).astype(jnp.float32)
        W = jax.random.normal(k3, (F_in, F_out), dtype=jnp.float32) * (1.414 * np.sqrt(2.0 / (F_in + F_out)))
        a = jax.random.normal(k4, (2 * F_out, 1), dtype=jnp.float32) * (1.414 * np.sqrt(2.0 / (2 * F_out + 1)))
        gamma = jnp.ones((F_out,), dtype=jnp.float32)
        beta = jnp.zeros((F_out,), dtype=jnp.float32)
        return {'h': h, 'adj': adj, 'W': W, 'a': a, 'gamma': gamma, 'beta': beta}
    _L3_gnn_all = _L3_gnn_setup()
    _L3_gnn_in = {k: v for k, v in _L3_gnn_all.items() if k in ('W', 'a', 'gamma', 'beta')}
    del _L3_gnn_all

    def _L3_ffn_setup():
        import jax, jax.numpy as jnp
        import numpy as np
        H, P, G, NS, K = (8, 64, 64, 64, 3)
        D_INNER = H * P
        CONV_DIM = D_INNER + 2 * NS
        D_IN_PROJ = 2 * D_INNER + 2 * NS + 2 * H

        def _hydra(u, in_w, conv_w, conv_b, dt_bias, A_log, Dp, fcD_w, norm_w, out_w):
            Bt, L, _ = u.shape
            zxbcdt = u @ in_w.T
            z = zxbcdt[..., :D_INNER]
            xBC = zxbcdt[..., D_INNER:D_INNER + CONV_DIM]
            dt = zxbcdt[..., -2 * H:]
            dt = jnp.concatenate([dt[..., :H], jnp.flip(dt[..., H:], axis=1)], axis=0)
            dt = jax.nn.softplus(dt + dt_bias)
            xp = jnp.pad(xBC, ((0, 0), (K - 1, 0), (0, 0)))
            xBC = sum((xp[:, k:k + L, :] * conv_w[:, k] for k in range(K))) + conv_b
            xBC = jax.nn.silu(xBC)
            x = xBC[..., :D_INNER]
            Bm = xBC[..., D_INNER:D_INNER + NS]
            Cm = xBC[..., D_INNER + NS:]
            x_og = x
            x2 = jnp.concatenate([x, jnp.flip(x, 1)], 0).reshape(2 * Bt, L, H, P)
            B2 = jnp.concatenate([Bm, jnp.flip(Bm, 1)], 0)
            C2 = jnp.concatenate([Cm, jnp.flip(Cm, 1)], 0)
            dA = jnp.exp(dt * -jnp.exp(A_log))
            dBx = jnp.einsum('blh,bln,blhp->blhpn', dt, B2, x2)

            def step(h, inp):
                dA_t, dBx_t, C_t = inp
                h = h * dA_t[:, :, None, None] + dBx_t
                return (h, jnp.einsum('bhpn,bn->bhp', h, C_t))
            h0 = jnp.zeros((2 * Bt, H, P, NS), u.dtype)
            _, ys = jax.lax.scan(step, h0, (dA.transpose(1, 0, 2), dBx.transpose(1, 0, 2, 3, 4), C2.transpose(1, 0, 2)))
            y = ys.transpose(1, 0, 2, 3).reshape(2 * Bt, L, D_INNER)
            y_fw, y_bw = (y[:Bt], jnp.flip(y[Bt:], 1))
            y = jnp.pad(y_fw[:, :-1], ((0, 0), (1, 0), (0, 0))) + jnp.pad(y_bw[:, 1:], ((0, 0), (0, 1), (0, 0)))
            y = y + x_og * jnp.repeat(x_og @ fcD_w.T + Dp, P, axis=-1)
            yg = y * jax.nn.silu(z)
            yg = yg * jax.lax.rsqrt(jnp.mean(jnp.square(yg), -1, keepdims=True) + 1e-05) * norm_w
            return yg @ out_w.T
        key = jax.random.key(seed)
        ks = jax.random.split(key, 10)
        dim, Bsz, N = (128, 4, 4096)
        s = 0.02
        return {'x': jax.random.normal(ks[0], (Bsz, N, dim), jnp.float32), 'W_fx': jax.random.normal(ks[1], (D_INNER, dim), jnp.float32) * s, 'b_fx': jnp.zeros((D_INNER,), jnp.float32), 'W_x': jax.random.normal(ks[2], (D_INNER, dim), jnp.float32) * s, 'b_x': jnp.zeros((D_INNER,), jnp.float32), 'W_slice': jax.random.normal(ks[3], (G, P), jnp.float32) * s, 'b_slice': jnp.zeros((G,), jnp.float32), 'temperature': jnp.full((1, H, 1, 1), 0.5, jnp.float32), 'hy_in_w': jax.random.normal(ks[4], (D_IN_PROJ, D_INNER), jnp.float32) * s, 'hy_conv_w': jax.random.normal(ks[5], (CONV_DIM, K), jnp.float32) * s, 'hy_conv_b': jnp.zeros((CONV_DIM,), jnp.float32), 'hy_dt_bias': jnp.log(jnp.expm1(jnp.full((H,), 0.01, jnp.float32))), 'hy_A_log': jnp.log(jnp.linspace(1.0, 16.0, H)).astype(jnp.float32), 'hy_D': jnp.ones((H,), jnp.float32), 'hy_fcD_w': jax.random.normal(ks[6], (H, D_INNER), jnp.float32) * s, 'hy_norm_w': jnp.ones((D_INNER,), jnp.float32), 'hy_out_w': jax.random.normal(ks[7], (D_INNER, D_INNER), jnp.float32) * s, 'out_w': jax.random.normal(ks[8], (dim, D_INNER), jnp.float32) * s, 'out_b': jnp.zeros((dim,), jnp.float32)}
    _L3_ffn_all = _L3_ffn_setup()
    _L3_ffn_in = {k: v for k, v in _L3_ffn_all.items() if k in ('W_fx', 'b_fx', 'W_x', 'b_x', 'W_slice', 'b_slice', 'temperature', 'hy_in_w', 'hy_conv_w', 'hy_conv_b', 'hy_dt_bias', 'hy_A_log', 'hy_D', 'hy_fcD_w', 'hy_norm_w', 'hy_out_w', 'out_w', 'out_b')}
    del _L3_ffn_all
    return {'x': x, 'adj': adj, 'L0_gnn_W': _L0_gnn_in['W'], 'L0_gnn_conv_w': _L0_gnn_in['conv_w'], 'L0_gnn_conv_b': _L0_gnn_in['conv_b'], 'L0_ffn_gate_w': _L0_ffn_in['gate_w'], 'L0_ffn_gate_b': _L0_ffn_in['gate_b'], 'L0_ffn_w1': _L0_ffn_in['w1'], 'L0_ffn_w2': _L0_ffn_in['w2'], 'L0_ffn_w3': _L0_ffn_in['w3'], 'L1_gnn_W1': _L1_gnn_in['W1'], 'L1_gnn_b1': _L1_gnn_in['b1'], 'L1_gnn_W2': _L1_gnn_in['W2'], 'L1_gnn_b2': _L1_gnn_in['b2'], 'L1_gnn_fusion_w': _L1_gnn_in['fusion_w'], 'L1_ffn_gate_w': _L1_ffn_in['gate_w'], 'L1_ffn_gate_b': _L1_ffn_in['gate_b'], 'L1_ffn_w1': _L1_ffn_in['w1'], 'L1_ffn_b1': _L1_ffn_in['b1'], 'L1_ffn_w2': _L1_ffn_in['w2'], 'L1_ffn_b2': _L1_ffn_in['b2'], 'L2_gnn_W_ioux': _L2_gnn_in['W_ioux'], 'L2_gnn_b_ioux': _L2_gnn_in['b_ioux'], 'L2_gnn_W_iouh': _L2_gnn_in['W_iouh'], 'L2_gnn_b_iouh': _L2_gnn_in['b_iouh'], 'L2_gnn_W_coux': _L2_gnn_in['W_coux'], 'L2_gnn_b_coux': _L2_gnn_in['b_coux'], 'L2_gnn_W_couh': _L2_gnn_in['W_couh'], 'L2_gnn_b_couh': _L2_gnn_in['b_couh'], 'L2_ffn_Wg': _L2_ffn_in['Wg'], 'L2_ffn_bg': _L2_ffn_in['bg'], 'L2_ffn_W1': _L2_ffn_in['W1'], 'L2_ffn_b1': _L2_ffn_in['b1'], 'L2_ffn_W2': _L2_ffn_in['W2'], 'L2_ffn_b2': _L2_ffn_in['b2'], 'L3_gnn_W': _L3_gnn_in['W'], 'L3_gnn_a': _L3_gnn_in['a'], 'L3_gnn_gamma': _L3_gnn_in['gamma'], 'L3_gnn_beta': _L3_gnn_in['beta'], 'L3_ffn_W_fx': _L3_ffn_in['W_fx'], 'L3_ffn_b_fx': _L3_ffn_in['b_fx'], 'L3_ffn_W_x': _L3_ffn_in['W_x'], 'L3_ffn_b_x': _L3_ffn_in['b_x'], 'L3_ffn_W_slice': _L3_ffn_in['W_slice'], 'L3_ffn_b_slice': _L3_ffn_in['b_slice'], 'L3_ffn_temperature': _L3_ffn_in['temperature'], 'L3_ffn_hy_in_w': _L3_ffn_in['hy_in_w'], 'L3_ffn_hy_conv_w': _L3_ffn_in['hy_conv_w'], 'L3_ffn_hy_conv_b': _L3_ffn_in['hy_conv_b'], 'L3_ffn_hy_dt_bias': _L3_ffn_in['hy_dt_bias'], 'L3_ffn_hy_A_log': _L3_ffn_in['hy_A_log'], 'L3_ffn_hy_D': _L3_ffn_in['hy_D'], 'L3_ffn_hy_fcD_w': _L3_ffn_in['hy_fcD_w'], 'L3_ffn_hy_norm_w': _L3_ffn_in['hy_norm_w'], 'L3_ffn_hy_out_w': _L3_ffn_in['hy_out_w'], 'L3_ffn_out_w': _L3_ffn_in['out_w'], 'L3_ffn_out_b': _L3_ffn_in['out_b']}

def reference(x, adj, L0_gnn_W, L0_gnn_conv_w, L0_gnn_conv_b, L0_ffn_gate_w, L0_ffn_gate_b, L0_ffn_w1, L0_ffn_w2, L0_ffn_w3, L1_gnn_W1, L1_gnn_b1, L1_gnn_W2, L1_gnn_b2, L1_gnn_fusion_w, L1_ffn_gate_w, L1_ffn_gate_b, L1_ffn_w1, L1_ffn_b1, L1_ffn_w2, L1_ffn_b2, L2_gnn_W_ioux, L2_gnn_b_ioux, L2_gnn_W_iouh, L2_gnn_b_iouh, L2_gnn_W_coux, L2_gnn_b_coux, L2_gnn_W_couh, L2_gnn_b_couh, L2_ffn_Wg, L2_ffn_bg, L2_ffn_W1, L2_ffn_b1, L2_ffn_W2, L2_ffn_b2, L3_gnn_W, L3_gnn_a, L3_gnn_gamma, L3_gnn_beta, L3_ffn_W_fx, L3_ffn_b_fx, L3_ffn_W_x, L3_ffn_b_x, L3_ffn_W_slice, L3_ffn_b_slice, L3_ffn_temperature, L3_ffn_hy_in_w, L3_ffn_hy_conv_w, L3_ffn_hy_conv_b, L3_ffn_hy_dt_bias, L3_ffn_hy_A_log, L3_ffn_hy_D, L3_ffn_hy_fcD_w, L3_ffn_hy_norm_w, L3_ffn_hy_out_w, L3_ffn_out_w, L3_ffn_out_b):
    import jax
    import jax.numpy as jnp

    def _L0_gnn_ref(h, adj, W, conv_w, conv_b):
        import jax, jax.numpy as jnp
        import numpy as np
        K = 4
        EPS = 1e-09
        LEAKY_SLOPE = 0.2
        h_trans = jnp.einsum('bni,oi->bno', h, W)
        row_sum = adj.sum(axis=2, keepdims=True) + EPS
        adj_norm = adj / row_sum
        curr = h_trans
        out = conv_w[0] * curr
        for k in range(1, K):
            curr = jnp.einsum('bnm,bmo->bno', adj_norm, curr)
            out = out + conv_w[k] * curr
        out = out + conv_b[0]
        return jnp.where(out >= 0, out, LEAKY_SLOPE * out)

    def _L0_ffn_ref(x, gate_w, gate_b, w1, w2, w3):
        import jax, jax.numpy as jnp
        import numpy as np
        D_MODEL = 128
        N_EXPERTS = 16
        HIDDEN = 256
        SCALE = 0.02
        n_experts = w1.shape[0]
        logits = jnp.einsum('bsd,de->bse', x, gate_w) + gate_b
        probs = jax.nn.softmax(logits, axis=-1)
        top_probs, top_idx = jax.lax.top_k(probs, 2)
        top_probs = top_probs / jnp.sum(top_probs, axis=-1, keepdims=True)
        dispatch = jnp.sum(jax.nn.one_hot(top_idx, n_experts, dtype=x.dtype) * top_probs[..., None], axis=-2)
        h1 = jnp.einsum('bsd,edh->bseh', x, w1)
        h2 = jnp.einsum('bsd,edh->bseh', x, w2)
        hidden = jax.nn.silu(h1) * h2
        expert_out = jnp.einsum('bseh,eho->bseo', hidden, w3)
        return jnp.einsum('bseo,bse->bso', expert_out, dispatch)

    def _L1_gnn_ref(x, adj, W1, b1, W2, b2, fusion_w):
        import jax, jax.numpy as jnp
        import numpy as np
        GROUPS = [list(range(25)), [0, 1, 2, 3, 4, 5, 6, 7, 8], [0, 9, 10, 11, 12, 13, 14], [6, 7, 8, 12, 13, 14], [3, 4, 5, 9, 10, 11]]
        B, N, D_IN, D_HID = (4096, 25, 128, 256)

        def _graph_conv(x, adj, W, b):
            n = adj.shape[-1]
            A = adj + jnp.eye(n, dtype=adj.dtype)
            deg = jnp.sum(A, axis=-1)
            deg_safe = jnp.where(deg == 0, 1.0, deg)
            dinv = jnp.where(deg == 0, 0.0, deg_safe ** (-0.5))
            norm_adj = dinv[:, :, None] * A * dinv[:, None, :]
            support = jnp.einsum('bnd,de->bne', x, W)
            out = jnp.einsum('bnm,bme->bne', norm_adj, support) + b
            return jax.nn.relu(out)
        norm_w = jax.nn.softmax(fusion_w)
        fused = jnp.zeros_like(x)
        for g, idx_list in enumerate(GROUPS):
            idx = jnp.asarray(idx_list)
            x_g = x[:, idx, :]
            adj_g = adj[:, idx][:, :, idx]
            h = _graph_conv(x_g, adj_g, W1[g], b1[g])
            out_g = _graph_conv(h, adj_g, W2[g], b2[g])
            fused = fused.at[:, idx, :].add(norm_w[g] * out_g)
        return fused

    def _L1_ffn_ref(h, gate_w, gate_b, w1, b1, w2, b2):
        import math
        import jax, jax.numpy as jnp
        import numpy as np
        CAPACITY_FACTOR = 1.25
        B, L, D = h.shape
        E = gate_w.shape[1]
        T = B * L
        C = max(1, math.ceil(CAPACITY_FACTOR * T / E))
        x = h.reshape(T, D)
        logits = x @ gate_w + gate_b
        probs = jax.nn.softmax(logits, axis=-1)
        idx = jnp.argmax(probs, axis=-1)
        prb = jnp.take_along_axis(probs, idx[:, None], axis=1)[:, 0]
        one_hot = jax.nn.one_hot(idx, E, dtype=jnp.float32)
        pos = (jnp.cumsum(one_hot, axis=0) * one_hot).sum(-1).astype(jnp.int32) - 1
        kept = pos < C
        pos_safe = jnp.where(kept, pos, C)
        buf = jnp.zeros((E, C, D), dtype=h.dtype).at[idx, pos_safe].set(x, mode='drop')
        hmid = jax.nn.relu(jnp.einsum('ecd,edf->ecf', buf, w1) + b1[:, None, :])
        ybuf = jnp.einsum('ecf,efd->ecd', hmid, w2) + b2[:, None, :]
        pos_g = jnp.minimum(pos, C - 1)
        y_tok = ybuf[idx, pos_g] * (prb * kept)[:, None]
        y = y_tok.reshape(B, L, D)
        y = jnp.nan_to_num(y, nan=0.0, posinf=10000.0, neginf=-10000.0)
        return y

    def _L2_gnn_ref(h_e, adj, W_ioux, b_ioux, W_iouh, b_iouh, W_coux, b_coux, W_couh, b_couh):
        import jax, jax.numpy as jnp
        import numpy as np
        B, N, D = (8, 256, 128)
        n = h_e.shape[1]
        d = jnp.sum(adj, axis=-1)
        dinv = jnp.where(d != 0, 1.0 / jnp.where(d != 0, d, 1.0), 0.0)
        norm_adjT = jnp.swapaxes(adj, 1, 2) * dinv[:, :, None]

        def step(h, i):
            x = jnp.take(h_e, i, axis=1)
            row = jnp.take(norm_adjT, i, axis=1)
            x_par = jnp.einsum('bj,bjd->bd', row, h)
            iou = x @ W_ioux.T + b_ioux + x_par @ W_iouh.T + b_iouh
            r, z = jnp.split(iou, 2, axis=1)
            r, z = (jax.nn.sigmoid(r), jax.nn.sigmoid(z))
            hc = jnp.tanh(x @ W_coux.T + b_coux + x_par * r @ W_couh.T + b_couh)
            h_new = z * x_par + (1.0 - z) * hc
            h = jax.lax.dynamic_update_slice(h, h_new[:, None, :], (0, i, 0))
            return (h, None)
        h_out, _ = jax.lax.scan(step, h_e, jnp.arange(n))
        return h_out

    def _L2_ffn_ref(x, Wg, bg, W1, b1, W2, b2):
        import jax, jax.numpy as jnp
        import numpy as np
        B, S, D, H, E, K = (8, 4096, 128, 512, 8, 2)
        gate_scores = jnp.einsum('bsd,ed->bse', x, Wg) + bg
        topk_scores, topk_idx = jax.lax.top_k(gate_scores, K)
        topk_probs = jax.nn.softmax(topk_scores, axis=-1)
        combine = jnp.sum(topk_probs[..., None] * jax.nn.one_hot(topk_idx, E, dtype=x.dtype), axis=-2)
        out = jnp.zeros_like(x)
        for e in range(E):
            h = jax.nn.relu(jnp.einsum('bsd,hd->bsh', x, W1[e]) + b1[e])
            y = jnp.einsum('bsh,dh->bsd', h, W2[e]) + b2[e]
            out = out + combine[..., e:e + 1] * y
        return out

    def _L3_gnn_ref(h, adj, W, a, gamma, beta):
        import jax, jax.numpy as jnp
        import numpy as np
        ALPHA = 0.2
        EPS = 1e-05
        NEG = -9000000000000000.0
        F_out = W.shape[1]
        Wh = jnp.matmul(h, W)
        a1 = a[:F_out, 0]
        a2 = a[F_out:, 0]
        s1 = jnp.einsum('bnf,f->bn', Wh, a1)
        s2 = jnp.einsum('bnf,f->bn', Wh, a2)
        e = s1[:, :, None] + s2[:, None, :]
        e = jnp.where(e > 0, e, ALPHA * e)
        e = jnp.where(adj > 0, e, NEG)
        attention = jax.nn.softmax(e, axis=2)
        h_prime = jnp.matmul(attention, Wh)
        mu = jnp.mean(h_prime, axis=-1, keepdims=True)
        var = jnp.mean(jnp.square(h_prime - mu), axis=-1, keepdims=True)
        hn = (h_prime - mu) / jnp.sqrt(var + EPS) * gamma + beta
        return jax.nn.gelu(hn, approximate=False)

    def _L3_ffn_ref(x, W_fx, b_fx, W_x, b_x, W_slice, b_slice, temperature, hy_in_w, hy_conv_w, hy_conv_b, hy_dt_bias, hy_A_log, hy_D, hy_fcD_w, hy_norm_w, hy_out_w, out_w, out_b):
        import jax, jax.numpy as jnp
        import numpy as np
        H, P, G, NS, K = (8, 64, 64, 64, 3)
        D_INNER = H * P
        CONV_DIM = D_INNER + 2 * NS
        D_IN_PROJ = 2 * D_INNER + 2 * NS + 2 * H

        def _hydra(u, in_w, conv_w, conv_b, dt_bias, A_log, Dp, fcD_w, norm_w, out_w):
            Bt, L, _ = u.shape
            zxbcdt = u @ in_w.T
            z = zxbcdt[..., :D_INNER]
            xBC = zxbcdt[..., D_INNER:D_INNER + CONV_DIM]
            dt = zxbcdt[..., -2 * H:]
            dt = jnp.concatenate([dt[..., :H], jnp.flip(dt[..., H:], axis=1)], axis=0)
            dt = jax.nn.softplus(dt + dt_bias)
            xp = jnp.pad(xBC, ((0, 0), (K - 1, 0), (0, 0)))
            xBC = sum((xp[:, k:k + L, :] * conv_w[:, k] for k in range(K))) + conv_b
            xBC = jax.nn.silu(xBC)
            x = xBC[..., :D_INNER]
            Bm = xBC[..., D_INNER:D_INNER + NS]
            Cm = xBC[..., D_INNER + NS:]
            x_og = x
            x2 = jnp.concatenate([x, jnp.flip(x, 1)], 0).reshape(2 * Bt, L, H, P)
            B2 = jnp.concatenate([Bm, jnp.flip(Bm, 1)], 0)
            C2 = jnp.concatenate([Cm, jnp.flip(Cm, 1)], 0)
            dA = jnp.exp(dt * -jnp.exp(A_log))
            dBx = jnp.einsum('blh,bln,blhp->blhpn', dt, B2, x2)

            def step(h, inp):
                dA_t, dBx_t, C_t = inp
                h = h * dA_t[:, :, None, None] + dBx_t
                return (h, jnp.einsum('bhpn,bn->bhp', h, C_t))
            h0 = jnp.zeros((2 * Bt, H, P, NS), u.dtype)
            _, ys = jax.lax.scan(step, h0, (dA.transpose(1, 0, 2), dBx.transpose(1, 0, 2, 3, 4), C2.transpose(1, 0, 2)))
            y = ys.transpose(1, 0, 2, 3).reshape(2 * Bt, L, D_INNER)
            y_fw, y_bw = (y[:Bt], jnp.flip(y[Bt:], 1))
            y = jnp.pad(y_fw[:, :-1], ((0, 0), (1, 0), (0, 0))) + jnp.pad(y_bw[:, 1:], ((0, 0), (0, 1), (0, 0)))
            y = y + x_og * jnp.repeat(x_og @ fcD_w.T + Dp, P, axis=-1)
            yg = y * jax.nn.silu(z)
            yg = yg * jax.lax.rsqrt(jnp.mean(jnp.square(yg), -1, keepdims=True) + 1e-05) * norm_w
            return yg @ out_w.T
        B, N, _ = x.shape
        fx = (x @ W_fx.T + b_fx).reshape(B, N, H, P).transpose(0, 2, 1, 3)
        xm = (x @ W_x.T + b_x).reshape(B, N, H, P).transpose(0, 2, 1, 3)
        temp = jnp.maximum(temperature, 1e-06)
        sw = jax.nn.softmax((xm @ W_slice.T + b_slice) / temp, axis=-1)
        snorm = sw.sum(2)
        st = jnp.einsum('bhnc,bhng->bhgc', fx, sw) / (snorm + 1e-05)[..., None]
        st = st.transpose(0, 2, 1, 3).reshape(B, G, D_INNER)
        ot = _hydra(st, hy_in_w, hy_conv_w, hy_conv_b, hy_dt_bias, hy_A_log, hy_D, hy_fcD_w, hy_norm_w, hy_out_w)
        ot = ot.reshape(B, G, H, P).transpose(0, 2, 1, 3)
        out = jnp.einsum('bhgc,bhng->bhnc', ot, sw).transpose(0, 2, 1, 3).reshape(B, N, D_INNER)
        return out @ out_w.T + out_b
    x = x + _L0_gnn_ref(_layernorm(x, axis=-1), adj, L0_gnn_W, L0_gnn_conv_w, L0_gnn_conv_b)
    x = x + _L0_ffn_ref(_layernorm(x, axis=-1), L0_ffn_gate_w, L0_ffn_gate_b, L0_ffn_w1, L0_ffn_w2, L0_ffn_w3)
    x = x + _L1_gnn_ref(_layernorm(x, axis=-1), adj, L1_gnn_W1, L1_gnn_b1, L1_gnn_W2, L1_gnn_b2, L1_gnn_fusion_w)
    x = x + _L1_ffn_ref(_layernorm(x, axis=-1), L1_ffn_gate_w, L1_ffn_gate_b, L1_ffn_w1, L1_ffn_b1, L1_ffn_w2, L1_ffn_b2)
    x = x + _L2_gnn_ref(_layernorm(x, axis=-1), adj, L2_gnn_W_ioux, L2_gnn_b_ioux, L2_gnn_W_iouh, L2_gnn_b_iouh, L2_gnn_W_coux, L2_gnn_b_coux, L2_gnn_W_couh, L2_gnn_b_couh)
    x = x + _L2_ffn_ref(_layernorm(x, axis=-1), L2_ffn_Wg, L2_ffn_bg, L2_ffn_W1, L2_ffn_b1, L2_ffn_W2, L2_ffn_b2)
    x = x + _L3_gnn_ref(_layernorm(x, axis=-1), adj, L3_gnn_W, L3_gnn_a, L3_gnn_gamma, L3_gnn_beta)
    x = x + _L3_ffn_ref(_layernorm(x, axis=-1), L3_ffn_W_fx, L3_ffn_b_fx, L3_ffn_W_x, L3_ffn_b_x, L3_ffn_W_slice, L3_ffn_b_slice, L3_ffn_temperature, L3_ffn_hy_in_w, L3_ffn_hy_conv_w, L3_ffn_hy_conv_b, L3_ffn_hy_dt_bias, L3_ffn_hy_A_log, L3_ffn_hy_D, L3_ffn_hy_fcD_w, L3_ffn_hy_norm_w, L3_ffn_hy_out_w, L3_ffn_out_w, L3_ffn_out_b)
    return x

_drawn_inputs = setup_inputs


def setup_inputs(seed=0):
    import zlib

    import numpy as np

    out = dict(_drawn_inputs(seed))
    spreads = {'L0_ffn_gate_b': (0.0, 0.536),
     'L1_gnn_b1': (0.0, 0.538),
     'L1_gnn_b2': (0.0, 0.431),
     'L1_gnn_fusion_w': (1.0, 0.6),
     'L1_ffn_gate_b': (0.0, 0.1),
     'L1_ffn_b1': (0.0, 0.329),
     'L1_ffn_b2': (0.0, 0.1),
     'L3_gnn_gamma': (1.0, 0.2),
     'L3_gnn_beta': (0.0, 0.1),
     'L3_ffn_b_fx': (0.0, 0.1),
     'L3_ffn_b_x': (0.0, 0.8),
     'L3_ffn_b_slice': (0.0, 0.8),
     'L3_ffn_temperature': (0.5, 0.6),
     'L3_ffn_hy_conv_b': (0.0, 0.1),
     'L3_ffn_hy_dt_bias': (-4.600166320800781, 0.6),
     'L3_ffn_hy_D': (1.0, 0.6),
     'L3_ffn_hy_norm_w': (1.0, 0.6),
     'L3_ffn_out_b': (0.0, 0.1)}
    factors = {'L0_ffn_gate_w': 3.353,
     'L0_ffn_w1': 3.021,
     'L0_ffn_w2': 3.437,
     'L0_ffn_w3': 3.311,
     'L2_gnn_b_ioux': 5.223,
     'L2_gnn_W_iouh': 3.237,
     'L2_gnn_b_iouh': 4.516,
     'L2_ffn_b1': 3.149,
     'L3_ffn_W_x': 8.0,
     'L3_ffn_W_slice': 8.0,
     'L3_ffn_hy_conv_w': 24.898,
     'L3_ffn_hy_A_log': 64.0,
     'L3_ffn_hy_fcD_w': 37.52}
    for name, (base, spread) in spreads.items():
        noise = np.random.default_rng([zlib.crc32(name.encode()), seed]).standard_normal(out[name].shape)
        drawn = base * np.exp(spread * noise) if base else spread * noise
        out[name] = jnp.asarray(drawn.astype(out[name].dtype))
    for name, factor in factors.items():
        out[name] = (out[name] * factor).astype(out[name].dtype)
    return out
```

```python
import concourse.bass as bass
import numpy as np
from concourse import mybir
from concourse.alu_op_type import AluOpType as ALU
from contextlib import ExitStack

F32 = mybir.dt.float32
U32 = mybir.dt.uint32
U8 = mybir.dt.uint8
ACT = mybir.ActivationFunctionType
AXX = mybir.AxisListType.X
AXXY = mybir.AxisListType.XY

B, N, D = 32, 256, 128
P = 128
HALVES = N // P
TILES = B * HALVES
CREDIT = 2
LN_EPS = 1e-5


def done(n):
    return n + (1 + CREDIT)


def freed(n):
    return n + 1


def dma_done(n, per=1):
    return n * (16 * per) + 16 * per + 16 * CREDIT


class Own:

    def __init__(self, eng, sem, turn, per):
        self.eng, self.sem, self.base, self.per, self.k = eng, sem, turn * per, per, 0

    def step(self, ins):
        self.mark(ins)
        self.join()

    def mark(self, ins):
        ins.then_inc(self.sem, 1)
        self.k += 1

    def join(self):
        self.eng.wait_ge(self.sem, self.base + self.k)

    def end(self):
        assert self.k == self.per, (self.k, self.per)


class Stage:

    def __init__(self, nc, name):
        self.nc, self.name, self.sems, self.ctx = nc, name, [], ExitStack()

    def __enter__(self):
        return self

    def sb(self, name, shape, dt=F32):
        return self.ctx.enter_context(self.nc.sbuf_tensor(self.name + "_" + name, list(shape), dt))

    def ps(self, name, shape, dt=F32):
        return self.ctx.enter_context(self.nc.psum_tensor(self.name + "_" + name, list(shape), dt))

    def sem(self, name, credit=0):
        s = self.nc.alloc_semaphore(self.name + "_" + name)
        if credit:
            self.nc.sync.sem_inc(s, credit)
        self.sems.append(s)
        return s

    def block(self):
        self.nc.all_engine_barrier()
        return self.nc.Block()

    def __exit__(self, *exc):
        self.ctx.close()
        self.nc.clear_and_free_semaphores(self.sems)
        self.nc.all_engine_barrier()


class Core:
    pass


def hold(eng, sem):
    eng.sem_inc(sem, 1)

USED = ["x", "adj_t", "L0_gnn_W_t", "L0_gnn_conv_w", "L0_gnn_conv_b",
        "L0_ffn_w12", "L0_ffn_w3", "L0_ffn_gate_w", "L0_ffn_gate_b",
        "L1_ffn_w1", "L1_ffn_w2", "L1_ffn_gate_w", "L1_ffn_gate_b", "L1_ffn_b1", "L1_ffn_b2",
        "L2_ffn_W1_t", "L2_ffn_W2_t", "L2_ffn_Wg_t", "L2_ffn_bg", "L2_ffn_b1", "L2_ffn_b2",
        "L1_gnn_W1", "L1_gnn_b1", "L1_gnn_W2", "L1_gnn_b2", "L1_gnn_fusion_w", "pair_mask", "row_mask",
        "adj", "L3_gnn_W", "L3_gnn_W_t", "L3_gnn_a2", "L3_gnn_gamma", "L3_gnn_beta",
        "L2_gnn_W_ioux_t", "L2_gnn_W_iouh_t", "L2_gnn_b_ioux", "L2_gnn_b_iouh",
        "L2_gnn_W_coux_t", "L2_gnn_W_couh_t", "L2_gnn_b_coux", "L2_gnn_b_couh",
        "L3_ffn_W_x", "L3_ffn_b_x", "L3_ffn_W_fx_t", "L3_ffn_b_fx", "L3_ffn_W_slice_t", "L3_ffn_b_slice", "L3_ffn_temperature",
        "L3_ffn_hy_in_w_t", "L3_ffn_hy_conv_w", "L3_ffn_hy_conv_b", "L3_ffn_hy_dt_bias", "L3_ffn_hy_A_log", "L3_ffn_hy_D",
        "L3_ffn_hy_fcD_w_t", "L3_ffn_hy_norm_w", "L3_ffn_hy_out_w_t", "L3_ffn_out_w_t", "L3_ffn_out_b", "col_mask", "lhs_mask"]


def load_inputs(nc, core, x):
    with Stage(nc, "load") as st:
        loaded = st.sem("x_loaded")
        zeroed = st.sem("identity_zeroed")
        with st.block() as block:
            @block.sync
            def _(sp):
                sp.dma_start(core.x[:], x.rearrange("b (h p) d -> p (b h) d", p=P)).then_inc(loaded, 16)
                sp.wait_ge(loaded, 16)

            @block.gpsimd
            def _(pool):
                nc.gpsimd.memset(core.ident[:], 0.0).then_inc(zeroed, 1)
                nc.gpsimd.memset(core.ones[:], 1.0)
                pool.wait_ge(zeroed, 1)
                nc.gpsimd.affine_select(out=core.ident[:], in_=core.ident[:], compare_op=ALU.not_equal, fill=1.0,
                                        base=0, pattern=[[-1, P]], channel_multiplier=1)


def layernorm_statistics(nc, core, name, of=None):
    of = core.x if of is None else of
    with Stage(nc, name) as st:
        GROUP = 4
        parts = st.sb("parts", [P, TILES, 6])
        half_gap = st.sb("half_gap", [P, TILES])
        root = st.sb("root", [P, TILES])
        parts_done, variance, rooted, own = [st.sem(n) for n in ("parts_done", "variance_ready", "root_ready", "vector_steps")]
        with st.block() as block:
            @block.vector
            def _(dve):
                with dve.Fori(0, TILES // GROUP) as i:
                    for k in range(GROUP):
                        last = nc.vector.bn_stats(parts[:, i * GROUP + k, :], of[:, i * GROUP + k, :])
                    last.then_inc(parts_done, 1)
                dve.wait_ge(parts_done, TILES // GROUP)
                even, odd = parts[:, :, 0:3], parts[:, :, 3:6]
                mine = Own(dve, own, 0, 7)
                mine.step(nc.vector.tensor_tensor(core.mean[:], even[:, :, 1], odd[:, :, 1], ALU.add))
                mine.step(nc.vector.tensor_scalar(core.mean[:], core.mean[:], 0.5, None, ALU.mult))
                mine.step(nc.vector.tensor_tensor(half_gap[:], core.mean[:], odd[:, :, 1], ALU.subtract))
                mine.step(nc.vector.tensor_tensor(half_gap[:], half_gap[:], half_gap[:], ALU.mult))
                mine.step(nc.vector.tensor_tensor(root[:], even[:, :, 2], odd[:, :, 2], ALU.add))
                mine.step(nc.vector.scalar_tensor_tensor(root[:], root[:], 1.0 / D, half_gap[:], ALU.mult, ALU.add))
                mine.step(nc.vector.tensor_scalar(root[:], root[:], LN_EPS, None, ALU.add))
                nc.vector.engine_nop().then_inc(variance, 1)
                dve.wait_ge(rooted, 1)
                nc.vector.reciprocal(core.rstd[:], root[:])

            @block.scalar
            def _(act):
                act.wait_ge(variance, 1)
                nc.scalar.activation(root[:], root[:], ACT.Sqrt).then_inc(rooted, 1)


def power_graph_block(nc, core, adj_t, w_t, conv_w, conv_b):
    POWERS = 4
    SLOPE = 0.2
    with Stage(nc, "power") as st:
        w = st.sb("w", [P, D])
        coef = st.sb("coef", [P, POWERS + 1])
        a_t = [st.sb(f"a_t{s}", [P, HALVES, N]) for s in range(2)]
        y = [st.sb(f"y{s}", [P, HALVES, D]) for s in range(2)]
        y_t = [st.sb(f"y_t{s}", [P, N]) for s in range(2)]
        cur = [st.sb(f"cur{s}", [P, HALVES, D + 4]) for s in range(2)]
        acc = [st.sb(f"acc{s}", [P, HALVES, D]) for s in range(2)]
        rinv = [st.sb(f"rinv{s}", [P, HALVES]) for s in range(2)]
        ps_t = [st.ps(f"ps_t{s}", [P, 512]) for s in range(2)]
        ps_c = [[st.ps(f"ps_c{s}{h}", [P, 512]) for h in range(2)] for s in range(2)]
        weights = st.sem("weights_loaded")
        adj_loaded = [st.sem(f"adj_loaded{s}") for s in range(2)]
        y_ready, y_t_ps, y_t_ready = [st.sem(n, CREDIT) for n in ("y_ready", "y_t_transposed", "y_t_ready")]
        prod = [st.sem(f"product{k}_ready", CREDIT) for k in range(POWERS)]
        cur_ready = [st.sem(f"power{k}_ready", CREDIT) for k in range(POWERS)]
        own = st.sem("vector_steps")
        passed = st.sem("passed")
        with st.block() as block:
            @block.sync
            def _(sp):
                sp.dma_start(w[:], w_t).then_inc(weights, 16)
                sp.dma_start(coef[:, 0:POWERS], conv_w.rearrange("(a k) -> a k", a=1).to_broadcast([P, POWERS])).then_inc(weights, 16)
                sp.dma_start(coef[:, POWERS:POWERS + 1], conv_b.rearrange("(a k) -> a k", a=1).to_broadcast([P, 1])).then_inc(weights, 16)
                with sp.Fori(0, B // 2) as i:
                    for s in range(2):
                        sp.wait_ge(prod[POWERS - 1], freed(i * 2 + s))
                        sp.dma_start(a_t[s][:], adj_t[i * 2 + s, :, :].rearrange("(h p) n -> p h n", p=P)).then_inc(adj_loaded[s], 16)

            @block.tensor
            def _(pe):
                pe.wait_ge(weights, 48)
                with pe.Fori(0, B // 2) as i:
                    for s in range(2):
                        pe.wait_ge(y_t_ready, freed(i * 2 + s))
                        pe.wait_ge(y_ready, done(i * 2 + s))
                        for h in range(HALVES):
                            last = nc.tensor.transpose(ps_t[s][:, h * P:(h + 1) * P], y[s][:, h, :], core.ident[:])
                        last.then_inc(y_t_ps, 1)
                    for s in range(2):
                        pe.wait_ge(y_t_ready, done(i * 2 + s))
                        pe.wait_ge(cur_ready[POWERS - 1], freed(i * 2 + s))
                        for h in range(HALVES):
                            last = nc.tensor.matmul(ps_c[s][h][:, 0:D], y_t[s][:, h * P:(h + 1) * P], w[:], start=True, stop=True)
                        last.then_inc(prod[0], 1)
                    for k in range(1, POWERS):
                        for s in range(2):
                            if k == 1:
                                pe.wait_ge(adj_loaded[s], i * 16 + 16)
                            pe.wait_ge(cur_ready[k - 1], done(i * 2 + s))
                            width = D + 1 if k == 1 else D
                            for h in range(HALVES):
                                for m in range(HALVES):
                                    last = nc.tensor.matmul(ps_c[s][h][:, 0:width], a_t[s][:, m, h * P:(h + 1) * P],
                                                            cur[s][:, m, 0:width], start=m == 0, stop=m == HALVES - 1)
                            last.then_inc(prod[k], 1)

            @block.scalar
            def _(act):
                with act.Fori(0, B // 2) as i:
                    for s in range(2):
                        act.wait_ge(y_t_ps, done(i * 2 + s))
                        act.wait_ge(prod[0], freed(i * 2 + s))
                        nc.scalar.copy(y_t[s][:], ps_t[s][:, 0:N]).then_inc(y_t_ready, 1)

            @block.vector
            def _(dve):
                for s in range(2):
                    nc.vector.memset(cur[s][:, :, D:D + 1], 1.0)
                dve.wait_ge(weights, 48)
                with dve.Fori(0, B // 2) as i:
                    mine = Own(dve, own, i, 2 * 14)
                    for s in range(2):
                        n = i * 2 + s
                        dve.wait_ge(y_t_ps, freed(n))
                        for h in range(HALVES):
                            t = n * 2 + h
                            last = nc.vector.tensor_scalar(y[s][:, h, :], core.x[:, t, :], core.mean[:, bass.ds(t, 1)],
                                                           core.rstd[:, bass.ds(t, 1)], ALU.subtract, ALU.mult)
                        last.then_inc(y_ready, 1)
                    for k in range(POWERS):
                        for s in range(2):
                            n = i * 2 + s
                            dve.wait_ge(prod[k], done(n))
                            if k == 1:
                                for h in range(HALVES):
                                    mine.step(nc.vector.tensor_scalar(rinv[s][:, h:h + 1], ps_c[s][h][:, D:D + 1], 1e-9, None, ALU.add))
                                mine.step(nc.vector.reciprocal(rinv[s][:], rinv[s][:]))
                            for h in range(HALVES):
                                if k == 0:
                                    last = nc.vector.tensor_scalar(cur[s][:, h, 0:D], ps_c[s][h][:, 0:D], 1.0, None, ALU.mult)
                                else:
                                    last = nc.vector.tensor_scalar(cur[s][:, h, 0:D], ps_c[s][h][:, 0:D], rinv[s][:, h:h + 1], None, ALU.mult)
                            last.then_inc(cur_ready[k], 1)
                            dve.wait_ge(cur_ready[k], done(n))
                            if k == 0:
                                mine.step(nc.vector.tensor_scalar(acc[s][:], cur[s][:, :, 0:D], coef[:, 0:1],
                                                                  coef[:, POWERS:POWERS + 1], ALU.mult, ALU.add))
                            else:
                                for h in range(HALVES):
                                    mine.step(nc.vector.scalar_tensor_tensor(acc[s][:, h, :], cur[s][:, h, 0:D], coef[:, k:k + 1],
                                                                             acc[s][:, h, :], ALU.mult, ALU.add))
                    for s in range(2):
                        n = i * 2 + s
                        for h in range(HALVES):
                            mine.step(nc.vector.scalar_tensor_tensor(acc[s][:, h, :], acc[s][:, h, :], SLOPE, acc[s][:, h, :], ALU.mult, ALU.max))
                        for h in range(HALVES):
                            mine.step(nc.vector.tensor_tensor(core.x[:, n * 2 + h, :], core.x[:, n * 2 + h, :], acc[s][:, h, :], ALU.add))
                    mine.end()


UP = 512
ROWS_MAX = (2 * B * N // P + 16) * P


def prepare_tables(nc, core):
    with Stage(nc, "table") as st:
        PART = 9 * P
        zeros = st.sb("zeros", [P, PART])
        zeroed, written = st.sem("zeros_ready"), st.sem("table_written")
        pieces = ROWS_MAX * D // (P * PART)
        flat = core.sorted_in.rearrange("(a p r) d -> a p (r d)", a=pieces, p=P)
        with st.block() as block:
            @block.vector
            def _(dve):
                nc.vector.memset(zeros[:], 0.0).then_inc(zeroed, 1)

            @block.sync
            def _(sp):
                sp.wait_ge(zeroed, 1)
                for a in range(pieces):
                    sp.dma_start(flat[a, :, :], zeros[:]).then_inc(written, 16)
                sp.wait_ge(written, 16 * pieces)


def expert_block(nc, core, name, w_up, w_down, gate_w, gate_b, b_up=None, b_down=None, top=2, capacity=None, guard=False):
    E = w_up.shape[0]
    gated = b_up is None
    HC = w_down.shape[1] // P
    Q = top * TILES + E
    assert Q % 2 == 0 and Q * P <= ROWS_MAX
    with Stage(nc, name) as keep:
        expert_of = keep.sb("expert_of_tile", [1, Q], U32)
        slot = [keep.sb(f"slot{k}", [P, TILES]) for k in range(top)]
        weight = [keep.sb(f"weight{k}", [P, TILES]) for k in range(top)]
        route(nc, core, name, E, top, Q, gate_w, gate_b, capacity, expert_of, slot, weight)
        scatter_tokens(nc, core, name, top, slot)
        run_experts(nc, core, name, E, Q, HC, gated, w_up, w_down, b_up, b_down, expert_of)
        gather_tokens(nc, core, name, top, Q, slot, weight, guard)


def route(nc, core, name, E, top, Q, gate_w, gate_b, capacity, expert_of, slot, weight):
    GROUP = 4
    BIG = 1e30
    MAGIC = float(2 ** 23)
    with Stage(nc, name + "_route") as st:
        gw = st.sb("gate_w", [P, E])
        gb = st.sb("gate_b", [P, E])
        y = [st.sb(f"y{s}", [P, GROUP, D]) for s in range(2)]
        y_t = [st.sb(f"y_t{s}", [P, GROUP * P]) for s in range(2)]
        logits = st.sb("logits", [P, TILES, E])
        ps_t = [st.ps(f"ps_t{s}", [P, 512]) for s in range(2)]
        ps_l = [st.ps(f"ps_l{s}", [P, 512]) for s in range(2)]
        weights = st.sem("weights_loaded")
        y_ready, y_t_ps, y_t_ready, logits_ps, logits_ready = [st.sem(n, CREDIT) for n in (
            "y_ready", "y_t_transposed", "y_t_ready", "logits_product", "logits_ready")]
        with st.block() as block:
            @block.sync
            def _(sp):
                sp.dma_start(gw[:], gate_w).then_inc(weights, 16)
                sp.dma_start(gb[:], gate_b.rearrange("(a k) -> a k", a=1).to_broadcast([P, E])).then_inc(weights, 16)

            @block.vector
            def _(dve):
                def normalise(n, s):
                    dve.wait_ge(y_t_ps, freed(n))
                    for k in range(GROUP):
                        t = n * GROUP + k
                        last = nc.vector.tensor_scalar(y[s][:, k, :], core.x[:, t, :], core.mean[:, bass.ds(t, 1)],
                                                       core.rstd[:, bass.ds(t, 1)], ALU.subtract, ALU.mult)
                    last.then_inc(y_ready, 1)

                def keep_logits(n, s):
                    dve.wait_ge(logits_ps, done(n))
                    nc.vector.tensor_tensor(logits[:, bass.ds(n * GROUP, GROUP), :],
                                            ps_l[s][:, 0:GROUP * E].rearrange("p (t e) -> p t e", e=E),
                                            gb[:].unsqueeze(1).to_broadcast([P, GROUP, E]), ALU.add).then_inc(logits_ready, 1)

                dve.wait_ge(weights, 32)
                normalise(0, 0)
                with dve.Fori(0, TILES // GROUP // 2 - 1) as i:
                    normalise(i * 2 + 1, 1)
                    keep_logits(i * 2, 0)
                    normalise(i * 2 + 2, 0)
                    keep_logits(i * 2 + 1, 1)
                n = TILES // GROUP - 2
                normalise(n + 1, 1)
                keep_logits(n, 0)
                keep_logits(n + 1, 1)

            @block.tensor
            def _(pe):
                pe.wait_ge(weights, 32)
                with pe.Fori(0, TILES // GROUP // 2) as i:
                    for s in range(2):
                        n = i * 2 + s
                        pe.wait_ge(y_t_ready, freed(n))
                        pe.wait_ge(y_ready, done(n))
                        for k in range(GROUP):
                            last = nc.tensor.transpose(ps_t[s][:, k * P:(k + 1) * P], y[s][:, k, :], core.ident[:])
                        last.then_inc(y_t_ps, 1)
                    for s in range(2):
                        n = i * 2 + s
                        pe.wait_ge(logits_ready, freed(n))
                        pe.wait_ge(y_t_ready, done(n))
                        for k in range(GROUP):
                            last = nc.tensor.matmul(ps_l[s][:, k * E:(k + 1) * E], y_t[s][:, k * P:(k + 1) * P], gw[:], start=True, stop=True)
                        last.then_inc(logits_ps, 1)

            @block.scalar
            def _(act):
                with act.Fori(0, TILES // GROUP // 2) as i:
                    for s in range(2):
                        n = i * 2 + s
                        act.wait_ge(logits_ps, freed(n))
                        act.wait_ge(y_t_ps, done(n))
                        nc.scalar.copy(y_t[s][:], ps_t[s][:]).then_inc(y_t_ready, 1)

        with Stage(nc, name + "_rank") as rk:
            upto = rk.sb("upto", [P, P])
            chosen = [rk.sb(f"chosen{k}", [P, TILES, E]) for k in range(top)]
            any_chosen = rk.sb("any_chosen", [P, TILES, E])
            wide = [rk.sb(f"wide{k}", [P, TILES, E]) for k in range(3)]
            number_i = rk.sb("expert_number_int", [P, E], mybir.dt.int32)
            number = rk.sb("expert_number", [P, E])
            row_i = rk.sb("first_row_int", [1, Q], mybir.dt.int32)
            row = rk.sb("first_row", [1, Q])
            at_or_behind = rk.sb("at_or_behind", [1, Q, E])
            tile_expert = rk.sb("tile_expert", [1, Q])
            best = [rk.sb(f"best{k}", [P, TILES]) for k in range(2)]
            small = [rk.sb(f"small{k}", [P, TILES]) for k in range(3)]
            share = [rk.sb(f"share{k}", [P, E]) for k in range(3)]
            ps_rank = [rk.ps(f"ps_rank{j}", [P, 512]) for j in range(2)]
            ps_total = [rk.ps(f"ps_total{j}", [P, 512]) for j in range(2)]
            consts, consts_step, picked, counted, exp_in, exp_out, own = [rk.sem(n) for n in (
                "constants_ready", "constants_step", "chosen_ready", "counts_ready", "exp_input_ready", "exp_ready", "vector_steps")]
            banks = TILES * E // 512
            per_bank = 512 // E
            with rk.block() as block:
                @block.gpsimd
                def _(pool):
                    nc.gpsimd.iota(number_i[:], pattern=[[1, E]], base=0, channel_multiplier=0).then_inc(consts, 1)
                    nc.gpsimd.iota(row_i[:], pattern=[[P, Q]], base=0, channel_multiplier=0).then_inc(consts, 1)
                    nc.gpsimd.memset(upto[:], 1.0).then_inc(consts_step, 1)
                    pool.wait_ge(consts_step, 1)
                    nc.gpsimd.affine_select(out=upto[:], in_=upto[:], compare_op=ALU.is_ge, fill=0.0, base=0,
                                            pattern=[[1, P]], channel_multiplier=-1).then_inc(consts, 1)

                @block.tensor
                def _(pe):
                    pe.wait_ge(consts, 3)
                    pe.wait_ge(picked, 1)
                    for j in range(banks):
                        pick = any_chosen[:, j * per_bank:(j + 1) * per_bank, :]
                        nc.tensor.matmul(ps_rank[j][:], upto[:], pick, start=True, stop=True)
                        nc.tensor.matmul(ps_total[j][:], core.ones[:], pick, start=True, stop=True).then_inc(counted, 1)

                @block.scalar
                def _(act):
                    act.wait_ge(exp_in, 1)
                    if top == 2:
                        nc.scalar.activation(small[0][:], small[0][:], ACT.Exp).then_inc(exp_out, 1)
                    else:
                        nc.scalar.activation(wide[0][:], wide[0][:], ACT.Exp).then_inc(exp_out, 1)

                @block.vector
                def _(dve):
                    v = nc.vector
                    mine = Own(dve, own, 0, 0)
                    each = lambda a: a.unsqueeze(2).to_broadcast([P, TILES, E])
                    tokens = lambda a: a.unsqueeze(1).to_broadcast([P, TILES, E])
                    dve.wait_ge(consts, 3)
                    mine.step(v.tensor_copy(number[:], number_i[:]))
                    mine.step(v.tensor_copy(row[:], row_i[:]))
                    scores = logits
                    for k in range(top):
                        mine.step(v.tensor_reduce(best[k][:], scores[:], AXX, ALU.max))
                        mine.step(v.tensor_tensor(wide[0][:], scores[:], each(best[k][:]), ALU.is_lt))
                        mine.step(v.tensor_scalar(wide[0][:], wide[0][:], float(E), None, ALU.mult))
                        mine.step(v.tensor_tensor(wide[0][:], wide[0][:], tokens(number[:]), ALU.add))
                        mine.step(v.tensor_reduce(small[0][:], wide[0][:], AXX, ALU.min))
                        mine.step(v.tensor_tensor(chosen[k][:], tokens(number[:]), each(small[0][:]), ALU.is_equal))
                        if k + 1 < top:
                            mine.step(v.tensor_scalar(wide[1][:], chosen[k][:], -BIG, None, ALU.mult))
                            mine.step(v.tensor_tensor(wide[1][:], wide[1][:], scores[:], ALU.add))
                            scores = wide[1]
                    if top == 2:
                        mine.step(v.tensor_tensor(any_chosen[:], chosen[0][:], chosen[1][:], ALU.add))
                        mine.step(v.tensor_tensor(small[0][:], best[1][:], best[0][:], ALU.subtract))
                    else:
                        mine.step(v.tensor_copy(any_chosen[:], chosen[0][:]))
                        mine.step(v.tensor_tensor(wide[0][:], logits[:], each(best[0][:]), ALU.subtract))
                    v.engine_nop().then_inc(picked, 1)
                    v.engine_nop().then_inc(exp_in, 1)
                    dve.wait_ge(exp_out, 1)
                    if top == 2:
                        mine.step(v.tensor_scalar(small[1][:], small[0][:], 1.0, None, ALU.add))
                        mine.step(v.reciprocal(weight[0][:], small[1][:]))
                        mine.step(v.tensor_tensor(weight[1][:], weight[0][:], small[0][:], ALU.mult))
                    else:
                        mine.step(v.tensor_reduce(small[1][:], wide[0][:], AXX, ALU.add))
                        mine.step(v.reciprocal(weight[0][:], small[1][:]))
                    dve.wait_ge(counted, banks)
                    for j in range(banks):
                        mine.step(v.tensor_copy(wide[0][:, j * per_bank:(j + 1) * per_bank, :],
                                                ps_total[j][:].rearrange("p (t e) -> p t e", e=E)))
                    a, b = wide[0], wide[1]
                    gap = 1
                    while gap < TILES:
                        mine.step(v.tensor_copy(b[:, 0:gap, :], a[:, 0:gap, :]))
                        mine.step(v.tensor_tensor(b[:, gap:, :], a[:, gap:, :], a[:, :TILES - gap, :], ALU.add))
                        a, b = b, a
                        gap *= 2
                    mine.step(v.tensor_scalar(share[0][:], a[:, TILES - 1, :], float(P - 1), 1.0 / P, ALU.add, ALU.mult))
                    mine.step(v.tensor_scalar(share[0][:], share[0][:], 0.5 - 0.5 / P, None, ALU.subtract))
                    mine.step(v.tensor_scalar(share[0][:], share[0][:], MAGIC, None, ALU.add))
                    mine.step(v.tensor_scalar(share[0][:], share[0][:], MAGIC, None, ALU.subtract))
                    mine.step(v.tensor_scalar(share[0][:], share[0][:], float(P), None, ALU.mult))
                    mine.step(v.tensor_copy(share[1][:], share[0][:]))
                    c, d = share[1], share[2]
                    gap = 1
                    while gap < E:
                        mine.step(v.tensor_copy(d[:, 0:gap], c[:, 0:gap]))
                        mine.step(v.tensor_tensor(d[:, gap:], c[:, gap:], c[:, :E - gap], ALU.add))
                        c, d = d, c
                        gap *= 2
                    mine.step(v.tensor_tensor(c[:], c[:], share[0][:], ALU.subtract))
                    for j in range(banks):
                        part = slice(j * per_bank, (j + 1) * per_bank)
                        mine.step(v.tensor_tensor(wide[2][:, part, :], a[:, part, :],
                                                  ps_total[j][:].rearrange("p (t e) -> p t e", e=E), ALU.subtract))
                        mine.step(v.tensor_tensor(wide[2][:, part, :], wide[2][:, part, :],
                                                  ps_rank[j][:].rearrange("p (t e) -> p t e", e=E), ALU.add))
                    if capacity is not None:
                        mine.step(v.tensor_tensor(b[:], chosen[0][:], wide[2][:], ALU.mult))
                        mine.step(v.tensor_reduce(small[0][:], b[:], AXX, ALU.add))
                        mine.step(v.tensor_scalar(small[0][:], small[0][:], float(capacity), None, ALU.is_le))
                        mine.step(v.tensor_tensor(weight[0][:], weight[0][:], small[0][:], ALU.mult))
                    mine.step(v.tensor_tensor(wide[2][:], wide[2][:], tokens(c[:]), ALU.add))
                    for k in range(top):
                        mine.step(v.tensor_tensor(b[:], chosen[k][:], wide[2][:], ALU.mult))
                        mine.step(v.tensor_reduce(slot[k][:], b[:], AXX, ALU.add))
                        mine.step(v.tensor_scalar(slot[k][:], slot[k][:], 1.0, None, ALU.subtract))
                    mine.step(v.tensor_tensor(at_or_behind[:], row[:].unsqueeze(2).to_broadcast([1, Q, E]),
                                              c[0:1, :].unsqueeze(1).to_broadcast([1, Q, E]), ALU.is_ge))
                    mine.step(v.tensor_reduce(tile_expert[:], at_or_behind[:], AXX, ALU.add))
                    mine.step(v.tensor_scalar(expert_of[:], tile_expert[:], 1.0, None, ALU.subtract))


def scatter_tokens(nc, core, name, top, slot):
    with Stage(nc, name + "_scatter") as st:
        y = [st.sb(f"y{s}", [P, D]) for s in range(2)]
        at = [[st.sb(f"at{s}{k}", [P, 1], U32) for k in range(top)] for s in range(2)]
        ready = st.sem("rows_ready", CREDIT)
        sent = [st.sem(f"rows_sent{s}") for s in range(2)]
        passed = st.sem("pool_passed")
        with st.block() as block:
            @block.vector
            def _(dve):
                def rows(t, s):
                    nc.vector.tensor_scalar(y[s][:], core.x[:, t, :], core.mean[:, bass.ds(t, 1)],
                                            core.rstd[:, bass.ds(t, 1)], ALU.subtract, ALU.mult)
                    for k in range(top):
                        last = nc.vector.tensor_scalar(at[s][k][:], slot[k][:, bass.ds(t, 1)], 0.0, None, ALU.add)
                    last.then_inc(ready, 1)

                rows(0, 0)
                rows(1, 1)
                with dve.Fori(1, TILES // 2) as i:
                    for s in range(2):
                        dve.wait_ge(sent[s], i * (16 * top))
                        rows(i * 2 + s, s)

            @block.gpsimd
            def _(pool):
                with pool.Fori(0, TILES // 2) as i:
                    for s in range(2):
                        pool.wait_ge(ready, done(i * 2 + s))
                        hold(pool, passed)
                        for k in range(top):
                            nc.gpsimd.indirect_dma_start(core.sorted_in, bass.IndirectOffsetOnAxis(ap=at[s][k][:], axis=0),
                                                         y[s][:], None).then_inc(sent[s], 16)
                for s in range(2):
                    pool.wait_ge(sent[s], 16 * top * (TILES // 2))


def gather_tokens(nc, core, name, top, Q, slot, weight, guard):
    with Stage(nc, name + "_gather") as st:
        rows = [[st.sb(f"rows{s}{k}", [P, D]) for k in range(top)] for s in range(2)]
        at = [[st.sb(f"at{s}{k}", [P, 1], U32) for k in range(top)] for s in range(2)]
        safe = st.sb("safe", [P, D])
        zero_or_nan = st.sb("zero_or_nan", [P, D])
        mask = st.sb("mask", [P, D], U8)
        at_ready, added = [st.sem(n, CREDIT) for n in ("indices_ready", "rows_added")]
        got = [st.sem(f"rows_got{s}") for s in range(2)]
        passed = st.sem("pool_passed")
        own, passed_v = st.sem("vector_steps"), st.sem("vector_passed")
        with st.block() as block:
            @block.gpsimd
            def _(pool):
                with pool.Fori(0, TILES // 2) as i:
                    for s in range(2):
                        pool.wait_ge(added, freed(i * 2 + s))
                        pool.wait_ge(at_ready, done(i * 2 + s))
                        hold(pool, passed)
                        for k in range(top):
                            nc.gpsimd.indirect_dma_start(rows[s][k][:], None, core.sorted_out[0:Q * P, :],
                                                         bass.IndirectOffsetOnAxis(ap=at[s][k][:], axis=0)).then_inc(got[s], 16)

            @block.vector
            def _(dve):
                def indices(n, i, s):
                    if not isinstance(n, int):
                        dve.wait_ge(got[s], i * (16 * top))
                    for k in range(top):
                        last = nc.vector.tensor_scalar(at[s][k][:], slot[k][:, bass.ds(n, 1)], 0.0, None, ALU.add)
                    last.then_inc(at_ready, 1)

                def add(n, i, s):
                    dve.wait_ge(got[s], i * (16 * top) + 16 * top)
                    mine = Own(dve, own, n, 8 if guard else top - 1)
                    if guard:
                        assert top == 1
                        y = rows[s][0]
                        mine.step(nc.vector.tensor_scalar(y[:], y[:], weight[0][:, bass.ds(n, 1)], None, ALU.mult))
                        mine.step(nc.vector.memset(safe[:], 0.0))
                        mine.step(nc.vector.tensor_tensor(mask[:], y[:], y[:], ALU.is_equal))
                        hold(dve, passed_v)
                        mine.step(nc.vector.copy_predicated(safe[:], mask[:], y[:]))
                        mine.step(nc.vector.tensor_scalar(y[:], safe[:], 1e4, -1e4, ALU.min, ALU.max))
                        mine.step(nc.vector.tensor_scalar(zero_or_nan[:], safe[:], 0.0, None, ALU.mult))
                        mine.step(nc.vector.tensor_tensor(mask[:], zero_or_nan[:], zero_or_nan[:], ALU.not_equal))
                        hold(dve, passed_v)
                        mine.step(nc.vector.copy_predicated(safe[:], mask[:], y[:]))
                        nc.vector.tensor_tensor(core.x[:, n, :], core.x[:, n, :], safe[:], ALU.add).then_inc(added, 1)
                    else:
                        for k in range(top):
                            last = nc.vector.scalar_tensor_tensor(core.x[:, n, :], rows[s][k][:], weight[k][:, bass.ds(n, 1)],
                                                                  core.x[:, n, :], ALU.mult, ALU.add)
                            if k + 1 < top:
                                mine.step(last)
                        last.then_inc(added, 1)
                    mine.end()

                indices(0, 0, 0)
                indices(1, 0, 1)
                with dve.Fori(0, TILES // 2 - 1) as i:
                    for s in range(2):
                        add(i * 2 + s, i, s)
                        indices(i * 2 + s + 2, i + 1, s)
                for s in range(2):
                    add(TILES - 2 + s, TILES // 2 - 1, s)


def run_experts(nc, core, name, E, Q, HC, gated, w_up, w_down, b_up, b_down, expert_of):
    with Stage(nc, name + "_experts") as st:
        wu = st.sb("w_up", [P, E * UP])
        wd = st.sb("w_down", [P, E * HC * D])
        if not gated:
            bu = st.sb("b_up", [P, E * UP])
            bd = st.sb("b_down", [P, E * D])
        g = [st.sb(f"rows{s}", [P, D]) for s in range(2)]
        g_t = [st.sb(f"rows_t{s}", [P, P]) for s in range(2)]
        silu = [st.sb(f"silu{s}", [P, HC * P]) for s in range(2)] if gated else None
        hid = [st.sb(f"hidden{s}", [P, HC * P]) for s in range(2)]
        hid_t = [st.sb(f"hidden_t{s}", [P, HC * P]) for s in range(2)]
        o = [st.sb(f"out{s}", [P, D]) for s in range(2)]
        ps_g = [st.ps(f"ps_rows{s}", [P, 512]) for s in range(2)]
        ps_u = [st.ps(f"ps_up{s}", [P, 512]) for s in range(2)]
        ps_h = [st.ps(f"ps_hidden{s}", [P, 512]) for s in range(2)]
        ps_o = [st.ps(f"ps_out{s}", [P, 512]) for s in range(2)]
        weights = st.sem("weights_loaded")
        g_loaded = [st.sem(f"rows_loaded{s}") for s in range(2)]
        stored = [st.sem(f"out_stored{s}", 16) for s in range(2)]
        g_t_ps, g_t_ready, up_done, silu_ready, hid_ready, hid_t_ps, hid_t_ready, down_done, o_ready = [
            st.sem(n, CREDIT) for n in ("rows_transposed", "rows_t_ready", "up_done", "silu_ready", "hidden_ready",
                                        "hidden_transposed", "hidden_t_ready", "down_done", "out_ready")]
        weight_loads = 2 if gated else 4

        def turns(eng, turn):
            def straight(n):
                turn(n, n // 2, n % 2, lambda d: 0 <= n + d < Q)
            straight(0)
            straight(1)
            with eng.Fori(1, Q // 2 - 1) as i:
                for s in range(2):
                    turn(i * 2 + s, i, s, lambda d: True)
            for n in (Q - 2, Q - 1, Q):
                straight(n)

        def pair(i, s, d):
            return i + (s + d) // 2, (s + d) % 2

        with st.block() as block:
            @block.sync
            def _(sp):
                sp.dma_start(wu[:].rearrange("p (e f) -> p e f", e=E), w_up.rearrange("e d f -> d e f")).then_inc(weights, 16)
                sp.dma_start(wd[:].rearrange("p (e c f) -> p e c f", e=E, c=HC),
                             w_down.rearrange("e (c p) f -> p e c f", p=P)).then_inc(weights, 16)
                if not gated:
                    sp.dma_start(bu[:], b_up.rearrange("(a e) f -> a (e f)", a=1).to_broadcast([P, E * UP])).then_inc(weights, 16)
                    sp.dma_start(bd[:], b_down.rearrange("(a e) f -> a (e f)", a=1).to_broadcast([P, E * D])).then_inc(weights, 16)

                def load(n, i, s):
                    sp.wait_ge(g_t_ps, freed(n))
                    sp.dma_start(g[s][:], core.sorted_in[bass.ds(n * P, P), :]).then_inc(g_loaded[s], 16)

                def turn(n, i, s, inside):
                    if inside(2):
                        load(n + 2, *pair(i, s, 2))
                    if inside(-1):
                        i1, s1 = pair(i, s, -1)
                        sp.wait_ge(o_ready, done(n - 1))
                        sp.dma_start(core.sorted_out[bass.ds((n - 1) * P, P), :], o[s1][:]).then_inc(stored[s1], 16)

                load(0, 0, 0)
                load(1, 0, 1)
                turns(sp, turn)
                for s in range(2):
                    sp.wait_ge(stored[s], 16 * (Q // 2 + 1))

            @block.tensor
            def _(pe):
                def expert(n):
                    e = pe.value_load(expert_of[0:1, bass.ds(n, 1)], min_val=0, max_val=E - 1)
                    return e

                def transpose_rows(n, i, s):
                    pe.wait_ge(g_t_ready, freed(n))
                    pe.wait_ge(g_loaded[s], i * 16 + 16)
                    nc.tensor.transpose(ps_g[s][:, 0:P], g[s][:], core.ident[:]).then_inc(g_t_ps, 1)

                def up(n, i, s):
                    e = expert(n)
                    pe.wait_ge(g_t_ready, done(n))
                    pe.wait_ge(hid_ready, freed(n))
                    nc.tensor.matmul(ps_u[s][:], g_t[s][:], wu[:, bass.ds(e * UP, UP)], start=True, stop=True).then_inc(up_done, 1)

                def turn(n, i, s, inside):
                    if inside(1):
                        up(n + 1, *pair(i, s, 1))
                    if inside(0):
                        pe.wait_ge(hid_ready, done(n))
                        pe.wait_ge(hid_t_ready, freed(n))
                        for c in range(HC):
                            last = nc.tensor.transpose(ps_h[s][:, c * P:(c + 1) * P], hid[s][:, c * P:(c + 1) * P], core.ident[:])
                        last.then_inc(hid_t_ps, 1)
                    if inside(2):
                        transpose_rows(n + 2, *pair(i, s, 2))
                    if inside(-1):
                        i1, s1 = pair(i, s, -1)
                        e = expert(n - 1)
                        pe.wait_ge(hid_t_ready, done(n - 1))
                        pe.wait_ge(o_ready, freed(n - 1))
                        for c in range(HC):
                            last = nc.tensor.matmul(ps_o[s1][:, 0:D], hid_t[s1][:, c * P:(c + 1) * P],
                                                    wd[:, bass.ds(e * (HC * D) + c * D, D)], start=c == 0, stop=c == HC - 1)
                        last.then_inc(down_done, 1)

                pe.wait_ge(weights, 16 * weight_loads)
                transpose_rows(0, 0, 0)
                transpose_rows(1, 0, 1)
                up(0, 0, 0)
                turns(pe, turn)

            @block.scalar
            def _(act):
                def rows_out(n, i, s):
                    act.wait_ge(g_t_ps, done(n))
                    act.wait_ge(up_done, freed(n))
                    nc.scalar.copy(g_t[s][:], ps_g[s][:, 0:P]).then_inc(g_t_ready, 1)

                def gate(n, i, s):
                    if gated:
                        act.wait_ge(up_done, done(n))
                        act.wait_ge(hid_ready, freed(n))
                        nc.scalar.activation(silu[s][:], ps_u[s][:, 0:HC * P], ACT.Silu).then_inc(silu_ready, 1)

                def turn(n, i, s, inside):
                    if inside(1):
                        gate(n + 1, *pair(i, s, 1))
                    if inside(0):
                        act.wait_ge(hid_t_ps, done(n))
                        act.wait_ge(down_done, freed(n))
                        nc.scalar.activation(hid_t[s][:], ps_h[s][:, 0:HC * P], ACT.Copy if gated else ACT.Relu).then_inc(hid_t_ready, 1)
                    if inside(2):
                        rows_out(n + 2, *pair(i, s, 2))

                rows_out(0, 0, 0)
                rows_out(1, 0, 1)
                gate(0, 0, 0)
                turns(act, turn)

            @block.vector
            def _(dve):
                def hidden(n, i, s):
                    dve.wait_ge(hid_t_ps, freed(n))
                    if gated:
                        dve.wait_ge(silu_ready, done(n))
                        nc.vector.tensor_tensor(hid[s][:], silu[s][:], ps_u[s][:, HC * P:2 * HC * P], ALU.mult).then_inc(hid_ready, 1)
                    else:
                        e = dve.value_load(expert_of[0:1, bass.ds(n, 1)], min_val=0, max_val=E - 1)
                        dve.wait_ge(up_done, done(n))
                        nc.vector.tensor_tensor(hid[s][:], ps_u[s][:], bu[:, bass.ds(e * UP, UP)], ALU.add).then_inc(hid_ready, 1)

                def turn(n, i, s, inside):
                    if inside(1):
                        hidden(n + 1, *pair(i, s, 1))
                    if inside(-1):
                        i1, s1 = pair(i, s, -1)
                        if not gated:
                            e = dve.value_load(expert_of[0:1, bass.ds(n - 1, 1)], min_val=0, max_val=E - 1)
                        dve.wait_ge(down_done, done(n - 1))
                        dve.wait_ge(stored[s1], i1 * 16 + 16)
                        if gated:
                            nc.vector.tensor_scalar(o[s1][:], ps_o[s1][:, 0:D], 1.0, None, ALU.mult).then_inc(o_ready, 1)
                        else:
                            nc.vector.tensor_tensor(o[s1][:], ps_o[s1][:, 0:D], bd[:, bass.ds(e * D, D)], ALU.add).then_inc(o_ready, 1)

                if not gated:
                    dve.wait_ge(weights, 16 * weight_loads)
                hidden(0, 0, 0)
                turns(dve, turn)


JOINTS = 25
GROUPS = [list(range(25)), [0, 1, 2, 3, 4, 5, 6, 7, 8], [0, 9, 10, 11, 12, 13, 14], [6, 7, 8, 12, 13, 14], [3, 4, 5, 9, 10, 11]]
QUAD = 32
SHARING = P // QUAD
PACKS = B // SHARING


def group_masks():
    member = np.zeros((len(GROUPS), QUAD), np.float32)
    for g, nodes in enumerate(GROUPS):
        member[g, nodes] = 1
    pairs = np.zeros((len(GROUPS), P, P), np.float32)
    for q in range(SHARING):
        part = slice(q * QUAD, (q + 1) * QUAD)
        pairs[:, part, part] = member[:, :, None] * member[:, None, :]
    return pairs, np.ascontiguousarray(np.tile(member, (1, SHARING)).T)


def grouped_graph_block(nc, core, adj_t, w1, b1, w2, b2, fusion_w, pair_mask, row_mask):
    G, HID = len(GROUPS), w1.shape[2]
    HC = HID // P
    HALF = PACKS // 2
    with Stage(nc, "groups") as st:
        a_t = st.sb("adj_t", [P, PACKS, P])
        a_g = st.sb("group_adj_t", [P, PACKS, P])
        masks = st.sb("pair_mask", [P, G, P])
        rows = st.sb("row_mask", [P, G])
        w1_sb = st.sb("w1", [P, G * HID])
        b1_sb = st.sb("b1", [P, G * HID])
        w2_sb = st.sb("w2", [P, G * HC * D])
        b2_sb = st.sb("b2", [P, G * D])
        fuse = st.sb("fusion", [P, G])
        stat = st.sb("fusion_stat", [P, 2])
        deg = st.sb("degree", [P, PACKS])
        empty = st.sb("empty", [P, PACKS])
        dinv = st.sb("dinv", [P, PACKS])
        y = st.sb("y", [P, PACKS, D])
        ys = st.sb("y_scaled", [P, PACKS, D])
        quad0 = st.sb("quad0", [QUAD, PACKS, D])
        u_t = [st.sb(f"spread_t{h}", [P, HALF * P]) for h in range(2)]
        hid = [st.sb(f"hidden{h}", [P, HALF, HID]) for h in range(2)]
        v_t = [st.sb(f"hidden_spread_t{h}", [P, HALF * HC * P]) for h in range(2)]
        out = st.sb("out", [P, HALF, D])
        fused = st.sb("fused", [P, PACKS, D])
        ps_d = st.ps("ps_degree", [P, 512])
        ps_u = st.ps("ps_spread", [P, 512])
        ps_h = [st.ps(f"ps_hidden{j}", [P, 512]) for j in range(2)]
        ps_v = [st.ps(f"ps_hidden_spread{j}", [P, 512]) for j in range(2)]
        ps_o = st.ps("ps_out", [P, 512])
        cleared, loaded, own, fuse_in, fuse_out = [st.sem(n) for n in ("cleared", "loaded", "vector_steps", "fusion_in", "fusion_exp")]
        a_ready, deg_ps, deg_ready, root_ready, ys_ready = [st.sem(n) for n in (
            "group_adj_ready", "degree_product", "degree_ready", "root_ready", "y_scaled_ready")]
        u_ps, u_ready, h_ps, h_ready, v_ps, v_ready, o_ps = [st.sem(n) for n in (
            "spread_product", "spread_ready", "hidden_product", "hidden_ready", "hidden_spread_product", "hidden_spread_ready", "out_product")]
        with st.block() as block:
            @block.gpsimd
            def _(pool):
                nc.gpsimd.memset(a_t[:], 0.0).then_inc(cleared, 1)
                nc.gpsimd.memset(fused[:], 0.0).then_inc(cleared, 1)

            LOADS = 7 + SHARING
            BEFORE = 6 + 2 * SHARING
            OWN = 4 + 2 + 1 + 2 * 3

            @block.sync
            def _(sp):
                def row(a, n):
                    return a.rearrange("(a n) -> a n", a=1).to_broadcast([P, n])
                sp.dma_start(w1_sb[:].rearrange("p (g f) -> p g f", g=G), w1.rearrange("g d f -> d g f")).then_inc(loaded, 16)
                sp.dma_start(w2_sb[:].rearrange("p (g c f) -> p g c f", g=G, c=HC), w2.rearrange("g (c p) f -> p g c f", p=P)).then_inc(loaded, 16)
                sp.dma_start(b1_sb[:], row(b1.rearrange("g f -> (g f)"), G * HID)).then_inc(loaded, 16)
                sp.dma_start(b2_sb[:], row(b2.rearrange("g f -> (g f)"), G * D)).then_inc(loaded, 16)
                sp.dma_start(fuse[:], row(fusion_w, G)).then_inc(loaded, 16)
                sp.dma_start(masks[:], pair_mask.rearrange("g p n -> p g n")).then_inc(loaded, 16)
                sp.dma_start(rows[:], row_mask).then_inc(loaded, 16)
                sp.wait_ge(cleared, 2)
                for q in range(SHARING):
                    src = adj_t.rearrange("(k q) m n -> q m k n", q=SHARING)[q, 0:JOINTS, :, 0:JOINTS]
                    sp.dma_start(a_t[q * QUAD:q * QUAD + JOINTS, :, q * QUAD:q * QUAD + JOINTS], src).then_inc(loaded, 16)

            @block.tensor
            def _(pe):
                mm = nc.tensor.matmul
                with pe.Fori(0, G) as g:
                    pe.wait_ge(a_ready, g + 1)
                    for k in range(PACKS):
                        last = mm(ps_d[:, k:k + 1], a_g[:, k, :], core.ones[:, 0:1], start=True, stop=True)
                    last.then_inc(deg_ps, 1)
                    pe.wait_ge(ys_ready, g + 1)
                    for h in range(2):
                        if h:
                            pe.wait_ge(u_ready, g * 2 + h)
                        for k in range(HALF):
                            last = mm(ps_u[:, k * P:(k + 1) * P], ys[:, h * HALF + k, :], a_g[:, h * HALF + k, :], start=True, stop=True)
                        last.then_inc(u_ps, 1)
                    for h in range(2):
                        pe.wait_ge(u_ready, g * 2 + h + 1)
                        if h:
                            pe.wait_ge(h_ready, g * 2 + h)
                        for k in range(HALF):
                            last = mm(ps_h[k // 2][:, k % 2 * HID:(k % 2 + 1) * HID], u_t[h][:, k * P:(k + 1) * P],
                                      w1_sb[:, bass.ds(g * HID, HID)], start=True, stop=True)
                        last.then_inc(h_ps, 1)
                    for h in range(2):
                        pe.wait_ge(h_ready, g * 2 + h + 1)
                        if h:
                            pe.wait_ge(v_ready, g * 2 + h)
                        for k in range(HALF):
                            for c in range(HC):
                                last = mm(ps_v[k // 2][:, (k % 2 * HC + c) * P:(k % 2 * HC + c + 1) * P],
                                          hid[h][:, k, c * P:(c + 1) * P], a_g[:, h * HALF + k, :], start=True, stop=True)
                        last.then_inc(v_ps, 1)
                    for h in range(2):
                        pe.wait_ge(v_ready, g * 2 + h + 1)
                        if h:
                            pe.wait_ge(own, g * OWN + (BEFORE + OWN - 5))
                        for k in range(HALF):
                            for c in range(HC):
                                last = mm(ps_o[:, k * D:(k + 1) * D], v_t[h][:, (k * HC + c) * P:(k * HC + c + 1) * P],
                                          w2_sb[:, bass.ds(g * (HC * D) + c * D, D)], start=c == 0, stop=c == HC - 1)
                        last.then_inc(o_ps, 1)

            @block.scalar
            def _(act):
                act.wait_ge(fuse_in, 1)
                nc.scalar.activation(fuse[:], fuse[:], ACT.Exp).then_inc(fuse_out, 1)
                with act.Fori(0, G) as g:
                    act.wait_ge(deg_ready, g + 1)
                    nc.scalar.activation(deg[:], deg[:], ACT.Sqrt).then_inc(root_ready, 1)
                    for h in range(2):
                        act.wait_ge(u_ps, g * 2 + h + 1)
                        nc.scalar.copy(u_t[h][:], ps_u[:]).then_inc(u_ready, 1)
                    for h in range(2):
                        act.wait_ge(v_ps, g * 2 + h + 1)
                        for j in range(2):
                            last = nc.scalar.copy(v_t[h][:, j * 512:(j + 1) * 512], ps_v[j][:])
                        last.then_inc(v_ready, 1)


            @block.vector
            def _(dve):
                v = nc.vector
                dve.wait_ge(loaded, 16 * LOADS)
                pre = Own(dve, own, 0, 0)
                pre.step(v.reduce_max(stat[:, 0:1], fuse[:], AXX))
                v.tensor_scalar(fuse[:], fuse[:], stat[:, 0:1], None, ALU.subtract).then_inc(fuse_in, 1)
                dve.wait_ge(fuse_out, 1)
                pre.step(v.reduce_sum(stat[:, 1:2], fuse[:], AXX))
                pre.step(v.reciprocal(stat[:, 1:2], stat[:, 1:2]))
                pre.step(v.tensor_scalar(fuse[:], fuse[:], stat[:, 1:2], None, ALU.mult))
                pre.step(v.tensor_tensor(fuse[:], fuse[:], rows[:], ALU.mult))
                pre.step(v.tensor_tensor(a_t[:], a_t[:], core.ident[:].unsqueeze(1).to_broadcast([P, PACKS, P]), ALU.add))
                for q in range(SHARING):
                    at = slice(q * HALVES, TILES, SHARING * HALVES)
                    pre.step(v.tensor_tensor(quad0[:], core.x[0:QUAD, at, :],
                                             core.mean[0:QUAD, at].unsqueeze(2).to_broadcast([QUAD, PACKS, D]), ALU.subtract))
                    pre.step(v.tensor_tensor(y[q * QUAD:(q + 1) * QUAD, :, :], quad0[:],
                                             core.rstd[0:QUAD, at].unsqueeze(2).to_broadcast([QUAD, PACKS, D]), ALU.mult))
                base = pre.k
                assert base == BEFORE
                with dve.Fori(0, G) as g:
                    mine = Own(dve, own, g, OWN)
                    mine.base = g * OWN + base
                    v.tensor_tensor(a_g[:], a_t[:], masks[:, bass.ds(g, 1), :].to_broadcast([P, PACKS, P]), ALU.mult).then_inc(a_ready, 1)
                    dve.wait_ge(deg_ps, g + 1)
                    mine.step(v.tensor_scalar(empty[:], ps_d[:, 0:PACKS], 0.0, None, ALU.is_equal))
                    v.tensor_tensor(deg[:], ps_d[:, 0:PACKS], empty[:], ALU.add).then_inc(deg_ready, 1)
                    mine.step(v.tensor_scalar(empty[:], empty[:], -1.0, 1.0, ALU.mult, ALU.add))
                    dve.wait_ge(root_ready, g + 1)
                    mine.step(v.reciprocal(dinv[:], deg[:]))
                    mine.step(v.tensor_tensor(dinv[:], dinv[:], empty[:], ALU.mult))
                    v.tensor_tensor(ys[:], y[:], dinv[:].unsqueeze(2).to_broadcast([P, PACKS, D]), ALU.mult).then_inc(ys_ready, 1)
                    for h in range(2):
                        dve.wait_ge(h_ps, g * 2 + h + 1)
                        for k in range(HALF):
                            last = v.scalar_tensor_tensor(hid[h][:, k, :], ps_h[k // 2][:, k % 2 * HID:(k % 2 + 1) * HID],
                                                          dinv[:, h * HALF + k:h * HALF + k + 1],
                                                          b1_sb[:, bass.ds(g * HID, HID)], ALU.mult, ALU.add)
                        mine.step(last)
                        for k in range(HALF):
                            last = v.tensor_scalar(hid[h][:, k, :], hid[h][:, k, :], 0.0, dinv[:, h * HALF + k:h * HALF + k + 1], ALU.max, ALU.mult)
                        last.then_inc(h_ready, 1)
                    mine.step(v.tensor_copy(stat[:, 0:1], fuse[:, bass.ds(g, 1)]))
                    for h in range(2):
                        dve.wait_ge(o_ps, g * 2 + h + 1)
                        for k in range(HALF):
                            last = v.scalar_tensor_tensor(out[:, k, :], ps_o[:, k * D:(k + 1) * D], dinv[:, h * HALF + k:h * HALF + k + 1],
                                                          b2_sb[:, bass.ds(g * D, D)], ALU.mult, ALU.add)
                        mine.step(last)
                        mine.step(v.tensor_scalar(out[:], out[:], 0.0, stat[:, 0:1], ALU.max, ALU.mult))
                        part = fused[:, h * HALF:(h + 1) * HALF, :]
                        mine.step(v.tensor_tensor(part, part, out[:], ALU.add))
                    mine.end()
                post = Own(dve, own, 0, 0)
                post.base = base + G * OWN
                for q in range(SHARING):
                    at = slice(q * HALVES, TILES, SHARING * HALVES)
                    post.step(v.tensor_copy(quad0[:], fused[q * QUAD:(q + 1) * QUAD, :, :]))
                    post.step(v.tensor_tensor(core.x[0:QUAD, at, :], core.x[0:QUAD, at, :], quad0[:], ALU.add))


def recurrent_block(nc, core, adj, adj_t, w_ioux_t, w_iouh_t, b_ioux, b_iouh, w_coux_t, w_couh_t, b_coux, b_couh):
    S = 16
    BLOCKS = P // S
    with Stage(nc, "recur") as keep:
        adj_sb = keep.sb("adj", [P, B, HALVES, N])
        h_t = keep.sb("h_t", [P, N, B])
        h = keep.sb("h", [P, HALVES, B, D])
        with Stage(nc, "recur_in") as st:
            a_t = [st.sb(f"adj_t{s}", [P, HALVES, N]) for s in range(2)]
            y = [st.sb(f"y{s}", [P, HALVES, D]) for s in range(2)]
            empty = [st.sb(f"empty{s}", [P, N]) for s in range(2)]
            inv = [st.sb(f"inv{s}", [P, N]) for s in range(2)]
            ps_d = [st.ps(f"ps_d{s}", [P, 512]) for s in range(2)]
            ps_y = [st.ps(f"ps_y{s}", [P, 512]) for s in range(2)]
            loaded = st.sem("adj_loaded")
            t_loaded = [st.sem(f"adj_t_loaded{s}") for s in range(2)]
            y_ready, y_kept, y_ps, y_t_kept, sums_ps, scaled = [st.sem(n, CREDIT) for n in (
                "y_ready", "y_kept", "y_transposed", "y_t_kept", "sums_product", "adj_scaled")]
            own, passed = st.sem("vector_steps"), st.sem("pool_passed")
            with st.block() as block:
                @block.sync
                def _(sp):
                    for k in range(4):
                        part = slice(k * (B // 4), (k + 1) * (B // 4))
                        sp.dma_start(adj_sb[:, part, :, :], adj[part, :, :].rearrange("b (h p) n -> p b h n", p=P)).then_inc(loaded, 16)
                    with sp.Fori(0, B // 2) as i:
                        for s in range(2):
                            sp.wait_ge(sums_ps, freed(i * 2 + s))
                            sp.dma_start(a_t[s][:], adj_t[i * 2 + s, :, :].rearrange("(h p) n -> p h n", p=P)).then_inc(t_loaded[s], 16)

                @block.tensor
                def _(pe):
                    with pe.Fori(0, B // 2) as i:
                        for s in range(2):
                            n = i * 2 + s
                            pe.wait_ge(y_t_kept, freed(n))
                            pe.wait_ge(y_ready, done(n))
                            for k in range(HALVES):
                                last = nc.tensor.transpose(ps_y[s][:, k * P:(k + 1) * P], y[s][:, k, :], core.ident[:])
                            last.then_inc(y_ps, 1)
                            pe.wait_ge(scaled, freed(n))
                            pe.wait_ge(t_loaded[s], i * 16 + 16)
                            for k in range(HALVES):
                                last = nc.tensor.matmul(ps_d[s][:, 0:N], core.ones[:], a_t[s][:, k, :], start=k == 0, stop=k == HALVES - 1)
                            last.then_inc(sums_ps, 1)

                @block.gpsimd
                def _(pool):
                    with pool.Fori(0, B // 2) as i:
                        for s in range(2):
                            n = i * 2 + s
                            pool.wait_ge(y_ready, done(n))
                            hold(pool, passed)
                            nc.gpsimd.tensor_copy(h[:, :, n, :], y[s][:]).then_inc(y_kept, 1)

                @block.vector
                def _(dve):
                    v = nc.vector
                    dve.wait_ge(loaded, 64)
                    with dve.Fori(0, B // 2) as i:
                        mine = Own(dve, own, i, 2 * 4)
                        for s in range(2):
                            n = i * 2 + s
                            dve.wait_ge(y_ps, freed(n))
                            dve.wait_ge(y_kept, freed(n))
                            for k in range(HALVES):
                                t = n * 2 + k
                                last = v.tensor_scalar(y[s][:, k, :], core.x[:, t, :], core.mean[:, bass.ds(t, 1)],
                                                       core.rstd[:, bass.ds(t, 1)], ALU.subtract, ALU.mult)
                            last.then_inc(y_ready, 1)
                        for s in range(2):
                            n = i * 2 + s
                            dve.wait_ge(y_ps, done(n))
                            v.tensor_scalar(h_t[:, :, n], ps_y[s][:, 0:N], 1.0, None, ALU.mult).then_inc(y_t_kept, 1)
                            dve.wait_ge(sums_ps, done(n))
                            mine.step(v.tensor_scalar(empty[s][:], ps_d[s][:, 0:N], 0.0, None, ALU.is_equal))
                            mine.step(v.tensor_tensor(inv[s][:], ps_d[s][:, 0:N], empty[s][:], ALU.add))
                            mine.step(v.reciprocal(inv[s][:], inv[s][:]))
                            mine.step(v.scalar_tensor_tensor(inv[s][:], empty[s][:], 0.0, inv[s][:], ALU.is_equal, ALU.mult))
                            v.tensor_tensor(adj_sb[:, n, :, :], adj_sb[:, n, :, :],
                                            inv[s][:].unsqueeze(1).to_broadcast([P, HALVES, N]), ALU.mult).then_inc(scaled, 1)
                        mine.end()

        with Stage(nc, "recur_scan") as st:
            wx = st.sb("wx", [P, 3, P])
            wh = st.sb("wh", [P, 3, P])
            bias = st.sb("bias", [P, 2, 3])
            pick = st.sb("pick", [P, S])
            sums = st.sb("sums", [P, S, B])
            r, z, xr, cand, keep_part, lag, open_part, fresh, delta = [st.sb(n, [P, B]) for n in (
                "reset", "update", "reset_sum", "candidate", "kept", "kept_minus_old", "one_minus_update", "fresh", "delta")]
            near = st.sb("near", [P, B])
            far = st.sb("far", [P, S, B])
            ps_sum = st.ps("ps_sums", [P, 512])
            ps_gate = [st.ps(f"ps_gates{k}", [P, 512]) for k in range(2)]
            ps_cand = st.ps("ps_candidate", [P, 512])
            ps_coef = [st.ps(f"ps_coefs{k}", [P, 512]) for k in range(2)]
            ps_back = [st.ps(f"ps_back{k}", [P, 512]) for k in range(2)]
            loaded, own, b_ready, pick_ready, sum_ps, sum_ready, h_final = [st.sem(n) for n in (
                "loaded", "vector_steps", "bias_ready", "pick_ready", "sums_product", "sums_ready", "states_final")]
            node_sum, gates_ps, r_ready, z_ready, xr_ready, cand_ps, cand_ready, coef_ps, spread = [st.sem(n) for n in (
                "node_sum_ready", "gates_product", "reset_ready", "update_ready", "reset_sum_ready", "candidate_product",
                "candidate_ready", "coefs_spread", "later_sums_ready")]
            back_ps = st.sem("states_transposed")
            GROUPS4 = B // 4
            copied = [st.sem(f"states_copied{k}", GROUPS4 // 2) for k in range(2)]
            passed = st.sem("vector_passed")
            with st.block() as block:
                @block.sync
                def _(sp):
                    col = lambda a, n: a.rearrange("(n p) -> p n", p=P)
                    sp.dma_start(wx[:, 0:2, :], w_ioux_t.rearrange("d (g f) -> d g f", g=2)).then_inc(loaded, 16)
                    sp.dma_start(wh[:, 0:2, :], w_iouh_t.rearrange("d (g f) -> d g f", g=2)).then_inc(loaded, 16)
                    sp.dma_start(wx[:, 2, :], w_coux_t).then_inc(loaded, 16)
                    sp.dma_start(wh[:, 2, :], w_couh_t).then_inc(loaded, 16)
                    with nc.allow_non_contiguous_dma("six columns of bias"):
                        sp.dma_start(bias[:, 0, 0:2], col(b_ioux, 2)).then_inc(loaded, 16)
                        sp.dma_start(bias[:, 1, 0:2], col(b_iouh, 2)).then_inc(loaded, 16)
                        sp.dma_start(bias[:, 0, 2:3], col(b_coux, 1)).then_inc(loaded, 16)
                        sp.dma_start(bias[:, 1, 2:3], col(b_couh, 1)).then_inc(loaded, 16)

                def block_of(half, k):
                    return k + half * BLOCKS

                @block.tensor
                def _(pe):
                    def mm(out, lhs, rhs, start=False, stop=False):
                        return nc.tensor.matmul(out, lhs, rhs, start=start, stop=stop, skip_group_check=True)

                    def own_parts(node, u):
                        for g in range(2):
                            mm(ps_gate[u % 2][:, g * B:(g + 1) * B], wx[:, g, :], h_t[:, node, :], start=g == 0)

                    def coefs(half, k, node, u):
                        later = S - 1 - u
                        n = block_of(half, k) * S + u
                        if u >= 2:
                            pe.wait_ge(spread, block_of(half, k) * (S - 1) + u - 1)
                        rhs = adj_sb[:, :, half, bass.ds(node + 1, later)].rearrange("p b i -> p i b")
                        mm(ps_coef[u % 2][:, 0:later * B], pick[:, u:u + 1].to_broadcast([P, P]), rhs, start=True, stop=True).then_inc(coef_ps, 1)

                    pe.wait_ge(loaded, 128)
                    for half in range(HALVES):
                        with pe.Fori(0, BLOCKS) as k:
                            n = block_of(half, k)
                            first = n * S
                            for c in range(2):
                                pe.wait_ge(copied[c], n * (GROUPS4 // 2) + GROUPS4 // 2)
                            for b in range(B):
                                for j in range(HALVES):
                                    last = mm(ps_sum[:, b:(S - 1) * B + b + 1:B], h[:, j, b, :], adj_sb[:, b, j, bass.ds(first, S)],
                                              start=j == 0, stop=j == HALVES - 1)
                            last.then_inc(sum_ps, 1)
                            pe.wait_ge(pick_ready, n + 1)
                            own_parts(first, 0)
                            coefs(half, k, first, 0)
                            for u in range(S):
                                node = first + u
                                if u == 0:
                                    pe.wait_ge(sum_ready, n + 1)
                                else:
                                    pe.wait_ge(node_sum, n * (S - 1) + u)
                                for g in range(2):
                                    last = mm(ps_gate[u % 2][:, g * B:(g + 1) * B], wh[:, g, :], sums[:, u, :])
                                last.then_inc(gates_ps, 1)
                                mm(ps_cand[:, 0:B], wx[:, 2, :], h_t[:, node, :], start=True)
                                if u + 1 < S:
                                    own_parts(node + 1, u + 1)
                                pe.wait_ge(xr_ready, node + 1)
                                mm(ps_cand[:, 0:B], wh[:, 2, :], xr[:], stop=True).then_inc(cand_ps, 1)
                                if u + 1 < S - 1:
                                    coefs(half, k, node + 1, u + 1)
                            pe.wait_ge(h_final, n + 1)
                            for q in range(GROUPS4):
                                pe.wait_ge(copied[q % 2], n * (GROUPS4 // 2) + GROUPS4 // 2 + q // 2)
                                for b in range(4):
                                    last = nc.tensor.transpose(ps_back[q % 2][:, b * D:(b + 1) * D], h_t[:, half * P:(half + 1) * P, q * 4 + b], core.ident[:])
                                last.then_inc(back_ps, 1)

                @block.scalar
                def _(act):
                    a = nc.scalar.activation
                    act.wait_ge(b_ready, 1)
                    for half in range(HALVES):
                        with act.Fori(0, BLOCKS) as k:
                            n = block_of(half, k)
                            act.wait_ge(sum_ps, n + 1)
                            nc.scalar.copy(sums[:].rearrange("p i b -> p (i b)"), ps_sum[:]).then_inc(sum_ready, 1)
                            for u in range(S):
                                t = n * S + u
                                ps = ps_gate[u % 2]
                                act.wait_ge(gates_ps, t + 1)
                                a(r[:], ps[:, 0:B], ACT.Sigmoid, bias=bias[:, 0, 0:1]).then_inc(r_ready, 1)
                                a(z[:], ps[:, B:2 * B], ACT.Sigmoid, bias=bias[:, 0, 1:2]).then_inc(z_ready, 1)
                                act.wait_ge(cand_ps, t + 1)
                                a(cand[:], ps_cand[:, 0:B], ACT.Tanh, bias=bias[:, 0, 2:3]).then_inc(cand_ready, 1)
                            for q in range(0, GROUPS4, 2):
                                act.wait_ge(back_ps, n * GROUPS4 + q + 1)
                                nc.scalar.copy(h[:, half, q * 4:q * 4 + 4, :], ps_back[0][:].rearrange("p (b d) -> p b d", b=4)).then_inc(copied[0], 1)

                @block.vector
                def _(dve):
                    v = nc.vector
                    dve.wait_ge(loaded, 128)
                    v.tensor_tensor(bias[:, 0, :], bias[:, 0, :], bias[:, 1, :], ALU.add).then_inc(b_ready, 1)
                    per = S * 5 + (S - 1) * 1 + (S - 2) * 1
                    for half in range(HALVES):
                        with dve.Fori(0, BLOCKS) as k:
                            n = block_of(half, k)
                            mine = Own(dve, own, n, per)
                            v.tensor_scalar(pick[:], core.ident[:, bass.ds(k * S, S)], 1.0, None, ALU.mult).then_inc(pick_ready, 1)
                            for u in range(S):
                                t = n * S + u
                                later = S - 1 - u
                                if u == 0:
                                    dve.wait_ge(sum_ready, n + 1)
                                dve.wait_ge(r_ready, t + 1)
                                v.tensor_tensor(xr[:], sums[:, u, :], r[:], ALU.mult).then_inc(xr_ready, 1)
                                dve.wait_ge(z_ready, t + 1)
                                mine.mark(v.tensor_scalar(open_part[:], z[:], -1.0, 1.0, ALU.mult, ALU.add))
                                mine.step(v.tensor_tensor(keep_part[:], sums[:, u, :], z[:], ALU.mult))
                                mine.step(v.tensor_tensor(lag[:], keep_part[:], h_t[:, t, :], ALU.subtract))
                                dve.wait_ge(cand_ready, t + 1)
                                mine.step(v.tensor_tensor(fresh[:], open_part[:], cand[:], ALU.mult))
                                mine.step(v.tensor_tensor(delta[:], fresh[:], lag[:], ALU.add))
                                if later:
                                    dve.wait_ge(coef_ps, n * (S - 1) + u + 1)
                                    mine.step(v.tensor_tensor(near[:], ps_coef[u % 2][:, 0:B], delta[:], ALU.mult))
                                    v.tensor_tensor(sums[:, u + 1, :], sums[:, u + 1, :], near[:], ALU.add).then_inc(node_sum, 1)
                                last = v.tensor_tensor(h_t[:, t, :], fresh[:], keep_part[:], ALU.add)
                                if not later:
                                    last.then_inc(h_final, 1)
                                if later > 1:
                                    mine.step(v.tensor_tensor(far[:, u + 2:, :], ps_coef[u % 2][:, B:later * B].rearrange("p (i b) -> p i b", b=B),
                                                              delta[:].unsqueeze(1).to_broadcast([P, later - 1, B]), ALU.mult))
                                    v.tensor_tensor(sums[:, u + 2:, :], sums[:, u + 2:, :], far[:, u + 2:, :], ALU.add).then_inc(spread, 1)
                                    dve.wait_ge(spread, n * (S - 1) + u + 1)
                                elif later == 1:
                                    last.then_inc(spread, 1)
                                    dve.wait_ge(spread, n * (S - 1) + u + 1)
                            mine.end()
                            for q in range(1, GROUPS4, 2):
                                dve.wait_ge(back_ps, n * GROUPS4 + q + 1)
                                v.tensor_scalar(h[:, half, q * 4:q * 4 + 4, :], ps_back[1][:].rearrange("p (b d) -> p b d", b=4), 1.0, None, ALU.mult).then_inc(copied[1], 1)
                    for c in range(2):
                        dve.wait_ge(copied[c], 2 * BLOCKS * (GROUPS4 // 2) + GROUPS4 // 2)
                    for half in range(HALVES):
                        part = core.x[:, half::2, :]
                        v.tensor_tensor(part, part, h[:, half, :, :], ALU.add)


def attention_block(nc, core, adj, w, w_t, a2, gamma, beta):
    SLOPE = 0.2
    MASKED = -9000000000000000.0
    with Stage(nc, "attend") as keep:
        attended = keep.sb("attended", [P, TILES, D])
        with Stage(nc, "attention") as st:
            w_sb = st.sb("w", [P, D + 4])
            w_t_sb = st.sb("w_t", [P, D])
            a_sb = st.sb("a", [P, 2])
            wa2 = st.sb("wa2", [P, P])
            adj_sb = [st.sb(f"adj{s}", [P, HALVES, N]) for s in range(2)]
            allow = [st.sb(f"allow{s}", [P, HALVES, N]) for s in range(2)]
            y = [st.sb(f"y{s}", [P, HALVES, D]) for s in range(2)]
            y_t = [st.sb(f"y_t{s}", [P, N]) for s in range(2)]
            wh = [st.sb(f"wh{s}", [P, HALVES, D + 2]) for s in range(2)]
            e = [st.sb(f"e{s}", [P, HALVES, N]) for s in range(2)]
            low = [st.sb(f"minus_max{s}", [P, HALVES]) for s in range(2)]
            total = [st.sb(f"total{s}", [P, HALVES]) for s in range(2)]
            p = [st.sb(f"p{s}", [P, HALVES, N]) for s in range(2)]
            p_t = [st.sb(f"p_t{s}", [P, HALVES, N]) for s in range(2)]
            ps_y = [st.ps(f"ps_y{s}", [P, 512]) for s in range(2)]
            ps_w = [st.ps(f"ps_w{s}", [P, 512]) for s in range(2)]
            ps_s = [st.ps(f"ps_s{s}", [P, 512]) for s in range(2)]
            ps_p = [st.ps(f"ps_p{s}", [P, 512]) for s in range(2)]
            weights, wa_ps, wa_ready, own, passed = [st.sem(n) for n in ("weights_loaded", "wa_product", "wa_ready", "vector_steps", "pool_passed")]
            adj_loaded = [st.sem(f"adj_loaded{s}") for s in range(2)]
            y_ready, y_ps, y_t_ready, wh_ps, wh_ready, s2_ps, allow_ready, e_ready, p_ready, p_ps, p_t_ready, out_ps, out_ready = [
                st.sem(n, CREDIT) for n in ("y_ready", "y_transposed", "y_t_ready", "wh_product", "wh_ready", "s2_product",
                                            "allow_ready", "e_ready", "p_ready", "p_transposed", "p_t_ready", "out_product", "out_ready")]
            with st.block() as block:
                @block.sync
                def _(sp):
                    sp.dma_start(w_sb[:, 0:D], w).then_inc(weights, 16)
                    sp.dma_start(w_t_sb[:], w_t).then_inc(weights, 16)
                    sp.dma_start(a_sb[:], a2).then_inc(weights, 16)
                    with sp.Fori(0, B // 2) as i:
                        for s in range(2):
                            sp.wait_ge(allow_ready, freed(i * 2 + s))
                            sp.dma_start(adj_sb[s][:], adj[i * 2 + s, :, :].rearrange("(h p) n -> p h n", p=P)).then_inc(adj_loaded[s], 16)

                @block.gpsimd
                def _(pool):
                    with pool.Fori(0, B // 2) as i:
                        for s in range(2):
                            pool.wait_ge(adj_loaded[s], i * 16 + 16)
                            pool.wait_ge(e_ready, freed(i * 2 + s))
                            hold(pool, passed)
                            nc.gpsimd.tensor_scalar(allow[s][:], adj_sb[s][:], 0.0, -2.0 * MASKED, ALU.is_gt, ALU.mult).then_inc(allow_ready, 1)

                @block.tensor
                def _(pe):
                    mm = nc.tensor.matmul
                    pe.wait_ge(weights, 48)
                    mm(ps_w[0][:, 0:2], w_t_sb[:], a_sb[:], start=True, stop=True).then_inc(wa_ps, 1)
                    pe.wait_ge(wa_ready, 1)
                    with pe.Fori(0, B // 2) as i:
                        for s in range(2):
                            pe.wait_ge(out_ready, freed(i * 2 + s))
                            pe.wait_ge(y_ready, done(i * 2 + s))
                            for h in range(HALVES):
                                last = nc.tensor.transpose(ps_y[s][:, h * P:(h + 1) * P], y[s][:, h, :], core.ident[:])
                            last.then_inc(y_ps, 1)
                        for s in range(2):
                            pe.wait_ge(y_t_ready, done(i * 2 + s))
                            pe.wait_ge(wh_ready, freed(i * 2 + s))
                            for h in range(HALVES):
                                last = mm(ps_w[s][:, h * (D + 2):(h + 1) * (D + 2)], y_t[s][:, h * P:(h + 1) * P], w_sb[:, 0:D + 2], start=True, stop=True)
                            last.then_inc(wh_ps, 1)
                            pe.wait_ge(e_ready, freed(i * 2 + s))
                            mm(ps_s[s][:, 0:N], wa2[:], y_t[s][:], start=True, stop=True).then_inc(s2_ps, 1)
                        for s in range(2):
                            pe.wait_ge(p_ready, done(i * 2 + s))
                            pe.wait_ge(p_t_ready, freed(i * 2 + s))
                            for j in range(HALVES):
                                for h in range(HALVES):
                                    last = nc.tensor.transpose(ps_p[s][:, j * N + h * P:j * N + (h + 1) * P], p[s][:, h, j * P:(j + 1) * P], core.ident[:])
                            last.then_inc(p_ps, 1)
                        for s in range(2):
                            pe.wait_ge(p_t_ready, done(i * 2 + s))
                            for h in range(HALVES):
                                for j in range(HALVES):
                                    last = mm(ps_y[s][:, N + h * D:N + (h + 1) * D], p_t[s][:, j, h * P:(h + 1) * P], wh[s][:, j, 0:D],
                                              start=j == 0, stop=j == HALVES - 1)
                            last.then_inc(out_ps, 1)

                @block.scalar
                def _(act):
                    with act.Fori(0, B // 2) as i:
                        for s in range(2):
                            act.wait_ge(s2_ps, freed(i * 2 + s))
                            act.wait_ge(y_ps, done(i * 2 + s))
                            nc.scalar.copy(y_t[s][:], ps_y[s][:, 0:N]).then_inc(y_t_ready, 1)
                        for s in range(2):
                            act.wait_ge(out_ps, freed(i * 2 + s))
                            act.wait_ge(wh_ps, done(i * 2 + s))
                            nc.scalar.copy(wh[s][:], ps_w[s][:, 0:2 * (D + 2)].rearrange("p (h d) -> p h d", h=HALVES)).then_inc(wh_ready, 1)
                        for s in range(2):
                            act.wait_ge(p_ps, freed(i * 2 + s))
                            act.wait_ge(out_ready, freed(i * 2 + s))
                            act.wait_ge(e_ready, done(i * 2 + s))
                            for h in range(HALVES):
                                last = nc.scalar.activation(p[s][:, h, :], e[s][:, h, :], ACT.Exp, bias=low[s][:, h:h + 1], accum_out=total[s][:, h:h + 1])
                            last.then_inc(p_ready, 1)
                        for s in range(2):
                            act.wait_ge(out_ps, freed(i * 2 + s))
                            act.wait_ge(p_ps, done(i * 2 + s))
                            nc.scalar.copy(p_t[s][:], ps_p[s][:].rearrange("p (h n) -> p h n", h=HALVES)).then_inc(p_t_ready, 1)

                @block.vector
                def _(dve):
                    v = nc.vector
                    dve.wait_ge(wa_ps, 1)
                    pre = Own(dve, own, 0, 0)
                    pre.step(v.tensor_copy(w_sb[:, D:D + 2], ps_w[0][:, 0:2]))
                    v.tensor_copy(wa2[:], w_sb[:, D + 1:D + 2].to_broadcast([P, P])).then_inc(wa_ready, 1)
                    with dve.Fori(0, B // 2) as i:
                        mine = Own(dve, own, i, 2 * (4 + 1))
                        mine.base = i * mine.per + 1
                        for s in range(2):
                            n = i * 2 + s
                            dve.wait_ge(y_ps, freed(n))
                            for h in range(HALVES):
                                t = n * 2 + h
                                last = v.tensor_scalar(y[s][:, h, :], core.x[:, t, :], core.mean[:, bass.ds(t, 1)],
                                                       core.rstd[:, bass.ds(t, 1)], ALU.subtract, ALU.mult)
                            last.then_inc(y_ready, 1)
                        for s in range(2):
                            n = i * 2 + s
                            dve.wait_ge(wh_ready, done(n))
                            dve.wait_ge(s2_ps, done(n))
                            dve.wait_ge(p_ready, freed(n))
                            for h in range(HALVES):
                                last = v.tensor_scalar(e[s][:, h, :], ps_s[s][:, 0:N], wh[s][:, h, D:D + 1], None, ALU.add)
                            mine.step(last)
                            mine.step(v.scalar_tensor_tensor(e[s][:], e[s][:], SLOPE, e[s][:], ALU.mult, ALU.max))
                            dve.wait_ge(allow_ready, done(n))
                            mine.step(v.scalar_tensor_tensor(e[s][:], allow[s][:], MASKED, e[s][:], ALU.add, ALU.min))
                            mine.step(v.tensor_reduce(low[s][:], e[s][:], AXX, ALU.max))
                            v.tensor_scalar(low[s][:], low[s][:], -1.0, None, ALU.mult).then_inc(e_ready, 1)
                        for s in range(2):
                            n = i * 2 + s
                            dve.wait_ge(p_ready, done(n))
                            dve.wait_ge(out_ps, done(n))
                            mine.step(v.reciprocal(total[s][:], total[s][:]))
                            for h in range(HALVES):
                                last = v.tensor_scalar(attended[:, n * 2 + h, :], ps_y[s][:, N + h * D:N + (h + 1) * D], total[s][:, h:h + 1], None, ALU.mult)
                            last.then_inc(out_ready, 1)
                        mine.end()
        layernorm_statistics(nc, core, "norm_attended", attended)
        GROUP = 4
        with Stage(nc, "gelu") as st:
            scale = st.sb("gamma", [P, D])
            shift = st.sb("beta", [P, D])
            z = [st.sb(f"z{s}", [P, GROUP, D]) for s in range(2)]
            loaded, own, own_pool = st.sem("loaded"), st.sem("vector_steps"), st.sem("pool_steps")
            z_ready, affine_ready, gelu_ready, added = [st.sem(n, CREDIT) for n in ("z_ready", "affine_ready", "gelu_ready", "added")]
            with st.block() as block:
                @block.sync
                def _(sp):
                    sp.dma_start(scale[:], gamma.rearrange("(a n) -> a n", a=1).to_broadcast([P, D])).then_inc(loaded, 16)
                    sp.dma_start(shift[:], beta.rearrange("(a n) -> a n", a=1).to_broadcast([P, D])).then_inc(loaded, 16)

                @block.gpsimd
                def _(pool):
                    pool.wait_ge(loaded, 32)
                    with pool.Fori(0, TILES // GROUP // 2) as i:
                        for s in range(2):
                            n = i * 2 + s
                            pool.wait_ge(z_ready, done(n))
                            nc.gpsimd.tensor_tensor(z[s][:], z[s][:], scale[:].unsqueeze(1).to_broadcast([P, GROUP, D]), ALU.mult).then_inc(own_pool, 1)
                            pool.wait_ge(own_pool, n + 1)
                            nc.gpsimd.tensor_tensor(z[s][:], z[s][:], shift[:].unsqueeze(1).to_broadcast([P, GROUP, D]), ALU.add).then_inc(affine_ready, 1)

                @block.scalar
                def _(act):
                    with act.Fori(0, TILES // GROUP // 2) as i:
                        for s in range(2):
                            n = i * 2 + s
                            act.wait_ge(affine_ready, done(n))
                            nc.scalar.activation(z[s][:], z[s][:], ACT.Gelu).then_inc(gelu_ready, 1)

                @block.vector
                def _(dve):
                    with dve.Fori(0, TILES // GROUP // 2) as i:
                        for s in range(2):
                            n = i * 2 + s
                            dve.wait_ge(added, freed(n))
                            for k in range(GROUP):
                                t = n * GROUP + k
                                last = nc.vector.tensor_scalar(z[s][:, k, :], attended[:, t, :], core.mean[:, bass.ds(t, 1)],
                                                               core.rstd[:, bass.ds(t, 1)], ALU.subtract, ALU.mult)
                            last.then_inc(z_ready, 1)
                        for s in range(2):
                            n = i * 2 + s
                            dve.wait_ge(gelu_ready, done(n))
                            part = core.x[:, bass.ds(n * GROUP, GROUP), :]
                            nc.vector.tensor_tensor(part, part, z[s][:], ALU.add).then_inc(added, 1)


HEADS, HD, SLICES, NS, KC = 8, 64, 64, 64, 3
INNER = HEADS * HD
CHUNKS = INNER // P
CONV = INNER + 2 * NS
FC = CONV // P
PAIRS = B // 2
DT0 = INNER + CONV


def order_masks():
    u, t = np.arange(SLICES)[:, None], np.arange(SLICES)[None, :]
    two = lambda m: np.tile(m, (2, 1)).astype(np.float32)
    block = lambda m: np.kron(np.eye(2), m).astype(np.float32)
    return np.stack([two(u < t), two(u > t)], 1), np.stack([block(u > t), block(u < t)], 1)


def slice_block(nc, core, a):
    with Stage(nc, "slice") as keep:
        core.u_t = keep.sb("u_t", [P, CHUNKS, B * SLICES])
        make_slices(nc, core, a)
        mix_slices(nc, core, a)
        spread_slices(nc, core, a)


def make_slices(nc, core, a):
    with Stage(nc, "make") as st:
        wx = st.sb("w_x", [P, CHUNKS, D])
        bx = st.sb("b_x", [P, CHUNKS])
        ws2 = st.sb("w_slice2", [P, P])
        bs = st.sb("b_slice", [P, SLICES])
        temp = st.sb("temperature", [P, HEADS])
        wl = st.sb("w_logits", [P, INNER])
        bl = st.sb("b_logits", [P, INNER])
        wf = st.sb("w_fx", [P, INNER])
        bf = st.sb("b_fx", [P, CHUNKS])
        y = [st.sb(f"y{s}", [P, HALVES, D]) for s in range(2)]
        y_t = [st.sb(f"y_t{s}", [P, N]) for s in range(2)]
        sw = [st.sb(f"sw{s}", [P, HALVES * HEADS, SLICES]) for s in range(2)]
        top = [st.sb(f"max{s}", [P, HALVES * HEADS]) for s in range(2)]
        rinv = st.sb("rinv", [P, INNER])
        ratio = st.sb("ratio", [P, INNER])
        mean_t = [st.sb(f"mean_t{s}", [P, INNER]) for s in range(2)]
        ps_y = [st.ps(f"ps_y{s}", [P, 512]) for s in range(2)]
        ps_l = [[st.ps(f"ps_logits{s}{h}", [P, 512]) for h in range(2)] for s in range(2)]
        ps_m = st.ps("ps_mean", [P, 512])
        ps_n = st.ps("ps_norm", [P, 512])
        cleared, loaded, own, w_ps, b_ps, w_ready, passed, own_pool = [st.sem(n) for n in (
            "cleared", "loaded", "vector_steps", "w_product", "b_product", "w_ready", "pool_passed", "pool_steps")]
        y_ready, y_ps, y_t_ready, logits_ps, top_ready, low_ready, exp_ready, total_ready, sw_ready, means_ps, means_ready, u_ps, u_ready = [
            st.sem(n, CREDIT) for n in ("y_ready", "y_transposed", "y_t_ready", "logits_product", "max_ready", "shifted", "exp_ready",
                                        "total_ready", "sw_ready", "means_product", "means_ready", "slices_product", "slices_ready")]
        stored = [st.sem(f"sw_stored{s}", 16) for s in range(2)]
        with st.block() as block:
            @block.sync
            def _(sp):
                def row(v, n):
                    return v.rearrange("(a n) -> a n", a=1).to_broadcast([P, n])
                sp.dma_start(wx[:], a["L3_ffn_W_x"].rearrange("(c p) d -> p c d", p=P)).then_inc(loaded, 16)
                sp.dma_start(wf[:], a["L3_ffn_W_fx_t"]).then_inc(loaded, 16)
                sp.dma_start(bs[:], row(a["L3_ffn_b_slice"], SLICES)).then_inc(loaded, 16)
                sp.dma_start(temp[:], row(a["L3_ffn_temperature"].rearrange("a h b c -> (a h b c)"), HEADS)).then_inc(loaded, 16)
                with nc.allow_non_contiguous_dma("bias columns"):
                    sp.dma_start(bx[:], a["L3_ffn_b_x"].rearrange("(c p) -> p c", p=P)).then_inc(loaded, 16)
                    sp.dma_start(bf[:], a["L3_ffn_b_fx"].rearrange("(c p) -> p c", p=P)).then_inc(loaded, 16)
                sp.wait_ge(cleared, 1)
                for k in range(2):
                    sp.dma_start(ws2[k * HD:(k + 1) * HD, k * SLICES:(k + 1) * SLICES], a["L3_ffn_W_slice_t"]).then_inc(loaded, 16)
                with sp.Fori(0, B // 2) as i:
                    for s in range(2):
                        sp.wait_ge(sw_ready, done(i * 2 + s))
                        sp.dma_start(core.sw[i * 2 + s, :, :], sw[s][:].rearrange("p a b -> p (a b)")).then_inc(stored[s], 16)
                for s in range(2):
                    sp.wait_ge(stored[s], 16 * (B // 2 + 1))

            @block.gpsimd
            def _(pool):
                nc.gpsimd.memset(ws2[:], 0.0).then_inc(cleared, 1)
                with pool.Fori(0, B // 2) as i:
                    for s in range(2):
                        each = top[s][:].unsqueeze(2).to_broadcast([P, HALVES * HEADS, SLICES])
                        pool.wait_ge(top_ready, done(i * 2 + s))
                        nc.gpsimd.tensor_tensor(sw[s][:], sw[s][:], each, ALU.subtract).then_inc(low_ready, 1)
                    for s in range(2):
                        each = top[s][:].unsqueeze(2).to_broadcast([P, HALVES * HEADS, SLICES])
                        pool.wait_ge(total_ready, done(i * 2 + s))
                        nc.gpsimd.tensor_tensor(sw[s][:], sw[s][:], each, ALU.mult).then_inc(sw_ready, 1)

            @block.tensor
            def _(pe):
                mm = nc.tensor.matmul
                pe.wait_ge(loaded, 128)
                for c in range(CHUNKS):
                    last = mm(ps_m[:, c * P:(c + 1) * P], wx[:, c, :], ws2[:], start=True, stop=True)
                last.then_inc(w_ps, 1)
                for c in range(CHUNKS):
                    last = mm(ps_n[:, c * P:(c + 1) * P], bx[:, c:c + 1].to_broadcast([P, P]), ws2[:], start=True, stop=True)
                last.then_inc(b_ps, 1)
                pe.wait_ge(w_ready, 1)
                with pe.Fori(0, B // 2) as i:
                    for s in range(2):
                        n = i * 2 + s
                        pe.wait_ge(u_ready, freed(n))
                        pe.wait_ge(y_ready, done(n))
                        for h in range(HALVES):
                            last = nc.tensor.transpose(ps_y[s][:, h * P:(h + 1) * P], y[s][:, h, :], core.ident[:])
                        last.then_inc(y_ps, 1)
                    for s in range(2):
                        n = i * 2 + s
                        pe.wait_ge(y_t_ready, done(n))
                        pe.wait_ge(top_ready, freed(n))
                        for h in range(HALVES):
                            last = mm(ps_l[s][h][:], y_t[s][:, h * P:(h + 1) * P], wl[:], start=True, stop=True)
                        last.then_inc(logits_ps, 1)
                    for s in range(2):
                        n = i * 2 + s
                        pe.wait_ge(sw_ready, done(n))
                        pe.wait_ge(means_ready, n + CREDIT)
                        for out, lhs in ((ps_m, None), (ps_n, core.ones)):
                            for h in range(HALVES):
                                rhs = sw[s][:, h * HEADS:(h + 1) * HEADS, :]
                                last = mm(out[:], y[s][:, h, :] if lhs is None else lhs[:], rhs, start=h == 0, stop=h == HALVES - 1)
                        last.then_inc(means_ps, 1)
                        pe.wait_ge(means_ready, done(n))
                        for c in range(CHUNKS):
                            last = mm(ps_y[s][:, c * P:(c + 1) * P], wf[:, c * P:(c + 1) * P], mean_t[s][:, c * P:(c + 1) * P], start=True, stop=True)
                        last.then_inc(u_ps, 1)

            @block.scalar
            def _(act):
                with act.Fori(0, B // 2) as i:
                    for s in range(2):
                        n = i * 2 + s
                        act.wait_ge(logits_ps, freed(n))
                        act.wait_ge(y_ps, done(n))
                        nc.scalar.copy(y_t[s][:], ps_y[s][:, 0:N]).then_inc(y_t_ready, 1)
                    for s in range(2):
                        n = i * 2 + s
                        act.wait_ge(low_ready, done(n))
                        nc.scalar.activation(sw[s][:], sw[s][:], ACT.Exp).then_inc(exp_ready, 1)

            @block.vector
            def _(dve):
                v = nc.vector
                dve.wait_ge(loaded, 128)
                heads = lambda ap: ap.rearrange("p (h g) -> p h g", h=HEADS)
                pre = Own(dve, own, 0, 0)
                pre.step(v.tensor_scalar(temp[:], temp[:], 1e-6, None, ALU.max))
                pre.step(v.reciprocal(temp[:], temp[:]))
                each_head = temp[:].unsqueeze(2).to_broadcast([P, HEADS, SLICES])
                dve.wait_ge(w_ps, 1)
                pre.step(v.tensor_tensor(heads(wl[:]), heads(ps_m[:]), each_head, ALU.mult))
                dve.wait_ge(b_ps, 1)
                pre.step(v.tensor_tensor(heads(bl[:]), heads(ps_n[:]), bs[:].unsqueeze(1).to_broadcast([P, HEADS, SLICES]), ALU.add))
                v.tensor_tensor(heads(bl[:]), heads(bl[:]), each_head, ALU.mult).then_inc(w_ready, 1)
                dve.wait_ge(w_ready, 1)
                before = pre.k
                with dve.Fori(0, B // 2) as i:
                    mine = Own(dve, own, i, 2 * (1 + 1 + 3))
                    mine.base = i * mine.per + before
                    for s in range(2):
                        n = i * 2 + s
                        dve.wait_ge(means_ps, freed(n))
                        for h in range(HALVES):
                            t = n * 2 + h
                            last = v.tensor_scalar(y[s][:, h, :], core.x[:, t, :], core.mean[:, bass.ds(t, 1)],
                                                   core.rstd[:, bass.ds(t, 1)], ALU.subtract, ALU.mult)
                        last.then_inc(y_ready, 1)
                    for s in range(2):
                        n = i * 2 + s
                        dve.wait_ge(logits_ps, done(n))
                        dve.wait_ge(stored[s], i * 16 + 16)
                        for h in range(HALVES):
                            last = v.tensor_tensor(sw[s][:, h * HEADS:(h + 1) * HEADS, :], heads(ps_l[s][h][:]), heads(bl[:]), ALU.add)
                        mine.step(last)
                        v.tensor_reduce(top[s][:], sw[s][:], AXX, ALU.max).then_inc(top_ready, 1)
                    for s in range(2):
                        n = i * 2 + s
                        dve.wait_ge(exp_ready, done(n))
                        mine.step(v.tensor_reduce(top[s][:], sw[s][:], AXX, ALU.add))
                        v.reciprocal(top[s][:], top[s][:]).then_inc(total_ready, 1)
                    for s in range(2):
                        n = i * 2 + s
                        dve.wait_ge(means_ps, done(n))
                        dve.wait_ge(u_ps, freed(n))
                        mine.step(v.tensor_scalar(rinv[:], ps_n[:], 1e-5, None, ALU.add))
                        mine.step(v.reciprocal(rinv[:], rinv[:]))
                        mine.mark(v.tensor_tensor(ratio[:], ps_n[:], rinv[:], ALU.mult))
                        v.tensor_tensor(mean_t[s][:], ps_m[:], rinv[:], ALU.mult).then_inc(means_ready, 1)
                        mine.join()
                        dve.wait_ge(u_ps, done(n))
                        for c in range(CHUNKS):
                            for k in range(2):
                                part = slice(k * HD, (k + 1) * HD)
                                at = c * P + k * SLICES
                                last = v.scalar_tensor_tensor(core.u_t[part, c, bass.ds(n * SLICES, SLICES)], ratio[part, at:at + SLICES],
                                                              bf[part, c:c + 1], ps_y[s][part, at:at + SLICES], ALU.mult, ALU.add)
                        last.then_inc(u_ready, 1)
                        dve.wait_ge(u_ready, done(n))
                    mine.end()


def mix_slices(nc, core, a):
    with Stage(nc, "mix") as keep:
        z = keep.sb("z", [P, PAIRS, INNER])
        xc = keep.sb("xbc_t", [P, FC, B * SLICES])
        dt = keep.sb("dt", [P, PAIRS, 2 * HEADS])
        decay = keep.sb("decay", [P, PAIRS, 2 * HEADS])
        project_slices(nc, core, a, z, xc, dt)
        time_steps(nc, core, a, dt, decay)
        scan_slices(nc, core, a, z, xc, dt, decay)


def project_slices(nc, core, a, z, xc, dt):
    BLOCK = 512
    GRAPHS = BLOCK // SLICES
    with Stage(nc, "project") as st:
        w = st.sb("in_w", [P, CHUNKS, DT0 + 2 * HEADS])
        cw = st.sb("conv_w", [P, FC, KC])
        cb = st.sb("conv_b", [P, FC])
        dtb = st.sb("dt_bias", [P, 2 * HEADS])
        ub = [st.sb(f"u{s}", [P, CHUNKS, P]) for s in range(2)]
        xp = [st.sb(f"padded{s}", [P, GRAPHS, KC - 1 + SLICES]) for s in range(2)]
        acc = [st.sb(f"acc{s}", [P, GRAPHS, SLICES]) for s in range(2)]
        ps_x = [st.ps(f"ps_x{s}", [P, 512]) for s in range(2)]
        ps_z = [st.ps(f"ps_z{s}", [P, 512]) for s in range(2)]
        ps_d = [st.ps(f"ps_dt{s}", [P, 512]) for s in range(2)]
        loaded, cleared, own, passed_a, passed_p = [st.sem(n) for n in ("loaded", "pads_cleared", "vector_steps", "scalar_passed", "pool_passed")]
        x_ps, x_ready, conv_ready, x_kept, ub_ready, z_ps, z_kept, d_kept = [st.sem(n, CREDIT) for n in (
            "x_product", "x_padded", "conv_ready", "x_kept", "u_ready", "z_product", "z_kept", "dt_kept")]
        with st.block() as block:
            @block.sync
            def _(sp):
                sp.dma_start(w[:], a["L3_ffn_hy_in_w_t"].rearrange("(c p) f -> p c f", p=P)).then_inc(loaded, 16)
                for k in range(2):
                    sp.dma_start(dtb[:, k * HEADS:(k + 1) * HEADS], a["L3_ffn_hy_dt_bias"].rearrange("(a n) -> a n", a=1).to_broadcast([P, HEADS])).then_inc(loaded, 16)
                with nc.allow_non_contiguous_dma("columns of the convolution"):
                    sp.dma_start(cw[:], a["L3_ffn_hy_conv_w"].rearrange("(c p) k -> p c k", p=P)).then_inc(loaded, 16)
                    sp.dma_start(cb[:], a["L3_ffn_hy_conv_b"].rearrange("(c p) -> p c", p=P)).then_inc(loaded, 16)

            @block.gpsimd
            def _(pool):
                for s in range(2):
                    nc.gpsimd.memset(xp[s][:], 0.0).then_inc(cleared, 1)
                with pool.Fori(0, PAIRS // 2) as i:
                    for s in range(2):
                        m = i * 2 + s
                        pool.wait_ge(z_ps, freed(m))
                        hold(pool, passed_p)
                        nc.gpsimd.tensor_copy(ub[s][:], core.u_t[:, :, bass.ds(m * P, P)]).then_inc(ub_ready, 1)

            @block.tensor
            def _(pe):
                mm = nc.tensor.matmul
                pe.wait_ge(loaded, 80)
                with pe.Fori(0, B * SLICES // BLOCK // 2) as i:
                    for j in range(2):
                        for f in range(FC):
                            s = (j * FC + f) % 2
                            n = i * (2 * FC) + j * FC + f
                            pe.wait_ge(x_ready, freed(n))
                            for c in range(CHUNKS):
                                last = mm(ps_x[s][:], w[:, c, INNER + f * P:INNER + (f + 1) * P],
                                          core.u_t[:, c, bass.ds((i * 2 + j) * BLOCK, BLOCK)], start=c == 0, stop=c == CHUNKS - 1)
                            last.then_inc(x_ps, 1)
                        for q in range(BLOCK // P):
                            s = q % 2
                            m = (i * 2 + j) * (BLOCK // P) + q
                            pe.wait_ge(ub_ready, done(m))
                            pe.wait_ge(z_kept, freed(m))
                            pe.wait_ge(d_kept, freed(m))
                            for c in range(CHUNKS):
                                mm(ps_z[s][:], ub[s][:, c, :], w[:, c, 0:INNER], start=c == 0, stop=c == CHUNKS - 1)
                            for c in range(CHUNKS):
                                last = mm(ps_d[s][:, 0:2 * HEADS], ub[s][:, c, :], w[:, c, DT0:DT0 + 2 * HEADS], start=c == 0, stop=c == CHUNKS - 1)
                            last.then_inc(z_ps, 1)

            @block.scalar
            def _(act):
                act.wait_ge(cleared, 2)
                act.wait_ge(loaded, 80)

                def pad(n, s):
                    act.wait_ge(conv_ready, freed(n))
                    act.wait_ge(x_ps, done(n))
                    nc.scalar.copy(xp[s][:, :, KC - 1:], ps_x[s][:].rearrange("p (b g) -> p b g", b=GRAPHS)).then_inc(x_ready, 1)

                def keep_x(n, s, f, j):
                    act.wait_ge(conv_ready, done(n))
                    hold(act, passed_a)
                    nc.scalar.activation(xc[:, f, bass.ds(j * BLOCK, BLOCK)], acc[s][:].rearrange("p b g -> p (b g)"),
                                         ACT.Silu, bias=cb[:, f:f + 1]).then_inc(x_kept, 1)

                with act.Fori(0, B * SLICES // BLOCK // 2) as i:
                    for j in range(2):
                        first = i * (2 * FC) + j * FC
                        pad(first, j * FC % 2)
                        for f in range(FC):
                            s = (j * FC + f) % 2
                            if f + 1 < FC:
                                pad(first + f + 1, 1 - s)
                            keep_x(first + f, s, f, i * 2 + j)
                        for q in range(BLOCK // P):
                            m = (i * 2 + j) * (BLOCK // P) + q
                            act.wait_ge(z_ps, done(m))
                            hold(act, passed_a)
                            nc.scalar.activation(z[:, m, :], ps_z[q % 2][:], ACT.Silu).then_inc(z_kept, 1)

            @block.vector
            def _(dve):
                v = nc.vector
                dve.wait_ge(loaded, 80)
                with dve.Fori(0, B * SLICES // BLOCK // 2) as i:
                    mine = Own(dve, own, i, 2 * FC * 2)
                    for j in range(2):
                        for f in range(FC):
                            s = (j * FC + f) % 2
                            n = i * (2 * FC) + j * FC + f
                            dve.wait_ge(x_ready, done(n))
                            dve.wait_ge(x_kept, freed(n))
                            mine.step(v.tensor_scalar(acc[s][:], xp[s][:, :, 0:SLICES], cw[:, f, 0:1], None, ALU.mult))
                            mine.step(v.scalar_tensor_tensor(acc[s][:], xp[s][:, :, 1:1 + SLICES], cw[:, f, 1:2], acc[s][:], ALU.mult, ALU.add))
                            v.scalar_tensor_tensor(acc[s][:], xp[s][:, :, 2:2 + SLICES], cw[:, f, 2:3], acc[s][:], ALU.mult, ALU.add).then_inc(conv_ready, 1)
                        for q in range(BLOCK // P):
                            m = (i * 2 + j) * (BLOCK // P) + q
                            dve.wait_ge(z_ps, done(m))
                            v.tensor_tensor(dt[:, m, :], ps_d[q % 2][:, 0:2 * HEADS], dtb[:], ALU.add).then_inc(d_kept, 1)
                    mine.end()


def time_steps(nc, core, a, dt, decay):
    STEEPEST = 69.0
    with Stage(nc, "steps") as st:
        rate = st.sb("rate", [P, 2 * HEADS])
        shape = [P, PAIRS, 2 * HEADS]
        t0, t1, t2, same = [st.sb(f"t{k}", shape) for k in range(4)]
        loaded, rate_in, own, t_ready, e_ready, w_ready, l_ready = [st.sem(n) for n in (
            "loaded", "rate_clamped", "vector_steps", "minus_abs_ready", "exp_ready", "one_plus_ready", "log_ready")]
        with st.block() as block:
            @block.sync
            def _(sp):
                for k in range(2):
                    sp.dma_start(rate[:, k * HEADS:(k + 1) * HEADS], a["L3_ffn_hy_A_log"].rearrange("(a n) -> a n", a=1).to_broadcast([P, HEADS])).then_inc(loaded, 16)

            @block.scalar
            def _(act):
                act.wait_ge(rate_in, 1)
                nc.scalar.activation(rate[:], rate[:], ACT.Exp)
                act.wait_ge(t_ready, 1)
                nc.scalar.activation(t0[:], t0[:], ACT.Exp).then_inc(e_ready, 1)
                act.wait_ge(w_ready, 1)
                nc.scalar.activation(t2[:], t1[:], ACT.Ln).then_inc(l_ready, 1)

            @block.vector
            def _(dve):
                v = nc.vector
                mine = Own(dve, own, 0, 0)
                dve.wait_ge(loaded, 32)
                v.tensor_scalar(rate[:], rate[:], STEEPEST, None, ALU.min).then_inc(rate_in, 1)
                mine.step(v.tensor_scalar(t0[:], dt[:], -1.0, None, ALU.mult))
                v.tensor_tensor(t0[:], t0[:], dt[:], ALU.min).then_inc(t_ready, 1)
                dve.wait_ge(e_ready, 1)
                v.tensor_scalar(t1[:], t0[:], 1.0, None, ALU.add).then_inc(w_ready, 1)
                dve.wait_ge(w_ready, 1)
                mine.step(v.tensor_scalar(same[:], t1[:], 1.0, None, ALU.is_equal))
                dve.wait_ge(l_ready, 1)
                mine.step(v.tensor_scalar(t1[:], t1[:], 1.0, None, ALU.subtract))
                mine.step(v.tensor_tensor(t1[:], t1[:], same[:], ALU.add))
                mine.step(v.tensor_tensor(t2[:], t2[:], same[:], ALU.add))
                mine.step(v.reciprocal(t1[:], t1[:]))
                mine.step(v.tensor_tensor(t2[:], t2[:], t1[:], ALU.mult))
                mine.step(v.tensor_tensor(t2[:], t2[:], t0[:], ALU.mult))
                mine.step(v.tensor_scalar(dt[:], dt[:], 0.0, None, ALU.max))
                mine.step(v.tensor_tensor(dt[:], dt[:], t2[:], ALU.add))
                mine.step(v.tensor_scalar(rate[:], rate[:], -1.0, None, ALU.mult))
                mine.step(v.tensor_tensor(decay[:], dt[:], rate[:].unsqueeze(1).to_broadcast(shape), ALU.mult))


def scan_slices(nc, core, a, z, xc, dt, decay):
    with Stage(nc, "scan") as st:
        col_mask = st.sb("col_mask", [P, 2, SLICES])
        row_mask = st.sb("row_mask", [P, 2, P])
        fc_w = st.sb("fc_w", [P, CHUNKS, HEADS])
        dp = st.sb("d", [P, HEADS])
        nw = st.sb("norm_w", [P, CHUNKS])
        ow = st.sb("out_w", [P, CHUNKS, INNER])
        xb = [st.sb(f"xbc{s}", [P, FC, P]) for s in range(2)]
        ct = [st.sb(f"c_t{s}", [NS, P]) for s in range(2)]
        part = [[st.sb(f"decay_part{s}{k}", [P, HEADS, SLICES]) for k in range(2)] for s in range(2)]
        xs = [st.sb(f"x{s}", [P, INNER]) for s in range(2)]
        fade = [[st.sb(f"fade{s}{k}", [P, HEADS, SLICES]) for k in range(2)] for s in range(2)]
        near = st.sb("cb", [P, 2, SLICES])
        mat = [st.sb(f"matrix{s}", [P, HEADS, P]) for s in range(2)]
        fcd = st.sb("fcd", [P, HEADS])
        yg = [st.sb(f"yg{s}", [P, INNER]) for s in range(2)]
        sq = st.sb("square", [P, INNER])
        ss = [st.sb(f"sum_square{s}", [P, 1]) for s in range(2)]
        yg_t = st.sb("yg_t", [P, CHUNKS, P])
        ps_x, ps_fc, ps_cb, ps_f, ps_b, ps_y, ps_g, ps_o = [st.ps(n, [P, 512]) for n in (
            "ps_x", "ps_fc", "ps_cb", "ps_forward", "ps_backward", "ps_y", "ps_gated", "ps_out")]
        loaded, cleared, own, own_pool, own_act, passed_a, passed_p = [st.sem(n) for n in (
            "loaded", "matrix_cleared", "vector_steps", "pool_steps", "log_ready", "scalar_passed", "pool_passed")]
        in_ready, x_ps, xs_ready, fade_ready, mat_ready, y_ps, yg_ready, ss_ready, ms_ready, rms_ready, ygs_ready, g_ps, g_ready, o_ps, o_kept = [
            st.sem(n, CREDIT) for n in ("inputs_ready", "inputs_product", "x_ready", "fade_ready", "matrix_ready", "y_product", "gated_ready",
                                        "square_sum_ready", "mean_square_ready", "rms_ready", "normed_ready", "gated_transposed",
                                        "gated_t_ready", "out_product", "out_kept")]
        with st.block() as block:
            @block.sync
            def _(sp):
                sp.dma_start(col_mask[:], a["col_mask"]).then_inc(loaded, 16)
                sp.dma_start(row_mask[:], a["lhs_mask"]).then_inc(loaded, 16)
                sp.dma_start(fc_w[:], a["L3_ffn_hy_fcD_w_t"].rearrange("(c p) h -> p c h", p=P)).then_inc(loaded, 16)
                sp.dma_start(dp[:], a["L3_ffn_hy_D"].rearrange("(a n) -> a n", a=1).to_broadcast([P, HEADS])).then_inc(loaded, 16)
                with nc.allow_non_contiguous_dma("weight columns"):
                    sp.dma_start(nw[:], a["L3_ffn_hy_norm_w"].rearrange("(c p) -> p c", p=P)).then_inc(loaded, 16)
                sp.dma_start(ow[:], a["L3_ffn_hy_out_w_t"].rearrange("(c p) f -> p c f", p=P)).then_inc(loaded, 16)

            @block.gpsimd
            def _(pool):
                g = nc.gpsimd
                for s in range(2):
                    g.memset(mat[s][:], 0.0).then_inc(cleared, 1)
                g.memset(near[:], 0.0).then_inc(cleared, 1)
                pool.wait_ge(loaded, 96)
                with pool.Fori(0, PAIRS // 2) as i:
                    for s in range(2):
                        m = i * 2 + s
                        pool.wait_ge(x_ps, freed(m))
                        hold(pool, passed_p)
                        g.tensor_copy(xb[s][:], xc[:, :, bass.ds(m * P, P)]).then_inc(own_pool, 1)
                        for k in range(2):
                            g.tensor_tensor(part[s][k][:], decay[:, m, k * HEADS:(k + 1) * HEADS].unsqueeze(2).to_broadcast([P, HEADS, SLICES]),
                                            col_mask[:, k, :].unsqueeze(1).to_broadcast([P, HEADS, SLICES]), ALU.mult).then_inc(own_pool, 1)
                        pool.wait_ge(own_pool, m * 3 + 3)
                        hold(pool, passed_p)
                        g.tensor_copy(ct[s][:], xb[s][NS:2 * NS, FC - 1, :]).then_inc(in_ready, 1)
                        pool.wait_ge(in_ready, done(m))
                        hold(pool, passed_p)

            @block.tensor
            def _(pe):
                mm = nc.tensor.matmul

                def inputs(m, s):
                    pe.wait_ge(in_ready, done(m))
                    pe.wait_ge(xs_ready, m + CREDIT)
                    pe.wait_ge(fade_ready, m + CREDIT)
                    pe.wait_ge(yg_ready, m + CREDIT)
                    for c in range(CHUNKS):
                        nc.tensor.transpose(ps_x[:, c * P:(c + 1) * P], xb[s][:, c, :], core.ident[:])
                    for c in range(CHUNKS):
                        mm(ps_fc[:, 0:HEADS], xb[s][:, c, :], fc_w[:, c, :], start=c == 0, stop=c == CHUNKS - 1)
                    mm(ps_cb[:, 0:P], xb[s][0:NS, FC - 1, :], ct[s][:], start=True, stop=True)
                    for k, out in enumerate((ps_f, ps_b)):
                        last = mm(out[:], row_mask[:, k, :], part[s][k][:], start=True, stop=True)
                    last.then_inc(x_ps, 1)

                def products(m, s):
                    pe.wait_ge(mat_ready, done(m))
                    pe.wait_ge(xs_ready, done(m))
                    for h in range(HEADS):
                        last = mm(ps_y[:, h * HD:(h + 1) * HD], mat[s][:, h, :], xs[s][:, h * HD:(h + 1) * HD], start=True, stop=True)
                    last.then_inc(y_ps, 1)

                def outputs(m, s):
                    pe.wait_ge(ygs_ready, done(m))
                    for c in range(CHUNKS):
                        last = nc.tensor.transpose(ps_g[:, c * P:(c + 1) * P], yg[s][:, c * P:(c + 1) * P], core.ident[:])
                    last.then_inc(g_ps, 1)
                    pe.wait_ge(g_ready, done(m))
                    pe.wait_ge(o_kept, m + CREDIT)
                    for f in range(CHUNKS):
                        for c in range(CHUNKS):
                            last = mm(ps_o[:, f * P:(f + 1) * P], ow[:, c, f * P:(f + 1) * P], yg_t[:, c, :], start=c == 0, stop=c == CHUNKS - 1)
                    last.then_inc(o_ps, 1)

                pe.wait_ge(loaded, 96)
                with pe.Fori(0, PAIRS // 2) as i:
                    for s in range(2):
                        inputs(i * 2 + s, s)
                        products(i * 2 + s, s)
                        outputs(i * 2 + s, s)

            @block.scalar
            def _(act):
                with act.Fori(0, PAIRS // 2) as i:
                    for s in range(2):
                        m = i * 2 + s
                        act.wait_ge(yg_ready, freed(m))
                        act.wait_ge(mat_ready, freed(m))
                        act.wait_ge(x_ps, done(m))
                        nc.scalar.copy(xs[s][:], ps_x[:]).then_inc(xs_ready, 1)
                        nc.scalar.activation(fade[s][0][:], ps_f[:].rearrange("p (h t) -> p h t", h=HEADS), ACT.Exp)
                        nc.scalar.activation(fade[s][1][:], ps_b[:].rearrange("p (h t) -> p h t", h=HEADS), ACT.Exp).then_inc(fade_ready, 1)
                        act.wait_ge(yg_ready, done(m))
                        nc.scalar.activation(sq[:], yg[s][:], ACT.Square, accum_out=ss[s][:]).then_inc(ss_ready, 1)
                        act.wait_ge(ms_ready, done(m))
                        nc.scalar.activation(ss[s][:], ss[s][:], ACT.Ln).then_inc(own_act, 1)
                        act.wait_ge(own_act, m + 1)
                        nc.scalar.activation(ss[s][:], ss[s][:], ACT.Exp, scale=-0.5).then_inc(rms_ready, 1)
                        act.wait_ge(o_ps, done(m))
                        hold(act, passed_a)
                        nc.scalar.copy(core.u_t[:, :, bass.ds(m * P, P)], ps_o[:].rearrange("p (c t) -> p c t", c=CHUNKS)).then_inc(o_kept, 1)

            @block.vector
            def _(dve):
                v = nc.vector
                per_head = lambda ap: ap.rearrange("p (h t) -> p h t", h=HEADS)
                dve.wait_ge(loaded, 96)
                dve.wait_ge(cleared, 3)
                with dve.Fori(0, PAIRS // 2) as i:
                    mine = Own(dve, own, i, 2 * (1 + 2 + 2 + 3))
                    for s in range(2):
                        m = i * 2 + s
                        dve.wait_ge(x_ps, done(m))
                        for q in range(2):
                            rows = slice(q * SLICES, (q + 1) * SLICES)
                            at = q * SLICES
                            v.tensor_tensor(near[rows, 0, 1:SLICES], ps_cb[rows, at:at + SLICES - 1], col_mask[rows, 0, 1:SLICES], ALU.mult)
                            last = v.tensor_tensor(near[rows, 1, 0:SLICES - 1], ps_cb[rows, at + 1:at + SLICES], col_mask[rows, 1, 0:SLICES - 1], ALU.mult)
                        mine.step(last)
                        dve.wait_ge(fade_ready, done(m))
                        for k in range(2):
                            last = v.tensor_tensor(fade[s][k][:], fade[s][k][:], near[:, k, :].unsqueeze(1).to_broadcast([P, HEADS, SLICES]), ALU.mult)
                            mine.mark(last)
                        mine.join()
                        for k in range(2):
                            last = v.tensor_tensor(fade[s][k][:], fade[s][k][:],
                                                   dt[:, m, k * HEADS:(k + 1) * HEADS].unsqueeze(2).to_broadcast([P, HEADS, SLICES]), ALU.mult)
                            mine.mark(last)
                        mine.join()
                        dve.wait_ge(y_ps, freed(m))
                        for q in range(2):
                            rows = slice(q * SLICES, (q + 1) * SLICES)
                            last = v.tensor_tensor(mat[s][rows, :, q * SLICES:(q + 1) * SLICES], fade[s][0][rows, :, :], fade[s][1][rows, :, :], ALU.add)
                        last.then_inc(mat_ready, 1)
                        mine.step(v.tensor_tensor(fcd[:], ps_fc[:, 0:HEADS], dp[:], ALU.add))
                        dve.wait_ge(xs_ready, done(m))
                        dve.wait_ge(g_ps, freed(m))
                        mine.step(v.tensor_tensor(per_head(yg[s][:]), per_head(xs[s][:]), fcd[:].unsqueeze(2).to_broadcast([P, HEADS, HD]), ALU.mult))
                        dve.wait_ge(y_ps, done(m))
                        mine.step(v.tensor_tensor(yg[s][:], ps_y[:], yg[s][:], ALU.add))
                        v.tensor_tensor(yg[s][:], yg[s][:], z[:, m, :], ALU.mult).then_inc(yg_ready, 1)
                        dve.wait_ge(ss_ready, done(m))
                        v.tensor_scalar(ss[s][:], ss[s][:], 1.0 / INNER, 1e-5, ALU.mult, ALU.add).then_inc(ms_ready, 1)
                        dve.wait_ge(rms_ready, done(m))
                        v.tensor_scalar(yg[s][:], yg[s][:], ss[s][:], None, ALU.mult).then_inc(ygs_ready, 1)
                        dve.wait_ge(g_ps, done(m))
                        v.tensor_tensor(yg_t[:], ps_g[:].rearrange("p (c t) -> p c t", c=CHUNKS), nw[:].unsqueeze(2).to_broadcast([P, CHUNKS, P]),
                                        ALU.mult).then_inc(g_ready, 1)
                    mine.end()


def spread_slices(nc, core, a):
    with Stage(nc, "spread") as st:
        w = st.sb("out_w", [P, CHUNKS, D])
        bias = st.sb("out_b", [P, D])
        sw = [st.sb(f"sw{s}", [P, HALVES, INNER]) for s in range(2)]
        sw_t = [[st.sb(f"sw_t{s}{h}", [P, CHUNKS, P]) for h in range(2)] for s in range(2)]
        diag = [st.sb(f"diagonal{s}", [P, CHUNKS, P]) for s in range(2)]
        vs = [st.sb(f"v{s}", [P, CHUNKS, D]) for s in range(2)]
        o = [st.sb(f"o{s}", [P, HALVES, D]) for s in range(2)]
        ps_v = [st.ps(f"ps_v{s}", [P, 512]) for s in range(2)]
        ps_s = [[st.ps(f"ps_sw{s}{h}", [P, 512]) for h in range(2)] for s in range(2)]
        ps_o = [st.ps(f"ps_o{s}", [P, 512]) for s in range(2)]
        loaded, cleared = st.sem("loaded"), st.sem("cleared")
        sw_loaded = [st.sem(f"sw_loaded{s}") for s in range(2)]
        diag_ready, v_ps, v_ready, sw_ps, sw_t_ready, o_ps, o_ready, added = [st.sem(n, CREDIT) for n in (
            "diagonal_ready", "v_product", "v_ready", "sw_transposed", "sw_t_ready", "out_product", "out_ready", "added")]
        with st.block() as block:
            @block.sync
            def _(sp):
                sp.dma_start(w[:], a["L3_ffn_out_w_t"].rearrange("(c p) f -> p c f", p=P)).then_inc(loaded, 16)
                sp.dma_start(bias[:], a["L3_ffn_out_b"].rearrange("(a n) -> a n", a=1).to_broadcast([P, D])).then_inc(loaded, 16)
                with sp.Fori(0, B // 2) as i:
                    for s in range(2):
                        n = i * 2 + s
                        sp.wait_ge(sw_ps, freed(n))
                        sp.dma_start(sw[s][:].rearrange("p h f -> p (h f)"), core.sw[n, :, :]).then_inc(sw_loaded[s], 16)

            @block.gpsimd
            def _(pool):
                for s in range(2):
                    nc.gpsimd.memset(diag[s][:], 0.0).then_inc(cleared, 1)

            @block.tensor
            def _(pe):
                mm = nc.tensor.matmul
                pe.wait_ge(loaded, 32)
                with pe.Fori(0, B // 2) as i:
                    for s in range(2):
                        n = i * 2 + s
                        pe.wait_ge(sw_loaded[s], i * 16 + 16)
                        pe.wait_ge(sw_t_ready, freed(n))
                        for h in range(HALVES):
                            for c in range(CHUNKS):
                                last = nc.tensor.transpose(ps_s[s][h][:, c * P:(c + 1) * P], sw[s][:, h, c * P:(c + 1) * P], core.ident[:])
                        last.then_inc(sw_ps, 1)
                        pe.wait_ge(diag_ready, done(n))
                        pe.wait_ge(v_ready, freed(n))
                        for c in range(CHUNKS):
                            last = mm(ps_v[s][:, c * D:(c + 1) * D], diag[s][:, c, :], w[:, c, :], start=True, stop=True)
                        last.then_inc(v_ps, 1)
                    for s in range(2):
                        n = i * 2 + s
                        pe.wait_ge(sw_t_ready, done(n))
                        pe.wait_ge(v_ready, done(n))
                        pe.wait_ge(o_ready, freed(n))
                        for h in range(HALVES):
                            for c in range(CHUNKS):
                                last = mm(ps_o[s][:, h * D:(h + 1) * D], sw_t[s][h][:, c, :], vs[s][:, c, :], start=c == 0, stop=c == CHUNKS - 1)
                        last.then_inc(o_ps, 1)

            @block.scalar
            def _(act):
                with act.Fori(0, B // 2) as i:
                    for s in range(2):
                        n = i * 2 + s
                        act.wait_ge(sw_ps, done(n))
                        act.wait_ge(o_ps, freed(n))
                        for h in range(HALVES):
                            last = nc.scalar.copy(sw_t[s][h][:], ps_s[s][h][:].rearrange("p (c n) -> p c n", c=CHUNKS))
                        last.then_inc(sw_t_ready, 1)
                        act.wait_ge(v_ps, done(n))
                        nc.scalar.copy(vs[s][:], ps_v[s][:].rearrange("p (c n) -> p c n", c=CHUNKS)).then_inc(v_ready, 1)

            @block.vector
            def _(dve):
                v = nc.vector
                dve.wait_ge(cleared, 2)
                dve.wait_ge(loaded, 32)
                with dve.Fori(0, B // 2) as i:
                    for s in range(2):
                        n = i * 2 + s
                        dve.wait_ge(v_ps, freed(n))
                        for k in range(2):
                            rows = slice(k * HD, (k + 1) * HD)
                            last = v.tensor_scalar(diag[s][rows, :, k * SLICES:(k + 1) * SLICES], core.u_t[rows, :, bass.ds(n * SLICES, SLICES)],
                                                   1.0, None, ALU.mult)
                        last.then_inc(diag_ready, 1)
                    for s in range(2):
                        n = i * 2 + s
                        dve.wait_ge(o_ps, done(n))
                        v.tensor_tensor(o[s][:], ps_o[s][:, 0:HALVES * D].rearrange("p (h d) -> p h d", h=HALVES),
                                        bias[:].unsqueeze(1).to_broadcast([P, HALVES, D]), ALU.add).then_inc(o_ready, 1)
                        dve.wait_ge(o_ready, done(n))
                        tiles = core.x[:, bass.ds(n * HALVES, HALVES), :]
                        v.tensor_tensor(tiles, tiles, o[s][:], ALU.add).then_inc(added, 1)
                        dve.wait_ge(added, done(n))


def store_output(nc, core, out):
    with Stage(nc, "store") as st:
        stored = st.sem("out_stored")
        with st.block() as block:
            @block.sync
            def _(sp):
                sp.dma_start(out.rearrange("b (h p) d -> p (b h) d", p=P), core.x[:]).then_inc(stored, 16)
                sp.wait_ge(stored, 16)


def build(nc, a, out):
    core = Core()
    with ExitStack() as ctx:
        core.x = ctx.enter_context(nc.sbuf_tensor("x", [P, TILES, D], F32))
        core.mean = ctx.enter_context(nc.sbuf_tensor("mean", [P, TILES], F32))
        core.rstd = ctx.enter_context(nc.sbuf_tensor("rstd", [P, TILES], F32))
        core.ident = ctx.enter_context(nc.sbuf_tensor("ident", [P, P], F32))
        core.ones = ctx.enter_context(nc.sbuf_tensor("ones", [P, P], F32))
        core.sorted_in = nc.dram_tensor("sorted_in", (ROWS_MAX, D), F32, kind="Internal").ap()
        core.sorted_out = nc.dram_tensor("sorted_out", (ROWS_MAX, D), F32, kind="Internal").ap()
        core.sw = nc.dram_tensor("slice_weights", (B, P, HALVES * INNER), F32, kind="Internal").ap()
        load_inputs(nc, core, a["x"])
        prepare_tables(nc, core)
        layernorm_statistics(nc, core, "norm0")
        power_graph_block(nc, core, a["adj_t"], a["L0_gnn_W_t"], a["L0_gnn_conv_w"], a["L0_gnn_conv_b"])
        layernorm_statistics(nc, core, "norm1")
        expert_block(nc, core, "glu", a["L0_ffn_w12"], a["L0_ffn_w3"], a["L0_ffn_gate_w"], a["L0_ffn_gate_b"])
        layernorm_statistics(nc, core, "norm2")
        grouped_graph_block(nc, core, a["adj_t"], a["L1_gnn_W1"], a["L1_gnn_b1"], a["L1_gnn_W2"], a["L1_gnn_b2"],
                            a["L1_gnn_fusion_w"], a["pair_mask"], a["row_mask"])
        layernorm_statistics(nc, core, "norm3")
        expert_block(nc, core, "top1", a["L1_ffn_w1"], a["L1_ffn_w2"], a["L1_ffn_gate_w"], a["L1_ffn_gate_b"],
                     a["L1_ffn_b1"], a["L1_ffn_b2"], top=1, capacity=-(-5 * B * N // (4 * 8)), guard=True)
        layernorm_statistics(nc, core, "norm4")
        recurrent_block(nc, core, a["adj"], a["adj_t"], a["L2_gnn_W_ioux_t"], a["L2_gnn_W_iouh_t"], a["L2_gnn_b_ioux"], a["L2_gnn_b_iouh"],
                        a["L2_gnn_W_coux_t"], a["L2_gnn_W_couh_t"], a["L2_gnn_b_coux"], a["L2_gnn_b_couh"])
        layernorm_statistics(nc, core, "norm5")
        expert_block(nc, core, "top2", a["L2_ffn_W1_t"], a["L2_ffn_W2_t"], a["L2_ffn_Wg_t"], a["L2_ffn_bg"],
                     a["L2_ffn_b1"], a["L2_ffn_b2"])
        layernorm_statistics(nc, core, "norm6")
        attention_block(nc, core, a["adj"], a["L3_gnn_W"], a["L3_gnn_W_t"], a["L3_gnn_a2"], a["L3_gnn_gamma"], a["L3_gnn_beta"])
        layernorm_statistics(nc, core, "norm7")
        slice_block(nc, core, a)
        store_output(nc, core, out)


def _laid_out(inputs):
    a = {k: np.asarray(v) for k, v in inputs.items()}
    a["adj_t"] = a["adj"].transpose(0, 2, 1)
    a["L0_gnn_W_t"] = a["L0_gnn_W"].T
    a["L0_ffn_w12"] = np.concatenate([a["L0_ffn_w1"], a["L0_ffn_w2"]], axis=2)
    a["L2_ffn_W1_t"] = a["L2_ffn_W1"].transpose(0, 2, 1)
    a["L2_ffn_W2_t"] = a["L2_ffn_W2"].transpose(0, 2, 1)
    a["L2_ffn_Wg_t"] = a["L2_ffn_Wg"].T
    a["pair_mask"], a["row_mask"] = group_masks()
    a["L3_gnn_W_t"] = a["L3_gnn_W"].T
    a["L3_gnn_a2"] = a["L3_gnn_a"].reshape(2, D).T
    for k in ("W_ioux", "W_iouh", "W_coux", "W_couh"):
        a["L2_gnn_" + k + "_t"] = a["L2_gnn_" + k].T
    for k in ("W_fx", "W_slice", "hy_in_w", "hy_fcD_w", "hy_out_w", "out_w"):
        a["L3_ffn_" + k + "_t"] = a["L3_ffn_" + k].T
    a["col_mask"], a["lhs_mask"] = order_masks()
    return {k: np.ascontiguousarray(a[k]) for k in USED}


def kernel(**inputs):
    import concourse.bacc as _bacc
    from concourse.bass_utils import run_bass_kernel_spmd as _run

    nc = _bacc.Bacc("TRN2", target_bir_lowering=False, num_devices=1)
    arrays = _laid_out(inputs)
    aps = {k: nc.dram_tensor("in_" + k, v.shape, mybir.dt.from_np(v.dtype), kind="ExternalInput").ap()
           for k, v in arrays.items()}
    out = nc.dram_tensor("out_0", (B, N, D), F32, kind="ExternalOutput").ap()
    build(nc, aps, out)
    r = _run(nc, [{"in_" + k: v for k, v in arrays.items()}], core_ids=[0])
    return r.results[0]["out_0"]
```

```python
import concourse.bass as bass
import numpy as np
from concourse import mybir
from concourse.alu_op_type import AluOpType as ALU
from contextlib import ExitStack

F32 = mybir.dt.float32
U32 = mybir.dt.uint32
U8 = mybir.dt.uint8
ACT = mybir.ActivationFunctionType
AXX = mybir.AxisListType.X
AXXY = mybir.AxisListType.XY

B, N, D = 32, 256, 128
P = 128
HALVES = N // P
TILES = B * HALVES
CREDIT = 2
LN_EPS = 1e-5


def done(n):
    return n + (1 + CREDIT)


def freed(n):
    return n + 1


def dma_done(n, per=1):
    return n * (16 * per) + 16 * per + 16 * CREDIT


class Own:

    def __init__(self, eng, sem, turn, per):
        self.eng, self.sem, self.base, self.per, self.k = eng, sem, turn * per, per, 0

    def step(self, ins):
        self.mark(ins)
        self.join()

    def mark(self, ins):
        ins.then_inc(self.sem, 1)
        self.k += 1

    def join(self):
        self.eng.wait_ge(self.sem, self.base + self.k)

    def end(self):
        assert self.k == self.per, (self.k, self.per)


class Stage:

    def __init__(self, nc, name):
        self.nc, self.name, self.sems, self.ctx = nc, name, [], ExitStack()

    def __enter__(self):
        return self

    def sb(self, name, shape, dt=F32):
        return self.ctx.enter_context(self.nc.sbuf_tensor(self.name + "_" + name, list(shape), dt))

    def ps(self, name, shape, dt=F32):
        return self.ctx.enter_context(self.nc.psum_tensor(self.name + "_" + name, list(shape), dt))

    def sem(self, name, credit=0):
        s = self.nc.alloc_semaphore(self.name + "_" + name)
        if credit:
            self.nc.sync.sem_inc(s, credit)
        self.sems.append(s)
        return s

    def block(self):
        self.nc.all_engine_barrier()
        return self.nc.Block()

    def __exit__(self, *exc):
        self.ctx.close()
        self.nc.clear_and_free_semaphores(self.sems)
        self.nc.all_engine_barrier()


class Core:
    pass


def hold(eng, sem):
    eng.sem_inc(sem, 1)

USED = ["x", "adj_t", "L0_gnn_W_t", "L0_gnn_conv_w", "L0_gnn_conv_b",
        "L0_ffn_w12", "L0_ffn_w3", "L0_ffn_gate_w", "L0_ffn_gate_b",
        "L1_ffn_w1", "L1_ffn_w2", "L1_ffn_gate_w", "L1_ffn_gate_b", "L1_ffn_b1", "L1_ffn_b2",
        "L2_ffn_W1_t", "L2_ffn_W2_t", "L2_ffn_Wg_t", "L2_ffn_bg", "L2_ffn_b1", "L2_ffn_b2",
        "L1_gnn_W1", "L1_gnn_b1", "L1_gnn_W2", "L1_gnn_b2", "L1_gnn_fusion_w", "pair_mask", "row_mask",
        "adj", "L3_gnn_W", "L3_gnn_W_t", "L3_gnn_a2", "L3_gnn_gamma", "L3_gnn_beta",
        "L2_gnn_W_ioux_t", "L2_gnn_W_iouh_t", "L2_gnn_b_ioux", "L2_gnn_b_iouh",
        "L2_gnn_W_coux_t", "L2_gnn_W_couh_t", "L2_gnn_b_coux", "L2_gnn_b_couh",
        "L3_ffn_W_x", "L3_ffn_b_x", "L3_ffn_W_fx_t", "L3_ffn_b_fx", "L3_ffn_W_slice_t", "L3_ffn_b_slice", "L3_ffn_temperature",
        "L3_ffn_hy_in_w_t", "L3_ffn_hy_conv_w", "L3_ffn_hy_conv_b", "L3_ffn_hy_dt_bias", "L3_ffn_hy_A_log", "L3_ffn_hy_D",
        "L3_ffn_hy_fcD_w_t", "L3_ffn_hy_norm_w", "L3_ffn_hy_out_w_t", "L3_ffn_out_w_t", "L3_ffn_out_b", "col_mask", "lhs_mask"]


def load_inputs(nc, core, x):
    with Stage(nc, "load") as st:
        loaded = st.sem("x_loaded")
        zeroed = st.sem("identity_zeroed")
        with st.block() as block:
            @block.sync
            def _(sp):
                sp.dma_start(core.x[:], x.rearrange("b (h p) d -> p (b h) d", p=P)).then_inc(loaded, 16)
                sp.wait_ge(loaded, 16)

            @block.gpsimd
            def _(pool):
                nc.gpsimd.memset(core.ident[:], 0.0).then_inc(zeroed, 1)
                nc.gpsimd.memset(core.ones[:], 1.0)
                pool.wait_ge(zeroed, 1)
                nc.gpsimd.affine_select(out=core.ident[:], in_=core.ident[:], compare_op=ALU.not_equal, fill=1.0,
                                        base=0, pattern=[[-1, P]], channel_multiplier=1)


def layernorm_statistics(nc, core, name, of=None):
    of = core.x if of is None else of
    with Stage(nc, name) as st:
        GROUP = 4
        parts = st.sb("parts", [P, TILES, 6])
        half_gap = st.sb("half_gap", [P, TILES])
        root = st.sb("root", [P, TILES])
        parts_done, variance, rooted, own = [st.sem(n) for n in ("parts_done", "variance_ready", "root_ready", "vector_steps")]
        with st.block() as block:
            @block.vector
            def _(dve):
                with dve.Fori(0, TILES // GROUP) as i:
                    for k in range(GROUP):
                        last = nc.vector.bn_stats(parts[:, i * GROUP + k, :], of[:, i * GROUP + k, :])
                    last.then_inc(parts_done, 1)
                dve.wait_ge(parts_done, TILES // GROUP)
                even, odd = parts[:, :, 0:3], parts[:, :, 3:6]
                mine = Own(dve, own, 0, 7)
                mine.step(nc.vector.tensor_tensor(core.mean[:], even[:, :, 1], odd[:, :, 1], ALU.add))
                mine.step(nc.vector.tensor_scalar(core.mean[:], core.mean[:], 0.5, None, ALU.mult))
                mine.step(nc.vector.tensor_tensor(half_gap[:], core.mean[:], odd[:, :, 1], ALU.subtract))
                mine.step(nc.vector.tensor_tensor(half_gap[:], half_gap[:], half_gap[:], ALU.mult))
                mine.step(nc.vector.tensor_tensor(root[:], even[:, :, 2], odd[:, :, 2], ALU.add))
                mine.step(nc.vector.scalar_tensor_tensor(root[:], root[:], 1.0 / D, half_gap[:], ALU.mult, ALU.add))
                mine.step(nc.vector.tensor_scalar(root[:], root[:], LN_EPS, None, ALU.add))
                nc.vector.engine_nop().then_inc(variance, 1)
                dve.wait_ge(rooted, 1)
                nc.vector.reciprocal(core.rstd[:], root[:])

            @block.scalar
            def _(act):
                act.wait_ge(variance, 1)
                nc.scalar.activation(root[:], root[:], ACT.Sqrt).then_inc(rooted, 1)


def power_graph_block(nc, core, adj_t, w_t, conv_w, conv_b):
    POWERS = 4
    SLOPE = 0.2
    with Stage(nc, "power") as st:
        w = st.sb("w", [P, D])
        coef = st.sb("coef", [P, POWERS + 1])
        a_t = [st.sb(f"a_t{s}", [P, HALVES, N]) for s in range(2)]
        y = [st.sb(f"y{s}", [P, HALVES, D]) for s in range(2)]
        y_t = [st.sb(f"y_t{s}", [P, N]) for s in range(2)]
        cur = [st.sb(f"cur{s}", [P, HALVES, D + 4]) for s in range(2)]
        acc = [st.sb(f"acc{s}", [P, HALVES, D]) for s in range(2)]
        rinv = [st.sb(f"rinv{s}", [P, HALVES]) for s in range(2)]
        ps_t = [st.ps(f"ps_t{s}", [P, 512]) for s in range(2)]
        ps_c = [[st.ps(f"ps_c{s}{h}", [P, 512]) for h in range(2)] for s in range(2)]
        weights = st.sem("weights_loaded")
        adj_loaded = [st.sem(f"adj_loaded{s}") for s in range(2)]
        y_ready, y_t_ps, y_t_ready = [st.sem(n, CREDIT) for n in ("y_ready", "y_t_transposed", "y_t_ready")]
        prod = [st.sem(f"product{k}_ready", CREDIT) for k in range(POWERS)]
        cur_ready = [st.sem(f"power{k}_ready", CREDIT) for k in range(POWERS)]
        own = st.sem("vector_steps")
        passed = st.sem("passed")
        with st.block() as block:
            @block.sync
            def _(sp):
                sp.dma_start(w[:], w_t).then_inc(weights, 16)
                sp.dma_start(coef[:, 0:POWERS], conv_w.rearrange("(a k) -> a k", a=1).to_broadcast([P, POWERS])).then_inc(weights, 16)
                sp.dma_start(coef[:, POWERS:POWERS + 1], conv_b.rearrange("(a k) -> a k", a=1).to_broadcast([P, 1])).then_inc(weights, 16)
                with sp.Fori(0, B // 2) as i:
                    for s in range(2):
                        sp.wait_ge(prod[POWERS - 1], freed(i * 2 + s))
                        sp.dma_start(a_t[s][:], adj_t[i * 2 + s, :, :].rearrange("(h p) n -> p h n", p=P)).then_inc(adj_loaded[s], 16)

            @block.tensor
            def _(pe):
                pe.wait_ge(weights, 48)
                with pe.Fori(0, B // 2) as i:
                    for s in range(2):
                        pe.wait_ge(y_t_ready, freed(i * 2 + s))
                        pe.wait_ge(y_ready, done(i * 2 + s))
                        for h in range(HALVES):
                            last = nc.tensor.transpose(ps_t[s][:, h * P:(h + 1) * P], y[s][:, h, :], core.ident[:])
                        last.then_inc(y_t_ps, 1)
                    for s in range(2):
                        pe.wait_ge(y_t_ready, done(i * 2 + s))
                        pe.wait_ge(cur_ready[POWERS - 1], freed(i * 2 + s))
                        for h in range(HALVES):
                            last = nc.tensor.matmul(ps_c[s][h][:, 0:D], y_t[s][:, h * P:(h + 1) * P], w[:], start=True, stop=True)
                        last.then_inc(prod[0], 1)
                    for k in range(1, POWERS):
                        for s in range(2):
                            if k == 1:
                                pe.wait_ge(adj_loaded[s], i * 16 + 16)
                            pe.wait_ge(cur_ready[k - 1], done(i * 2 + s))
                            width = D + 1 if k == 1 else D
                            for h in range(HALVES):
                                for m in range(HALVES):
                                    last = nc.tensor.matmul(ps_c[s][h][:, 0:width], a_t[s][:, m, h * P:(h + 1) * P],
                                                            cur[s][:, m, 0:width], start=m == 0, stop=m == HALVES - 1)
                            last.then_inc(prod[k], 1)

            @block.scalar
            def _(act):
                with act.Fori(0, B // 2) as i:
                    for s in range(2):
                        act.wait_ge(y_t_ps, done(i * 2 + s))
                        act.wait_ge(prod[0], freed(i * 2 + s))
                        nc.scalar.copy(y_t[s][:], ps_t[s][:, 0:N]).then_inc(y_t_ready, 1)

            @block.vector
            def _(dve):
                for s in range(2):
                    nc.vector.memset(cur[s][:, :, D:D + 1], 1.0)
                dve.wait_ge(weights, 48)
                with dve.Fori(0, B // 2) as i:
                    mine = Own(dve, own, i, 2 * 14)
                    for s in range(2):
                        n = i * 2 + s
                        dve.wait_ge(y_t_ps, freed(n))
                        for h in range(HALVES):
                            t = n * 2 + h
                            last = nc.vector.tensor_scalar(y[s][:, h, :], core.x[:, t, :], core.mean[:, bass.ds(t, 1)],
                                                           core.rstd[:, bass.ds(t, 1)], ALU.subtract, ALU.mult)
                        last.then_inc(y_ready, 1)
                    for k in range(POWERS):
                        for s in range(2):
                            n = i * 2 + s
                            dve.wait_ge(prod[k], done(n))
                            if k == 1:
                                for h in range(HALVES):
                                    mine.step(nc.vector.tensor_scalar(rinv[s][:, h:h + 1], ps_c[s][h][:, D:D + 1], 1e-9, None, ALU.add))
                                mine.step(nc.vector.reciprocal(rinv[s][:], rinv[s][:]))
                            for h in range(HALVES):
                                if k == 0:
                                    last = nc.vector.tensor_scalar(cur[s][:, h, 0:D], ps_c[s][h][:, 0:D], 1.0, None, ALU.mult)
                                else:
                                    last = nc.vector.tensor_scalar(cur[s][:, h, 0:D], ps_c[s][h][:, 0:D], rinv[s][:, h:h + 1], None, ALU.mult)
                            last.then_inc(cur_ready[k], 1)
                            dve.wait_ge(cur_ready[k], done(n))
                            if k == 0:
                                mine.step(nc.vector.tensor_scalar(acc[s][:], cur[s][:, :, 0:D], coef[:, 0:1],
                                                                  coef[:, POWERS:POWERS + 1], ALU.mult, ALU.add))
                            else:
                                for h in range(HALVES):
                                    mine.step(nc.vector.scalar_tensor_tensor(acc[s][:, h, :], cur[s][:, h, 0:D], coef[:, k:k + 1],
                                                                             acc[s][:, h, :], ALU.mult, ALU.add))
                    for s in range(2):
                        n = i * 2 + s
                        for h in range(HALVES):
                            mine.step(nc.vector.scalar_tensor_tensor(acc[s][:, h, :], acc[s][:, h, :], SLOPE, acc[s][:, h, :], ALU.mult, ALU.max))
                        for h in range(HALVES):
                            mine.step(nc.vector.tensor_tensor(core.x[:, n * 2 + h, :], core.x[:, n * 2 + h, :], acc[s][:, h, :], ALU.add))
                    mine.end()


TURNS = 4
UP = 512
ROWS_MAX = (2 * B * N // P + 16) * P


def prepare_tables(nc, core):
    with Stage(nc, "table") as st:
        PART = 9 * P
        zeros = st.sb("zeros", [P, PART])
        zeroed, written = st.sem("zeros_ready"), st.sem("table_written")
        pieces = ROWS_MAX * D // (P * PART)
        flat = core.sorted_in.rearrange("(a p r) d -> a p (r d)", a=pieces, p=P)
        with st.block() as block:
            @block.vector
            def _(dve):
                nc.vector.memset(zeros[:], 0.0).then_inc(zeroed, 1)

            @block.sync
            def _(sp):
                sp.wait_ge(zeroed, 1)
                for a in range(pieces):
                    sp.dma_start(flat[a, :, :], zeros[:]).then_inc(written, 16)
                sp.wait_ge(written, 16 * pieces)


def expert_block(nc, core, name, w_up, w_down, gate_w, gate_b, b_up=None, b_down=None, top=2, capacity=None, guard=False):
    E = w_up.shape[0]
    gated = b_up is None
    HC = w_down.shape[1] // P
    Q = top * TILES + E
    assert Q % TURNS == 0 and Q * P <= ROWS_MAX
    with Stage(nc, name) as keep:
        expert_of = keep.sb("experts_of_turns", [1, Q // TURNS + 1, 8], U32)
        wu = keep.sb("w_up", [P, E * UP])
        wd = keep.sb("w_down", [P, E * HC * D])
        bu, bd = (None, None) if gated else (keep.sb("b_up", [P, E * UP]), keep.sb("b_down", [P, E * D]))
        weights = keep.sem("expert_weights_loaded")

        def load_weights(sp):
            sp.dma_start(wu[:].rearrange("p (e f) -> p e f", e=E), w_up.rearrange("e d f -> d e f")).then_inc(weights, 16)
            sp.dma_start(wd[:].rearrange("p (e c f) -> p e c f", e=E, c=HC),
                         w_down.rearrange("e (c p) f -> p e c f", p=P)).then_inc(weights, 16)
            if not gated:
                sp.dma_start(bu[:], b_up.rearrange("(a e) f -> a (e f)", a=1).to_broadcast([P, E * UP])).then_inc(weights, 16)
                sp.dma_start(bd[:], b_down.rearrange("(a e) f -> a (e f)", a=1).to_broadcast([P, E * D])).then_inc(weights, 16)

        slot = [keep.sb(f"slot{k}", [P, TILES]) for k in range(top)]
        weight = [keep.sb(f"weight{k}", [P, TILES]) for k in range(top)]
        route(nc, core, name, E, top, Q, gate_w, gate_b, capacity, expert_of, slot, weight, load_weights)
        scatter_tokens(nc, core, name, top, slot)
        run_experts(nc, core, name, E, Q, HC, gated, wu, wd, bu, bd, weights, 2 if gated else 4, expert_of)
        gather_tokens(nc, core, name, top, Q, slot, weight, guard)


def route(nc, core, name, E, top, Q, gate_w, gate_b, capacity, expert_of, slot, weight, load_weights):
    GROUP = 4
    BIG = 1e30
    MAGIC = float(2 ** 23)
    with Stage(nc, name + "_route") as st:
        gw = st.sb("gate_w", [P, E])
        gb = st.sb("gate_b", [P, E])
        y = [st.sb(f"y{s}", [P, GROUP, D]) for s in range(2)]
        y_t = [st.sb(f"y_t{s}", [P, GROUP * P]) for s in range(2)]
        logits = st.sb("logits", [P, TILES, E])
        ps_t = [st.ps(f"ps_t{s}", [P, 512]) for s in range(2)]
        ps_l = [st.ps(f"ps_l{s}", [P, 512]) for s in range(2)]
        weights = st.sem("weights_loaded")
        y_ready, y_t_ps, y_t_ready, logits_ps, logits_ready = [st.sem(n, CREDIT) for n in (
            "y_ready", "y_t_transposed", "y_t_ready", "logits_product", "logits_ready")]
        with st.block() as block:
            @block.sync
            def _(sp):
                sp.dma_start(gw[:], gate_w).then_inc(weights, 16)
                sp.dma_start(gb[:], gate_b.rearrange("(a k) -> a k", a=1).to_broadcast([P, E])).then_inc(weights, 16)
                load_weights(sp)

            @block.vector
            def _(dve):
                def normalise(n, s):
                    dve.wait_ge(y_t_ps, freed(n))
                    for k in range(GROUP):
                        t = n * GROUP + k
                        last = nc.vector.tensor_scalar(y[s][:, k, :], core.x[:, t, :], core.mean[:, bass.ds(t, 1)],
                                                       core.rstd[:, bass.ds(t, 1)], ALU.subtract, ALU.mult)
                    last.then_inc(y_ready, 1)

                def keep_logits(n, s):
                    dve.wait_ge(logits_ps, done(n))
                    nc.vector.tensor_tensor(logits[:, bass.ds(n * GROUP, GROUP), :],
                                            ps_l[s][:, 0:GROUP * E].rearrange("p (t e) -> p t e", e=E),
                                            gb[:].unsqueeze(1).to_broadcast([P, GROUP, E]), ALU.add).then_inc(logits_ready, 1)

                dve.wait_ge(weights, 32)
                normalise(0, 0)
                with dve.Fori(0, TILES // GROUP // 2 - 1) as i:
                    normalise(i * 2 + 1, 1)
                    keep_logits(i * 2, 0)
                    normalise(i * 2 + 2, 0)
                    keep_logits(i * 2 + 1, 1)
                n = TILES // GROUP - 2
                normalise(n + 1, 1)
                keep_logits(n, 0)
                keep_logits(n + 1, 1)

            @block.tensor
            def _(pe):
                pe.wait_ge(weights, 32)
                with pe.Fori(0, TILES // GROUP // 2) as i:
                    for s in range(2):
                        n = i * 2 + s
                        pe.wait_ge(y_t_ready, freed(n))
                        pe.wait_ge(y_ready, done(n))
                        for k in range(GROUP):
                            last = nc.tensor.transpose(ps_t[s][:, k * P:(k + 1) * P], y[s][:, k, :], core.ident[:])
                        last.then_inc(y_t_ps, 1)
                    for s in range(2):
                        n = i * 2 + s
                        pe.wait_ge(logits_ready, freed(n))
                        pe.wait_ge(y_t_ready, done(n))
                        for k in range(GROUP):
                            last = nc.tensor.matmul(ps_l[s][:, k * E:(k + 1) * E], y_t[s][:, k * P:(k + 1) * P], gw[:], start=True, stop=True)
                        last.then_inc(logits_ps, 1)

            @block.scalar
            def _(act):
                with act.Fori(0, TILES // GROUP // 2) as i:
                    for s in range(2):
                        n = i * 2 + s
                        act.wait_ge(logits_ps, freed(n))
                        act.wait_ge(y_t_ps, done(n))
                        nc.scalar.copy(y_t[s][:], ps_t[s][:]).then_inc(y_t_ready, 1)

        with Stage(nc, name + "_rank") as rk:
            upto = rk.sb("upto", [P, P])
            chosen = [rk.sb(f"chosen{k}", [P, TILES, E]) for k in range(top)]
            any_chosen = rk.sb("any_chosen", [P, TILES, E])
            wide = [rk.sb(f"wide{k}", [P, TILES, E]) for k in range(3)]
            number_i = rk.sb("expert_number_int", [P, E], mybir.dt.int32)
            number = rk.sb("expert_number", [P, E])
            row_i = rk.sb("first_row_int", [1, Q], mybir.dt.int32)
            row = rk.sb("first_row", [1, Q])
            at_or_behind = rk.sb("at_or_behind", [1, Q, E])
            tile_expert = rk.sb("tile_expert", [1, Q])
            best = [rk.sb(f"best{k}", [P, TILES]) for k in range(2)]
            small = [rk.sb(f"small{k}", [P, TILES]) for k in range(3)]
            share = [rk.sb(f"share{k}", [P, E]) for k in range(3)]
            ps_rank = [rk.ps(f"ps_rank{j}", [P, 512]) for j in range(2)]
            ps_total = [rk.ps(f"ps_total{j}", [P, 512]) for j in range(2)]
            consts, consts_step, picked, counted, exp_in, exp_out, own = [rk.sem(n) for n in (
                "constants_ready", "constants_step", "chosen_ready", "counts_ready", "exp_input_ready", "exp_ready", "vector_steps")]
            banks = TILES * E // 512
            per_bank = 512 // E
            with rk.block() as block:
                @block.gpsimd
                def _(pool):
                    nc.gpsimd.iota(number_i[:], pattern=[[1, E]], base=0, channel_multiplier=0).then_inc(consts, 1)
                    nc.gpsimd.iota(row_i[:], pattern=[[P, Q]], base=0, channel_multiplier=0).then_inc(consts, 1)
                    nc.gpsimd.memset(upto[:], 1.0).then_inc(consts_step, 1)
                    pool.wait_ge(consts_step, 1)
                    nc.gpsimd.affine_select(out=upto[:], in_=upto[:], compare_op=ALU.is_ge, fill=0.0, base=0,
                                            pattern=[[1, P]], channel_multiplier=-1).then_inc(consts, 1)

                @block.tensor
                def _(pe):
                    pe.wait_ge(consts, 3)
                    pe.wait_ge(picked, 1)
                    for j in range(banks):
                        pick = any_chosen[:, j * per_bank:(j + 1) * per_bank, :]
                        nc.tensor.matmul(ps_rank[j][:], upto[:], pick, start=True, stop=True)
                        nc.tensor.matmul(ps_total[j][:], core.ones[:], pick, start=True, stop=True).then_inc(counted, 1)

                @block.scalar
                def _(act):
                    act.wait_ge(exp_in, 1)
                    if top == 2:
                        nc.scalar.activation(small[0][:], small[0][:], ACT.Exp).then_inc(exp_out, 1)
                    else:
                        nc.scalar.activation(wide[0][:], wide[0][:], ACT.Exp).then_inc(exp_out, 1)

                @block.vector
                def _(dve):
                    v = nc.vector
                    mine = Own(dve, own, 0, 0)
                    each = lambda a: a.unsqueeze(2).to_broadcast([P, TILES, E])
                    tokens = lambda a: a.unsqueeze(1).to_broadcast([P, TILES, E])
                    dve.wait_ge(consts, 3)
                    mine.step(v.tensor_copy(number[:], number_i[:]))
                    mine.step(v.tensor_copy(row[:], row_i[:]))
                    scores = logits
                    for k in range(top):
                        mine.step(v.tensor_reduce(best[k][:], scores[:], AXX, ALU.max))
                        mine.step(v.tensor_tensor(wide[0][:], scores[:], each(best[k][:]), ALU.is_lt))
                        mine.step(v.tensor_scalar(wide[0][:], wide[0][:], float(E), None, ALU.mult))
                        mine.step(v.tensor_tensor(wide[0][:], wide[0][:], tokens(number[:]), ALU.add))
                        mine.step(v.tensor_reduce(small[0][:], wide[0][:], AXX, ALU.min))
                        mine.step(v.tensor_tensor(chosen[k][:], tokens(number[:]), each(small[0][:]), ALU.is_equal))
                        if k + 1 < top:
                            mine.step(v.tensor_scalar(wide[1][:], chosen[k][:], -BIG, None, ALU.mult))
                            mine.step(v.tensor_tensor(wide[1][:], wide[1][:], scores[:], ALU.add))
                            scores = wide[1]
                    if top == 2:
                        mine.step(v.tensor_tensor(any_chosen[:], chosen[0][:], chosen[1][:], ALU.add))
                        mine.step(v.tensor_tensor(small[0][:], best[1][:], best[0][:], ALU.subtract))
                    else:
                        mine.step(v.tensor_copy(any_chosen[:], chosen[0][:]))
                        mine.step(v.tensor_tensor(wide[0][:], logits[:], each(best[0][:]), ALU.subtract))
                    v.engine_nop().then_inc(picked, 1)
                    v.engine_nop().then_inc(exp_in, 1)
                    dve.wait_ge(exp_out, 1)
                    if top == 2:
                        mine.step(v.tensor_scalar(small[1][:], small[0][:], 1.0, None, ALU.add))
                        mine.step(v.reciprocal(weight[0][:], small[1][:]))
                        mine.step(v.tensor_tensor(weight[1][:], weight[0][:], small[0][:], ALU.mult))
                    else:
                        mine.step(v.tensor_reduce(small[1][:], wide[0][:], AXX, ALU.add))
                        mine.step(v.reciprocal(weight[0][:], small[1][:]))
                    dve.wait_ge(counted, banks)
                    for j in range(banks):
                        mine.step(v.tensor_copy(wide[0][:, j * per_bank:(j + 1) * per_bank, :],
                                                ps_total[j][:].rearrange("p (t e) -> p t e", e=E)))
                    a, b = wide[0], wide[1]
                    gap = 1
                    while gap < TILES:
                        mine.step(v.tensor_copy(b[:, 0:gap, :], a[:, 0:gap, :]))
                        mine.step(v.tensor_tensor(b[:, gap:, :], a[:, gap:, :], a[:, :TILES - gap, :], ALU.add))
                        a, b = b, a
                        gap *= 2
                    mine.step(v.tensor_scalar(share[0][:], a[:, TILES - 1, :], float(P - 1), 1.0 / P, ALU.add, ALU.mult))
                    mine.step(v.tensor_scalar(share[0][:], share[0][:], 0.5 - 0.5 / P, None, ALU.subtract))
                    mine.step(v.tensor_scalar(share[0][:], share[0][:], MAGIC, None, ALU.add))
                    mine.step(v.tensor_scalar(share[0][:], share[0][:], MAGIC, None, ALU.subtract))
                    mine.step(v.tensor_scalar(share[0][:], share[0][:], float(P), None, ALU.mult))
                    mine.step(v.tensor_copy(share[1][:], share[0][:]))
                    c, d = share[1], share[2]
                    gap = 1
                    while gap < E:
                        mine.step(v.tensor_copy(d[:, 0:gap], c[:, 0:gap]))
                        mine.step(v.tensor_tensor(d[:, gap:], c[:, gap:], c[:, :E - gap], ALU.add))
                        c, d = d, c
                        gap *= 2
                    mine.step(v.tensor_tensor(c[:], c[:], share[0][:], ALU.subtract))
                    for j in range(banks):
                        part = slice(j * per_bank, (j + 1) * per_bank)
                        mine.step(v.tensor_tensor(wide[2][:, part, :], a[:, part, :],
                                                  ps_total[j][:].rearrange("p (t e) -> p t e", e=E), ALU.subtract))
                        mine.step(v.tensor_tensor(wide[2][:, part, :], wide[2][:, part, :],
                                                  ps_rank[j][:].rearrange("p (t e) -> p t e", e=E), ALU.add))
                    if capacity is not None:
                        mine.step(v.tensor_tensor(b[:], chosen[0][:], wide[2][:], ALU.mult))
                        mine.step(v.tensor_reduce(small[0][:], b[:], AXX, ALU.add))
                        mine.step(v.tensor_scalar(small[0][:], small[0][:], float(capacity), None, ALU.is_le))
                        mine.step(v.tensor_tensor(weight[0][:], weight[0][:], small[0][:], ALU.mult))
                    mine.step(v.tensor_tensor(wide[2][:], wide[2][:], tokens(c[:]), ALU.add))
                    for k in range(top):
                        mine.step(v.tensor_tensor(b[:], chosen[k][:], wide[2][:], ALU.mult))
                        mine.step(v.tensor_reduce(slot[k][:], b[:], AXX, ALU.add))
                        mine.step(v.tensor_scalar(slot[k][:], slot[k][:], 1.0, None, ALU.subtract))
                    mine.step(v.tensor_tensor(at_or_behind[:], row[:].unsqueeze(2).to_broadcast([1, Q, E]),
                                              c[0:1, :].unsqueeze(1).to_broadcast([1, Q, E]), ALU.is_ge))
                    mine.step(v.tensor_reduce(tile_expert[:], at_or_behind[:], AXX, ALU.add))
                    mine.step(v.memset(expert_of[:], 0))
                    for j in range(TURNS + 2):
                        tiles = slice(j - 1 if j else TURNS - 1, Q, TURNS)
                        first = 1 if j == 0 else 0
                        count = len(range(Q)[tiles])
                        mine.step(v.tensor_scalar(expert_of[:, first:first + count, j], tile_expert[:, tiles], 1.0, None, ALU.subtract))


def scatter_tokens(nc, core, name, top, slot):
    with Stage(nc, name + "_scatter") as st:
        y = [st.sb(f"y{s}", [P, D]) for s in range(2)]
        at = [[st.sb(f"at{s}{k}", [P, 1], U32) for k in range(top)] for s in range(2)]
        ready = st.sem("rows_ready", CREDIT)
        sent = [st.sem(f"rows_sent{s}") for s in range(2)]
        passed = st.sem("pool_passed")
        with st.block() as block:
            @block.vector
            def _(dve):
                def rows(t, s):
                    nc.vector.tensor_scalar(y[s][:], core.x[:, t, :], core.mean[:, bass.ds(t, 1)],
                                            core.rstd[:, bass.ds(t, 1)], ALU.subtract, ALU.mult)
                    for k in range(top):
                        last = nc.vector.tensor_scalar(at[s][k][:], slot[k][:, bass.ds(t, 1)], 0.0, None, ALU.add)
                    last.then_inc(ready, 1)

                rows(0, 0)
                rows(1, 1)
                with dve.Fori(1, TILES // 2) as i:
                    for s in range(2):
                        dve.wait_ge(sent[s], i * (16 * top))
                        rows(i * 2 + s, s)

            @block.gpsimd
            def _(pool):
                with pool.Fori(0, TILES // 2) as i:
                    for s in range(2):
                        pool.wait_ge(ready, done(i * 2 + s))
                        hold(pool, passed)
                        for k in range(top):
                            nc.gpsimd.indirect_dma_start(core.sorted_in, bass.IndirectOffsetOnAxis(ap=at[s][k][:], axis=0),
                                                         y[s][:], None).then_inc(sent[s], 16)
                for s in range(2):
                    pool.wait_ge(sent[s], 16 * top * (TILES // 2))


def gather_tokens(nc, core, name, top, Q, slot, weight, guard):
    with Stage(nc, name + "_gather") as st:
        rows = [[st.sb(f"rows{s}{k}", [P, D]) for k in range(top)] for s in range(2)]
        at = [[st.sb(f"at{s}{k}", [P, 1], U32) for k in range(top)] for s in range(2)]
        safe = st.sb("safe", [P, D])
        zero_or_nan = st.sb("zero_or_nan", [P, D])
        mask = st.sb("mask", [P, D], U8)
        at_ready, added = [st.sem(n, CREDIT) for n in ("indices_ready", "rows_added")]
        got = [st.sem(f"rows_got{s}") for s in range(2)]
        passed = st.sem("pool_passed")
        own, passed_v = st.sem("vector_steps"), st.sem("vector_passed")
        with st.block() as block:
            @block.gpsimd
            def _(pool):
                with pool.Fori(0, TILES // 2) as i:
                    for s in range(2):
                        pool.wait_ge(added, freed(i * 2 + s))
                        pool.wait_ge(at_ready, done(i * 2 + s))
                        hold(pool, passed)
                        for k in range(top):
                            nc.gpsimd.indirect_dma_start(rows[s][k][:], None, core.sorted_out[0:Q * P, :],
                                                         bass.IndirectOffsetOnAxis(ap=at[s][k][:], axis=0)).then_inc(got[s], 16)

            @block.vector
            def _(dve):
                def indices(n, i, s):
                    if not isinstance(n, int):
                        dve.wait_ge(got[s], i * (16 * top))
                    for k in range(top):
                        last = nc.vector.tensor_scalar(at[s][k][:], slot[k][:, bass.ds(n, 1)], 0.0, None, ALU.add)
                    last.then_inc(at_ready, 1)

                def add(n, i, s):
                    dve.wait_ge(got[s], i * (16 * top) + 16 * top)
                    mine = Own(dve, own, n, 8 if guard else top - 1)
                    if guard:
                        assert top == 1
                        y = rows[s][0]
                        mine.step(nc.vector.tensor_scalar(y[:], y[:], weight[0][:, bass.ds(n, 1)], None, ALU.mult))
                        mine.step(nc.vector.memset(safe[:], 0.0))
                        mine.step(nc.vector.tensor_tensor(mask[:], y[:], y[:], ALU.is_equal))
                        hold(dve, passed_v)
                        mine.step(nc.vector.copy_predicated(safe[:], mask[:], y[:]))
                        mine.step(nc.vector.tensor_scalar(y[:], safe[:], 1e4, -1e4, ALU.min, ALU.max))
                        mine.step(nc.vector.tensor_scalar(zero_or_nan[:], safe[:], 0.0, None, ALU.mult))
                        mine.step(nc.vector.tensor_tensor(mask[:], zero_or_nan[:], zero_or_nan[:], ALU.not_equal))
                        hold(dve, passed_v)
                        mine.step(nc.vector.copy_predicated(safe[:], mask[:], y[:]))
                        nc.vector.tensor_tensor(core.x[:, n, :], core.x[:, n, :], safe[:], ALU.add).then_inc(added, 1)
                    else:
                        for k in range(top):
                            last = nc.vector.scalar_tensor_tensor(core.x[:, n, :], rows[s][k][:], weight[k][:, bass.ds(n, 1)],
                                                                  core.x[:, n, :], ALU.mult, ALU.add)
                            if k + 1 < top:
                                mine.step(last)
                        last.then_inc(added, 1)
                    mine.end()

                indices(0, 0, 0)
                indices(1, 0, 1)
                with dve.Fori(0, TILES // 2 - 1) as i:
                    for s in range(2):
                        add(i * 2 + s, i, s)
                        indices(i * 2 + s + 2, i + 1, s)
                for s in range(2):
                    add(TILES - 2 + s, TILES // 2 - 1, s)


def run_experts(nc, core, name, E, Q, HC, gated, wu, wd, bu, bd, weights, weight_loads, expert_of):
    with Stage(nc, name + "_experts") as st:
        g = [st.sb(f"rows{k}", [P, 2, D]) for k in range(2)]
        g_t = [st.sb(f"rows_t{s}", [P, P]) for s in range(2)]
        silu = [st.sb(f"silu{s}", [P, HC * P]) for s in range(2)] if gated else None
        hid = [st.sb(f"hidden{s}", [P, HC * P]) for s in range(2)]
        hid_t = [st.sb(f"hidden_t{s}", [P, HC * P]) for s in range(2)]
        o = [st.sb(f"out{k}", [P, 2, D]) for k in range(2)]
        ps_g = [st.ps(f"ps_rows{s}", [P, 512]) for s in range(2)]
        ps_u = [st.ps(f"ps_up{s}", [P, 512]) for s in range(2)]
        ps_h = [st.ps(f"ps_hidden{s}", [P, 512]) for s in range(2)]
        ps_o = [st.ps(f"ps_out{s}", [P, 512]) for s in range(2)]
        g_loaded = [st.sem(f"rows_loaded{k}") for k in range(2)]
        stored = [st.sem(f"out_stored{k}", 16) for k in range(2)]
        g_t_ps, g_t_ready, up_done, silu_ready, hid_ready, hid_t_ps, hid_t_ready, down_done, o_ready = [
            st.sem(n, CREDIT) for n in ("rows_transposed", "rows_t_ready", "up_done", "silu_ready", "hidden_ready",
                                        "hidden_transposed", "hidden_t_ready", "down_done", "out_ready")]
        def load_experts(eng, i):
            if eng is not nc.tensor and (gated or eng is not nc.vector):
                return [None] * 8
            _, e = nc.values_load_multi_w_load_instructions(
                expert_of[0:1, i if isinstance(i, int) else bass.ds(i, 1), :], engines=(eng.engine,), min_val=0, max_val=E - 1,
                skip_runtime_bounds_check_because="each is a count from 1 to E less 1")
            return e

        def turns(eng, turn):
            def of(experts, s):
                return lambda d: experts[s + 1 + d]

            experts = load_experts(eng, 0)
            for s in range(TURNS):
                turn(s, 0, s, lambda d: 0 <= s + d, of(experts, s))
            with eng.Fori(1, Q // TURNS - 1) as i:
                experts = load_experts(eng, i)
                for s in range(TURNS):
                    turn(i * TURNS + s, i, s, lambda d: True, of(experts, s))
            for i in (Q // TURNS - 1, Q // TURNS):
                experts = load_experts(eng, i)
                for s in range(TURNS if i * TURNS < Q else 1):
                    turn(i * TURNS + s, i, s, lambda d: i * TURNS + s + d < Q, of(experts, s))

        def other(i, s, d):
            return i + (s + d) // TURNS, (s + d) % TURNS

        with st.block() as block:
            @block.sync
            def _(sp):
                def load(n, i, k):
                    sp.dma_start(g[k][:], core.sorted_in[bass.ds(n * P, 2 * P), :].rearrange("(t p) d -> p t d", p=P)).then_inc(g_loaded[k], 16)

                def turn(n, i, s, inside, e):
                    if s % 2 == 0 and inside(4):
                        sp.wait_ge(g_t_ps, done(n + 1))
                        load(n + 4, i + 1, s // 2)
                    if s % 2 == 0 and inside(-1):
                        i1, s1 = other(i, s, -1)
                        sp.wait_ge(o_ready, done(n - 1))
                        sp.dma_start(core.sorted_out[bass.ds((n - 2) * P, 2 * P), :].rearrange("(t p) d -> p t d", p=P),
                                     o[s1 // 2][:]).then_inc(stored[s1 // 2], 16)

                load(0, 0, 0)
                load(2, 0, 1)
                turns(sp, turn)
                for k in range(2):
                    sp.wait_ge(stored[k], 16 * (Q // TURNS + 1))

            @block.tensor
            def _(pe):
                def transpose_rows(n, i, s):
                    pe.wait_ge(g_t_ready, freed(n))
                    pe.wait_ge(g_loaded[s // 2], i * 16 + 16)
                    nc.tensor.transpose(ps_g[s % 2][:, 0:P], g[s // 2][:, s % 2, :], core.ident[:]).then_inc(g_t_ps, 1)

                def up(n, i, s, e):
                    pe.wait_ge(g_t_ready, done(n))
                    pe.wait_ge(hid_ready, freed(n))
                    nc.tensor.matmul(ps_u[s % 2][:], g_t[s % 2][:], wu[:, bass.ds(e * UP, UP)], start=True, stop=True).then_inc(up_done, 1)

                def turn(n, i, s, inside, e):
                    if inside(1):
                        up(n + 1, *other(i, s, 1), e(1))
                    if inside(0):
                        pe.wait_ge(hid_ready, done(n))
                        pe.wait_ge(hid_t_ready, freed(n))
                        for c in range(HC):
                            last = nc.tensor.transpose(ps_h[s % 2][:, c * P:(c + 1) * P], hid[s % 2][:, c * P:(c + 1) * P], core.ident[:])
                        last.then_inc(hid_t_ps, 1)
                    if inside(2):
                        transpose_rows(n + 2, *other(i, s, 2))
                    if inside(-1):
                        i1, s1 = other(i, s, -1)
                        pe.wait_ge(hid_t_ready, done(n - 1))
                        pe.wait_ge(o_ready, freed(n - 1))
                        for c in range(HC):
                            last = nc.tensor.matmul(ps_o[s1 % 2][:, 0:D], hid_t[s1 % 2][:, c * P:(c + 1) * P],
                                                    wd[:, bass.ds(e(-1) * (HC * D) + c * D, D)], start=c == 0, stop=c == HC - 1)
                        last.then_inc(down_done, 1)

                pe.wait_ge(weights, 16 * weight_loads)
                transpose_rows(0, 0, 0)
                transpose_rows(1, 0, 1)
                up(0, 0, 0, load_experts(pe, 0)[1])
                turns(pe, turn)

            @block.scalar
            def _(act):
                def rows_out(n, i, s):
                    act.wait_ge(g_t_ps, done(n))
                    act.wait_ge(up_done, freed(n))
                    nc.scalar.copy(g_t[s % 2][:], ps_g[s % 2][:, 0:P]).then_inc(g_t_ready, 1)

                def gate(n, i, s):
                    if gated:
                        act.wait_ge(up_done, done(n))
                        act.wait_ge(hid_ready, freed(n))
                        nc.scalar.activation(silu[s % 2][:], ps_u[s % 2][:, 0:HC * P], ACT.Silu).then_inc(silu_ready, 1)

                def turn(n, i, s, inside, e):
                    if inside(1):
                        gate(n + 1, *other(i, s, 1))
                    if inside(0):
                        act.wait_ge(hid_t_ps, done(n))
                        act.wait_ge(down_done, freed(n))
                        nc.scalar.activation(hid_t[s % 2][:], ps_h[s % 2][:, 0:HC * P], ACT.Copy if gated else ACT.Relu).then_inc(hid_t_ready, 1)
                    if inside(2):
                        rows_out(n + 2, *other(i, s, 2))

                rows_out(0, 0, 0)
                rows_out(1, 0, 1)
                gate(0, 0, 0)
                turns(act, turn)

            @block.vector
            def _(dve):
                def hidden(n, i, s, e):
                    dve.wait_ge(hid_t_ps, freed(n))
                    if gated:
                        dve.wait_ge(silu_ready, done(n))
                        nc.vector.tensor_tensor(hid[s % 2][:], silu[s % 2][:], ps_u[s % 2][:, HC * P:2 * HC * P], ALU.mult).then_inc(hid_ready, 1)
                    else:
                        dve.wait_ge(up_done, done(n))
                        nc.vector.tensor_tensor(hid[s % 2][:], ps_u[s % 2][:], bu[:, bass.ds(e * UP, UP)], ALU.add).then_inc(hid_ready, 1)

                def turn(n, i, s, inside, e):
                    if inside(1):
                        hidden(n + 1, *other(i, s, 1), e(1))
                    if inside(-1):
                        i1, s1 = other(i, s, -1)
                        dve.wait_ge(down_done, done(n - 1))
                        if s1 % 2 == 0:
                            dve.wait_ge(stored[s1 // 2], i1 * 16 + 16)
                        if gated:
                            nc.vector.tensor_scalar(o[s1 // 2][:, s1 % 2, :], ps_o[s1 % 2][:, 0:D], 1.0, None, ALU.mult).then_inc(o_ready, 1)
                        else:
                            nc.vector.tensor_tensor(o[s1 // 2][:, s1 % 2, :], ps_o[s1 % 2][:, 0:D], bd[:, bass.ds(e(-1) * D, D)], ALU.add).then_inc(o_ready, 1)

                if not gated:
                    dve.wait_ge(weights, 16 * weight_loads)
                hidden(0, 0, 0, load_experts(dve, 0)[1])
                turns(dve, turn)


JOINTS = 25
GROUPS = [list(range(25)), [0, 1, 2, 3, 4, 5, 6, 7, 8], [0, 9, 10, 11, 12, 13, 14], [6, 7, 8, 12, 13, 14], [3, 4, 5, 9, 10, 11]]
QUAD = 32
SHARING = P // QUAD
PACKS = B // SHARING


def group_masks():
    member = np.zeros((len(GROUPS), QUAD), np.float32)
    for g, nodes in enumerate(GROUPS):
        member[g, nodes] = 1
    pairs = np.zeros((len(GROUPS), P, P), np.float32)
    for q in range(SHARING):
        part = slice(q * QUAD, (q + 1) * QUAD)
        pairs[:, part, part] = member[:, :, None] * member[:, None, :]
    return pairs, np.ascontiguousarray(np.tile(member, (1, SHARING)).T)


def grouped_graph_block(nc, core, adj_t, w1, b1, w2, b2, fusion_w, pair_mask, row_mask):
    G, HID = len(GROUPS), w1.shape[2]
    HC = HID // P
    HALF = PACKS // 2
    with Stage(nc, "groups") as st:
        a_t = st.sb("adj_t", [P, PACKS, P])
        a_g = st.sb("group_adj_t", [P, PACKS, P])
        masks = st.sb("pair_mask", [P, G, P])
        rows = st.sb("row_mask", [P, G])
        w1_sb = st.sb("w1", [P, G * HID])
        b1_sb = st.sb("b1", [P, G * HID])
        w2_sb = st.sb("w2", [P, G * HC * D])
        b2_sb = st.sb("b2", [P, G * D])
        fuse = st.sb("fusion", [P, G])
        stat = st.sb("fusion_stat", [P, 2])
        deg = st.sb("degree", [P, PACKS])
        empty = st.sb("empty", [P, PACKS])
        dinv = st.sb("dinv", [P, PACKS])
        y = st.sb("y", [P, PACKS, D])
        ys = st.sb("y_scaled", [P, PACKS, D])
        quad0 = st.sb("quad0", [QUAD, PACKS, D])
        u_t = [st.sb(f"spread_t{h}", [P, HALF * P]) for h in range(2)]
        hid = [st.sb(f"hidden{h}", [P, HALF, HID]) for h in range(2)]
        v_t = [st.sb(f"hidden_spread_t{h}", [P, HALF * HC * P]) for h in range(2)]
        out = st.sb("out", [P, HALF, D])
        fused = st.sb("fused", [P, PACKS, D])
        ps_d = st.ps("ps_degree", [P, 512])
        ps_u = st.ps("ps_spread", [P, 512])
        ps_h = [st.ps(f"ps_hidden{j}", [P, 512]) for j in range(2)]
        ps_v = [st.ps(f"ps_hidden_spread{j}", [P, 512]) for j in range(2)]
        ps_o = st.ps("ps_out", [P, 512])
        cleared, loaded, own, fuse_in, fuse_out = [st.sem(n) for n in ("cleared", "loaded", "vector_steps", "fusion_in", "fusion_exp")]
        a_ready, deg_ps, deg_ready, root_ready, ys_ready = [st.sem(n) for n in (
            "group_adj_ready", "degree_product", "degree_ready", "root_ready", "y_scaled_ready")]
        u_ps, u_ready, h_ps, h_ready, v_ps, v_ready, o_ps = [st.sem(n) for n in (
            "spread_product", "spread_ready", "hidden_product", "hidden_ready", "hidden_spread_product", "hidden_spread_ready", "out_product")]
        with st.block() as block:
            @block.gpsimd
            def _(pool):
                nc.gpsimd.memset(a_t[:], 0.0).then_inc(cleared, 1)
                nc.gpsimd.memset(fused[:], 0.0).then_inc(cleared, 1)

            LOADS = 7 + SHARING
            BEFORE = 6 + 2 * SHARING
            OWN = 4 + 2 + 1 + 2 * 3

            @block.sync
            def _(sp):
                def row(a, n):
                    return a.rearrange("(a n) -> a n", a=1).to_broadcast([P, n])
                sp.dma_start(w1_sb[:].rearrange("p (g f) -> p g f", g=G), w1.rearrange("g d f -> d g f")).then_inc(loaded, 16)
                sp.dma_start(w2_sb[:].rearrange("p (g c f) -> p g c f", g=G, c=HC), w2.rearrange("g (c p) f -> p g c f", p=P)).then_inc(loaded, 16)
                sp.dma_start(b1_sb[:], row(b1.rearrange("g f -> (g f)"), G * HID)).then_inc(loaded, 16)
                sp.dma_start(b2_sb[:], row(b2.rearrange("g f -> (g f)"), G * D)).then_inc(loaded, 16)
                sp.dma_start(fuse[:], row(fusion_w, G)).then_inc(loaded, 16)
                sp.dma_start(masks[:], pair_mask.rearrange("g p n -> p g n")).then_inc(loaded, 16)
                sp.dma_start(rows[:], row_mask).then_inc(loaded, 16)
                sp.wait_ge(cleared, 2)
                for q in range(SHARING):
                    src = adj_t.rearrange("(k q) m n -> q m k n", q=SHARING)[q, 0:JOINTS, :, 0:JOINTS]
                    sp.dma_start(a_t[q * QUAD:q * QUAD + JOINTS, :, q * QUAD:q * QUAD + JOINTS], src).then_inc(loaded, 16)

            @block.tensor
            def _(pe):
                mm = nc.tensor.matmul
                with pe.Fori(0, G) as g:
                    pe.wait_ge(a_ready, g + 1)
                    for k in range(PACKS):
                        last = mm(ps_d[:, k:k + 1], a_g[:, k, :], core.ones[:, 0:1], start=True, stop=True)
                    last.then_inc(deg_ps, 1)
                    pe.wait_ge(ys_ready, g + 1)
                    for h in range(2):
                        if h:
                            pe.wait_ge(u_ready, g * 2 + h)
                        for k in range(HALF):
                            last = mm(ps_u[:, k * P:(k + 1) * P], ys[:, h * HALF + k, :], a_g[:, h * HALF + k, :], start=True, stop=True)
                        last.then_inc(u_ps, 1)
                    for h in range(2):
                        pe.wait_ge(u_ready, g * 2 + h + 1)
                        if h:
                            pe.wait_ge(h_ready, g * 2 + h)
                        for k in range(HALF):
                            last = mm(ps_h[k // 2][:, k % 2 * HID:(k % 2 + 1) * HID], u_t[h][:, k * P:(k + 1) * P],
                                      w1_sb[:, bass.ds(g * HID, HID)], start=True, stop=True)
                        last.then_inc(h_ps, 1)
                    for h in range(2):
                        pe.wait_ge(h_ready, g * 2 + h + 1)
                        if h:
                            pe.wait_ge(v_ready, g * 2 + h)
                        for k in range(HALF):
                            for c in range(HC):
                                last = mm(ps_v[k // 2][:, (k % 2 * HC + c) * P:(k % 2 * HC + c + 1) * P],
                                          hid[h][:, k, c * P:(c + 1) * P], a_g[:, h * HALF + k, :], start=True, stop=True)
                        last.then_inc(v_ps, 1)
                    for h in range(2):
                        pe.wait_ge(v_ready, g * 2 + h + 1)
                        if h:
                            pe.wait_ge(own, g * OWN + (BEFORE + OWN - 5))
                        for k in range(HALF):
                            for c in range(HC):
                                last = mm(ps_o[:, k * D:(k + 1) * D], v_t[h][:, (k * HC + c) * P:(k * HC + c + 1) * P],
                                          w2_sb[:, bass.ds(g * (HC * D) + c * D, D)], start=c == 0, stop=c == HC - 1)
                        last.then_inc(o_ps, 1)

            @block.scalar
            def _(act):
                act.wait_ge(fuse_in, 1)
                nc.scalar.activation(fuse[:], fuse[:], ACT.Exp).then_inc(fuse_out, 1)
                with act.Fori(0, G) as g:
                    act.wait_ge(deg_ready, g + 1)
                    nc.scalar.activation(deg[:], deg[:], ACT.Sqrt).then_inc(root_ready, 1)
                    for h in range(2):
                        act.wait_ge(u_ps, g * 2 + h + 1)
                        nc.scalar.copy(u_t[h][:], ps_u[:]).then_inc(u_ready, 1)
                    for h in range(2):
                        act.wait_ge(v_ps, g * 2 + h + 1)
                        for j in range(2):
                            last = nc.scalar.copy(v_t[h][:, j * 512:(j + 1) * 512], ps_v[j][:])
                        last.then_inc(v_ready, 1)


            @block.vector
            def _(dve):
                v = nc.vector
                dve.wait_ge(loaded, 16 * LOADS)
                pre = Own(dve, own, 0, 0)
                pre.step(v.reduce_max(stat[:, 0:1], fuse[:], AXX))
                v.tensor_scalar(fuse[:], fuse[:], stat[:, 0:1], None, ALU.subtract).then_inc(fuse_in, 1)
                dve.wait_ge(fuse_out, 1)
                pre.step(v.reduce_sum(stat[:, 1:2], fuse[:], AXX))
                pre.step(v.reciprocal(stat[:, 1:2], stat[:, 1:2]))
                pre.step(v.tensor_scalar(fuse[:], fuse[:], stat[:, 1:2], None, ALU.mult))
                pre.step(v.tensor_tensor(fuse[:], fuse[:], rows[:], ALU.mult))
                pre.step(v.tensor_tensor(a_t[:], a_t[:], core.ident[:].unsqueeze(1).to_broadcast([P, PACKS, P]), ALU.add))
                for q in range(SHARING):
                    at = slice(q * HALVES, TILES, SHARING * HALVES)
                    pre.step(v.tensor_tensor(quad0[:], core.x[0:QUAD, at, :],
                                             core.mean[0:QUAD, at].unsqueeze(2).to_broadcast([QUAD, PACKS, D]), ALU.subtract))
                    pre.step(v.tensor_tensor(y[q * QUAD:(q + 1) * QUAD, :, :], quad0[:],
                                             core.rstd[0:QUAD, at].unsqueeze(2).to_broadcast([QUAD, PACKS, D]), ALU.mult))
                base = pre.k
                assert base == BEFORE
                with dve.Fori(0, G) as g:
                    mine = Own(dve, own, g, OWN)
                    mine.base = g * OWN + base
                    v.tensor_tensor(a_g[:], a_t[:], masks[:, bass.ds(g, 1), :].to_broadcast([P, PACKS, P]), ALU.mult).then_inc(a_ready, 1)
                    dve.wait_ge(deg_ps, g + 1)
                    mine.step(v.tensor_scalar(empty[:], ps_d[:, 0:PACKS], 0.0, None, ALU.is_equal))
                    v.tensor_tensor(deg[:], ps_d[:, 0:PACKS], empty[:], ALU.add).then_inc(deg_ready, 1)
                    mine.step(v.tensor_scalar(empty[:], empty[:], -1.0, 1.0, ALU.mult, ALU.add))
                    dve.wait_ge(root_ready, g + 1)
                    mine.step(v.reciprocal(dinv[:], deg[:]))
                    mine.step(v.tensor_tensor(dinv[:], dinv[:], empty[:], ALU.mult))
                    v.tensor_tensor(ys[:], y[:], dinv[:].unsqueeze(2).to_broadcast([P, PACKS, D]), ALU.mult).then_inc(ys_ready, 1)
                    for h in range(2):
                        dve.wait_ge(h_ps, g * 2 + h + 1)
                        for k in range(HALF):
                            last = v.scalar_tensor_tensor(hid[h][:, k, :], ps_h[k // 2][:, k % 2 * HID:(k % 2 + 1) * HID],
                                                          dinv[:, h * HALF + k:h * HALF + k + 1],
                                                          b1_sb[:, bass.ds(g * HID, HID)], ALU.mult, ALU.add)
                        mine.step(last)
                        for k in range(HALF):
                            last = v.tensor_scalar(hid[h][:, k, :], hid[h][:, k, :], 0.0, dinv[:, h * HALF + k:h * HALF + k + 1], ALU.max, ALU.mult)
                        last.then_inc(h_ready, 1)
                    mine.step(v.tensor_copy(stat[:, 0:1], fuse[:, bass.ds(g, 1)]))
                    for h in range(2):
                        dve.wait_ge(o_ps, g * 2 + h + 1)
                        for k in range(HALF):
                            last = v.scalar_tensor_tensor(out[:, k, :], ps_o[:, k * D:(k + 1) * D], dinv[:, h * HALF + k:h * HALF + k + 1],
                                                          b2_sb[:, bass.ds(g * D, D)], ALU.mult, ALU.add)
                        mine.step(last)
                        mine.step(v.tensor_scalar(out[:], out[:], 0.0, stat[:, 0:1], ALU.max, ALU.mult))
                        part = fused[:, h * HALF:(h + 1) * HALF, :]
                        mine.step(v.tensor_tensor(part, part, out[:], ALU.add))
                    mine.end()
                post = Own(dve, own, 0, 0)
                post.base = base + G * OWN
                for q in range(SHARING):
                    at = slice(q * HALVES, TILES, SHARING * HALVES)
                    post.step(v.tensor_copy(quad0[:], fused[q * QUAD:(q + 1) * QUAD, :, :]))
                    post.step(v.tensor_tensor(core.x[0:QUAD, at, :], core.x[0:QUAD, at, :], quad0[:], ALU.add))


S = 16
BLOCKS = P // S
QUARTER = P // B


def recurrent_block(nc, core, adj, w_ioux_t, w_iouh_t, b_ioux, b_iouh, w_coux_t, w_couh_t, b_coux, b_couh):
    with Stage(nc, "recur") as keep:
        near_adj = [keep.sb(f"adj_within{h}", [P, B, P]) for h in range(HALVES)]
        cross_adj = keep.sb("adj_across", [P, B, P])
        y_t = keep.sb("y_t", [P, N, B])
        base = keep.sb("base", [P, N, B])
        recurrent_base(nc, core, adj, near_adj, cross_adj, y_t, base)
        with Stage(nc, "recur_states") as st:
            changes = st.sb("changes", [P, B, D])
            for half in range(HALVES):
                scan_half(nc, core, half, near_adj[half], y_t, base, changes,
                          w_ioux_t, w_iouh_t, b_ioux, b_iouh, w_coux_t, w_couh_t, b_coux, b_couh)
                if half == 0:
                    carry_changes(nc, core, cross_adj, base, changes)


def recurrent_base(nc, core, adj, near_adj, cross_adj, y_t, base):
    with Stage(nc, "recur_in") as st:
        back_adj = st.sb("adj_back", [P, B, P])
        part = [[near_adj[0], cross_adj], [back_adj, near_adj[1]]]
        y = [st.sb(f"y{s}", [P, HALVES, D]) for s in range(2)]
        degree = [st.sb(f"degree{k}", [P, HALVES, B]) for k in range(2)]
        empty = st.sb("empty", [P, HALVES, B])
        inv = st.sb("inv", [P, HALVES, B])
        diagonal = [st.sb(f"diagonal{s}", [P, HALVES, P]) for s in range(2)]
        scale = [st.sb(f"scale{s}", [P, N]) for s in range(2)]
        ps_s = [st.ps(f"ps_scale{s}", [P, 512]) for s in range(2)]
        ps_y = [st.ps(f"ps_y{s}", [P, 512]) for s in range(2)]
        ps_b = [st.ps(f"ps_base{s}", [P, 512]) for s in range(2)]
        loaded = st.sem("adj_loaded")
        inv_ready = st.sem("inv_ready")
        y_ready, x_added, y_ps, y_t_kept, diagonal_ready, scale_ps, base_ps, scaled = [st.sem(n, CREDIT) for n in (
            "y_ready", "x_added", "y_transposed", "y_t_kept", "diagonal_ready", "scale_spread", "base_product", "adj_scaled")]
        own, own_turn, inv_done, passed, passed_a = st.sem("vector_first_steps"), st.sem("vector_steps"), st.sem("inv_done"), st.sem("pool_passed"), st.sem("scalar_passed")
        with st.block() as block:
            @block.sync
            def _(sp):
                for j in range(HALVES):
                    for i in range(HALVES):
                        sp.dma_start(part[j][i][:], adj[:, j * P:(j + 1) * P, i * P:(i + 1) * P].rearrange("b p n -> p b n")).then_inc(loaded, 16)

            @block.tensor
            def _(pe):
                pe.wait_ge(loaded, 64)
                with pe.Fori(0, B // 2) as i:
                    for s in range(2):
                        n = i * 2 + s
                        pe.wait_ge(y_t_kept, freed(n))
                        pe.wait_ge(y_ready, done(n))
                        for k in range(HALVES):
                            last = nc.tensor.transpose(ps_y[s][:, k * P:(k + 1) * P], y[s][:, k, :], core.ident[:])
                        last.then_inc(y_ps, 1)
                        pe.wait_ge(scaled, freed(n))
                        pe.wait_ge(diagonal_ready, done(n))
                        nc.tensor.matmul(ps_s[s][:, 0:N], core.ones[:], diagonal[s][:].rearrange("p h i -> p (h i)"), start=True, stop=True).then_inc(scale_ps, 1)
                        for k in range(HALVES):
                            for j in range(HALVES):
                                last = nc.tensor.matmul(ps_b[s][:, k * P:(k + 1) * P], y[s][:, j, :], part[j][k][:, n, :],
                                                        start=j == 0, stop=j == HALVES - 1)
                        last.then_inc(base_ps, 1)

            @block.gpsimd
            def _(pool):
                with pool.Fori(0, B // 2) as i:
                    for s in range(2):
                        n = i * 2 + s
                        pool.wait_ge(y_ready, done(n))
                        hold(pool, passed)
                        here = core.x[:, bass.ds(n * HALVES, HALVES), :]
                        nc.gpsimd.tensor_tensor(here, here, y[s][:], ALU.add).then_inc(x_added, 1)

            @block.scalar
            def _(act):
                act.wait_ge(inv_ready, 1)
                with act.Fori(0, B // 2) as i:
                    for s in range(2):
                        n = i * 2 + s
                        act.wait_ge(scale_ps, freed(n))
                        hold(act, passed_a)
                        for k in range(HALVES):
                            last = nc.scalar.activation(diagonal[s][:, k, :], core.ident[:], ACT.Copy, scale=inv[:, k, bass.ds(n, 1)])
                        last.then_inc(diagonal_ready, 1)
                    for s in range(2):
                        n = i * 2 + s
                        act.wait_ge(y_ps, done(n))
                        hold(act, passed_a)
                        nc.scalar.activation(y_t[:, :, n], ps_y[s][:, 0:N], ACT.Copy).then_inc(y_t_kept, 1)

            @block.vector
            def _(dve):
                v = nc.vector
                first = Own(dve, own, 0, 4)
                for j in range(HALVES):
                    dve.wait_ge(loaded, 64)
                    for i in range(HALVES):
                        last = v.tensor_reduce(degree[i][:, j, :], part[j][i][:], AXX, ALU.add)
                first.step(last)
                first.step(v.tensor_tensor(degree[0][:], degree[0][:], degree[1][:], ALU.add))
                first.step(v.tensor_scalar(empty[:], degree[0][:], 0.0, None, ALU.is_equal))
                first.step(v.tensor_tensor(inv[:], degree[0][:], empty[:], ALU.add))
                v.reciprocal(inv[:], inv[:]).then_inc(inv_done, 1)
                dve.wait_ge(inv_done, 1)
                v.scalar_tensor_tensor(inv[:], empty[:], 0.0, inv[:], ALU.is_equal, ALU.mult).then_inc(inv_ready, 1)
                with dve.Fori(0, B // 2) as i:
                    mine = Own(dve, own_turn, i, 2)
                    for s in range(2):
                        n = i * 2 + s
                        dve.wait_ge(base_ps, freed(n))
                        dve.wait_ge(x_added, freed(n))
                        for k in range(HALVES):
                            t = n * 2 + k
                            last = v.tensor_scalar(y[s][:, k, :], core.x[:, t, :], core.mean[:, bass.ds(t, 1)],
                                                   core.rstd[:, bass.ds(t, 1)], ALU.subtract, ALU.mult)
                        last.then_inc(y_ready, 1)
                    for s in range(2):
                        n = i * 2 + s
                        dve.wait_ge(scale_ps, done(n))
                        mine.step(v.tensor_scalar(scale[s][:], ps_s[s][:, 0:N], 1.0, None, ALU.mult))
                        dve.wait_ge(base_ps, done(n))
                        v.tensor_tensor(base[:, :, n], ps_b[s][:, 0:N], scale[s][:], ALU.mult)
                        for a, k in ((near_adj[0], 0), (cross_adj, 1), (near_adj[1], 1)):
                            last = v.tensor_tensor(a[:, n, :], a[:, n, :], scale[s][:, k * P:(k + 1) * P], ALU.mult)
                        last.then_inc(scaled, 1)
                    mine.end()


def carry_changes(nc, core, cross_adj, base, changes):
    FOUR = 512 // P
    with Stage(nc, "recur_carry") as st:
        ps = [st.ps(f"ps_part{s}", [P, 512]) for s in range(2)]
        multiplied, added = [st.sem(n, CREDIT) for n in ("part_product", "part_added")]
        with st.block() as block:
            @block.tensor
            def _(pe):
                for q in range(B // FOUR):
                    pe.wait_ge(added, freed(q))
                    for k in range(FOUR):
                        b = q * FOUR + k
                        last = nc.tensor.matmul(ps[q % 2][:, k * P:(k + 1) * P], changes[:, b, :], cross_adj[:, b, :], start=True, stop=True)
                    last.then_inc(multiplied, 1)

            @block.vector
            def _(dve):
                for q in range(B // FOUR):
                    dve.wait_ge(multiplied, done(q))
                    here = base[:, P:N, q * FOUR:(q + 1) * FOUR]
                    nc.vector.tensor_tensor(here, here, ps[q % 2][:].rearrange("p (b i) -> p i b", b=FOUR), ALU.add).then_inc(added, 1)


def scan_half(nc, core, half, adj, y_t, base, changes, w_ioux_t, w_iouh_t, b_ioux, b_iouh, w_coux_t, w_couh_t, b_coux, b_couh):
    HALF_S = S // 2
    GROUPS = S // QUARTER
    MOVES = 16 * GROUPS
    EARLIER = {2: (0, 1), 3: (0, 1), 4: (0, 2), 5: (0, 2), 6: (1, 3), 7: (1, 3), 8: (0, 3), 9: (0, 3), 10: (0, 4), 11: (0, 4), 12: (0, 4)}
    assert sum(a + b for a, b in EARLIER.values()) == B
    with Stage(nc, f"recur_scan{half}") as st:
        wx = st.sb("wx", [P, 3, P])
        wh = st.sb("wh", [P, 3, P])
        bias = st.sb("bias", [P, 2, 3])
        same_graph = st.sb("same_graph", [P, B])
        pick = [st.sb(f"pick{p}", [P, S]) for p in range(2)]
        sums = [st.sb(f"sums{p}", [P, S, B]) for p in range(2)]
        delta = [st.sb(f"delta{p}", [P, S, B]) for p in range(2)]
        delta_t = [st.sb(f"delta_t{p}", [P, GROUPS, D]) for p in range(2)]
        rows = [st.sb(f"adj_rows{p}", [P, GROUPS, S]) for p in range(2)]
        spread_adj = st.sb("adj_spread", [P, GROUPS, S, B])
        r, xr, cand, keep_part, lag, minus_slope, offset, minus_fresh = [st.sb(n, [P, B]) for n in (
            "reset", "reset_sum", "candidate", "kept", "kept_minus_old", "minus_slope", "offset", "minus_fresh")]
        z = [st.sb(f"update{k}", [P, B]) for k in range(2)]
        near = st.sb("near", [P, B])
        far = st.sb("far", [P, S, B])
        ps_rc = [st.ps(f"ps_reset_candidate{k}", [P, 2, HALF_S, B]) for k in range(2)]
        ps_z = [st.ps(f"ps_update{k}", [P, 512]) for k in range(2)]
        ps_coef = [st.ps(f"ps_coefs{k}", [P, 512]) for k in range(2)]
        ps_sum = st.ps("ps_sums", [P, 512])
        ps_tr = st.ps("ps_delta_t", [P, 512])
        loaded, copied, own, b_ready, consts = [st.sem(n) for n in ("loaded", "adj_copied", "vector_steps", "bias_ready", "constants_ready")]
        rows_loaded = [st.sem(f"adj_rows_loaded{p}") for p in range(2)]
        node_sum, r_ps, z_ps, r_ready, z_ready, xr_ready, cand_ps, cand_ready, spread = [st.sem(n) for n in (
            "node_sum_ready", "reset_product", "update_product", "reset_ready", "update_ready", "reset_sum_ready",
            "candidate_product", "candidate_ready", "coefs_used")]
        delta_ready, tr_ps, tr_ready, earlier_ps, sums_taken, pick_ready = [st.sem(n) for n in (
            "delta_ready", "delta_transposed", "delta_t_ready", "earlier_changes_product", "sums_taken", "pick_ready")]
        coef_ps = st.sem("coefs_product", 2 * (S - 1))
        pushed = st.sem("delta_product", GROUPS)
        spread_ready = st.sem("adj_spread_ready", 2 * GROUPS)
        moved = st.sem("changes_moved", 2 * MOVES)
        passed = st.sem("pool_passed")

        def following(i, p):
            return i * 2 + 1 if p == 0 else ((i + 1) % (BLOCKS // 2)) * 2

        with st.block() as block:
            @block.sync
            def _(sp):
                col = lambda a, n: a.rearrange("(n p) -> p n", p=P)
                sp.dma_start(core.adj_rows.rearrange("(p b) i -> p b i", b=B), adj[:]).then_inc(copied, 16)
                sp.dma_start(wx[:, 0:2, :], w_ioux_t.rearrange("d (g f) -> d g f", g=2)).then_inc(loaded, 16)
                sp.dma_start(wh[:, 0:2, :], w_iouh_t.rearrange("d (g f) -> d g f", g=2)).then_inc(loaded, 16)
                sp.dma_start(wx[:, 2, :], w_coux_t).then_inc(loaded, 16)
                sp.dma_start(wh[:, 2, :], w_couh_t).then_inc(loaded, 16)
                with nc.allow_non_contiguous_dma("six columns of bias"):
                    sp.dma_start(bias[:, 0, 0:2], col(b_ioux, 2)).then_inc(loaded, 16)
                    sp.dma_start(bias[:, 1, 0:2], col(b_iouh, 2)).then_inc(loaded, 16)
                    sp.dma_start(bias[:, 0, 2:3], col(b_coux, 1)).then_inc(loaded, 16)
                    sp.dma_start(bias[:, 1, 2:3], col(b_couh, 1)).then_inc(loaded, 16)
                sp.wait_ge(copied, 16)
                for n in range(BLOCKS):
                    p = n % 2
                    sp.wait_ge(spread_ready, n * GROUPS + GROUPS)
                    sp.dma_start(rows[p][:], core.adj_rows[n * S * B:(n + 1) * S * B, (n + 1) % BLOCKS * S:(n + 1) % BLOCKS * S + S]
                                 .rearrange("(g p) i -> p g i", p=P)).then_inc(rows_loaded[p], 16)
                    sp.wait_ge(earlier_ps, n + 1)
                    sp.wait_ge(tr_ready, n * GROUPS + GROUPS)
                    for g in range(GROUPS):
                        sp.dma_start(changes[n * S + g * QUARTER:n * S + (g + 1) * QUARTER, :, :], delta_t[p][:, g, :]).then_inc(moved, 16)

            @block.gpsimd
            def _(pool):
                nc.gpsimd.memset(changes[:], 0.0).then_inc(consts, 1)
                pool.wait_ge(consts, 2)
                with pool.Fori(0, BLOCKS // 2) as i:
                    for p in range(2):
                        n = i * 2 + p
                        pool.wait_ge(coef_ps, n * (S - 1) + S - 1)
                        hold(pool, passed)
                        nc.gpsimd.tensor_copy(pick[p][:], core.ident[:, bass.ds(n * S, S)]).then_inc(pick_ready, 1)
                        pool.wait_ge(rows_loaded[p], i * 16 + 16)
                        for g in range(GROUPS):
                            pool.wait_ge(pushed, n * GROUPS + g + 1)
                            hold(pool, passed)
                            nc.gpsimd.tensor_tensor(spread_adj[:, g, :, :], rows[p][:, g, :].unsqueeze(2).to_broadcast([P, S, B]),
                                                    same_graph[:].unsqueeze(1).to_broadcast([P, S, B]), ALU.mult).then_inc(spread_ready, 1)

                nc.gpsimd.tensor_copy(pick[0][:], core.ident[:, 0:S]).then_inc(pick_ready, 1)

            @block.tensor
            def _(pe):
                def mm(out, lhs, rhs, start=False, stop=False):
                    return nc.tensor.matmul(out, lhs, rhs, start=start, stop=stop, skip_group_check=True)

                def own_part(n, k, piece):
                    gate, q = (0, 0, 2, 2, 1, 1)[piece], piece % 2
                    nodes = slice(q * QUARTER, (q + 1) * QUARTER)
                    rhs = y_t[:, bass.ds(n * S + (half * P + k * HALF_S + q * QUARTER), QUARTER), :]
                    if gate == 1:
                        mm(ps_z[k][:, q * P:(q + 1) * P], wx[:, 1, :], rhs, start=piece == 4)
                    else:
                        mm(ps_rc[k][:, gate // 2, nodes, :], wx[:, gate, :], rhs, start=piece == 0)

                def coefs(n, p, u, before):
                    later = S - 1 - u
                    if before is not None:
                        pe.wait_ge(spread, before)
                    rhs = adj[:, :, bass.ds(n * S + (u + 1), later)].rearrange("p b i -> p i b")
                    mm(ps_coef[u % 2][:, 0:later * B], pick[p][:, u:u + 1].to_broadcast([P, P]), rhs, start=True, stop=True).then_inc(coef_ps, 1)

                def transpose_delta(n, p, g):
                    pe.wait_ge(delta_ready, n * GROUPS + g + 1)
                    nc.tensor.transpose(ps_tr[:, g * P:(g + 1) * P], delta[p][:, g * QUARTER:(g + 1) * QUARTER, :].rearrange("p i b -> p (i b)"),
                                        core.ident[:]).then_inc(tr_ps, 1)

                def push(n, p, g):
                    pe.wait_ge(spread_ready, n * GROUPS + g + 1 + 2 * GROUPS)
                    pe.wait_ge(tr_ready, n * GROUPS + g + 1)
                    return mm(ps_sum[:], delta_t[p][:, g, :], spread_adj[:, g, :, :].rearrange("p i b -> p (i b)"), stop=g == GROUPS - 1)

                pe.wait_ge(loaded, 128)
                for piece in range(6):
                    own_part(0, 0, piece)
                pe.wait_ge(pick_ready, 1)
                coefs(0, 0, 0, None)
                with pe.Fori(0, BLOCKS // 2) as i:
                    for p in range(2):
                        n = i * 2 + p
                        after = following(i, p)
                        graphs = iter(range(B))

                        def earlier(count):
                            for _ in range(count):
                                g = next(graphs)
                                last = mm(ps_sum[:, g:(S - 1) * B + g + 1:B], changes[:, g, :], adj[:, g, bass.ds(after * S, S)], start=g == 0)
                                if g == B - 1:
                                    last.then_inc(earlier_ps, 1)

                        for u in range(S):
                            t = n * S + u
                            pe.wait_ge(node_sum, t + 1)
                            part, v = ps_rc[u // HALF_S], u % HALF_S
                            mm(part[:, 0, v, :], wh[:, 0, :], sums[p][:, u, :]).then_inc(r_ps, 1)
                            mm(ps_z[u // HALF_S][:, v * B:(v + 1) * B], wh[:, 1, :], sums[p][:, u, :]).then_inc(z_ps, 1)
                            if u < 6:
                                own_part(n, 1, u)
                            elif HALF_S <= u < HALF_S + 6:
                                own_part(after, 0, u - HALF_S)
                            if u in EARLIER:
                                earlier(EARLIER[u][0])
                            pe.wait_ge(xr_ready, t + 1)
                            mm(part[:, 1, v, :], wh[:, 2, :], xr[:]).then_inc(cand_ps, 1)
                            if u + 1 < S - 1:
                                coefs(n, p, u + 1, n * (S - 1) + u if u >= 1 else None)
                            if u == S - 1:
                                pe.wait_ge(pick_ready, n + 2)
                                coefs(after, 1 - p, 0, n * (S - 1) + S - 1)
                            if u == min(EARLIER):
                                pe.wait_ge(consts, 2)
                                pe.wait_ge(moved, n * MOVES + 2 * MOVES)
                                pe.wait_ge(sums_taken, n + 1)
                            if u in EARLIER:
                                earlier(EARLIER[u][1])
                            if u % QUARTER == 1 and u > QUARTER:
                                transpose_delta(n, p, u // QUARTER - 1)
                            if u > S - GROUPS:
                                push(n, p, u - (S - GROUPS + 1)).then_inc(pushed, 1)
                        transpose_delta(n, p, GROUPS - 1)
                        push(n, p, GROUPS - 1).then_inc(pushed, 1)

            @block.scalar
            def _(act):
                a = nc.scalar.activation
                act.wait_ge(b_ready, 1)
                with act.Fori(0, BLOCKS // 2) as i:
                    for p in range(2):
                        for u in range(S):
                            t = (i * 2 + p) * S + u
                            part, v = ps_rc[u // HALF_S], u % HALF_S
                            act.wait_ge(r_ps, t + 1)
                            a(r[:], part[:, 0, v, :], ACT.Sigmoid, bias=bias[:, 0, 0:1]).then_inc(r_ready, 1)
                            act.wait_ge(z_ps, t + 1)
                            a(z[u % 2][:], ps_z[u // HALF_S][:, v * B:(v + 1) * B], ACT.Sigmoid, bias=bias[:, 0, 1:2]).then_inc(z_ready, 1)
                            act.wait_ge(cand_ps, t + 1)
                            a(cand[:], part[:, 1, v, :], ACT.Tanh, bias=bias[:, 0, 2:3]).then_inc(cand_ready, 1)

            @block.vector
            def _(dve):
                v = nc.vector
                v.tensor_reduce(same_graph[:], core.ident[:].rearrange("p (j b) -> p b j", b=B), AXX, ALU.add).then_inc(consts, 1)
                v.tensor_scalar(sums[0][:], base[:, half * P:half * P + S, :], 1.0, None, ALU.mult).then_inc(node_sum, 1)
                v.engine_nop().then_inc(sums_taken, 1)
                dve.wait_ge(loaded, 128)
                v.tensor_tensor(bias[:, 0, :], bias[:, 0, :], bias[:, 1, :], ALU.add).then_inc(b_ready, 1)
                dve.wait_ge(node_sum, 1)
                per = S * 3 + (S - 1) * 4 + (S - 2) * 2 - (GROUPS - 1)
                with dve.Fori(0, BLOCKS // 2) as i:
                    for p in range(2):
                        n = i * 2 + p
                        mine = Own(dve, own, n, per)

                        def keep_delta_t(g):
                            dve.wait_ge(tr_ps, n * GROUPS + g + 1)
                            if g == 0:
                                dve.wait_ge(moved, n * MOVES + MOVES)
                            v.tensor_scalar(delta_t[p][:, g, :], ps_tr[:, g * P:(g + 1) * P], 1.0, None, ALU.mult).then_inc(tr_ready, 1)

                        for u in range(S):
                            t = n * S + u
                            later = S - 1 - u
                            coef = ps_coef[u % 2]
                            dve.wait_ge(r_ready, t + 1)
                            v.tensor_tensor(xr[:], sums[p][:, u, :], r[:], ALU.mult).then_inc(xr_ready, 1)
                            dve.wait_ge(z_ready, t + 1)
                            mine.step(v.tensor_tensor(keep_part[:], sums[p][:, u, :], z[u % 2][:], ALU.mult))
                            mine.mark(v.tensor_tensor(lag[:], keep_part[:], y_t[:, half * P + t, :], ALU.subtract))
                            if later:
                                dve.wait_ge(coef_ps, n * (S - 1) + u + 1 + 2 * (S - 1))
                                mine.step(v.scalar_tensor_tensor(minus_slope[:], z[u % 2][:], 1.0, coef[:, 0:B], ALU.subtract, ALU.mult))
                                mine.step(v.tensor_tensor(near[:], lag[:], coef[:, 0:B], ALU.mult))
                                mine.step(v.tensor_tensor(offset[:], sums[p][:, u + 1, :], near[:], ALU.add))
                            dve.wait_ge(cand_ready, t + 1)
                            if later:
                                mine.step(v.tensor_tensor(near[:], minus_slope[:], cand[:], ALU.mult))
                                v.tensor_tensor(sums[p][:, u + 1, :], offset[:], near[:], ALU.subtract).then_inc(node_sum, 1)
                            else:
                                mine.join()
                            mine.step(v.scalar_tensor_tensor(minus_fresh[:], z[u % 2][:], 1.0, cand[:], ALU.subtract, ALU.mult))
                            last = v.tensor_tensor(delta[p][:, u, :], lag[:], minus_fresh[:], ALU.subtract)
                            if u % QUARTER == QUARTER - 1:
                                last.then_inc(delta_ready, 1)
                            if later > 1:
                                if u % QUARTER == QUARTER - 1:
                                    dve.wait_ge(delta_ready, n * GROUPS + u // QUARTER + 1)
                                else:
                                    mine.step(last)
                                v.tensor_tensor(far[:, u + 2:, :], coef[:, B:later * B].rearrange("p (i b) -> p i b", b=B),
                                                delta[p][:, u, :].unsqueeze(1).to_broadcast([P, later - 1, B]), ALU.mult).then_inc(spread, 1)
                                dve.wait_ge(spread, n * (S - 1) + u + 1)
                                mine.mark(v.tensor_tensor(sums[p][:, u + 2:, :], sums[p][:, u + 2:, :], far[:, u + 2:, :], ALU.add))
                            elif later == 1:
                                v.engine_nop().then_inc(spread, 1)
                            if u % QUARTER == 2 and u > QUARTER:
                                keep_delta_t(u // QUARTER - 1)
                        mine.end()
                        keep_delta_t(GROUPS - 1)
                        dve.wait_ge(pushed, n * GROUPS + 2 * GROUPS)
                        first = following(i, p) * S + half * P
                        ps = ps_sum[:].rearrange("p (i b) -> p i b", b=B)
                        v.tensor_tensor(sums[1 - p][:, 0, :], ps[:, 0, :], base[:, first, :], ALU.add).then_inc(node_sum, 1)
                        v.tensor_tensor(sums[1 - p][:, 1:, :], ps[:, 1:, :], base[:, bass.ds(first + 1, S - 1), :], ALU.add).then_inc(sums_taken, 1)
                        dve.wait_ge(node_sum, n * S + S + 1)
                        dve.wait_ge(sums_taken, n + 2)
                dve.wait_ge(moved, BLOCKS * MOVES + 2 * MOVES)
                part = core.x[:, half::2, :]
                v.tensor_tensor(part, part, changes[:], ALU.add)


def attention_block(nc, core, adj, w, w_t, a2, gamma, beta):
    SLOPE = 0.2
    MASKED = -9000000000000000.0
    with Stage(nc, "attend") as keep:
        attended = keep.sb("attended", [P, TILES, D])
        with Stage(nc, "attention") as st:
            w_sb = st.sb("w", [P, D + 4])
            w_t_sb = st.sb("w_t", [P, D])
            a_sb = st.sb("a", [P, 2])
            wa2 = st.sb("wa2", [P, P])
            adj_sb = [st.sb(f"adj{s}", [P, HALVES, N]) for s in range(2)]
            allow = [st.sb(f"allow{s}", [P, HALVES, N]) for s in range(2)]
            y = [st.sb(f"y{s}", [P, HALVES, D]) for s in range(2)]
            y_t = [st.sb(f"y_t{s}", [P, N]) for s in range(2)]
            wh = [st.sb(f"wh{s}", [P, HALVES, D + 2]) for s in range(2)]
            e = [st.sb(f"e{s}", [P, HALVES, N]) for s in range(2)]
            low = [st.sb(f"minus_max{s}", [P, HALVES]) for s in range(2)]
            total = [st.sb(f"total{s}", [P, HALVES]) for s in range(2)]
            p = [st.sb(f"p{s}", [P, HALVES, N]) for s in range(2)]
            p_t = [st.sb(f"p_t{s}", [P, HALVES, N]) for s in range(2)]
            ps_y = [st.ps(f"ps_y{s}", [P, 512]) for s in range(2)]
            ps_w = [st.ps(f"ps_w{s}", [P, 512]) for s in range(2)]
            ps_s = [st.ps(f"ps_s{s}", [P, 512]) for s in range(2)]
            ps_p = [st.ps(f"ps_p{s}", [P, 512]) for s in range(2)]
            weights, wa_ps, wa_ready, own, passed = [st.sem(n) for n in ("weights_loaded", "wa_product", "wa_ready", "vector_steps", "pool_passed")]
            adj_loaded = [st.sem(f"adj_loaded{s}") for s in range(2)]
            y_ready, y_ps, y_t_ready, wh_ps, wh_ready, s2_ps, allow_ready, e_ready, p_ready, p_ps, p_t_ready, out_ps, out_ready = [
                st.sem(n, CREDIT) for n in ("y_ready", "y_transposed", "y_t_ready", "wh_product", "wh_ready", "s2_product",
                                            "allow_ready", "e_ready", "p_ready", "p_transposed", "p_t_ready", "out_product", "out_ready")]
            with st.block() as block:
                @block.sync
                def _(sp):
                    sp.dma_start(w_sb[:, 0:D], w).then_inc(weights, 16)
                    sp.dma_start(w_t_sb[:], w_t).then_inc(weights, 16)
                    sp.dma_start(a_sb[:], a2).then_inc(weights, 16)
                    with sp.Fori(0, B // 2) as i:
                        for s in range(2):
                            sp.wait_ge(allow_ready, freed(i * 2 + s))
                            sp.dma_start(adj_sb[s][:], adj[i * 2 + s, :, :].rearrange("(h p) n -> p h n", p=P)).then_inc(adj_loaded[s], 16)

                @block.gpsimd
                def _(pool):
                    with pool.Fori(0, B // 2) as i:
                        for s in range(2):
                            pool.wait_ge(adj_loaded[s], i * 16 + 16)
                            pool.wait_ge(e_ready, freed(i * 2 + s))
                            hold(pool, passed)
                            nc.gpsimd.tensor_scalar(allow[s][:], adj_sb[s][:], 0.0, -2.0 * MASKED, ALU.is_gt, ALU.mult).then_inc(allow_ready, 1)

                @block.tensor
                def _(pe):
                    mm = nc.tensor.matmul
                    pe.wait_ge(weights, 48)
                    mm(ps_w[0][:, 0:2], w_t_sb[:], a_sb[:], start=True, stop=True).then_inc(wa_ps, 1)
                    pe.wait_ge(wa_ready, 1)
                    with pe.Fori(0, B // 2) as i:
                        for s in range(2):
                            pe.wait_ge(out_ready, freed(i * 2 + s))
                            pe.wait_ge(y_ready, done(i * 2 + s))
                            for h in range(HALVES):
                                last = nc.tensor.transpose(ps_y[s][:, h * P:(h + 1) * P], y[s][:, h, :], core.ident[:])
                            last.then_inc(y_ps, 1)
                        for s in range(2):
                            pe.wait_ge(y_t_ready, done(i * 2 + s))
                            pe.wait_ge(wh_ready, freed(i * 2 + s))
                            for h in range(HALVES):
                                last = mm(ps_w[s][:, h * (D + 2):(h + 1) * (D + 2)], y_t[s][:, h * P:(h + 1) * P], w_sb[:, 0:D + 2], start=True, stop=True)
                            last.then_inc(wh_ps, 1)
                            pe.wait_ge(e_ready, freed(i * 2 + s))
                            mm(ps_s[s][:, 0:N], wa2[:], y_t[s][:], start=True, stop=True).then_inc(s2_ps, 1)
                        for s in range(2):
                            pe.wait_ge(p_ready, done(i * 2 + s))
                            pe.wait_ge(p_t_ready, freed(i * 2 + s))
                            for j in range(HALVES):
                                for h in range(HALVES):
                                    last = nc.tensor.transpose(ps_p[s][:, j * N + h * P:j * N + (h + 1) * P], p[s][:, h, j * P:(j + 1) * P], core.ident[:])
                            last.then_inc(p_ps, 1)
                        for s in range(2):
                            pe.wait_ge(p_t_ready, done(i * 2 + s))
                            for h in range(HALVES):
                                for j in range(HALVES):
                                    last = mm(ps_y[s][:, N + h * D:N + (h + 1) * D], p_t[s][:, j, h * P:(h + 1) * P], wh[s][:, j, 0:D],
                                              start=j == 0, stop=j == HALVES - 1)
                            last.then_inc(out_ps, 1)

                @block.scalar
                def _(act):
                    with act.Fori(0, B // 2) as i:
                        for s in range(2):
                            act.wait_ge(s2_ps, freed(i * 2 + s))
                            act.wait_ge(y_ps, done(i * 2 + s))
                            nc.scalar.copy(y_t[s][:], ps_y[s][:, 0:N]).then_inc(y_t_ready, 1)
                        for s in range(2):
                            act.wait_ge(out_ps, freed(i * 2 + s))
                            act.wait_ge(wh_ps, done(i * 2 + s))
                            nc.scalar.copy(wh[s][:], ps_w[s][:, 0:2 * (D + 2)].rearrange("p (h d) -> p h d", h=HALVES)).then_inc(wh_ready, 1)
                        for s in range(2):
                            act.wait_ge(p_ps, freed(i * 2 + s))
                            act.wait_ge(out_ready, freed(i * 2 + s))
                            act.wait_ge(e_ready, done(i * 2 + s))
                            for h in range(HALVES):
                                last = nc.scalar.activation(p[s][:, h, :], e[s][:, h, :], ACT.Exp, bias=low[s][:, h:h + 1], accum_out=total[s][:, h:h + 1])
                            last.then_inc(p_ready, 1)
                        for s in range(2):
                            act.wait_ge(out_ps, freed(i * 2 + s))
                            act.wait_ge(p_ps, done(i * 2 + s))
                            nc.scalar.copy(p_t[s][:], ps_p[s][:].rearrange("p (h n) -> p h n", h=HALVES)).then_inc(p_t_ready, 1)

                @block.vector
                def _(dve):
                    v = nc.vector
                    dve.wait_ge(wa_ps, 1)
                    pre = Own(dve, own, 0, 0)
                    pre.step(v.tensor_copy(w_sb[:, D:D + 2], ps_w[0][:, 0:2]))
                    v.tensor_copy(wa2[:], w_sb[:, D + 1:D + 2].to_broadcast([P, P])).then_inc(wa_ready, 1)
                    with dve.Fori(0, B // 2) as i:
                        mine = Own(dve, own, i, 2 * (4 + 1))
                        mine.base = i * mine.per + 1
                        for s in range(2):
                            n = i * 2 + s
                            dve.wait_ge(y_ps, freed(n))
                            for h in range(HALVES):
                                t = n * 2 + h
                                last = v.tensor_scalar(y[s][:, h, :], core.x[:, t, :], core.mean[:, bass.ds(t, 1)],
                                                       core.rstd[:, bass.ds(t, 1)], ALU.subtract, ALU.mult)
                            last.then_inc(y_ready, 1)
                        for s in range(2):
                            n = i * 2 + s
                            dve.wait_ge(wh_ready, done(n))
                            dve.wait_ge(s2_ps, done(n))
                            dve.wait_ge(p_ready, freed(n))
                            for h in range(HALVES):
                                last = v.tensor_scalar(e[s][:, h, :], ps_s[s][:, 0:N], wh[s][:, h, D:D + 1], None, ALU.add)
                            mine.step(last)
                            mine.step(v.scalar_tensor_tensor(e[s][:], e[s][:], SLOPE, e[s][:], ALU.mult, ALU.max))
                            dve.wait_ge(allow_ready, done(n))
                            mine.step(v.scalar_tensor_tensor(e[s][:], allow[s][:], MASKED, e[s][:], ALU.add, ALU.min))
                            mine.step(v.tensor_reduce(low[s][:], e[s][:], AXX, ALU.max))
                            v.tensor_scalar(low[s][:], low[s][:], -1.0, None, ALU.mult).then_inc(e_ready, 1)
                        for s in range(2):
                            n = i * 2 + s
                            dve.wait_ge(p_ready, done(n))
                            dve.wait_ge(out_ps, done(n))
                            mine.step(v.reciprocal(total[s][:], total[s][:]))
                            for h in range(HALVES):
                                last = v.tensor_scalar(attended[:, n * 2 + h, :], ps_y[s][:, N + h * D:N + (h + 1) * D], total[s][:, h:h + 1], None, ALU.mult)
                            last.then_inc(out_ready, 1)
                        mine.end()
        layernorm_statistics(nc, core, "norm_attended", attended)
        GROUP = 4
        with Stage(nc, "gelu") as st:
            scale = st.sb("gamma", [P, D])
            shift = st.sb("beta", [P, D])
            z = [st.sb(f"z{s}", [P, GROUP, D]) for s in range(2)]
            loaded, own, own_pool = st.sem("loaded"), st.sem("vector_steps"), st.sem("pool_steps")
            z_ready, affine_ready, gelu_ready, added = [st.sem(n, CREDIT) for n in ("z_ready", "affine_ready", "gelu_ready", "added")]
            with st.block() as block:
                @block.sync
                def _(sp):
                    sp.dma_start(scale[:], gamma.rearrange("(a n) -> a n", a=1).to_broadcast([P, D])).then_inc(loaded, 16)
                    sp.dma_start(shift[:], beta.rearrange("(a n) -> a n", a=1).to_broadcast([P, D])).then_inc(loaded, 16)

                @block.gpsimd
                def _(pool):
                    pool.wait_ge(loaded, 32)
                    with pool.Fori(0, TILES // GROUP // 2) as i:
                        for s in range(2):
                            n = i * 2 + s
                            pool.wait_ge(z_ready, done(n))
                            nc.gpsimd.tensor_tensor(z[s][:], z[s][:], scale[:].unsqueeze(1).to_broadcast([P, GROUP, D]), ALU.mult).then_inc(own_pool, 1)
                            pool.wait_ge(own_pool, n + 1)
                            nc.gpsimd.tensor_tensor(z[s][:], z[s][:], shift[:].unsqueeze(1).to_broadcast([P, GROUP, D]), ALU.add).then_inc(affine_ready, 1)

                @block.scalar
                def _(act):
                    with act.Fori(0, TILES // GROUP // 2) as i:
                        for s in range(2):
                            n = i * 2 + s
                            act.wait_ge(affine_ready, done(n))
                            nc.scalar.activation(z[s][:], z[s][:], ACT.Gelu).then_inc(gelu_ready, 1)

                @block.vector
                def _(dve):
                    with dve.Fori(0, TILES // GROUP // 2) as i:
                        for s in range(2):
                            n = i * 2 + s
                            dve.wait_ge(added, freed(n))
                            for k in range(GROUP):
                                t = n * GROUP + k
                                last = nc.vector.tensor_scalar(z[s][:, k, :], attended[:, t, :], core.mean[:, bass.ds(t, 1)],
                                                               core.rstd[:, bass.ds(t, 1)], ALU.subtract, ALU.mult)
                            last.then_inc(z_ready, 1)
                        for s in range(2):
                            n = i * 2 + s
                            dve.wait_ge(gelu_ready, done(n))
                            part = core.x[:, bass.ds(n * GROUP, GROUP), :]
                            nc.vector.tensor_tensor(part, part, z[s][:], ALU.add).then_inc(added, 1)


HEADS, HD, SLICES, NS, KC = 8, 64, 64, 64, 3
INNER = HEADS * HD
CHUNKS = INNER // P
CONV = INNER + 2 * NS
FC = CONV // P
PAIRS = B // 2
DT0 = INNER + CONV


def order_masks():
    u, t = np.arange(SLICES)[:, None], np.arange(SLICES)[None, :]
    two = lambda m: np.tile(m, (2, 1)).astype(np.float32)
    block = lambda m: np.kron(np.eye(2), m).astype(np.float32)
    return np.stack([two(u < t), two(u > t)], 1), np.stack([block(u > t), block(u < t)], 1)


def slice_block(nc, core, a):
    with Stage(nc, "slice") as keep:
        core.u_t = keep.sb("u_t", [P, CHUNKS, B * SLICES])
        make_slices(nc, core, a)
        mix_slices(nc, core, a)
        spread_slices(nc, core, a)


def make_slices(nc, core, a):
    with Stage(nc, "make") as st:
        wx = st.sb("w_x", [P, CHUNKS, D])
        bx = st.sb("b_x", [P, CHUNKS])
        ws2 = st.sb("w_slice2", [P, P])
        bs = st.sb("b_slice", [P, SLICES])
        temp = st.sb("temperature", [P, HEADS])
        wl = st.sb("w_logits", [P, INNER])
        bl = st.sb("b_logits", [P, INNER])
        wf = st.sb("w_fx", [P, INNER])
        bf = st.sb("b_fx", [P, CHUNKS])
        y = [st.sb(f"y{s}", [P, HALVES, D]) for s in range(2)]
        y_t = [st.sb(f"y_t{s}", [P, N]) for s in range(2)]
        sw = [st.sb(f"sw{s}", [P, HALVES * HEADS, SLICES]) for s in range(2)]
        top = [st.sb(f"max{s}", [P, HALVES * HEADS]) for s in range(2)]
        rinv = st.sb("rinv", [P, INNER])
        ratio = st.sb("ratio", [P, INNER])
        mean_t = [st.sb(f"mean_t{s}", [P, INNER]) for s in range(2)]
        ps_y = [st.ps(f"ps_y{s}", [P, 512]) for s in range(2)]
        ps_l = [[st.ps(f"ps_logits{s}{h}", [P, 512]) for h in range(2)] for s in range(2)]
        ps_m = st.ps("ps_mean", [P, 512])
        ps_n = st.ps("ps_norm", [P, 512])
        cleared, loaded, own, w_ps, b_ps, w_ready, passed, own_pool = [st.sem(n) for n in (
            "cleared", "loaded", "vector_steps", "w_product", "b_product", "w_ready", "pool_passed", "pool_steps")]
        y_ready, y_ps, y_t_ready, logits_ps, top_ready, low_ready, exp_ready, total_ready, sw_ready, means_ps, means_ready, u_ps, u_ready = [
            st.sem(n, CREDIT) for n in ("y_ready", "y_transposed", "y_t_ready", "logits_product", "max_ready", "shifted", "exp_ready",
                                        "total_ready", "sw_ready", "means_product", "means_ready", "slices_product", "slices_ready")]
        stored = [st.sem(f"sw_stored{s}", 16) for s in range(2)]
        with st.block() as block:
            @block.sync
            def _(sp):
                def row(v, n):
                    return v.rearrange("(a n) -> a n", a=1).to_broadcast([P, n])
                sp.dma_start(wx[:], a["L3_ffn_W_x"].rearrange("(c p) d -> p c d", p=P)).then_inc(loaded, 16)
                sp.dma_start(wf[:], a["L3_ffn_W_fx_t"]).then_inc(loaded, 16)
                sp.dma_start(bs[:], row(a["L3_ffn_b_slice"], SLICES)).then_inc(loaded, 16)
                sp.dma_start(temp[:], row(a["L3_ffn_temperature"].rearrange("a h b c -> (a h b c)"), HEADS)).then_inc(loaded, 16)
                with nc.allow_non_contiguous_dma("bias columns"):
                    sp.dma_start(bx[:], a["L3_ffn_b_x"].rearrange("(c p) -> p c", p=P)).then_inc(loaded, 16)
                    sp.dma_start(bf[:], a["L3_ffn_b_fx"].rearrange("(c p) -> p c", p=P)).then_inc(loaded, 16)
                sp.wait_ge(cleared, 1)
                for k in range(2):
                    sp.dma_start(ws2[k * HD:(k + 1) * HD, k * SLICES:(k + 1) * SLICES], a["L3_ffn_W_slice_t"]).then_inc(loaded, 16)
                with sp.Fori(0, B // 2) as i:
                    for s in range(2):
                        sp.wait_ge(sw_ready, done(i * 2 + s))
                        sp.dma_start(core.sw[i * 2 + s, :, :], sw[s][:].rearrange("p a b -> p (a b)")).then_inc(stored[s], 16)
                for s in range(2):
                    sp.wait_ge(stored[s], 16 * (B // 2 + 1))

            @block.gpsimd
            def _(pool):
                nc.gpsimd.memset(ws2[:], 0.0).then_inc(cleared, 1)
                with pool.Fori(0, B // 2) as i:
                    for s in range(2):
                        each = top[s][:].unsqueeze(2).to_broadcast([P, HALVES * HEADS, SLICES])
                        pool.wait_ge(top_ready, done(i * 2 + s))
                        nc.gpsimd.tensor_tensor(sw[s][:], sw[s][:], each, ALU.subtract).then_inc(low_ready, 1)
                    for s in range(2):
                        each = top[s][:].unsqueeze(2).to_broadcast([P, HALVES * HEADS, SLICES])
                        pool.wait_ge(total_ready, done(i * 2 + s))
                        nc.gpsimd.tensor_tensor(sw[s][:], sw[s][:], each, ALU.mult).then_inc(sw_ready, 1)

            @block.tensor
            def _(pe):
                mm = nc.tensor.matmul
                pe.wait_ge(loaded, 128)
                for c in range(CHUNKS):
                    last = mm(ps_m[:, c * P:(c + 1) * P], wx[:, c, :], ws2[:], start=True, stop=True)
                last.then_inc(w_ps, 1)
                for c in range(CHUNKS):
                    last = mm(ps_n[:, c * P:(c + 1) * P], bx[:, c:c + 1].to_broadcast([P, P]), ws2[:], start=True, stop=True)
                last.then_inc(b_ps, 1)
                pe.wait_ge(w_ready, 1)
                with pe.Fori(0, B // 2) as i:
                    for s in range(2):
                        n = i * 2 + s
                        pe.wait_ge(u_ready, freed(n))
                        pe.wait_ge(y_ready, done(n))
                        for h in range(HALVES):
                            last = nc.tensor.transpose(ps_y[s][:, h * P:(h + 1) * P], y[s][:, h, :], core.ident[:])
                        last.then_inc(y_ps, 1)
                    for s in range(2):
                        n = i * 2 + s
                        pe.wait_ge(y_t_ready, done(n))
                        pe.wait_ge(top_ready, freed(n))
                        for h in range(HALVES):
                            last = mm(ps_l[s][h][:], y_t[s][:, h * P:(h + 1) * P], wl[:], start=True, stop=True)
                        last.then_inc(logits_ps, 1)
                    for s in range(2):
                        n = i * 2 + s
                        pe.wait_ge(sw_ready, done(n))
                        pe.wait_ge(means_ready, n + CREDIT)
                        for out, lhs in ((ps_m, None), (ps_n, core.ones)):
                            for h in range(HALVES):
                                rhs = sw[s][:, h * HEADS:(h + 1) * HEADS, :]
                                last = mm(out[:], y[s][:, h, :] if lhs is None else lhs[:], rhs, start=h == 0, stop=h == HALVES - 1)
                        last.then_inc(means_ps, 1)
                        pe.wait_ge(means_ready, done(n))
                        for c in range(CHUNKS):
                            last = mm(ps_y[s][:, c * P:(c + 1) * P], wf[:, c * P:(c + 1) * P], mean_t[s][:, c * P:(c + 1) * P], start=True, stop=True)
                        last.then_inc(u_ps, 1)

            @block.scalar
            def _(act):
                with act.Fori(0, B // 2) as i:
                    for s in range(2):
                        n = i * 2 + s
                        act.wait_ge(logits_ps, freed(n))
                        act.wait_ge(y_ps, done(n))
                        nc.scalar.copy(y_t[s][:], ps_y[s][:, 0:N]).then_inc(y_t_ready, 1)
                    for s in range(2):
                        n = i * 2 + s
                        act.wait_ge(low_ready, done(n))
                        nc.scalar.activation(sw[s][:], sw[s][:], ACT.Exp).then_inc(exp_ready, 1)

            @block.vector
            def _(dve):
                v = nc.vector
                dve.wait_ge(loaded, 128)
                heads = lambda ap: ap.rearrange("p (h g) -> p h g", h=HEADS)
                pre = Own(dve, own, 0, 0)
                pre.step(v.tensor_scalar(temp[:], temp[:], 1e-6, None, ALU.max))
                pre.step(v.reciprocal(temp[:], temp[:]))
                each_head = temp[:].unsqueeze(2).to_broadcast([P, HEADS, SLICES])
                dve.wait_ge(w_ps, 1)
                pre.step(v.tensor_tensor(heads(wl[:]), heads(ps_m[:]), each_head, ALU.mult))
                dve.wait_ge(b_ps, 1)
                pre.step(v.tensor_tensor(heads(bl[:]), heads(ps_n[:]), bs[:].unsqueeze(1).to_broadcast([P, HEADS, SLICES]), ALU.add))
                v.tensor_tensor(heads(bl[:]), heads(bl[:]), each_head, ALU.mult).then_inc(w_ready, 1)
                dve.wait_ge(w_ready, 1)
                before = pre.k
                with dve.Fori(0, B // 2) as i:
                    mine = Own(dve, own, i, 2 * (1 + 1 + 3))
                    mine.base = i * mine.per + before
                    for s in range(2):
                        n = i * 2 + s
                        dve.wait_ge(means_ps, freed(n))
                        for h in range(HALVES):
                            t = n * 2 + h
                            last = v.tensor_scalar(y[s][:, h, :], core.x[:, t, :], core.mean[:, bass.ds(t, 1)],
                                                   core.rstd[:, bass.ds(t, 1)], ALU.subtract, ALU.mult)
                        last.then_inc(y_ready, 1)
                    for s in range(2):
                        n = i * 2 + s
                        dve.wait_ge(logits_ps, done(n))
                        dve.wait_ge(stored[s], i * 16 + 16)
                        for h in range(HALVES):
                            last = v.tensor_tensor(sw[s][:, h * HEADS:(h + 1) * HEADS, :], heads(ps_l[s][h][:]), heads(bl[:]), ALU.add)
                        mine.step(last)
                        v.tensor_reduce(top[s][:], sw[s][:], AXX, ALU.max).then_inc(top_ready, 1)
                    for s in range(2):
                        n = i * 2 + s
                        dve.wait_ge(exp_ready, done(n))
                        mine.step(v.tensor_reduce(top[s][:], sw[s][:], AXX, ALU.add))
                        v.reciprocal(top[s][:], top[s][:]).then_inc(total_ready, 1)
                    for s in range(2):
                        n = i * 2 + s
                        dve.wait_ge(means_ps, done(n))
                        dve.wait_ge(u_ps, freed(n))
                        mine.step(v.tensor_scalar(rinv[:], ps_n[:], 1e-5, None, ALU.add))
                        mine.step(v.reciprocal(rinv[:], rinv[:]))
                        mine.mark(v.tensor_tensor(ratio[:], ps_n[:], rinv[:], ALU.mult))
                        v.tensor_tensor(mean_t[s][:], ps_m[:], rinv[:], ALU.mult).then_inc(means_ready, 1)
                        mine.join()
                        dve.wait_ge(u_ps, done(n))
                        for c in range(CHUNKS):
                            for k in range(2):
                                part = slice(k * HD, (k + 1) * HD)
                                at = c * P + k * SLICES
                                last = v.scalar_tensor_tensor(core.u_t[part, c, bass.ds(n * SLICES, SLICES)], ratio[part, at:at + SLICES],
                                                              bf[part, c:c + 1], ps_y[s][part, at:at + SLICES], ALU.mult, ALU.add)
                        last.then_inc(u_ready, 1)
                        dve.wait_ge(u_ready, done(n))
                    mine.end()


def mix_slices(nc, core, a):
    with Stage(nc, "mix") as keep:
        z = keep.sb("z", [P, PAIRS, INNER])
        xc = keep.sb("xbc_t", [P, FC, B * SLICES])
        dt = keep.sb("dt", [P, PAIRS, 2 * HEADS])
        decay = keep.sb("decay", [P, PAIRS, 2 * HEADS])
        project_slices(nc, core, a, z, xc, dt)
        time_steps(nc, core, a, dt, decay)
        scan_slices(nc, core, a, z, xc, dt, decay)


def project_slices(nc, core, a, z, xc, dt):
    BLOCK = 512
    GRAPHS = BLOCK // SLICES
    with Stage(nc, "project") as st:
        w = st.sb("in_w", [P, CHUNKS, DT0 + 2 * HEADS])
        cw = st.sb("conv_w", [P, FC, KC])
        cb = st.sb("conv_b", [P, FC])
        dtb = st.sb("dt_bias", [P, 2 * HEADS])
        ub = [st.sb(f"u{s}", [P, CHUNKS, P]) for s in range(2)]
        xp = [st.sb(f"padded{s}", [P, GRAPHS, KC - 1 + SLICES]) for s in range(2)]
        acc = [st.sb(f"acc{s}", [P, GRAPHS, SLICES]) for s in range(2)]
        ps_x = [st.ps(f"ps_x{s}", [P, 512]) for s in range(2)]
        ps_z = [st.ps(f"ps_z{s}", [P, 512]) for s in range(2)]
        ps_d = [st.ps(f"ps_dt{s}", [P, 512]) for s in range(2)]
        loaded, cleared, own, passed_a, passed_p = [st.sem(n) for n in ("loaded", "pads_cleared", "vector_steps", "scalar_passed", "pool_passed")]
        x_ps, x_ready, conv_ready, x_kept, ub_ready, z_ps, z_kept, d_kept = [st.sem(n, CREDIT) for n in (
            "x_product", "x_padded", "conv_ready", "x_kept", "u_ready", "z_product", "z_kept", "dt_kept")]
        with st.block() as block:
            @block.sync
            def _(sp):
                sp.dma_start(w[:], a["L3_ffn_hy_in_w_t"].rearrange("(c p) f -> p c f", p=P)).then_inc(loaded, 16)
                for k in range(2):
                    sp.dma_start(dtb[:, k * HEADS:(k + 1) * HEADS], a["L3_ffn_hy_dt_bias"].rearrange("(a n) -> a n", a=1).to_broadcast([P, HEADS])).then_inc(loaded, 16)
                with nc.allow_non_contiguous_dma("columns of the convolution"):
                    sp.dma_start(cw[:], a["L3_ffn_hy_conv_w"].rearrange("(c p) k -> p c k", p=P)).then_inc(loaded, 16)
                    sp.dma_start(cb[:], a["L3_ffn_hy_conv_b"].rearrange("(c p) -> p c", p=P)).then_inc(loaded, 16)

            @block.gpsimd
            def _(pool):
                for s in range(2):
                    nc.gpsimd.memset(xp[s][:], 0.0).then_inc(cleared, 1)
                with pool.Fori(0, PAIRS // 2) as i:
                    for s in range(2):
                        m = i * 2 + s
                        pool.wait_ge(z_ps, freed(m))
                        hold(pool, passed_p)
                        nc.gpsimd.tensor_copy(ub[s][:], core.u_t[:, :, bass.ds(m * P, P)]).then_inc(ub_ready, 1)

            @block.tensor
            def _(pe):
                mm = nc.tensor.matmul
                pe.wait_ge(loaded, 80)
                with pe.Fori(0, B * SLICES // BLOCK // 2) as i:
                    for j in range(2):
                        for f in range(FC):
                            s = (j * FC + f) % 2
                            n = i * (2 * FC) + j * FC + f
                            pe.wait_ge(x_ready, freed(n))
                            for c in range(CHUNKS):
                                last = mm(ps_x[s][:], w[:, c, INNER + f * P:INNER + (f + 1) * P],
                                          core.u_t[:, c, bass.ds((i * 2 + j) * BLOCK, BLOCK)], start=c == 0, stop=c == CHUNKS - 1)
                            last.then_inc(x_ps, 1)
                        for q in range(BLOCK // P):
                            s = q % 2
                            m = (i * 2 + j) * (BLOCK // P) + q
                            pe.wait_ge(ub_ready, done(m))
                            pe.wait_ge(z_kept, freed(m))
                            pe.wait_ge(d_kept, freed(m))
                            for c in range(CHUNKS):
                                mm(ps_z[s][:], ub[s][:, c, :], w[:, c, 0:INNER], start=c == 0, stop=c == CHUNKS - 1)
                            for c in range(CHUNKS):
                                last = mm(ps_d[s][:, 0:2 * HEADS], ub[s][:, c, :], w[:, c, DT0:DT0 + 2 * HEADS], start=c == 0, stop=c == CHUNKS - 1)
                            last.then_inc(z_ps, 1)

            @block.scalar
            def _(act):
                act.wait_ge(cleared, 2)
                act.wait_ge(loaded, 80)

                def pad(n, s):
                    act.wait_ge(conv_ready, freed(n))
                    act.wait_ge(x_ps, done(n))
                    nc.scalar.copy(xp[s][:, :, KC - 1:], ps_x[s][:].rearrange("p (b g) -> p b g", b=GRAPHS)).then_inc(x_ready, 1)

                def keep_x(n, s, f, j):
                    act.wait_ge(conv_ready, done(n))
                    hold(act, passed_a)
                    nc.scalar.activation(xc[:, f, bass.ds(j * BLOCK, BLOCK)], acc[s][:].rearrange("p b g -> p (b g)"),
                                         ACT.Silu, bias=cb[:, f:f + 1]).then_inc(x_kept, 1)

                with act.Fori(0, B * SLICES // BLOCK // 2) as i:
                    for j in range(2):
                        first = i * (2 * FC) + j * FC
                        pad(first, j * FC % 2)
                        for f in range(FC):
                            s = (j * FC + f) % 2
                            if f + 1 < FC:
                                pad(first + f + 1, 1 - s)
                            keep_x(first + f, s, f, i * 2 + j)
                        for q in range(BLOCK // P):
                            m = (i * 2 + j) * (BLOCK // P) + q
                            act.wait_ge(z_ps, done(m))
                            hold(act, passed_a)
                            nc.scalar.activation(z[:, m, :], ps_z[q % 2][:], ACT.Silu).then_inc(z_kept, 1)

            @block.vector
            def _(dve):
                v = nc.vector
                dve.wait_ge(loaded, 80)
                with dve.Fori(0, B * SLICES // BLOCK // 2) as i:
                    mine = Own(dve, own, i, 2 * FC * 2)
                    for j in range(2):
                        for f in range(FC):
                            s = (j * FC + f) % 2
                            n = i * (2 * FC) + j * FC + f
                            dve.wait_ge(x_ready, done(n))
                            dve.wait_ge(x_kept, freed(n))
                            mine.step(v.tensor_scalar(acc[s][:], xp[s][:, :, 0:SLICES], cw[:, f, 0:1], None, ALU.mult))
                            mine.step(v.scalar_tensor_tensor(acc[s][:], xp[s][:, :, 1:1 + SLICES], cw[:, f, 1:2], acc[s][:], ALU.mult, ALU.add))
                            v.scalar_tensor_tensor(acc[s][:], xp[s][:, :, 2:2 + SLICES], cw[:, f, 2:3], acc[s][:], ALU.mult, ALU.add).then_inc(conv_ready, 1)
                        for q in range(BLOCK // P):
                            m = (i * 2 + j) * (BLOCK // P) + q
                            dve.wait_ge(z_ps, done(m))
                            v.tensor_tensor(dt[:, m, :], ps_d[q % 2][:, 0:2 * HEADS], dtb[:], ALU.add).then_inc(d_kept, 1)
                    mine.end()


def time_steps(nc, core, a, dt, decay):
    STEEPEST = 69.0
    with Stage(nc, "steps") as st:
        rate = st.sb("rate", [P, 2 * HEADS])
        shape = [P, PAIRS, 2 * HEADS]
        t0, t1, t2, same = [st.sb(f"t{k}", shape) for k in range(4)]
        loaded, rate_in, own, t_ready, e_ready, w_ready, l_ready = [st.sem(n) for n in (
            "loaded", "rate_clamped", "vector_steps", "minus_abs_ready", "exp_ready", "one_plus_ready", "log_ready")]
        with st.block() as block:
            @block.sync
            def _(sp):
                for k in range(2):
                    sp.dma_start(rate[:, k * HEADS:(k + 1) * HEADS], a["L3_ffn_hy_A_log"].rearrange("(a n) -> a n", a=1).to_broadcast([P, HEADS])).then_inc(loaded, 16)

            @block.scalar
            def _(act):
                act.wait_ge(rate_in, 1)
                nc.scalar.activation(rate[:], rate[:], ACT.Exp)
                act.wait_ge(t_ready, 1)
                nc.scalar.activation(t0[:], t0[:], ACT.Exp).then_inc(e_ready, 1)
                act.wait_ge(w_ready, 1)
                nc.scalar.activation(t2[:], t1[:], ACT.Ln).then_inc(l_ready, 1)

            @block.vector
            def _(dve):
                v = nc.vector
                mine = Own(dve, own, 0, 0)
                dve.wait_ge(loaded, 32)
                v.tensor_scalar(rate[:], rate[:], STEEPEST, None, ALU.min).then_inc(rate_in, 1)
                mine.step(v.tensor_scalar(t0[:], dt[:], -1.0, None, ALU.mult))
                v.tensor_tensor(t0[:], t0[:], dt[:], ALU.min).then_inc(t_ready, 1)
                dve.wait_ge(e_ready, 1)
                v.tensor_scalar(t1[:], t0[:], 1.0, None, ALU.add).then_inc(w_ready, 1)
                dve.wait_ge(w_ready, 1)
                mine.step(v.tensor_scalar(same[:], t1[:], 1.0, None, ALU.is_equal))
                dve.wait_ge(l_ready, 1)
                mine.step(v.tensor_scalar(t1[:], t1[:], 1.0, None, ALU.subtract))
                mine.step(v.tensor_tensor(t1[:], t1[:], same[:], ALU.add))
                mine.step(v.tensor_tensor(t2[:], t2[:], same[:], ALU.add))
                mine.step(v.reciprocal(t1[:], t1[:]))
                mine.step(v.tensor_tensor(t2[:], t2[:], t1[:], ALU.mult))
                mine.step(v.tensor_tensor(t2[:], t2[:], t0[:], ALU.mult))
                mine.step(v.tensor_scalar(dt[:], dt[:], 0.0, None, ALU.max))
                mine.step(v.tensor_tensor(dt[:], dt[:], t2[:], ALU.add))
                mine.step(v.tensor_scalar(rate[:], rate[:], -1.0, None, ALU.mult))
                mine.step(v.tensor_tensor(decay[:], dt[:], rate[:].unsqueeze(1).to_broadcast(shape), ALU.mult))


def scan_slices(nc, core, a, z, xc, dt, decay):
    with Stage(nc, "scan") as st:
        col_mask = st.sb("col_mask", [P, 2, SLICES])
        row_mask = st.sb("row_mask", [P, 2, P])
        fc_w = st.sb("fc_w", [P, CHUNKS, HEADS])
        dp = st.sb("d", [P, HEADS])
        nw = st.sb("norm_w", [P, CHUNKS])
        ow = st.sb("out_w", [P, CHUNKS, INNER])
        xb = [st.sb(f"xbc{s}", [P, FC, P]) for s in range(2)]
        ct = [st.sb(f"c_t{s}", [NS, P]) for s in range(2)]
        part = [[st.sb(f"decay_part{s}{k}", [P, HEADS, SLICES]) for k in range(2)] for s in range(2)]
        xs = [st.sb(f"x{s}", [P, INNER]) for s in range(2)]
        fade = [[st.sb(f"fade{s}{k}", [P, HEADS, SLICES]) for k in range(2)] for s in range(2)]
        near = st.sb("cb", [P, 2, SLICES])
        mat = [st.sb(f"matrix{s}", [P, HEADS, P]) for s in range(2)]
        fcd = st.sb("fcd", [P, HEADS])
        yg = [st.sb(f"yg{s}", [P, INNER]) for s in range(2)]
        sq = st.sb("square", [P, INNER])
        ss = [st.sb(f"sum_square{s}", [P, 1]) for s in range(2)]
        yg_t = st.sb("yg_t", [P, CHUNKS, P])
        ps_x, ps_fc, ps_cb, ps_f, ps_b, ps_y, ps_g, ps_o = [st.ps(n, [P, 512]) for n in (
            "ps_x", "ps_fc", "ps_cb", "ps_forward", "ps_backward", "ps_y", "ps_gated", "ps_out")]
        loaded, cleared, own, own_pool, own_act, passed_a, passed_p = [st.sem(n) for n in (
            "loaded", "matrix_cleared", "vector_steps", "pool_steps", "log_ready", "scalar_passed", "pool_passed")]
        in_ready, x_ps, xs_ready, fade_ready, mat_ready, y_ps, yg_ready, ss_ready, ms_ready, rms_ready, ygs_ready, g_ps, g_ready, o_ps, o_kept = [
            st.sem(n, CREDIT) for n in ("inputs_ready", "inputs_product", "x_ready", "fade_ready", "matrix_ready", "y_product", "gated_ready",
                                        "square_sum_ready", "mean_square_ready", "rms_ready", "normed_ready", "gated_transposed",
                                        "gated_t_ready", "out_product", "out_kept")]
        with st.block() as block:
            @block.sync
            def _(sp):
                sp.dma_start(col_mask[:], a["col_mask"]).then_inc(loaded, 16)
                sp.dma_start(row_mask[:], a["lhs_mask"]).then_inc(loaded, 16)
                sp.dma_start(fc_w[:], a["L3_ffn_hy_fcD_w_t"].rearrange("(c p) h -> p c h", p=P)).then_inc(loaded, 16)
                sp.dma_start(dp[:], a["L3_ffn_hy_D"].rearrange("(a n) -> a n", a=1).to_broadcast([P, HEADS])).then_inc(loaded, 16)
                with nc.allow_non_contiguous_dma("weight columns"):
                    sp.dma_start(nw[:], a["L3_ffn_hy_norm_w"].rearrange("(c p) -> p c", p=P)).then_inc(loaded, 16)
                sp.dma_start(ow[:], a["L3_ffn_hy_out_w_t"].rearrange("(c p) f -> p c f", p=P)).then_inc(loaded, 16)

            @block.gpsimd
            def _(pool):
                g = nc.gpsimd
                for s in range(2):
                    g.memset(mat[s][:], 0.0).then_inc(cleared, 1)
                g.memset(near[:], 0.0).then_inc(cleared, 1)
                pool.wait_ge(loaded, 96)
                with pool.Fori(0, PAIRS // 2) as i:
                    for s in range(2):
                        m = i * 2 + s
                        pool.wait_ge(x_ps, freed(m))
                        hold(pool, passed_p)
                        g.tensor_copy(xb[s][:], xc[:, :, bass.ds(m * P, P)]).then_inc(own_pool, 1)
                        for k in range(2):
                            g.tensor_tensor(part[s][k][:], decay[:, m, k * HEADS:(k + 1) * HEADS].unsqueeze(2).to_broadcast([P, HEADS, SLICES]),
                                            col_mask[:, k, :].unsqueeze(1).to_broadcast([P, HEADS, SLICES]), ALU.mult).then_inc(own_pool, 1)
                        pool.wait_ge(own_pool, m * 3 + 3)
                        hold(pool, passed_p)
                        g.tensor_copy(ct[s][:], xb[s][NS:2 * NS, FC - 1, :]).then_inc(in_ready, 1)
                        pool.wait_ge(in_ready, done(m))
                        hold(pool, passed_p)

            @block.tensor
            def _(pe):
                mm = nc.tensor.matmul

                def inputs(m, s):
                    pe.wait_ge(in_ready, done(m))
                    pe.wait_ge(xs_ready, m + CREDIT)
                    pe.wait_ge(fade_ready, m + CREDIT)
                    pe.wait_ge(yg_ready, m + CREDIT)
                    for c in range(CHUNKS):
                        nc.tensor.transpose(ps_x[:, c * P:(c + 1) * P], xb[s][:, c, :], core.ident[:])
                    for c in range(CHUNKS):
                        mm(ps_fc[:, 0:HEADS], xb[s][:, c, :], fc_w[:, c, :], start=c == 0, stop=c == CHUNKS - 1)
                    mm(ps_cb[:, 0:P], xb[s][0:NS, FC - 1, :], ct[s][:], start=True, stop=True)
                    for k, out in enumerate((ps_f, ps_b)):
                        last = mm(out[:], row_mask[:, k, :], part[s][k][:], start=True, stop=True)
                    last.then_inc(x_ps, 1)

                def products(m, s):
                    pe.wait_ge(mat_ready, done(m))
                    pe.wait_ge(xs_ready, done(m))
                    for h in range(HEADS):
                        last = mm(ps_y[:, h * HD:(h + 1) * HD], mat[s][:, h, :], xs[s][:, h * HD:(h + 1) * HD], start=True, stop=True)
                    last.then_inc(y_ps, 1)

                def outputs(m, s):
                    pe.wait_ge(ygs_ready, done(m))
                    for c in range(CHUNKS):
                        last = nc.tensor.transpose(ps_g[:, c * P:(c + 1) * P], yg[s][:, c * P:(c + 1) * P], core.ident[:])
                    last.then_inc(g_ps, 1)
                    pe.wait_ge(g_ready, done(m))
                    pe.wait_ge(o_kept, m + CREDIT)
                    for f in range(CHUNKS):
                        for c in range(CHUNKS):
                            last = mm(ps_o[:, f * P:(f + 1) * P], ow[:, c, f * P:(f + 1) * P], yg_t[:, c, :], start=c == 0, stop=c == CHUNKS - 1)
                    last.then_inc(o_ps, 1)

                pe.wait_ge(loaded, 96)
                with pe.Fori(0, PAIRS // 2) as i:
                    for s in range(2):
                        inputs(i * 2 + s, s)
                        products(i * 2 + s, s)
                        outputs(i * 2 + s, s)

            @block.scalar
            def _(act):
                with act.Fori(0, PAIRS // 2) as i:
                    for s in range(2):
                        m = i * 2 + s
                        act.wait_ge(yg_ready, freed(m))
                        act.wait_ge(mat_ready, freed(m))
                        act.wait_ge(x_ps, done(m))
                        nc.scalar.copy(xs[s][:], ps_x[:]).then_inc(xs_ready, 1)
                        nc.scalar.activation(fade[s][0][:], ps_f[:].rearrange("p (h t) -> p h t", h=HEADS), ACT.Exp)
                        nc.scalar.activation(fade[s][1][:], ps_b[:].rearrange("p (h t) -> p h t", h=HEADS), ACT.Exp).then_inc(fade_ready, 1)
                        act.wait_ge(yg_ready, done(m))
                        nc.scalar.activation(sq[:], yg[s][:], ACT.Square, accum_out=ss[s][:]).then_inc(ss_ready, 1)
                        act.wait_ge(ms_ready, done(m))
                        nc.scalar.activation(ss[s][:], ss[s][:], ACT.Ln).then_inc(own_act, 1)
                        act.wait_ge(own_act, m + 1)
                        nc.scalar.activation(ss[s][:], ss[s][:], ACT.Exp, scale=-0.5).then_inc(rms_ready, 1)
                        act.wait_ge(o_ps, done(m))
                        hold(act, passed_a)
                        nc.scalar.copy(core.u_t[:, :, bass.ds(m * P, P)], ps_o[:].rearrange("p (c t) -> p c t", c=CHUNKS)).then_inc(o_kept, 1)

            @block.vector
            def _(dve):
                v = nc.vector
                per_head = lambda ap: ap.rearrange("p (h t) -> p h t", h=HEADS)
                dve.wait_ge(loaded, 96)
                dve.wait_ge(cleared, 3)
                with dve.Fori(0, PAIRS // 2) as i:
                    mine = Own(dve, own, i, 2 * (1 + 2 + 2 + 3))
                    for s in range(2):
                        m = i * 2 + s
                        dve.wait_ge(x_ps, done(m))
                        for q in range(2):
                            rows = slice(q * SLICES, (q + 1) * SLICES)
                            at = q * SLICES
                            v.tensor_tensor(near[rows, 0, 1:SLICES], ps_cb[rows, at:at + SLICES - 1], col_mask[rows, 0, 1:SLICES], ALU.mult)
                            last = v.tensor_tensor(near[rows, 1, 0:SLICES - 1], ps_cb[rows, at + 1:at + SLICES], col_mask[rows, 1, 0:SLICES - 1], ALU.mult)
                        mine.step(last)
                        dve.wait_ge(fade_ready, done(m))
                        for k in range(2):
                            last = v.tensor_tensor(fade[s][k][:], fade[s][k][:], near[:, k, :].unsqueeze(1).to_broadcast([P, HEADS, SLICES]), ALU.mult)
                            mine.mark(last)
                        mine.join()
                        for k in range(2):
                            last = v.tensor_tensor(fade[s][k][:], fade[s][k][:],
                                                   dt[:, m, k * HEADS:(k + 1) * HEADS].unsqueeze(2).to_broadcast([P, HEADS, SLICES]), ALU.mult)
                            mine.mark(last)
                        mine.join()
                        dve.wait_ge(y_ps, freed(m))
                        for q in range(2):
                            rows = slice(q * SLICES, (q + 1) * SLICES)
                            last = v.tensor_tensor(mat[s][rows, :, q * SLICES:(q + 1) * SLICES], fade[s][0][rows, :, :], fade[s][1][rows, :, :], ALU.add)
                        last.then_inc(mat_ready, 1)
                        mine.step(v.tensor_tensor(fcd[:], ps_fc[:, 0:HEADS], dp[:], ALU.add))
                        dve.wait_ge(xs_ready, done(m))
                        dve.wait_ge(g_ps, freed(m))
                        mine.step(v.tensor_tensor(per_head(yg[s][:]), per_head(xs[s][:]), fcd[:].unsqueeze(2).to_broadcast([P, HEADS, HD]), ALU.mult))
                        dve.wait_ge(y_ps, done(m))
                        mine.step(v.tensor_tensor(yg[s][:], ps_y[:], yg[s][:], ALU.add))
                        v.tensor_tensor(yg[s][:], yg[s][:], z[:, m, :], ALU.mult).then_inc(yg_ready, 1)
                        dve.wait_ge(ss_ready, done(m))
                        v.tensor_scalar(ss[s][:], ss[s][:], 1.0 / INNER, 1e-5, ALU.mult, ALU.add).then_inc(ms_ready, 1)
                        dve.wait_ge(rms_ready, done(m))
                        v.tensor_scalar(yg[s][:], yg[s][:], ss[s][:], None, ALU.mult).then_inc(ygs_ready, 1)
                        dve.wait_ge(g_ps, done(m))
                        v.tensor_tensor(yg_t[:], ps_g[:].rearrange("p (c t) -> p c t", c=CHUNKS), nw[:].unsqueeze(2).to_broadcast([P, CHUNKS, P]),
                                        ALU.mult).then_inc(g_ready, 1)
                    mine.end()


def spread_slices(nc, core, a):
    with Stage(nc, "spread") as st:
        w = st.sb("out_w", [P, CHUNKS, D])
        bias = st.sb("out_b", [P, D])
        sw = [st.sb(f"sw{s}", [P, HALVES, INNER]) for s in range(2)]
        sw_t = [[st.sb(f"sw_t{s}{h}", [P, CHUNKS, P]) for h in range(2)] for s in range(2)]
        diag = [st.sb(f"diagonal{s}", [P, CHUNKS, P]) for s in range(2)]
        vs = [st.sb(f"v{s}", [P, CHUNKS, D]) for s in range(2)]
        o = [st.sb(f"o{s}", [P, HALVES, D]) for s in range(2)]
        ps_v = [st.ps(f"ps_v{s}", [P, 512]) for s in range(2)]
        ps_s = [[st.ps(f"ps_sw{s}{h}", [P, 512]) for h in range(2)] for s in range(2)]
        ps_o = [st.ps(f"ps_o{s}", [P, 512]) for s in range(2)]
        loaded, cleared = st.sem("loaded"), st.sem("cleared")
        sw_loaded = [st.sem(f"sw_loaded{s}") for s in range(2)]
        diag_ready, v_ps, v_ready, sw_ps, sw_t_ready, o_ps, o_ready, added = [st.sem(n, CREDIT) for n in (
            "diagonal_ready", "v_product", "v_ready", "sw_transposed", "sw_t_ready", "out_product", "out_ready", "added")]
        with st.block() as block:
            @block.sync
            def _(sp):
                sp.dma_start(w[:], a["L3_ffn_out_w_t"].rearrange("(c p) f -> p c f", p=P)).then_inc(loaded, 16)
                sp.dma_start(bias[:], a["L3_ffn_out_b"].rearrange("(a n) -> a n", a=1).to_broadcast([P, D])).then_inc(loaded, 16)
                with sp.Fori(0, B // 2) as i:
                    for s in range(2):
                        n = i * 2 + s
                        sp.wait_ge(sw_ps, freed(n))
                        sp.dma_start(sw[s][:].rearrange("p h f -> p (h f)"), core.sw[n, :, :]).then_inc(sw_loaded[s], 16)

            @block.gpsimd
            def _(pool):
                for s in range(2):
                    nc.gpsimd.memset(diag[s][:], 0.0).then_inc(cleared, 1)

            @block.tensor
            def _(pe):
                mm = nc.tensor.matmul
                pe.wait_ge(loaded, 32)
                with pe.Fori(0, B // 2) as i:
                    for s in range(2):
                        n = i * 2 + s
                        pe.wait_ge(sw_loaded[s], i * 16 + 16)
                        pe.wait_ge(sw_t_ready, freed(n))
                        for h in range(HALVES):
                            for c in range(CHUNKS):
                                last = nc.tensor.transpose(ps_s[s][h][:, c * P:(c + 1) * P], sw[s][:, h, c * P:(c + 1) * P], core.ident[:])
                        last.then_inc(sw_ps, 1)
                        pe.wait_ge(diag_ready, done(n))
                        pe.wait_ge(v_ready, freed(n))
                        for c in range(CHUNKS):
                            last = mm(ps_v[s][:, c * D:(c + 1) * D], diag[s][:, c, :], w[:, c, :], start=True, stop=True)
                        last.then_inc(v_ps, 1)
                    for s in range(2):
                        n = i * 2 + s
                        pe.wait_ge(sw_t_ready, done(n))
                        pe.wait_ge(v_ready, done(n))
                        pe.wait_ge(o_ready, freed(n))
                        for h in range(HALVES):
                            for c in range(CHUNKS):
                                last = mm(ps_o[s][:, h * D:(h + 1) * D], sw_t[s][h][:, c, :], vs[s][:, c, :], start=c == 0, stop=c == CHUNKS - 1)
                        last.then_inc(o_ps, 1)

            @block.scalar
            def _(act):
                with act.Fori(0, B // 2) as i:
                    for s in range(2):
                        n = i * 2 + s
                        act.wait_ge(sw_ps, done(n))
                        act.wait_ge(o_ps, freed(n))
                        for h in range(HALVES):
                            last = nc.scalar.copy(sw_t[s][h][:], ps_s[s][h][:].rearrange("p (c n) -> p c n", c=CHUNKS))
                        last.then_inc(sw_t_ready, 1)
                        act.wait_ge(v_ps, done(n))
                        nc.scalar.copy(vs[s][:], ps_v[s][:].rearrange("p (c n) -> p c n", c=CHUNKS)).then_inc(v_ready, 1)

            @block.vector
            def _(dve):
                v = nc.vector
                dve.wait_ge(cleared, 2)
                dve.wait_ge(loaded, 32)
                with dve.Fori(0, B // 2) as i:
                    for s in range(2):
                        n = i * 2 + s
                        dve.wait_ge(v_ps, freed(n))
                        for k in range(2):
                            rows = slice(k * HD, (k + 1) * HD)
                            last = v.tensor_scalar(diag[s][rows, :, k * SLICES:(k + 1) * SLICES], core.u_t[rows, :, bass.ds(n * SLICES, SLICES)],
                                                   1.0, None, ALU.mult)
                        last.then_inc(diag_ready, 1)
                    for s in range(2):
                        n = i * 2 + s
                        dve.wait_ge(o_ps, done(n))
                        v.tensor_tensor(o[s][:], ps_o[s][:, 0:HALVES * D].rearrange("p (h d) -> p h d", h=HALVES),
                                        bias[:].unsqueeze(1).to_broadcast([P, HALVES, D]), ALU.add).then_inc(o_ready, 1)
                        dve.wait_ge(o_ready, done(n))
                        tiles = core.x[:, bass.ds(n * HALVES, HALVES), :]
                        v.tensor_tensor(tiles, tiles, o[s][:], ALU.add).then_inc(added, 1)
                        dve.wait_ge(added, done(n))


def store_output(nc, core, out):
    with Stage(nc, "store") as st:
        stored = st.sem("out_stored")
        with st.block() as block:
            @block.sync
            def _(sp):
                sp.dma_start(out.rearrange("b (h p) d -> p (b h) d", p=P), core.x[:]).then_inc(stored, 16)
                sp.wait_ge(stored, 16)


def build(nc, a, out):
    core = Core()
    with ExitStack() as ctx:
        core.x = ctx.enter_context(nc.sbuf_tensor("x", [P, TILES, D], F32))
        core.mean = ctx.enter_context(nc.sbuf_tensor("mean", [P, TILES], F32))
        core.rstd = ctx.enter_context(nc.sbuf_tensor("rstd", [P, TILES], F32))
        core.ident = ctx.enter_context(nc.sbuf_tensor("ident", [P, P], F32))
        core.ones = ctx.enter_context(nc.sbuf_tensor("ones", [P, P], F32))
        core.sorted_in = nc.dram_tensor("sorted_in", (ROWS_MAX, D), F32, kind="Internal").ap()
        core.sorted_out = nc.dram_tensor("sorted_out", (ROWS_MAX, D), F32, kind="Internal").ap()
        core.adj_rows = nc.dram_tensor("adj_rows", (P * B, P), F32, kind="Internal").ap()
        core.sw = nc.dram_tensor("slice_weights", (B, P, HALVES * INNER), F32, kind="Internal").ap()
        load_inputs(nc, core, a["x"])
        prepare_tables(nc, core)
        layernorm_statistics(nc, core, "norm0")
        power_graph_block(nc, core, a["adj_t"], a["L0_gnn_W_t"], a["L0_gnn_conv_w"], a["L0_gnn_conv_b"])
        layernorm_statistics(nc, core, "norm1")
        expert_block(nc, core, "glu", a["L0_ffn_w12"], a["L0_ffn_w3"], a["L0_ffn_gate_w"], a["L0_ffn_gate_b"])
        layernorm_statistics(nc, core, "norm2")
        grouped_graph_block(nc, core, a["adj_t"], a["L1_gnn_W1"], a["L1_gnn_b1"], a["L1_gnn_W2"], a["L1_gnn_b2"],
                            a["L1_gnn_fusion_w"], a["pair_mask"], a["row_mask"])
        layernorm_statistics(nc, core, "norm3")
        expert_block(nc, core, "top1", a["L1_ffn_w1"], a["L1_ffn_w2"], a["L1_ffn_gate_w"], a["L1_ffn_gate_b"],
                     a["L1_ffn_b1"], a["L1_ffn_b2"], top=1, capacity=-(-5 * B * N // (4 * 8)), guard=True)
        layernorm_statistics(nc, core, "norm4")
        recurrent_block(nc, core, a["adj"], a["L2_gnn_W_ioux_t"], a["L2_gnn_W_iouh_t"], a["L2_gnn_b_ioux"], a["L2_gnn_b_iouh"],
                        a["L2_gnn_W_coux_t"], a["L2_gnn_W_couh_t"], a["L2_gnn_b_coux"], a["L2_gnn_b_couh"])
        layernorm_statistics(nc, core, "norm5")
        expert_block(nc, core, "top2", a["L2_ffn_W1_t"], a["L2_ffn_W2_t"], a["L2_ffn_Wg_t"], a["L2_ffn_bg"],
                     a["L2_ffn_b1"], a["L2_ffn_b2"])
        layernorm_statistics(nc, core, "norm6")
        attention_block(nc, core, a["adj"], a["L3_gnn_W"], a["L3_gnn_W_t"], a["L3_gnn_a2"], a["L3_gnn_gamma"], a["L3_gnn_beta"])
        layernorm_statistics(nc, core, "norm7")
        slice_block(nc, core, a)
        store_output(nc, core, out)


def _laid_out(inputs):
    a = {k: np.asarray(v) for k, v in inputs.items()}
    a["adj_t"] = a["adj"].transpose(0, 2, 1)
    a["L0_gnn_W_t"] = a["L0_gnn_W"].T
    a["L0_ffn_w12"] = np.concatenate([a["L0_ffn_w1"], a["L0_ffn_w2"]], axis=2)
    a["L2_ffn_W1_t"] = a["L2_ffn_W1"].transpose(0, 2, 1)
    a["L2_ffn_W2_t"] = a["L2_ffn_W2"].transpose(0, 2, 1)
    a["L2_ffn_Wg_t"] = a["L2_ffn_Wg"].T
    a["pair_mask"], a["row_mask"] = group_masks()
    a["L3_gnn_W_t"] = a["L3_gnn_W"].T
    a["L3_gnn_a2"] = a["L3_gnn_a"].reshape(2, D).T
    for k in ("W_ioux", "W_iouh", "W_coux", "W_couh"):
        a["L2_gnn_" + k + "_t"] = a["L2_gnn_" + k].T
    for k in ("W_fx", "W_slice", "hy_in_w", "hy_fcD_w", "hy_out_w", "out_w"):
        a["L3_ffn_" + k + "_t"] = a["L3_ffn_" + k].T
    a["col_mask"], a["lhs_mask"] = order_masks()
    return {k: np.ascontiguousarray(a[k]) for k in USED}


def kernel(**inputs):
    import concourse.bacc as _bacc
    from concourse.bass_utils import run_bass_kernel_spmd as _run

    nc = _bacc.Bacc("TRN2", target_bir_lowering=False, num_devices=1)
    arrays = _laid_out(inputs)
    aps = {k: nc.dram_tensor("in_" + k, v.shape, mybir.dt.from_np(v.dtype), kind="ExternalInput").ap()
           for k, v in arrays.items()}
    out = nc.dram_tensor("out_0", (B, N, D), F32, kind="ExternalOutput").ap()
    build(nc, aps, out)
    r = _run(nc, [{"in_" + k: v for k, v in arrays.items()}], core_ids=[0])
    return r.results[0]["out_0"]
```

```python
import concourse.bass as bass
import numpy as np
from concourse import mybir
from concourse.alu_op_type import AluOpType as ALU
from contextlib import ExitStack

F32 = mybir.dt.float32
U32 = mybir.dt.uint32
U8 = mybir.dt.uint8
ACT = mybir.ActivationFunctionType
AXX = mybir.AxisListType.X

B, N, D = 32, 256, 128
P = 128
HALVES = N // P
TILES = B * HALVES
CREDIT = 2
LN_EPS = 1e-5


def done(n):
    return n + (1 + CREDIT)


def freed(n):
    return n + 1


class Own:

    def __init__(self, eng, sem, turn, per):
        self.eng, self.sem, self.base, self.per, self.k = eng, sem, turn * per, per, 0

    def step(self, ins):
        self.mark(ins)
        self.join()

    def mark(self, ins):
        ins.then_inc(self.sem, 1)
        self.k += 1

    def join(self):
        self.eng.wait_ge(self.sem, self.base + self.k)

    def end(self):
        assert self.k == self.per, (self.k, self.per)


class Stage:

    def __init__(self, nc, name):
        self.nc, self.name, self.sems, self.ctx = nc, name, [], ExitStack()

    def __enter__(self):
        return self

    def sb(self, name, shape, dt=F32):
        return self.ctx.enter_context(self.nc.sbuf_tensor(self.name + "_" + name, list(shape), dt))

    def ps(self, name, shape, dt=F32):
        return self.ctx.enter_context(self.nc.psum_tensor(self.name + "_" + name, list(shape), dt))

    def sem(self, name, credit=0):
        s = self.nc.alloc_semaphore(self.name + "_" + name)
        if credit:
            self.nc.sync.sem_inc(s, credit)
        self.sems.append(s)
        return s

    def block(self):
        self.nc.all_engine_barrier()
        return self.nc.Block()

    def __exit__(self, *exc):
        self.ctx.close()
        self.nc.clear_and_free_semaphores(self.sems)
        self.nc.all_engine_barrier()


class Core:
    pass


def hold(eng, sem):
    eng.sem_inc(sem, 1)

USED = ["x", "adj_t", "L0_gnn_W_t", "L0_gnn_conv_w", "L0_gnn_conv_b",
        "L0_ffn_w12", "L0_ffn_w3", "L0_ffn_gate_w", "L0_ffn_gate_b",
        "L1_ffn_w1", "L1_ffn_w2", "L1_ffn_gate_w", "L1_ffn_gate_b", "L1_ffn_b1", "L1_ffn_b2",
        "L2_ffn_W1_t", "L2_ffn_W2_t", "L2_ffn_Wg_t", "L2_ffn_bg", "L2_ffn_b1", "L2_ffn_b2",
        "L1_gnn_W1", "L1_gnn_b1", "L1_gnn_W2", "L1_gnn_b2", "L1_gnn_fusion_w", "pair_mask", "row_mask",
        "adj", "L3_gnn_W", "L3_gnn_W_t", "L3_gnn_a2", "L3_gnn_gamma", "L3_gnn_beta",
        "L2_gnn_W_ioux_t", "L2_gnn_W_iouh_t", "L2_gnn_b_ioux", "L2_gnn_b_iouh",
        "L2_gnn_W_coux_t", "L2_gnn_W_couh_t", "L2_gnn_b_coux", "L2_gnn_b_couh",
        "L3_ffn_W_x", "L3_ffn_b_x", "L3_ffn_W_fx_t", "L3_ffn_b_fx", "L3_ffn_W_slice_t", "L3_ffn_b_slice", "L3_ffn_temperature",
        "L3_ffn_hy_in_w_t", "L3_ffn_hy_conv_w", "L3_ffn_hy_conv_b", "L3_ffn_hy_dt_bias", "L3_ffn_hy_A_log", "L3_ffn_hy_D",
        "L3_ffn_hy_fcD_w_t", "L3_ffn_hy_norm_w", "L3_ffn_hy_out_w_t", "L3_ffn_out_w_t", "L3_ffn_out_b", "col_mask", "lhs_mask"]


def load_inputs(nc, core, x):
    with Stage(nc, "load") as st:
        loaded = st.sem("x_loaded")
        zeroed = st.sem("identity_zeroed")
        with st.block() as block:
            @block.sync
            def _(sp):
                sp.dma_start(core.x[:], x.rearrange("b (h p) d -> p (b h) d", p=P)).then_inc(loaded, 16)
                sp.wait_ge(loaded, 16)

            @block.gpsimd
            def _(pool):
                nc.gpsimd.memset(core.ident[:], 0.0).then_inc(zeroed, 1)
                nc.gpsimd.memset(core.ones[:], 1.0)
                pool.wait_ge(zeroed, 1)
                nc.gpsimd.affine_select(out=core.ident[:], in_=core.ident[:], compare_op=ALU.not_equal, fill=1.0,
                                        base=0, pattern=[[-1, P]], channel_multiplier=1)


def layernorm_statistics(nc, core, name, of=None, parts_known=False):
    of = core.x if of is None else of
    with Stage(nc, name) as st:
        GROUP = 16
        parts = core.parts
        half_gap = st.sb("half_gap", [P, TILES])
        root = st.sb("root", [P, TILES])
        parts_done, variance, rooted, own = [st.sem(n) for n in ("parts_done", "variance_ready", "root_ready", "vector_steps")]
        with st.block() as block:
            @block.vector
            def _(dve):
                if not parts_known:
                    with dve.Fori(0, TILES // GROUP) as i:
                        for k in range(GROUP):
                            last = nc.vector.bn_stats(parts[:, i * GROUP + k, :], of[:, i * GROUP + k, :])
                        last.then_inc(parts_done, 1)
                    dve.wait_ge(parts_done, TILES // GROUP)
                even, odd = parts[:, :, 0:3], parts[:, :, 3:6]
                mine = Own(dve, own, 0, 7)
                mine.step(nc.vector.tensor_tensor(core.mean[:], even[:, :, 1], odd[:, :, 1], ALU.add))
                mine.step(nc.vector.tensor_scalar(core.mean[:], core.mean[:], 0.5, None, ALU.mult))
                mine.step(nc.vector.tensor_tensor(half_gap[:], core.mean[:], odd[:, :, 1], ALU.subtract))
                mine.step(nc.vector.tensor_tensor(half_gap[:], half_gap[:], half_gap[:], ALU.mult))
                mine.step(nc.vector.tensor_tensor(root[:], even[:, :, 2], odd[:, :, 2], ALU.add))
                mine.step(nc.vector.scalar_tensor_tensor(root[:], root[:], 1.0 / D, half_gap[:], ALU.mult, ALU.add))
                mine.step(nc.vector.tensor_scalar(root[:], root[:], LN_EPS, None, ALU.add))
                nc.vector.engine_nop().then_inc(variance, 1)
                dve.wait_ge(rooted, 1)
                nc.vector.reciprocal(core.rstd[:], root[:])

            @block.scalar
            def _(act):
                act.wait_ge(variance, 1)
                nc.scalar.activation(root[:], root[:], ACT.Sqrt).then_inc(rooted, 1)


def power_graph_block(nc, core, adj_t, w_t, conv_w, conv_b):
    POWERS = 4
    SLOPE = 0.2
    with Stage(nc, "power") as st:
        w = st.sb("w", [P, D])
        coef = st.sb("coef", [P, POWERS + 1])
        a_t = [st.sb(f"a_t{s}", [P, HALVES, N]) for s in range(2)]
        y = [st.sb(f"y{s}", [P, HALVES, D]) for s in range(2)]
        y_t = [st.sb(f"y_t{s}", [P, N]) for s in range(2)]
        cur = [st.sb(f"cur{s}", [P, HALVES, D + 4]) for s in range(2)]
        acc = [st.sb(f"acc{s}", [P, HALVES, D]) for s in range(2)]
        rinv = [st.sb(f"rinv{s}", [P, HALVES]) for s in range(2)]
        ps_t = [st.ps(f"ps_t{s}", [P, 512]) for s in range(2)]
        ps_c = [[st.ps(f"ps_c{s}{h}", [P, 512]) for h in range(2)] for s in range(2)]
        weights = st.sem("weights_loaded")
        adj_loaded = [st.sem(f"adj_loaded{s}") for s in range(2)]
        y_ready, y_t_ps, y_t_ready = [st.sem(n, CREDIT) for n in ("y_ready", "y_t_transposed", "y_t_ready")]
        prod = [st.sem(f"product{k}_ready", CREDIT) for k in range(POWERS)]
        cur_ready = [st.sem(f"power{k}_ready", CREDIT) for k in range(POWERS)]
        rinv_ready, acc_ready, x_added = [st.sem(n, CREDIT) for n in ("rinv_ready", "sum_ready", "x_added")]
        cur_added = [st.sem(f"powers_added{s}", CREDIT) for s in range(2)]
        own = st.sem("vector_steps")
        passed = st.sem("pool_passed")
        with st.block() as block:
            @block.sync
            def _(sp):
                sp.dma_start(w[:], w_t).then_inc(weights, 16)
                sp.dma_start(coef[:, 0:POWERS], conv_w.rearrange("(a k) -> a k", a=1).to_broadcast([P, POWERS])).then_inc(weights, 16)
                sp.dma_start(coef[:, POWERS:POWERS + 1], conv_b.rearrange("(a k) -> a k", a=1).to_broadcast([P, 1])).then_inc(weights, 16)
                with sp.Fori(0, B // 2) as i:
                    for s in range(2):
                        sp.wait_ge(prod[POWERS - 1], freed(i * 2 + s))
                        sp.dma_start(a_t[s][:], adj_t[i * 2 + s, :, :].rearrange("(h p) n -> p h n", p=P)).then_inc(adj_loaded[s], 16)

            def loop(eng, turn):
                with eng.Fori(0, B // 2 - 1) as i:
                    turn(i, True)
                turn(B // 2 - 1, False)

            @block.tensor
            def _(pe):
                def transposes(i):
                    for s in range(2):
                        pe.wait_ge(y_t_ready, freed(i * 2 + s))
                        pe.wait_ge(y_ready, done(i * 2 + s))
                        for h in range(HALVES):
                            last = nc.tensor.transpose(ps_t[s][:, h * P:(h + 1) * P], y[s][:, h, :], core.ident[:])
                        last.then_inc(y_t_ps, 1)

                def turn(i, more):
                    for s in range(2):
                        pe.wait_ge(y_t_ready, done(i * 2 + s))
                        pe.wait_ge(cur_ready[POWERS - 1], freed(i * 2 + s))
                        for h in range(HALVES):
                            last = nc.tensor.matmul(ps_c[s][h][:, 0:D], y_t[s][:, h * P:(h + 1) * P], w[:], start=True, stop=True)
                        last.then_inc(prod[0], 1)
                    for k in range(1, POWERS):
                        for s in range(2):
                            if k == 1:
                                pe.wait_ge(adj_loaded[s], i * 16 + 16)
                            pe.wait_ge(cur_ready[k - 1], done(i * 2 + s))
                            width = D + 1 if k == 1 else D
                            for h in range(HALVES):
                                for m in range(HALVES):
                                    last = nc.tensor.matmul(ps_c[s][h][:, 0:width], a_t[s][:, m, h * P:(h + 1) * P],
                                                            cur[s][:, m, 0:width], start=m == 0, stop=m == HALVES - 1)
                            last.then_inc(prod[k], 1)
                        if k == 2 and more:
                            transposes(i + 1)

                pe.wait_ge(weights, 48)
                transposes(0)
                loop(pe, turn)

            @block.scalar
            def _(act):
                def keep_y_t(i):
                    for s in range(2):
                        act.wait_ge(y_t_ps, done(i * 2 + s))
                        act.wait_ge(prod[0], freed(i * 2 + s))
                        nc.scalar.copy(y_t[s][:], ps_t[s][:, 0:N]).then_inc(y_t_ready, 1)

                def turn(i, more):
                    for k in range(POWERS):
                        for s in range(2):
                            n = i * 2 + s
                            act.wait_ge(cur_added[s], i * POWERS + (k + CREDIT))
                            act.wait_ge(rinv_ready if k == 1 else prod[k], done(n))
                            for h in range(HALVES):
                                last = nc.scalar.activation(cur[s][:, h, 0:D], ps_c[s][h][:, 0:D], ACT.Copy,
                                                            scale=1.0 if k == 0 else rinv[s][:, h:h + 1])
                            last.then_inc(cur_ready[k], 1)
                        if k == 2 and more:
                            keep_y_t(i + 1)

                keep_y_t(0)
                loop(act, turn)

            @block.gpsimd
            def _(pool):
                with pool.Fori(0, B // 2) as i:
                    for s in range(2):
                        n = i * 2 + s
                        pool.wait_ge(acc_ready, done(n))
                        hold(pool, passed)
                        here = core.x[:, bass.ds(n * HALVES, HALVES), :]
                        nc.gpsimd.tensor_tensor(here, here, acc[s][:], ALU.add).then_inc(x_added, 1)

            @block.vector
            def _(dve):
                def normalise(i):
                    for s in range(2):
                        n = i * 2 + s
                        dve.wait_ge(y_t_ps, freed(n))
                        for h in range(HALVES):
                            t = n * 2 + h
                            last = nc.vector.tensor_scalar(y[s][:, h, :], core.x[:, t, :], core.mean[:, bass.ds(t, 1)],
                                                           core.rstd[:, bass.ds(t, 1)], ALU.subtract, ALU.mult)
                        last.then_inc(y_ready, 1)

                def turn(i, more):
                    mine = Own(dve, own, i, 2)
                    for k in range(POWERS):
                        if k == 1:
                            for s in range(2):
                                dve.wait_ge(prod[1], done(i * 2 + s))
                                for h in range(HALVES):
                                    last = nc.vector.tensor_scalar(rinv[s][:, h:h + 1], ps_c[s][h][:, D:D + 1], 1e-9, None, ALU.add)
                                mine.step(last)
                                nc.vector.reciprocal(rinv[s][:], rinv[s][:]).then_inc(rinv_ready, 1)
                            if more:
                                normalise(i + 1)
                        for s in range(2):
                            n = i * 2 + s
                            dve.wait_ge(cur_ready[k], done(n))
                            if k == 0:
                                dve.wait_ge(x_added, freed(n))
                                last = nc.vector.tensor_scalar(acc[s][:], cur[s][:, :, 0:D], coef[:, 0:1], coef[:, POWERS:POWERS + 1], ALU.mult, ALU.add)
                            else:
                                dve.wait_ge(cur_added[s], i * POWERS + (k + CREDIT))
                                last = nc.vector.scalar_tensor_tensor(acc[s][:], cur[s][:, :, 0:D], coef[:, k:k + 1], acc[s][:], ALU.mult, ALU.add)
                            last.then_inc(cur_added[s], 1)
                    for s in range(2):
                        dve.wait_ge(cur_added[s], i * POWERS + (POWERS + CREDIT))
                        nc.vector.scalar_tensor_tensor(acc[s][:], acc[s][:], SLOPE, acc[s][:], ALU.mult, ALU.max).then_inc(acc_ready, 1)
                    mine.end()

                for s in range(2):
                    nc.vector.memset(cur[s][:, :, D:D + 1], 1.0)
                dve.wait_ge(weights, 48)
                normalise(0)
                loop(dve, turn)


TURNS = 4
UP = 512
ROWS_MAX = (2 * B * N // P + 16) * P


def start_tables(nc, core, st):
    PART = 9 * P
    zeros = st.sb("zeros", [P, PART])
    zeroed, written = st.sem("zeros_ready"), st.sem("table_written")
    pieces = ROWS_MAX * D // (P * PART)
    flat = core.sorted_in.rearrange("(a p r) d -> a p (r d)", a=pieces, p=P)
    with st.block() as block:
        @block.vector
        def _(dve):
            nc.vector.memset(zeros[:], 0.0).then_inc(zeroed, 1)

        @block.sync
        def _(sp):
            sp.wait_ge(zeroed, 1)
            for a in range(pieces):
                sp.dma_start(flat[a, :, :], zeros[:]).then_inc(written, 16)
    return written, 16 * pieces


def finish_tables(nc, st, written, count):
    with st.block() as block:
        @block.sync
        def _(sp):
            sp.wait_ge(written, count)


def expert_block(nc, core, name, w_up, w_down, gate_w, gate_b, b_up=None, b_down=None, top=2, capacity=None, guard=False):
    E = w_up.shape[0]
    gated = b_up is None
    HC = w_down.shape[1] // P
    Q = top * TILES + E
    assert Q % TURNS == 0 and Q * P <= ROWS_MAX
    with Stage(nc, name) as keep:
        expert_of = keep.sb("experts_of_turns", [1, Q // TURNS + 1, 8], U32)
        wu = keep.sb("w_up", [P, E * UP])
        wd = keep.sb("w_down", [P, E * HC * D])
        bu, bd = (None, None) if gated else (keep.sb("b_up", [P, E * UP]), keep.sb("b_down", [P, E * D]))
        weights = keep.sem("expert_weights_loaded")

        def load_weights(sp):
            sp.dma_start(wu[:].rearrange("p (e f) -> p e f", e=E), w_up.rearrange("e d f -> d e f")).then_inc(weights, 16)
            sp.dma_start(wd[:].rearrange("p (e c f) -> p e c f", e=E, c=HC),
                         w_down.rearrange("e (c p) f -> p e c f", p=P)).then_inc(weights, 16)
            if not gated:
                sp.dma_start(bu[:], b_up.rearrange("(a e) f -> a (e f)", a=1).to_broadcast([P, E * UP])).then_inc(weights, 16)
                sp.dma_start(bd[:], b_down.rearrange("(a e) f -> a (e f)", a=1).to_broadcast([P, E * D])).then_inc(weights, 16)

        slot = [keep.sb(f"slot{k}", [P, TILES]) for k in range(top)]
        weight = [keep.sb(f"weight{k}", [P, TILES]) for k in range(top)]
        route(nc, core, name, E, top, Q, gate_w, gate_b, capacity, expert_of, slot, weight, load_weights)
        scatter_tokens(nc, core, name, top, slot)
        run_experts(nc, core, name, E, Q, HC, gated, wu, wd, bu, bd, weights, 2 if gated else 4, expert_of)
        gather_tokens(nc, core, name, top, Q, slot, weight, guard)


def route(nc, core, name, E, top, Q, gate_w, gate_b, capacity, expert_of, slot, weight, load_weights):
    GROUP = 4
    BIG = 1e30
    MAGIC = float(2 ** 23)
    with Stage(nc, name + "_route") as st:
        gw = st.sb("gate_w", [P, E])
        gb = st.sb("gate_b", [P, E])
        y = [st.sb(f"y{s}", [P, GROUP, D]) for s in range(2)]
        y_t = [st.sb(f"y_t{s}", [P, GROUP * P]) for s in range(2)]
        logits = st.sb("logits", [P, TILES, E])
        ps_t = [st.ps(f"ps_t{s}", [P, 512]) for s in range(2)]
        ps_l = [st.ps(f"ps_l{s}", [P, 512]) for s in range(2)]
        weights = st.sem("weights_loaded")
        y_ready, y_t_ps, y_t_ready, logits_ps, logits_ready = [st.sem(n, CREDIT) for n in (
            "y_ready", "y_t_transposed", "y_t_ready", "logits_product", "logits_ready")]
        with st.block() as block:
            @block.sync
            def _(sp):
                sp.dma_start(gw[:], gate_w).then_inc(weights, 16)
                sp.dma_start(gb[:], gate_b.rearrange("(a k) -> a k", a=1).to_broadcast([P, E])).then_inc(weights, 16)
                load_weights(sp)

            @block.vector
            def _(dve):
                def normalise(n, s):
                    dve.wait_ge(y_t_ps, freed(n))
                    for k in range(GROUP):
                        t = n * GROUP + k
                        last = nc.vector.tensor_scalar(y[s][:, k, :], core.x[:, t, :], core.mean[:, bass.ds(t, 1)],
                                                       core.rstd[:, bass.ds(t, 1)], ALU.subtract, ALU.mult)
                    last.then_inc(y_ready, 1)

                def keep_logits(n, s):
                    dve.wait_ge(logits_ps, done(n))
                    nc.vector.tensor_tensor(logits[:, bass.ds(n * GROUP, GROUP), :],
                                            ps_l[s][:, 0:GROUP * E].rearrange("p (t e) -> p t e", e=E),
                                            gb[:].unsqueeze(1).to_broadcast([P, GROUP, E]), ALU.add).then_inc(logits_ready, 1)

                dve.wait_ge(weights, 32)
                normalise(0, 0)
                with dve.Fori(0, TILES // GROUP // 2 - 1) as i:
                    normalise(i * 2 + 1, 1)
                    keep_logits(i * 2, 0)
                    normalise(i * 2 + 2, 0)
                    keep_logits(i * 2 + 1, 1)
                n = TILES // GROUP - 2
                normalise(n + 1, 1)
                keep_logits(n, 0)
                keep_logits(n + 1, 1)

            @block.tensor
            def _(pe):
                pe.wait_ge(weights, 32)
                with pe.Fori(0, TILES // GROUP // 2) as i:
                    for s in range(2):
                        n = i * 2 + s
                        pe.wait_ge(y_t_ready, freed(n))
                        pe.wait_ge(y_ready, done(n))
                        for k in range(GROUP):
                            last = nc.tensor.transpose(ps_t[s][:, k * P:(k + 1) * P], y[s][:, k, :], core.ident[:])
                        last.then_inc(y_t_ps, 1)
                    for s in range(2):
                        n = i * 2 + s
                        pe.wait_ge(logits_ready, freed(n))
                        pe.wait_ge(y_t_ready, done(n))
                        for k in range(GROUP):
                            last = nc.tensor.matmul(ps_l[s][:, k * E:(k + 1) * E], y_t[s][:, k * P:(k + 1) * P], gw[:], start=True, stop=True)
                        last.then_inc(logits_ps, 1)

            @block.scalar
            def _(act):
                with act.Fori(0, TILES // GROUP // 2) as i:
                    for s in range(2):
                        n = i * 2 + s
                        act.wait_ge(logits_ps, freed(n))
                        act.wait_ge(y_t_ps, done(n))
                        nc.scalar.copy(y_t[s][:], ps_t[s][:]).then_inc(y_t_ready, 1)

        with Stage(nc, name + "_rank") as rk:
            upto = rk.sb("upto", [P, P])
            chosen = [rk.sb(f"chosen{k}", [P, TILES, E]) for k in range(top)]
            any_chosen = rk.sb("any_chosen", [P, TILES, E])
            wide = [rk.sb(f"wide{k}", [P, TILES, E]) for k in range(3)]
            number_i = rk.sb("expert_number_int", [P, E], mybir.dt.int32)
            number = rk.sb("expert_number", [P, E])
            row_i = rk.sb("first_row_int", [1, Q], mybir.dt.int32)
            row = rk.sb("first_row", [1, Q])
            at_or_behind = rk.sb("at_or_behind", [1, Q, E])
            tile_expert = rk.sb("tile_expert", [1, Q])
            best = [rk.sb(f"best{k}", [P, TILES]) for k in range(2)]
            small = [rk.sb(f"small{k}", [P, TILES]) for k in range(3)]
            share = [rk.sb(f"share{k}", [P, E]) for k in range(3)]
            ps_rank = [rk.ps(f"ps_rank{j}", [P, 512]) for j in range(2)]
            ps_total = [rk.ps(f"ps_total{j}", [P, 512]) for j in range(2)]
            consts, consts_step, picked, counted, exp_in, exp_out, own = [rk.sem(n) for n in (
                "constants_ready", "constants_step", "chosen_ready", "counts_ready", "exp_input_ready", "exp_ready", "vector_steps")]
            banks = TILES * E // 512
            per_bank = 512 // E
            with rk.block() as block:
                @block.gpsimd
                def _(pool):
                    nc.gpsimd.iota(number_i[:], pattern=[[1, E]], base=0, channel_multiplier=0).then_inc(consts, 1)
                    nc.gpsimd.iota(row_i[:], pattern=[[P, Q]], base=0, channel_multiplier=0).then_inc(consts, 1)
                    nc.gpsimd.memset(upto[:], 1.0).then_inc(consts_step, 1)
                    pool.wait_ge(consts_step, 1)
                    nc.gpsimd.affine_select(out=upto[:], in_=upto[:], compare_op=ALU.is_ge, fill=0.0, base=0,
                                            pattern=[[1, P]], channel_multiplier=-1).then_inc(consts, 1)

                @block.tensor
                def _(pe):
                    pe.wait_ge(consts, 3)
                    pe.wait_ge(picked, 1)
                    for j in range(banks):
                        pick = any_chosen[:, j * per_bank:(j + 1) * per_bank, :]
                        nc.tensor.matmul(ps_rank[j][:], upto[:], pick, start=True, stop=True)
                        nc.tensor.matmul(ps_total[j][:], core.ones[:], pick, start=True, stop=True).then_inc(counted, 1)

                @block.scalar
                def _(act):
                    act.wait_ge(exp_in, 1)
                    if top == 2:
                        nc.scalar.activation(small[0][:], small[0][:], ACT.Exp).then_inc(exp_out, 1)
                    else:
                        nc.scalar.activation(wide[0][:], wide[0][:], ACT.Exp).then_inc(exp_out, 1)

                @block.vector
                def _(dve):
                    v = nc.vector
                    mine = Own(dve, own, 0, 0)
                    each = lambda a: a.unsqueeze(2).to_broadcast([P, TILES, E])
                    tokens = lambda a: a.unsqueeze(1).to_broadcast([P, TILES, E])
                    dve.wait_ge(consts, 3)
                    mine.step(v.tensor_copy(number[:], number_i[:]))
                    mine.step(v.tensor_copy(row[:], row_i[:]))
                    scores = logits
                    for k in range(top):
                        mine.step(v.tensor_reduce(best[k][:], scores[:], AXX, ALU.max))
                        mine.step(v.tensor_tensor(wide[0][:], scores[:], each(best[k][:]), ALU.is_lt))
                        mine.step(v.tensor_scalar(wide[0][:], wide[0][:], float(E), None, ALU.mult))
                        mine.step(v.tensor_tensor(wide[0][:], wide[0][:], tokens(number[:]), ALU.add))
                        mine.step(v.tensor_reduce(small[0][:], wide[0][:], AXX, ALU.min))
                        mine.step(v.tensor_tensor(chosen[k][:], tokens(number[:]), each(small[0][:]), ALU.is_equal))
                        if k + 1 < top:
                            mine.step(v.tensor_scalar(wide[1][:], chosen[k][:], -BIG, None, ALU.mult))
                            mine.step(v.tensor_tensor(wide[1][:], wide[1][:], scores[:], ALU.add))
                            scores = wide[1]
                    if top == 2:
                        mine.step(v.tensor_tensor(any_chosen[:], chosen[0][:], chosen[1][:], ALU.add))
                        mine.step(v.tensor_tensor(small[0][:], best[1][:], best[0][:], ALU.subtract))
                    else:
                        mine.step(v.tensor_copy(any_chosen[:], chosen[0][:]))
                        mine.step(v.tensor_tensor(wide[0][:], logits[:], each(best[0][:]), ALU.subtract))
                    v.engine_nop().then_inc(picked, 1)
                    v.engine_nop().then_inc(exp_in, 1)
                    dve.wait_ge(exp_out, 1)
                    if top == 2:
                        mine.step(v.tensor_scalar(small[1][:], small[0][:], 1.0, None, ALU.add))
                        mine.step(v.reciprocal(weight[0][:], small[1][:]))
                        mine.step(v.tensor_tensor(weight[1][:], weight[0][:], small[0][:], ALU.mult))
                    else:
                        mine.step(v.tensor_reduce(small[1][:], wide[0][:], AXX, ALU.add))
                        mine.step(v.reciprocal(weight[0][:], small[1][:]))
                    dve.wait_ge(counted, banks)
                    for j in range(banks):
                        mine.step(v.tensor_copy(wide[0][:, j * per_bank:(j + 1) * per_bank, :],
                                                ps_total[j][:].rearrange("p (t e) -> p t e", e=E)))
                    a, b = wide[0], wide[1]
                    gap = 1
                    while gap < TILES:
                        mine.step(v.tensor_copy(b[:, 0:gap, :], a[:, 0:gap, :]))
                        mine.step(v.tensor_tensor(b[:, gap:, :], a[:, gap:, :], a[:, :TILES - gap, :], ALU.add))
                        a, b = b, a
                        gap *= 2
                    mine.step(v.tensor_scalar(share[0][:], a[:, TILES - 1, :], float(P - 1), 1.0 / P, ALU.add, ALU.mult))
                    mine.step(v.tensor_scalar(share[0][:], share[0][:], 0.5 - 0.5 / P, None, ALU.subtract))
                    mine.step(v.tensor_scalar(share[0][:], share[0][:], MAGIC, None, ALU.add))
                    mine.step(v.tensor_scalar(share[0][:], share[0][:], MAGIC, None, ALU.subtract))
                    mine.step(v.tensor_scalar(share[0][:], share[0][:], float(P), None, ALU.mult))
                    mine.step(v.tensor_copy(share[1][:], share[0][:]))
                    c, d = share[1], share[2]
                    gap = 1
                    while gap < E:
                        mine.step(v.tensor_copy(d[:, 0:gap], c[:, 0:gap]))
                        mine.step(v.tensor_tensor(d[:, gap:], c[:, gap:], c[:, :E - gap], ALU.add))
                        c, d = d, c
                        gap *= 2
                    mine.step(v.tensor_tensor(c[:], c[:], share[0][:], ALU.subtract))
                    for j in range(banks):
                        part = slice(j * per_bank, (j + 1) * per_bank)
                        mine.step(v.tensor_tensor(wide[2][:, part, :], a[:, part, :],
                                                  ps_total[j][:].rearrange("p (t e) -> p t e", e=E), ALU.subtract))
                        mine.step(v.tensor_tensor(wide[2][:, part, :], wide[2][:, part, :],
                                                  ps_rank[j][:].rearrange("p (t e) -> p t e", e=E), ALU.add))
                    if capacity is not None:
                        mine.step(v.tensor_tensor(b[:], chosen[0][:], wide[2][:], ALU.mult))
                        mine.step(v.tensor_reduce(small[0][:], b[:], AXX, ALU.add))
                        mine.step(v.tensor_scalar(small[0][:], small[0][:], float(capacity), None, ALU.is_le))
                        mine.step(v.tensor_tensor(weight[0][:], weight[0][:], small[0][:], ALU.mult))
                    mine.step(v.tensor_tensor(wide[2][:], wide[2][:], tokens(c[:]), ALU.add))
                    for k in range(top):
                        mine.step(v.tensor_tensor(b[:], chosen[k][:], wide[2][:], ALU.mult))
                        mine.step(v.tensor_reduce(slot[k][:], b[:], AXX, ALU.add))
                        mine.step(v.tensor_scalar(slot[k][:], slot[k][:], 1.0, None, ALU.subtract))
                    mine.step(v.tensor_tensor(at_or_behind[:], row[:].unsqueeze(2).to_broadcast([1, Q, E]),
                                              c[0:1, :].unsqueeze(1).to_broadcast([1, Q, E]), ALU.is_ge))
                    mine.step(v.tensor_reduce(tile_expert[:], at_or_behind[:], AXX, ALU.add))
                    mine.step(v.memset(expert_of[:], 0))
                    for j in range(TURNS + 2):
                        tiles = slice(j - 1 if j else TURNS - 1, Q, TURNS)
                        first = 1 if j == 0 else 0
                        count = len(range(Q)[tiles])
                        mine.step(v.tensor_scalar(expert_of[:, first:first + count, j], tile_expert[:, tiles], 1.0, None, ALU.subtract))


MOVED = 4


def scatter_tokens(nc, core, name, top, slot):
    with Stage(nc, name + "_scatter") as st:
        y = [st.sb(f"y{s}", [P, MOVED, D]) for s in range(2)]
        at = [[st.sb(f"at{s}{k}", [P, MOVED], U32) for k in range(top)] for s in range(2)]
        ready = st.sem("rows_ready", CREDIT)
        sent = [st.sem(f"rows_sent{s}") for s in range(2)]
        passed = st.sem("pool_passed")
        per = 16 * top * MOVED
        with st.block() as block:
            @block.vector
            def _(dve):
                def rows(n, s):
                    for j in range(MOVED):
                        t = n * MOVED + j
                        nc.vector.tensor_scalar(y[s][:, j, :], core.x[:, t, :], core.mean[:, bass.ds(t, 1)],
                                                core.rstd[:, bass.ds(t, 1)], ALU.subtract, ALU.mult)
                    for k in range(top):
                        last = nc.vector.tensor_scalar(at[s][k][:], slot[k][:, bass.ds(n * MOVED, MOVED)], 0.0, None, ALU.add)
                    last.then_inc(ready, 1)

                rows(0, 0)
                rows(1, 1)
                with dve.Fori(1, TILES // MOVED // 2) as i:
                    for s in range(2):
                        dve.wait_ge(sent[s], i * per)
                        rows(i * 2 + s, s)

            @block.gpsimd
            def _(pool):
                with pool.Fori(0, TILES // MOVED // 2) as i:
                    for s in range(2):
                        pool.wait_ge(ready, done(i * 2 + s))
                        hold(pool, passed)
                        for j in range(MOVED):
                            for k in range(top):
                                nc.gpsimd.indirect_dma_start(core.sorted_in, bass.IndirectOffsetOnAxis(ap=at[s][k][:, j:j + 1], axis=0),
                                                             y[s][:, j, :], None).then_inc(sent[s], 16)
                for s in range(2):
                    pool.wait_ge(sent[s], per * (TILES // MOVED // 2))


def gather_tokens(nc, core, name, top, Q, slot, weight, guard):
    with Stage(nc, name + "_gather") as st:
        rows = [[st.sb(f"rows{s}{k}", [P, MOVED, D]) for k in range(top)] for s in range(2)]
        at = [[st.sb(f"at{s}{k}", [P, MOVED], U32) for k in range(top)] for s in range(2)]
        safe = st.sb("safe", [P, MOVED, D])
        zero_or_nan = st.sb("zero_or_nan", [P, MOVED, D])
        mask = st.sb("mask", [P, MOVED, D], U8)
        at_ready, added = [st.sem(n, CREDIT) for n in ("indices_ready", "rows_added")]
        got = [st.sem(f"rows_got{s}") for s in range(2)]
        passed = st.sem("pool_passed")
        own, passed_v = st.sem("vector_steps"), st.sem("vector_passed")
        per = 16 * top * MOVED
        last_i = TILES // MOVED // 2 - 1
        with st.block() as block:
            @block.gpsimd
            def _(pool):
                with pool.Fori(0, TILES // MOVED // 2) as i:
                    for s in range(2):
                        pool.wait_ge(added, freed(i * 2 + s))
                        pool.wait_ge(at_ready, done(i * 2 + s))
                        hold(pool, passed)
                        for j in range(MOVED):
                            for k in range(top):
                                nc.gpsimd.indirect_dma_start(rows[s][k][:, j, :], None, core.sorted_out[0:Q * P, :],
                                                             bass.IndirectOffsetOnAxis(ap=at[s][k][:, j:j + 1], axis=0)).then_inc(got[s], 16)

            @block.vector
            def _(dve):
                def indices(n, i, s):
                    if not isinstance(n, int):
                        dve.wait_ge(got[s], i * per)
                    for k in range(top):
                        last = nc.vector.tensor_scalar(at[s][k][:], slot[k][:, bass.ds(n * MOVED, MOVED)], 0.0, None, ALU.add)
                    last.then_inc(at_ready, 1)

                def add(n, i, s):
                    dve.wait_ge(got[s], i * per + per)
                    mine = Own(dve, own, n, 8 if guard else top - 1)
                    here = core.x[:, bass.ds(n * MOVED, MOVED), :]
                    if guard:
                        assert top == 1
                        y = rows[s][0]
                        mine.step(nc.vector.tensor_tensor(y[:], y[:], weight[0][:, bass.ds(n * MOVED, MOVED)].unsqueeze(2).to_broadcast([P, MOVED, D]), ALU.mult))
                        mine.step(nc.vector.memset(safe[:], 0.0))
                        mine.step(nc.vector.tensor_tensor(mask[:], y[:], y[:], ALU.is_equal))
                        hold(dve, passed_v)
                        mine.step(nc.vector.copy_predicated(safe[:], mask[:], y[:]))
                        mine.step(nc.vector.tensor_scalar(y[:], safe[:], 1e4, -1e4, ALU.min, ALU.max))
                        mine.step(nc.vector.tensor_scalar(zero_or_nan[:], safe[:], 0.0, None, ALU.mult))
                        mine.step(nc.vector.tensor_tensor(mask[:], zero_or_nan[:], zero_or_nan[:], ALU.not_equal))
                        hold(dve, passed_v)
                        mine.step(nc.vector.copy_predicated(safe[:], mask[:], y[:]))
                        nc.vector.tensor_tensor(here, here, safe[:], ALU.add).then_inc(added, 1)
                    else:
                        for k in range(top):
                            for j in range(MOVED):
                                t = n * MOVED + j
                                last = nc.vector.scalar_tensor_tensor(core.x[:, t, :], rows[s][k][:, j, :], weight[k][:, bass.ds(t, 1)],
                                                                      core.x[:, t, :], ALU.mult, ALU.add)
                            if k + 1 < top:
                                mine.step(last)
                        last.then_inc(added, 1)
                    mine.end()
                    dve.wait_ge(added, done(n))
                    for j in range(MOVED):
                        nc.vector.bn_stats(core.parts[:, n * MOVED + j, :], core.x[:, n * MOVED + j, :])

                indices(0, 0, 0)
                indices(1, 0, 1)
                with dve.Fori(0, last_i) as i:
                    for s in range(2):
                        add(i * 2 + s, i, s)
                        indices(i * 2 + s + 2, i + 1, s)
                for s in range(2):
                    add(last_i * 2 + s, last_i, s)


def run_experts(nc, core, name, E, Q, HC, gated, wu, wd, bu, bd, weights, weight_loads, expert_of):
    with Stage(nc, name + "_experts") as st:
        g = [st.sb(f"rows{k}", [P, 2, D]) for k in range(2)]
        g_t = [st.sb(f"rows_t{s}", [P, P]) for s in range(2)]
        silu = [st.sb(f"silu{s}", [P, HC * P]) for s in range(2)] if gated else None
        hid = [st.sb(f"hidden{s}", [P, HC * P]) for s in range(2)]
        hid_t = [st.sb(f"hidden_t{s}", [P, HC * P]) for s in range(2)]
        o = [st.sb(f"out{k}", [P, 2, D]) for k in range(2)]
        ps_g = [st.ps(f"ps_rows{s}", [P, 512]) for s in range(2)]
        ps_u = [st.ps(f"ps_up{s}", [P, 512]) for s in range(2)]
        ps_h = [st.ps(f"ps_hidden{s}", [P, 512]) for s in range(2)]
        ps_o = [st.ps(f"ps_out{s}", [P, 512]) for s in range(2)]
        g_loaded = [st.sem(f"rows_loaded{k}") for k in range(2)]
        stored = [st.sem(f"out_stored{k}", 16) for k in range(2)]
        g_t_ps, g_t_ready, up_done, silu_ready, hid_ready, hid_t_ps, hid_t_ready, down_done, o_ready = [
            st.sem(n, CREDIT) for n in ("rows_transposed", "rows_t_ready", "up_done", "silu_ready", "hidden_ready",
                                        "hidden_transposed", "hidden_t_ready", "down_done", "out_ready")]
        def load_experts(eng, i):
            if eng is not nc.tensor and (gated or eng is not nc.vector):
                return [None] * 8
            _, e = nc.values_load_multi_w_load_instructions(
                expert_of[0:1, i if isinstance(i, int) else bass.ds(i, 1), :], engines=(eng.engine,), min_val=0, max_val=E - 1,
                skip_runtime_bounds_check_because="each is a count from 1 to E less 1")
            return e

        def turns(eng, turn):
            def of(experts, s):
                return lambda d: experts[s + 1 + d]

            experts = load_experts(eng, 0)
            for s in range(TURNS):
                turn(s, 0, s, lambda d: 0 <= s + d, of(experts, s))
            with eng.Fori(1, Q // TURNS - 1) as i:
                experts = load_experts(eng, i)
                for s in range(TURNS):
                    turn(i * TURNS + s, i, s, lambda d: True, of(experts, s))
            for i in (Q // TURNS - 1, Q // TURNS):
                experts = load_experts(eng, i)
                for s in range(TURNS if i * TURNS < Q else 1):
                    turn(i * TURNS + s, i, s, lambda d: i * TURNS + s + d < Q, of(experts, s))

        def other(i, s, d):
            return i + (s + d) // TURNS, (s + d) % TURNS

        with st.block() as block:
            @block.sync
            def _(sp):
                def load(n, i, k):
                    sp.dma_start(g[k][:], core.sorted_in[bass.ds(n * P, 2 * P), :].rearrange("(t p) d -> p t d", p=P)).then_inc(g_loaded[k], 16)

                def turn(n, i, s, inside, e):
                    if s % 2 == 0 and inside(4):
                        sp.wait_ge(g_t_ps, done(n + 1))
                        load(n + 4, i + 1, s // 2)
                    if s % 2 == 0 and inside(-1):
                        i1, s1 = other(i, s, -1)
                        sp.wait_ge(o_ready, done(n - 1))
                        sp.dma_start(core.sorted_out[bass.ds((n - 2) * P, 2 * P), :].rearrange("(t p) d -> p t d", p=P),
                                     o[s1 // 2][:]).then_inc(stored[s1 // 2], 16)

                load(0, 0, 0)
                load(2, 0, 1)
                turns(sp, turn)
                for k in range(2):
                    sp.wait_ge(stored[k], 16 * (Q // TURNS + 1))

            @block.tensor
            def _(pe):
                def transpose_rows(n, i, s):
                    pe.wait_ge(g_t_ready, freed(n))
                    pe.wait_ge(g_loaded[s // 2], i * 16 + 16)
                    nc.tensor.transpose(ps_g[s % 2][:, 0:P], g[s // 2][:, s % 2, :], core.ident[:]).then_inc(g_t_ps, 1)

                def up(n, i, s, e):
                    pe.wait_ge(g_t_ready, done(n))
                    pe.wait_ge(hid_ready, freed(n))
                    nc.tensor.matmul(ps_u[s % 2][:], g_t[s % 2][:], wu[:, bass.ds(e * UP, UP)], start=True, stop=True).then_inc(up_done, 1)

                def turn(n, i, s, inside, e):
                    if inside(2):
                        transpose_rows(n + 2, *other(i, s, 2))
                    if inside(1):
                        up(n + 1, *other(i, s, 1), e(1))
                    if inside(0):
                        pe.wait_ge(hid_ready, done(n))
                        pe.wait_ge(hid_t_ready, freed(n))
                        for c in range(HC):
                            last = nc.tensor.transpose(ps_h[s % 2][:, c * P:(c + 1) * P], hid[s % 2][:, c * P:(c + 1) * P], core.ident[:])
                        last.then_inc(hid_t_ps, 1)
                    if inside(-1):
                        i1, s1 = other(i, s, -1)
                        pe.wait_ge(hid_t_ready, done(n - 1))
                        pe.wait_ge(o_ready, freed(n - 1))
                        for c in range(HC):
                            last = nc.tensor.matmul(ps_o[s1 % 2][:, 0:D], hid_t[s1 % 2][:, c * P:(c + 1) * P],
                                                    wd[:, bass.ds(e(-1) * (HC * D) + c * D, D)], start=c == 0, stop=c == HC - 1)
                        last.then_inc(down_done, 1)

                pe.wait_ge(weights, 16 * weight_loads)
                transpose_rows(0, 0, 0)
                transpose_rows(1, 0, 1)
                up(0, 0, 0, load_experts(pe, 0)[1])
                turns(pe, turn)

            @block.scalar
            def _(act):
                def rows_out(n, i, s):
                    act.wait_ge(g_t_ps, done(n))
                    act.wait_ge(up_done, freed(n))
                    nc.scalar.copy(g_t[s % 2][:], ps_g[s % 2][:, 0:P]).then_inc(g_t_ready, 1)

                def gate(n, i, s):
                    if gated:
                        act.wait_ge(up_done, done(n))
                        act.wait_ge(hid_ready, freed(n))
                        nc.scalar.activation(silu[s % 2][:], ps_u[s % 2][:, 0:HC * P], ACT.Silu).then_inc(silu_ready, 1)

                def turn(n, i, s, inside, e):
                    if inside(2):
                        rows_out(n + 2, *other(i, s, 2))
                    if inside(1):
                        gate(n + 1, *other(i, s, 1))
                    if inside(0):
                        act.wait_ge(hid_t_ps, done(n))
                        act.wait_ge(down_done, freed(n))
                        nc.scalar.activation(hid_t[s % 2][:], ps_h[s % 2][:, 0:HC * P], ACT.Copy if gated else ACT.Relu).then_inc(hid_t_ready, 1)

                rows_out(0, 0, 0)
                rows_out(1, 0, 1)
                gate(0, 0, 0)
                turns(act, turn)

            @block.vector
            def _(dve):
                def hidden(n, i, s, e):
                    dve.wait_ge(hid_t_ps, freed(n))
                    if gated:
                        dve.wait_ge(silu_ready, done(n))
                        nc.vector.tensor_tensor(hid[s % 2][:], silu[s % 2][:], ps_u[s % 2][:, HC * P:2 * HC * P], ALU.mult).then_inc(hid_ready, 1)
                    else:
                        dve.wait_ge(up_done, done(n))
                        nc.vector.tensor_tensor(hid[s % 2][:], ps_u[s % 2][:], bu[:, bass.ds(e * UP, UP)], ALU.add).then_inc(hid_ready, 1)

                def turn(n, i, s, inside, e):
                    if inside(1):
                        hidden(n + 1, *other(i, s, 1), e(1))
                    if inside(-1):
                        i1, s1 = other(i, s, -1)
                        dve.wait_ge(down_done, done(n - 1))
                        if s1 % 2 == 0:
                            dve.wait_ge(stored[s1 // 2], i1 * 16 + 16)
                        if gated:
                            nc.vector.tensor_scalar(o[s1 // 2][:, s1 % 2, :], ps_o[s1 % 2][:, 0:D], 1.0, None, ALU.mult).then_inc(o_ready, 1)
                        else:
                            nc.vector.tensor_tensor(o[s1 // 2][:, s1 % 2, :], ps_o[s1 % 2][:, 0:D], bd[:, bass.ds(e(-1) * D, D)], ALU.add).then_inc(o_ready, 1)

                if not gated:
                    dve.wait_ge(weights, 16 * weight_loads)
                hidden(0, 0, 0, load_experts(dve, 0)[1])
                turns(dve, turn)


JOINTS = 25
GROUPS = [list(range(25)), [0, 1, 2, 3, 4, 5, 6, 7, 8], [0, 9, 10, 11, 12, 13, 14], [6, 7, 8, 12, 13, 14], [3, 4, 5, 9, 10, 11]]
QUAD = 32
SHARING = P // QUAD
PACKS = B // SHARING


def group_masks():
    member = np.zeros((len(GROUPS), QUAD), np.float32)
    for g, nodes in enumerate(GROUPS):
        member[g, nodes] = 1
    pairs = np.zeros((len(GROUPS), P, P), np.float32)
    for q in range(SHARING):
        part = slice(q * QUAD, (q + 1) * QUAD)
        pairs[:, part, part] = member[:, :, None] * member[:, None, :]
    return pairs, np.ascontiguousarray(np.tile(member, (1, SHARING)).T)


def grouped_graph_block(nc, core, adj_t, w1, b1, w2, b2, fusion_w, pair_mask, row_mask):
    G, HID = len(GROUPS), w1.shape[2]
    HC = HID // P
    HALF = PACKS // 2
    with Stage(nc, "groups") as st:
        a_t = st.sb("adj_t", [P, PACKS, P])
        a_g = st.sb("group_adj_t", [P, PACKS, P])
        masks = st.sb("pair_mask", [P, G, P])
        rows = st.sb("row_mask", [P, G])
        w1_sb = st.sb("w1", [P, G * HID])
        b1_sb = st.sb("b1", [P, G * HID])
        w2_sb = st.sb("w2", [P, G * HC * D])
        b2_sb = st.sb("b2", [P, G * D])
        fuse = st.sb("fusion", [P, G])
        stat = st.sb("fusion_stat", [P, 2])
        deg = st.sb("degree", [P, PACKS])
        empty = st.sb("empty", [P, PACKS])
        dinv = st.sb("dinv", [P, PACKS])
        y = st.sb("y", [P, PACKS, D])
        ys = st.sb("y_scaled", [P, PACKS, D])
        quad0 = st.sb("quad0", [QUAD, PACKS, D])
        u_t = [st.sb(f"spread_t{h}", [P, HALF * P]) for h in range(2)]
        hid = [st.sb(f"hidden{h}", [P, HALF, HID]) for h in range(2)]
        v_t = [st.sb(f"hidden_spread_t{h}", [P, HALF * HC * P]) for h in range(2)]
        out = st.sb("out", [P, HALF, D])
        fused = st.sb("fused", [P, PACKS, D])
        ps_d = st.ps("ps_degree", [P, 512])
        ps_u = st.ps("ps_spread", [P, 512])
        ps_h = [st.ps(f"ps_hidden{j}", [P, 512]) for j in range(2)]
        ps_v = [st.ps(f"ps_hidden_spread{j}", [P, 512]) for j in range(2)]
        ps_o = st.ps("ps_out", [P, 512])
        cleared, loaded, own, fuse_in, fuse_out = [st.sem(n) for n in ("cleared", "loaded", "vector_steps", "fusion_in", "fusion_exp")]
        a_ready, deg_ps, deg_ready, root_ready, ys_ready = [st.sem(n) for n in (
            "group_adj_ready", "degree_product", "degree_ready", "root_ready", "y_scaled_ready")]
        u_ps, u_ready, h_ps, h_ready, v_ps, v_ready, o_ps = [st.sem(n) for n in (
            "spread_product", "spread_ready", "hidden_product", "hidden_ready", "hidden_spread_product", "hidden_spread_ready", "out_product")]
        with st.block() as block:
            @block.gpsimd
            def _(pool):
                nc.gpsimd.memset(a_t[:], 0.0).then_inc(cleared, 1)
                nc.gpsimd.memset(fused[:], 0.0).then_inc(cleared, 1)

            LOADS = 7 + SHARING
            BEFORE = 6 + 2 * SHARING
            OWN = 4 + 2 + 1 + 2 * 3

            @block.sync
            def _(sp):
                def row(a, n):
                    return a.rearrange("(a n) -> a n", a=1).to_broadcast([P, n])
                sp.dma_start(w1_sb[:].rearrange("p (g f) -> p g f", g=G), w1.rearrange("g d f -> d g f")).then_inc(loaded, 16)
                sp.dma_start(w2_sb[:].rearrange("p (g c f) -> p g c f", g=G, c=HC), w2.rearrange("g (c p) f -> p g c f", p=P)).then_inc(loaded, 16)
                sp.dma_start(b1_sb[:], row(b1.rearrange("g f -> (g f)"), G * HID)).then_inc(loaded, 16)
                sp.dma_start(b2_sb[:], row(b2.rearrange("g f -> (g f)"), G * D)).then_inc(loaded, 16)
                sp.dma_start(fuse[:], row(fusion_w, G)).then_inc(loaded, 16)
                sp.dma_start(masks[:], pair_mask.rearrange("g p n -> p g n")).then_inc(loaded, 16)
                sp.dma_start(rows[:], row_mask).then_inc(loaded, 16)
                sp.wait_ge(cleared, 2)
                for q in range(SHARING):
                    src = adj_t.rearrange("(k q) m n -> q m k n", q=SHARING)[q, 0:JOINTS, :, 0:JOINTS]
                    sp.dma_start(a_t[q * QUAD:q * QUAD + JOINTS, :, q * QUAD:q * QUAD + JOINTS], src).then_inc(loaded, 16)

            @block.tensor
            def _(pe):
                mm = nc.tensor.matmul
                with pe.Fori(0, G) as g:
                    pe.wait_ge(a_ready, g + 1)
                    for k in range(PACKS):
                        last = mm(ps_d[:, k:k + 1], a_g[:, k, :], core.ones[:, 0:1], start=True, stop=True)
                    last.then_inc(deg_ps, 1)
                    pe.wait_ge(ys_ready, g + 1)
                    for h in range(2):
                        if h:
                            pe.wait_ge(u_ready, g * 2 + h)
                        for k in range(HALF):
                            last = mm(ps_u[:, k * P:(k + 1) * P], ys[:, h * HALF + k, :], a_g[:, h * HALF + k, :], start=True, stop=True)
                        last.then_inc(u_ps, 1)
                    for h in range(2):
                        pe.wait_ge(u_ready, g * 2 + h + 1)
                        if h:
                            pe.wait_ge(h_ready, g * 2 + h)
                        for k in range(HALF):
                            last = mm(ps_h[k // 2][:, k % 2 * HID:(k % 2 + 1) * HID], u_t[h][:, k * P:(k + 1) * P],
                                      w1_sb[:, bass.ds(g * HID, HID)], start=True, stop=True)
                        last.then_inc(h_ps, 1)
                    for h in range(2):
                        pe.wait_ge(h_ready, g * 2 + h + 1)
                        if h:
                            pe.wait_ge(v_ready, g * 2 + h)
                        for k in range(HALF):
                            for c in range(HC):
                                last = mm(ps_v[k // 2][:, (k % 2 * HC + c) * P:(k % 2 * HC + c + 1) * P],
                                          hid[h][:, k, c * P:(c + 1) * P], a_g[:, h * HALF + k, :], start=True, stop=True)
                        last.then_inc(v_ps, 1)
                    for h in range(2):
                        pe.wait_ge(v_ready, g * 2 + h + 1)
                        if h:
                            pe.wait_ge(own, g * OWN + (BEFORE + OWN - 5))
                        for k in range(HALF):
                            for c in range(HC):
                                last = mm(ps_o[:, k * D:(k + 1) * D], v_t[h][:, (k * HC + c) * P:(k * HC + c + 1) * P],
                                          w2_sb[:, bass.ds(g * (HC * D) + c * D, D)], start=c == 0, stop=c == HC - 1)
                        last.then_inc(o_ps, 1)

            @block.scalar
            def _(act):
                act.wait_ge(fuse_in, 1)
                nc.scalar.activation(fuse[:], fuse[:], ACT.Exp).then_inc(fuse_out, 1)
                with act.Fori(0, G) as g:
                    act.wait_ge(deg_ready, g + 1)
                    nc.scalar.activation(deg[:], deg[:], ACT.Sqrt).then_inc(root_ready, 1)
                    for h in range(2):
                        act.wait_ge(u_ps, g * 2 + h + 1)
                        nc.scalar.copy(u_t[h][:], ps_u[:]).then_inc(u_ready, 1)
                    for h in range(2):
                        act.wait_ge(v_ps, g * 2 + h + 1)
                        for j in range(2):
                            last = nc.scalar.copy(v_t[h][:, j * 512:(j + 1) * 512], ps_v[j][:])
                        last.then_inc(v_ready, 1)


            @block.vector
            def _(dve):
                v = nc.vector
                dve.wait_ge(loaded, 16 * LOADS)
                pre = Own(dve, own, 0, 0)
                pre.step(v.reduce_max(stat[:, 0:1], fuse[:], AXX))
                v.tensor_scalar(fuse[:], fuse[:], stat[:, 0:1], None, ALU.subtract).then_inc(fuse_in, 1)
                dve.wait_ge(fuse_out, 1)
                pre.step(v.reduce_sum(stat[:, 1:2], fuse[:], AXX))
                pre.step(v.reciprocal(stat[:, 1:2], stat[:, 1:2]))
                pre.step(v.tensor_scalar(fuse[:], fuse[:], stat[:, 1:2], None, ALU.mult))
                pre.step(v.tensor_tensor(fuse[:], fuse[:], rows[:], ALU.mult))
                pre.step(v.tensor_tensor(a_t[:], a_t[:], core.ident[:].unsqueeze(1).to_broadcast([P, PACKS, P]), ALU.add))
                for q in range(SHARING):
                    at = slice(q * HALVES, TILES, SHARING * HALVES)
                    pre.step(v.tensor_tensor(quad0[:], core.x[0:QUAD, at, :],
                                             core.mean[0:QUAD, at].unsqueeze(2).to_broadcast([QUAD, PACKS, D]), ALU.subtract))
                    pre.step(v.tensor_tensor(y[q * QUAD:(q + 1) * QUAD, :, :], quad0[:],
                                             core.rstd[0:QUAD, at].unsqueeze(2).to_broadcast([QUAD, PACKS, D]), ALU.mult))
                base = pre.k
                assert base == BEFORE
                with dve.Fori(0, G) as g:
                    mine = Own(dve, own, g, OWN)
                    mine.base = g * OWN + base
                    v.tensor_tensor(a_g[:], a_t[:], masks[:, bass.ds(g, 1), :].to_broadcast([P, PACKS, P]), ALU.mult).then_inc(a_ready, 1)
                    dve.wait_ge(deg_ps, g + 1)
                    mine.step(v.tensor_scalar(empty[:], ps_d[:, 0:PACKS], 0.0, None, ALU.is_equal))
                    v.tensor_tensor(deg[:], ps_d[:, 0:PACKS], empty[:], ALU.add).then_inc(deg_ready, 1)
                    mine.step(v.tensor_scalar(empty[:], empty[:], -1.0, 1.0, ALU.mult, ALU.add))
                    dve.wait_ge(root_ready, g + 1)
                    mine.step(v.reciprocal(dinv[:], deg[:]))
                    mine.step(v.tensor_tensor(dinv[:], dinv[:], empty[:], ALU.mult))
                    v.tensor_tensor(ys[:], y[:], dinv[:].unsqueeze(2).to_broadcast([P, PACKS, D]), ALU.mult).then_inc(ys_ready, 1)
                    for h in range(2):
                        dve.wait_ge(h_ps, g * 2 + h + 1)
                        for k in range(HALF):
                            last = v.scalar_tensor_tensor(hid[h][:, k, :], ps_h[k // 2][:, k % 2 * HID:(k % 2 + 1) * HID],
                                                          dinv[:, h * HALF + k:h * HALF + k + 1],
                                                          b1_sb[:, bass.ds(g * HID, HID)], ALU.mult, ALU.add)
                        mine.step(last)
                        for k in range(HALF):
                            last = v.tensor_scalar(hid[h][:, k, :], hid[h][:, k, :], 0.0, dinv[:, h * HALF + k:h * HALF + k + 1], ALU.max, ALU.mult)
                        last.then_inc(h_ready, 1)
                    mine.step(v.tensor_copy(stat[:, 0:1], fuse[:, bass.ds(g, 1)]))
                    for h in range(2):
                        dve.wait_ge(o_ps, g * 2 + h + 1)
                        for k in range(HALF):
                            last = v.scalar_tensor_tensor(out[:, k, :], ps_o[:, k * D:(k + 1) * D], dinv[:, h * HALF + k:h * HALF + k + 1],
                                                          b2_sb[:, bass.ds(g * D, D)], ALU.mult, ALU.add)
                        mine.step(last)
                        mine.step(v.tensor_scalar(out[:], out[:], 0.0, stat[:, 0:1], ALU.max, ALU.mult))
                        part = fused[:, h * HALF:(h + 1) * HALF, :]
                        mine.step(v.tensor_tensor(part, part, out[:], ALU.add))
                    mine.end()
                post = Own(dve, own, 0, 0)
                post.base = base + G * OWN
                for q in range(SHARING):
                    at = slice(q * HALVES, TILES, SHARING * HALVES)
                    post.step(v.tensor_copy(quad0[:], fused[q * QUAD:(q + 1) * QUAD, :, :]))
                    post.step(v.tensor_tensor(core.x[0:QUAD, at, :], core.x[0:QUAD, at, :], quad0[:], ALU.add))


S = 16
BLOCKS = P // S
QUARTER = P // B


def start_adjacency(nc, st, adj):
    quarters = [[st.sb(f"adj{j}{i}", [P, B, P]) for i in range(HALVES)] for j in range(HALVES)]
    loaded = st.sem("adj_loaded")
    with st.block() as block:
        @block.sync
        def _(sp):
            for j in range(HALVES):
                for i in range(HALVES):
                    sp.dma_start(quarters[j][i][:], adj[:, j * P:(j + 1) * P, i * P:(i + 1) * P].rearrange("b p n -> p b n")).then_inc(loaded, 16)
    return quarters, loaded


def recurrent_block(nc, core, quarters, loaded, w_ioux_t, w_iouh_t, b_ioux, b_iouh, w_coux_t, w_couh_t, b_coux, b_couh):
    with Stage(nc, "recur") as keep:
        near_adj = [quarters[h][h] for h in range(HALVES)]
        cross_adj = quarters[0][1]
        y_t = keep.sb("y_t", [P, N, B])
        base = keep.sb("base", [P, N, B])
        recurrent_base(nc, core, quarters, loaded, y_t, base)
        changes = quarters[1][0]
        for half in range(HALVES):
            scan_half(nc, core, half, near_adj[half], y_t, base, changes,
                      w_ioux_t, w_iouh_t, b_ioux, b_iouh, w_coux_t, w_couh_t, b_coux, b_couh)
            if half == 0:
                carry_changes(nc, core, cross_adj, base, changes)


def recurrent_base(nc, core, part, loaded, y_t, base):
    with Stage(nc, "recur_in") as st:
        y = [st.sb(f"y{s}", [P, HALVES, D]) for s in range(2)]
        degree = [st.sb(f"degree{k}", [P, HALVES, B]) for k in range(2)]
        empty = st.sb("empty", [P, HALVES, B])
        inv = st.sb("inv", [P, HALVES, B])
        diagonal = [st.sb(f"diagonal{s}", [P, HALVES, P]) for s in range(2)]
        scale = [st.sb(f"scale{s}", [P, N]) for s in range(2)]
        ps_s = [st.ps(f"ps_scale{s}", [P, 512]) for s in range(2)]
        ps_y = [st.ps(f"ps_y{s}", [P, 512]) for s in range(2)]
        ps_b = [st.ps(f"ps_base{s}", [P, 512]) for s in range(2)]
        inv_ready = st.sem("inv_ready")
        y_ready, x_added, y_ps, y_t_kept, diagonal_ready, scale_ps, base_ps, scaled = [st.sem(n, CREDIT) for n in (
            "y_ready", "x_added", "y_transposed", "y_t_kept", "diagonal_ready", "scale_spread", "base_product", "adj_scaled")]
        own, own_turn, inv_done, passed, passed_a = st.sem("vector_first_steps"), st.sem("vector_steps"), st.sem("inv_done"), st.sem("pool_passed"), st.sem("scalar_passed")
        with st.block() as block:
            @block.tensor
            def _(pe):
                pe.wait_ge(loaded, 64)
                with pe.Fori(0, B // 2) as i:
                    for s in range(2):
                        n = i * 2 + s
                        pe.wait_ge(y_t_kept, freed(n))
                        pe.wait_ge(y_ready, done(n))
                        for k in range(HALVES):
                            last = nc.tensor.transpose(ps_y[s][:, k * P:(k + 1) * P], y[s][:, k, :], core.ident[:])
                        last.then_inc(y_ps, 1)
                        pe.wait_ge(scaled, freed(n))
                        pe.wait_ge(diagonal_ready, done(n))
                        nc.tensor.matmul(ps_s[s][:, 0:N], core.ones[:], diagonal[s][:].rearrange("p h i -> p (h i)"), start=True, stop=True).then_inc(scale_ps, 1)
                        for k in range(HALVES):
                            for j in range(HALVES):
                                last = nc.tensor.matmul(ps_b[s][:, k * P:(k + 1) * P], y[s][:, j, :], part[j][k][:, n, :],
                                                        start=j == 0, stop=j == HALVES - 1)
                        last.then_inc(base_ps, 1)

            @block.gpsimd
            def _(pool):
                with pool.Fori(0, B // 2) as i:
                    for s in range(2):
                        n = i * 2 + s
                        pool.wait_ge(y_ready, done(n))
                        hold(pool, passed)
                        here = core.x[:, bass.ds(n * HALVES, HALVES), :]
                        nc.gpsimd.tensor_tensor(here, here, y[s][:], ALU.add).then_inc(x_added, 1)

            @block.scalar
            def _(act):
                act.wait_ge(inv_ready, 1)
                with act.Fori(0, B // 2) as i:
                    for s in range(2):
                        n = i * 2 + s
                        act.wait_ge(scale_ps, freed(n))
                        hold(act, passed_a)
                        for k in range(HALVES):
                            last = nc.scalar.activation(diagonal[s][:, k, :], core.ident[:], ACT.Copy, scale=inv[:, k, bass.ds(n, 1)])
                        last.then_inc(diagonal_ready, 1)
                    for s in range(2):
                        n = i * 2 + s
                        act.wait_ge(y_ps, done(n))
                        hold(act, passed_a)
                        nc.scalar.activation(y_t[:, :, n], ps_y[s][:, 0:N], ACT.Copy).then_inc(y_t_kept, 1)

            @block.vector
            def _(dve):
                v = nc.vector
                first = Own(dve, own, 0, 4)
                for j in range(HALVES):
                    dve.wait_ge(loaded, 64)
                    for i in range(HALVES):
                        last = v.tensor_reduce(degree[i][:, j, :], part[j][i][:], AXX, ALU.add)
                first.step(last)
                first.step(v.tensor_tensor(degree[0][:], degree[0][:], degree[1][:], ALU.add))
                first.step(v.tensor_scalar(empty[:], degree[0][:], 0.0, None, ALU.is_equal))
                first.step(v.tensor_tensor(inv[:], degree[0][:], empty[:], ALU.add))
                v.reciprocal(inv[:], inv[:]).then_inc(inv_done, 1)
                dve.wait_ge(inv_done, 1)
                v.scalar_tensor_tensor(inv[:], empty[:], 0.0, inv[:], ALU.is_equal, ALU.mult).then_inc(inv_ready, 1)
                with dve.Fori(0, B // 2) as i:
                    mine = Own(dve, own_turn, i, 2)
                    for s in range(2):
                        n = i * 2 + s
                        dve.wait_ge(base_ps, freed(n))
                        dve.wait_ge(x_added, freed(n))
                        for k in range(HALVES):
                            t = n * 2 + k
                            last = v.tensor_scalar(y[s][:, k, :], core.x[:, t, :], core.mean[:, bass.ds(t, 1)],
                                                   core.rstd[:, bass.ds(t, 1)], ALU.subtract, ALU.mult)
                        last.then_inc(y_ready, 1)
                    for s in range(2):
                        n = i * 2 + s
                        dve.wait_ge(scale_ps, done(n))
                        mine.step(v.tensor_scalar(scale[s][:], ps_s[s][:, 0:N], 1.0, None, ALU.mult))
                        dve.wait_ge(base_ps, done(n))
                        v.tensor_tensor(base[:, :, n], ps_b[s][:, 0:N], scale[s][:], ALU.mult)
                        for a, k in ((part[0][0], 0), (part[0][1], 1), (part[1][1], 1)):
                            last = v.tensor_tensor(a[:, n, :], a[:, n, :], scale[s][:, k * P:(k + 1) * P], ALU.mult)
                        last.then_inc(scaled, 1)
                    mine.end()


def carry_changes(nc, core, cross_adj, base, changes):
    FOUR = 512 // P
    with Stage(nc, "recur_carry") as st:
        ps = [st.ps(f"ps_part{s}", [P, 512]) for s in range(2)]
        multiplied, added = [st.sem(n, CREDIT) for n in ("part_product", "part_added")]
        with st.block() as block:
            @block.tensor
            def _(pe):
                for q in range(B // FOUR):
                    pe.wait_ge(added, freed(q))
                    for k in range(FOUR):
                        b = q * FOUR + k
                        last = nc.tensor.matmul(ps[q % 2][:, k * P:(k + 1) * P], changes[:, b, :], cross_adj[:, b, :], start=True, stop=True)
                    last.then_inc(multiplied, 1)

            @block.vector
            def _(dve):
                for q in range(B // FOUR):
                    dve.wait_ge(multiplied, done(q))
                    here = base[:, P:N, q * FOUR:(q + 1) * FOUR]
                    nc.vector.tensor_tensor(here, here, ps[q % 2][:].rearrange("p (b i) -> p i b", b=FOUR), ALU.add).then_inc(added, 1)


def scan_half(nc, core, half, adj, y_t, base, changes, w_ioux_t, w_iouh_t, b_ioux, b_iouh, w_coux_t, w_couh_t, b_coux, b_couh):
    HALF_S = S // 2
    GROUPS = S // QUARTER
    MOVES = 16 * GROUPS
    EARLIER = {2: (0, 1), 3: (0, 1), 4: (0, 2), 5: (0, 2), 6: (1, 3), 7: (1, 3), 8: (0, 3), 9: (0, 3), 10: (0, 4), 11: (0, 4), 12: (0, 4)}
    assert sum(a + b for a, b in EARLIER.values()) == B
    with Stage(nc, f"recur_scan{half}") as st:
        wx = st.sb("wx", [P, 3, P])
        wh = st.sb("wh", [P, 3, P])
        bias = st.sb("bias", [P, 2, 3])
        same_graph = st.sb("same_graph", [P, B])
        pick = [st.sb(f"pick{p}", [P, S]) for p in range(2)]
        sums = [st.sb(f"sums{p}", [P, S, B]) for p in range(2)]
        delta = [st.sb(f"delta{p}", [P, S, B]) for p in range(2)]
        delta_t = [st.sb(f"delta_t{p}", [P, GROUPS, D]) for p in range(2)]
        rows = [st.sb(f"adj_rows{p}", [P, GROUPS, S]) for p in range(2)]
        spread_adj = st.sb("adj_spread", [P, GROUPS, S, B])
        r, xr, cand, keep_part, lag, minus_slope, offset, minus_fresh = [st.sb(n, [P, B]) for n in (
            "reset", "reset_sum", "candidate", "kept", "kept_minus_old", "minus_slope", "offset", "minus_fresh")]
        z = [st.sb(f"update{k}", [P, B]) for k in range(2)]
        near = st.sb("near", [P, B])
        far = st.sb("far", [P, S, B])
        ps_rc = [st.ps(f"ps_reset_candidate{k}", [P, 2, HALF_S, B]) for k in range(2)]
        ps_z = [st.ps(f"ps_update{k}", [P, 512]) for k in range(2)]
        ps_coef = [st.ps(f"ps_coefs{k}", [P, 512]) for k in range(2)]
        ps_sum = st.ps("ps_sums", [P, 512])
        ps_tr = st.ps("ps_delta_t", [P, 512])
        loaded, copied, own, b_ready, consts = [st.sem(n) for n in ("loaded", "adj_copied", "vector_steps", "bias_ready", "constants_ready")]
        rows_loaded = [st.sem(f"adj_rows_loaded{p}") for p in range(2)]
        node_sum, r_ps, z_ps, r_ready, z_ready, xr_ready, cand_ps, cand_ready, spread = [st.sem(n) for n in (
            "node_sum_ready", "reset_product", "update_product", "reset_ready", "update_ready", "reset_sum_ready",
            "candidate_product", "candidate_ready", "coefs_used")]
        delta_ready, tr_ps, tr_ready, earlier_ps, sums_taken, pick_ready = [st.sem(n) for n in (
            "delta_ready", "delta_transposed", "delta_t_ready", "earlier_changes_product", "sums_taken", "pick_ready")]
        coef_ps = st.sem("coefs_product", 2 * (S - 1))
        pushed = st.sem("delta_product", GROUPS)
        spread_ready = st.sem("adj_spread_ready", 2 * GROUPS)
        moved = st.sem("changes_moved", 2 * MOVES)
        passed = st.sem("pool_passed")

        def following(i, p):
            return i * 2 + 1 if p == 0 else ((i + 1) % (BLOCKS // 2)) * 2

        with st.block() as block:
            @block.sync
            def _(sp):
                col = lambda a, n: a.rearrange("(n p) -> p n", p=P)
                sp.dma_start(core.adj_rows.rearrange("(p b) i -> p b i", b=B), adj[:]).then_inc(copied, 16)
                sp.dma_start(wx[:, 0:2, :], w_ioux_t.rearrange("d (g f) -> d g f", g=2)).then_inc(loaded, 16)
                sp.dma_start(wh[:, 0:2, :], w_iouh_t.rearrange("d (g f) -> d g f", g=2)).then_inc(loaded, 16)
                sp.dma_start(wx[:, 2, :], w_coux_t).then_inc(loaded, 16)
                sp.dma_start(wh[:, 2, :], w_couh_t).then_inc(loaded, 16)
                with nc.allow_non_contiguous_dma("six columns of bias"):
                    sp.dma_start(bias[:, 0, 0:2], col(b_ioux, 2)).then_inc(loaded, 16)
                    sp.dma_start(bias[:, 1, 0:2], col(b_iouh, 2)).then_inc(loaded, 16)
                    sp.dma_start(bias[:, 0, 2:3], col(b_coux, 1)).then_inc(loaded, 16)
                    sp.dma_start(bias[:, 1, 2:3], col(b_couh, 1)).then_inc(loaded, 16)
                sp.wait_ge(copied, 16)
                for n in range(BLOCKS):
                    p = n % 2
                    sp.wait_ge(spread_ready, n * GROUPS + GROUPS)
                    sp.dma_start(rows[p][:], core.adj_rows[n * S * B:(n + 1) * S * B, (n + 1) % BLOCKS * S:(n + 1) % BLOCKS * S + S]
                                 .rearrange("(g p) i -> p g i", p=P)).then_inc(rows_loaded[p], 16)
                    sp.wait_ge(earlier_ps, n + 1)
                    sp.wait_ge(tr_ready, n * GROUPS + GROUPS)
                    for g in range(GROUPS):
                        sp.dma_start(changes[n * S + g * QUARTER:n * S + (g + 1) * QUARTER, :, :], delta_t[p][:, g, :]).then_inc(moved, 16)

            @block.gpsimd
            def _(pool):
                nc.gpsimd.memset(changes[:], 0.0).then_inc(consts, 1)
                pool.wait_ge(consts, 2)
                with pool.Fori(0, BLOCKS // 2) as i:
                    for p in range(2):
                        n = i * 2 + p
                        pool.wait_ge(coef_ps, n * (S - 1) + S - 1)
                        hold(pool, passed)
                        nc.gpsimd.tensor_copy(pick[p][:], core.ident[:, bass.ds(n * S, S)]).then_inc(pick_ready, 1)
                        pool.wait_ge(rows_loaded[p], i * 16 + 16)
                        for g in range(GROUPS):
                            pool.wait_ge(pushed, n * GROUPS + g + 1)
                            hold(pool, passed)
                            nc.gpsimd.tensor_tensor(spread_adj[:, g, :, :], rows[p][:, g, :].unsqueeze(2).to_broadcast([P, S, B]),
                                                    same_graph[:].unsqueeze(1).to_broadcast([P, S, B]), ALU.mult).then_inc(spread_ready, 1)

                nc.gpsimd.tensor_copy(pick[0][:], core.ident[:, 0:S]).then_inc(pick_ready, 1)

            @block.tensor
            def _(pe):
                def mm(out, lhs, rhs, start=False, stop=False):
                    return nc.tensor.matmul(out, lhs, rhs, start=start, stop=stop, skip_group_check=True)

                def own_part(n, k, piece):
                    gate, q = (0, 0, 2, 2, 1, 1)[piece], piece % 2
                    nodes = slice(q * QUARTER, (q + 1) * QUARTER)
                    rhs = y_t[:, bass.ds(n * S + (half * P + k * HALF_S + q * QUARTER), QUARTER), :]
                    if gate == 1:
                        mm(ps_z[k][:, q * P:(q + 1) * P], wx[:, 1, :], rhs, start=piece == 4)
                    else:
                        mm(ps_rc[k][:, gate // 2, nodes, :], wx[:, gate, :], rhs, start=piece == 0)

                def coefs(n, p, u, before):
                    later = S - 1 - u
                    if before is not None:
                        pe.wait_ge(spread, before)
                    rhs = adj[:, :, bass.ds(n * S + (u + 1), later)].rearrange("p b i -> p i b")
                    mm(ps_coef[u % 2][:, 0:later * B], pick[p][:, u:u + 1].to_broadcast([P, P]), rhs, start=True, stop=True).then_inc(coef_ps, 1)

                def transpose_delta(n, p, g):
                    pe.wait_ge(delta_ready, n * GROUPS + g + 1)
                    nc.tensor.transpose(ps_tr[:, g * P:(g + 1) * P], delta[p][:, g * QUARTER:(g + 1) * QUARTER, :].rearrange("p i b -> p (i b)"),
                                        core.ident[:]).then_inc(tr_ps, 1)

                def push(n, p, g):
                    pe.wait_ge(spread_ready, n * GROUPS + g + 1 + 2 * GROUPS)
                    pe.wait_ge(tr_ready, n * GROUPS + g + 1)
                    return mm(ps_sum[:], delta_t[p][:, g, :], spread_adj[:, g, :, :].rearrange("p i b -> p (i b)"), stop=g == GROUPS - 1)

                pe.wait_ge(loaded, 128)
                for piece in range(6):
                    own_part(0, 0, piece)
                pe.wait_ge(pick_ready, 1)
                coefs(0, 0, 0, None)
                with pe.Fori(0, BLOCKS // 2) as i:
                    for p in range(2):
                        n = i * 2 + p
                        after = following(i, p)
                        graphs = iter(range(B))

                        def earlier(count):
                            for _ in range(count):
                                g = next(graphs)
                                last = mm(ps_sum[:, g:(S - 1) * B + g + 1:B], changes[:, g, :], adj[:, g, bass.ds(after * S, S)], start=g == 0)
                                if g == B - 1:
                                    last.then_inc(earlier_ps, 1)

                        for u in range(S):
                            t = n * S + u
                            pe.wait_ge(node_sum, t + 1)
                            part, v = ps_rc[u // HALF_S], u % HALF_S
                            mm(part[:, 0, v, :], wh[:, 0, :], sums[p][:, u, :]).then_inc(r_ps, 1)
                            mm(ps_z[u // HALF_S][:, v * B:(v + 1) * B], wh[:, 1, :], sums[p][:, u, :]).then_inc(z_ps, 1)
                            if u < 6:
                                own_part(n, 1, u)
                            elif HALF_S <= u < HALF_S + 6:
                                own_part(after, 0, u - HALF_S)
                            if u in EARLIER:
                                earlier(EARLIER[u][0])
                            pe.wait_ge(xr_ready, t + 1)
                            mm(part[:, 1, v, :], wh[:, 2, :], xr[:]).then_inc(cand_ps, 1)
                            if u + 1 < S - 1:
                                coefs(n, p, u + 1, n * (S - 1) + u if u >= 1 else None)
                            if u == S - 1:
                                pe.wait_ge(pick_ready, n + 2)
                                coefs(after, 1 - p, 0, n * (S - 1) + S - 1)
                            if u == min(EARLIER):
                                pe.wait_ge(consts, 2)
                                pe.wait_ge(moved, n * MOVES + 2 * MOVES)
                                pe.wait_ge(sums_taken, n + 1)
                            if u in EARLIER:
                                earlier(EARLIER[u][1])
                            if u % QUARTER == 1 and u > QUARTER:
                                transpose_delta(n, p, u // QUARTER - 1)
                            if u > S - GROUPS:
                                push(n, p, u - (S - GROUPS + 1)).then_inc(pushed, 1)
                        transpose_delta(n, p, GROUPS - 1)
                        push(n, p, GROUPS - 1).then_inc(pushed, 1)

            @block.scalar
            def _(act):
                a = nc.scalar.activation
                act.wait_ge(b_ready, 1)
                with act.Fori(0, BLOCKS // 2) as i:
                    for p in range(2):
                        for u in range(S):
                            t = (i * 2 + p) * S + u
                            part, v = ps_rc[u // HALF_S], u % HALF_S
                            act.wait_ge(r_ps, t + 1)
                            a(r[:], part[:, 0, v, :], ACT.Sigmoid, bias=bias[:, 0, 0:1]).then_inc(r_ready, 1)
                            act.wait_ge(z_ps, t + 1)
                            a(z[u % 2][:], ps_z[u // HALF_S][:, v * B:(v + 1) * B], ACT.Sigmoid, bias=bias[:, 0, 1:2]).then_inc(z_ready, 1)
                            act.wait_ge(cand_ps, t + 1)
                            a(cand[:], part[:, 1, v, :], ACT.Tanh, bias=bias[:, 0, 2:3]).then_inc(cand_ready, 1)

            @block.vector
            def _(dve):
                v = nc.vector
                v.tensor_reduce(same_graph[:], core.ident[:].rearrange("p (j b) -> p b j", b=B), AXX, ALU.add).then_inc(consts, 1)
                v.tensor_scalar(sums[0][:], base[:, half * P:half * P + S, :], 1.0, None, ALU.mult).then_inc(node_sum, 1)
                v.engine_nop().then_inc(sums_taken, 1)
                dve.wait_ge(loaded, 128)
                v.tensor_tensor(bias[:, 0, :], bias[:, 0, :], bias[:, 1, :], ALU.add).then_inc(b_ready, 1)
                dve.wait_ge(node_sum, 1)
                per = S * 3 + (S - 1) * 4 + (S - 2) * 2 - (GROUPS - 1)
                with dve.Fori(0, BLOCKS // 2) as i:
                    for p in range(2):
                        n = i * 2 + p
                        mine = Own(dve, own, n, per)

                        def keep_delta_t(g):
                            dve.wait_ge(tr_ps, n * GROUPS + g + 1)
                            if g == 0:
                                dve.wait_ge(moved, n * MOVES + MOVES)
                            v.tensor_scalar(delta_t[p][:, g, :], ps_tr[:, g * P:(g + 1) * P], 1.0, None, ALU.mult).then_inc(tr_ready, 1)

                        for u in range(S):
                            t = n * S + u
                            later = S - 1 - u
                            coef = ps_coef[u % 2]
                            dve.wait_ge(r_ready, t + 1)
                            v.tensor_tensor(xr[:], sums[p][:, u, :], r[:], ALU.mult).then_inc(xr_ready, 1)
                            dve.wait_ge(z_ready, t + 1)
                            mine.step(v.tensor_tensor(keep_part[:], sums[p][:, u, :], z[u % 2][:], ALU.mult))
                            mine.mark(v.tensor_tensor(lag[:], keep_part[:], y_t[:, half * P + t, :], ALU.subtract))
                            if later:
                                dve.wait_ge(coef_ps, n * (S - 1) + u + 1 + 2 * (S - 1))
                                mine.step(v.scalar_tensor_tensor(minus_slope[:], z[u % 2][:], 1.0, coef[:, 0:B], ALU.subtract, ALU.mult))
                                mine.step(v.tensor_tensor(near[:], lag[:], coef[:, 0:B], ALU.mult))
                                mine.step(v.tensor_tensor(offset[:], sums[p][:, u + 1, :], near[:], ALU.add))
                            dve.wait_ge(cand_ready, t + 1)
                            if later:
                                mine.step(v.tensor_tensor(near[:], minus_slope[:], cand[:], ALU.mult))
                                v.tensor_tensor(sums[p][:, u + 1, :], offset[:], near[:], ALU.subtract).then_inc(node_sum, 1)
                            else:
                                mine.join()
                            mine.step(v.scalar_tensor_tensor(minus_fresh[:], z[u % 2][:], 1.0, cand[:], ALU.subtract, ALU.mult))
                            last = v.tensor_tensor(delta[p][:, u, :], lag[:], minus_fresh[:], ALU.subtract)
                            if u % QUARTER == QUARTER - 1:
                                last.then_inc(delta_ready, 1)
                            if later > 1:
                                if u % QUARTER == QUARTER - 1:
                                    dve.wait_ge(delta_ready, n * GROUPS + u // QUARTER + 1)
                                else:
                                    mine.step(last)
                                v.tensor_tensor(far[:, u + 2:, :], coef[:, B:later * B].rearrange("p (i b) -> p i b", b=B),
                                                delta[p][:, u, :].unsqueeze(1).to_broadcast([P, later - 1, B]), ALU.mult).then_inc(spread, 1)
                                dve.wait_ge(spread, n * (S - 1) + u + 1)
                                mine.mark(v.tensor_tensor(sums[p][:, u + 2:, :], sums[p][:, u + 2:, :], far[:, u + 2:, :], ALU.add))
                            elif later == 1:
                                v.engine_nop().then_inc(spread, 1)
                            if u % QUARTER == 2 and u > QUARTER:
                                keep_delta_t(u // QUARTER - 1)
                        mine.end()
                        keep_delta_t(GROUPS - 1)
                        dve.wait_ge(pushed, n * GROUPS + 2 * GROUPS)
                        first = following(i, p) * S + half * P
                        ps = ps_sum[:].rearrange("p (i b) -> p i b", b=B)
                        v.tensor_tensor(sums[1 - p][:, 0, :], ps[:, 0, :], base[:, first, :], ALU.add).then_inc(node_sum, 1)
                        v.tensor_tensor(sums[1 - p][:, 1:, :], ps[:, 1:, :], base[:, bass.ds(first + 1, S - 1), :], ALU.add).then_inc(sums_taken, 1)
                        dve.wait_ge(node_sum, n * S + S + 1)
                        dve.wait_ge(sums_taken, n + 2)
                dve.wait_ge(moved, BLOCKS * MOVES + 2 * MOVES)
                part = core.x[:, half::2, :]
                v.tensor_tensor(part, part, changes[:], ALU.add)


def attention_block(nc, core, adj, w, w_t, a2, gamma, beta):
    SLOPE = 0.2
    MASKED = -9000000000000000.0
    with Stage(nc, "attend") as keep:
        attended = keep.sb("attended", [P, TILES, D])
        with Stage(nc, "attention") as st:
            w_sb = st.sb("w", [P, D + 4])
            w_t_sb = st.sb("w_t", [P, D])
            a_sb = st.sb("a", [P, 2])
            wa2 = st.sb("wa2", [P, P])
            adj_sb = [st.sb(f"adj{s}", [P, HALVES, N]) for s in range(2)]
            allow = [st.sb(f"allow{s}", [P, HALVES, N]) for s in range(2)]
            y = [st.sb(f"y{s}", [P, HALVES, D]) for s in range(2)]
            y_t = [st.sb(f"y_t{s}", [P, N]) for s in range(2)]
            wh = [st.sb(f"wh{s}", [P, HALVES, D + 2]) for s in range(2)]
            e = [st.sb(f"e{s}", [P, HALVES, N]) for s in range(2)]
            low = [st.sb(f"minus_max{s}", [P, HALVES]) for s in range(2)]
            total = [st.sb(f"total{s}", [P, HALVES]) for s in range(2)]
            p = [st.sb(f"p{s}", [P, HALVES, N]) for s in range(2)]
            p_t = [st.sb(f"p_t{s}", [P, HALVES, N]) for s in range(2)]
            ps_y = [st.ps(f"ps_y{s}", [P, 512]) for s in range(2)]
            ps_w = [st.ps(f"ps_w{s}", [P, 512]) for s in range(2)]
            ps_s = [st.ps(f"ps_s{s}", [P, 512]) for s in range(2)]
            ps_p = [st.ps(f"ps_p{s}", [P, 512]) for s in range(2)]
            weights, wa_ps, wa_ready, first, own, passed, passed_a = [st.sem(n) for n in (
                "weights_loaded", "wa_product", "wa_ready", "first_step", "vector_steps", "pool_passed", "scalar_passed")]
            inv_ready, raw_ready = st.sem("total_inverted", CREDIT), st.sem("scores_ready", CREDIT)
            adj_loaded = [st.sem(f"adj_loaded{s}") for s in range(2)]
            y_ready, y_ps, y_t_ready, wh_ps, wh_ready, s2_ps, allow_ready, e_ready, p_ready, p_ps, p_t_ready, out_ps, out_ready = [
                st.sem(n, CREDIT) for n in ("y_ready", "y_transposed", "y_t_ready", "wh_product", "wh_ready", "s2_product",
                                            "allow_ready", "e_ready", "p_ready", "p_transposed", "p_t_ready", "out_product", "out_ready")]
            with st.block() as block:
                @block.sync
                def _(sp):
                    sp.dma_start(w_sb[:, 0:D], w).then_inc(weights, 16)
                    sp.dma_start(w_t_sb[:], w_t).then_inc(weights, 16)
                    sp.dma_start(a_sb[:], a2).then_inc(weights, 16)
                    with sp.Fori(0, B // 2) as i:
                        for s in range(2):
                            sp.wait_ge(allow_ready, freed(i * 2 + s))
                            sp.dma_start(adj_sb[s][:], adj[i * 2 + s, :, :].rearrange("(h p) n -> p h n", p=P)).then_inc(adj_loaded[s], 16)

                @block.gpsimd
                def _(pool):
                    with pool.Fori(0, B // 2) as i:
                        for s in range(2):
                            pool.wait_ge(adj_loaded[s], i * 16 + 16)
                            pool.wait_ge(e_ready, freed(i * 2 + s))
                            hold(pool, passed)
                            nc.gpsimd.tensor_scalar(allow[s][:], adj_sb[s][:], 0.0, -2.0 * MASKED, ALU.is_gt, ALU.mult).then_inc(allow_ready, 1)

                def loop(eng, turn):
                    with eng.Fori(0, B // 2 - 1) as i:
                        turn(i, True)
                    turn(B // 2 - 1, False)

                @block.tensor
                def _(pe):
                    mm = nc.tensor.matmul

                    def transposes(i):
                        for s in range(2):
                            pe.wait_ge(y_t_ready, freed(i * 2 + s))
                            pe.wait_ge(y_ready, done(i * 2 + s))
                            for h in range(HALVES):
                                last = nc.tensor.transpose(ps_y[s][:, h * P:(h + 1) * P], y[s][:, h, :], core.ident[:])
                            last.then_inc(y_ps, 1)

                    def turn(i, more):
                        for s in range(2):
                            pe.wait_ge(y_t_ready, done(i * 2 + s))
                            pe.wait_ge(wh_ready, freed(i * 2 + s))
                            for h in range(HALVES):
                                last = mm(ps_w[s][:, h * (D + 2):(h + 1) * (D + 2)], y_t[s][:, h * P:(h + 1) * P], w_sb[:, 0:D + 2], start=True, stop=True)
                            last.then_inc(wh_ps, 1)
                            pe.wait_ge(e_ready, freed(i * 2 + s))
                            pe.wait_ge(out_ready, freed(i * 2 + s))
                            mm(ps_s[s][:, 0:N], wa2[:], y_t[s][:], start=True, stop=True).then_inc(s2_ps, 1)
                        if more:
                            transposes(i + 1)
                        for s in range(2):
                            pe.wait_ge(p_ready, done(i * 2 + s))
                            pe.wait_ge(p_t_ready, freed(i * 2 + s))
                            for j in range(HALVES):
                                for h in range(HALVES):
                                    last = nc.tensor.transpose(ps_p[s][:, j * N + h * P:j * N + (h + 1) * P], p[s][:, h, j * P:(j + 1) * P], core.ident[:])
                            last.then_inc(p_ps, 1)
                        for s in range(2):
                            pe.wait_ge(p_t_ready, done(i * 2 + s))
                            pe.wait_ge(e_ready, done(i * 2 + s))
                            for h in range(HALVES):
                                for j in range(HALVES):
                                    last = mm(ps_s[s][:, N + h * D:N + (h + 1) * D], p_t[s][:, j, h * P:(h + 1) * P], wh[s][:, j, 0:D],
                                              start=j == 0, stop=j == HALVES - 1)
                            last.then_inc(out_ps, 1)

                    pe.wait_ge(weights, 48)
                    mm(ps_w[0][:, 0:2], w_t_sb[:], a_sb[:], start=True, stop=True).then_inc(wa_ps, 1)
                    pe.wait_ge(wa_ready, 1)
                    transposes(0)
                    loop(pe, turn)

                @block.scalar
                def _(act):
                    def keep_y_t(i):
                        for s in range(2):
                            act.wait_ge(s2_ps, freed(i * 2 + s))
                            act.wait_ge(y_ps, done(i * 2 + s))
                            nc.scalar.copy(y_t[s][:], ps_y[s][:, 0:N]).then_inc(y_t_ready, 1)

                    def turn(i, more):
                        for s in range(2):
                            act.wait_ge(out_ps, freed(i * 2 + s))
                            act.wait_ge(wh_ps, done(i * 2 + s))
                            nc.scalar.copy(wh[s][:], ps_w[s][:, 0:2 * (D + 2)].rearrange("p (h d) -> p h d", h=HALVES)).then_inc(wh_ready, 1)
                        for s in range(2):
                            act.wait_ge(wh_ready, done(i * 2 + s))
                            act.wait_ge(s2_ps, done(i * 2 + s))
                            for h in range(HALVES):
                                last = nc.scalar.activation(e[s][:, h, :], ps_s[s][:, 0:N], ACT.Identity, bias=wh[s][:, h, D:D + 1])
                            last.then_inc(raw_ready, 1)
                        if more:
                            keep_y_t(i + 1)
                        for s in range(2):
                            act.wait_ge(p_ps, freed(i * 2 + s))
                            act.wait_ge(out_ready, freed(i * 2 + s))
                            act.wait_ge(e_ready, done(i * 2 + s))
                            for h in range(HALVES):
                                last = nc.scalar.activation(p[s][:, h, :], e[s][:, h, :], ACT.Exp, bias=low[s][:, h:h + 1], accum_out=total[s][:, h:h + 1])
                            last.then_inc(p_ready, 1)
                        for s in range(2):
                            act.wait_ge(out_ps, freed(i * 2 + s))
                            act.wait_ge(p_ps, done(i * 2 + s))
                            nc.scalar.copy(p_t[s][:], ps_p[s][:].rearrange("p (h n) -> p h n", h=HALVES)).then_inc(p_t_ready, 1)
                        for s in range(2):
                            n = i * 2 + s
                            act.wait_ge(inv_ready, done(n))
                            act.wait_ge(out_ps, done(n))
                            hold(act, passed_a)
                            for h in range(HALVES):
                                last = nc.scalar.activation(attended[:, n * 2 + h, :], ps_s[s][:, N + h * D:N + (h + 1) * D], ACT.Copy, scale=total[s][:, h:h + 1])
                            last.then_inc(out_ready, 1)

                    keep_y_t(0)
                    loop(act, turn)

                @block.vector
                def _(dve):
                    v = nc.vector
                    dve.wait_ge(wa_ps, 1)
                    v.tensor_copy(w_sb[:, D:D + 2], ps_w[0][:, 0:2]).then_inc(first, 1)
                    dve.wait_ge(first, 1)
                    v.tensor_copy(wa2[:], w_sb[:, D + 1:D + 2].to_broadcast([P, P])).then_inc(wa_ready, 1)

                    def normalise(i):
                        for s in range(2):
                            n = i * 2 + s
                            dve.wait_ge(y_ps, freed(n))
                            for h in range(HALVES):
                                t = n * 2 + h
                                last = v.tensor_scalar(y[s][:, h, :], core.x[:, t, :], core.mean[:, bass.ds(t, 1)],
                                                       core.rstd[:, bass.ds(t, 1)], ALU.subtract, ALU.mult)
                            last.then_inc(y_ready, 1)

                    def turn(i, more):
                        mine = Own(dve, own, i, 2 * 3)
                        if more:
                            normalise(i + 1)
                        for s in range(2):
                            n = i * 2 + s
                            dve.wait_ge(raw_ready, done(n))
                            dve.wait_ge(p_ready, freed(n))
                            mine.step(v.scalar_tensor_tensor(e[s][:], e[s][:], SLOPE, e[s][:], ALU.mult, ALU.max))
                            dve.wait_ge(allow_ready, done(n))
                            mine.step(v.scalar_tensor_tensor(e[s][:], allow[s][:], MASKED, e[s][:], ALU.add, ALU.min))
                            mine.step(v.tensor_reduce(low[s][:], e[s][:], AXX, ALU.max))
                            v.tensor_scalar(low[s][:], low[s][:], -1.0, None, ALU.mult).then_inc(e_ready, 1)
                        for s in range(2):
                            dve.wait_ge(p_ready, done(i * 2 + s))
                            v.reciprocal(total[s][:], total[s][:]).then_inc(inv_ready, 1)
                        mine.end()

                    normalise(0)
                    loop(dve, turn)
        layernorm_statistics(nc, core, "norm_attended", attended)
        GROUP, SLOTS = 4, 4
        with Stage(nc, "gelu") as st:
            scale = st.sb("gamma", [P, D])
            shift = st.sb("beta", [P, D])
            z = [st.sb(f"z{s}", [P, GROUP, D]) for s in range(SLOTS)]
            loaded, own = st.sem("loaded"), st.sem("vector_steps")
            z_ready, affine_ready, gelu_ready, added = [st.sem(n, CREDIT) for n in ("z_ready", "affine_ready", "gelu_ready", "added")]
            with st.block() as block:
                @block.sync
                def _(sp):
                    sp.dma_start(scale[:], gamma.rearrange("(a n) -> a n", a=1).to_broadcast([P, D])).then_inc(loaded, 16)
                    sp.dma_start(shift[:], beta.rearrange("(a n) -> a n", a=1).to_broadcast([P, D])).then_inc(loaded, 16)

                @block.gpsimd
                def _(pool):
                    pool.wait_ge(loaded, 32)
                    with pool.Fori(0, TILES // GROUP // SLOTS) as i:
                        for s in range(SLOTS):
                            n = i * SLOTS + s
                            pool.wait_ge(z_ready, done(n))
                            nc.gpsimd.tensor_tensor(z[s][:], z[s][:], shift[:].unsqueeze(1).to_broadcast([P, GROUP, D]), ALU.add).then_inc(affine_ready, 1)

                @block.scalar
                def _(act):
                    with act.Fori(0, TILES // GROUP // SLOTS) as i:
                        for s in range(SLOTS):
                            n = i * SLOTS + s
                            act.wait_ge(affine_ready, done(n))
                            nc.scalar.activation(z[s][:], z[s][:], ACT.Gelu).then_inc(gelu_ready, 1)

                @block.vector
                def _(dve):
                    dve.wait_ge(loaded, 32)
                    with dve.Fori(0, TILES // GROUP // SLOTS) as i:
                        mine = Own(dve, own, i, SLOTS)
                        dve.wait_ge(added, i * SLOTS + CREDIT)
                        for s in range(SLOTS):
                            n = i * SLOTS + s
                            for k in range(GROUP):
                                t = n * GROUP + k
                                last = nc.vector.tensor_scalar(z[s][:, k, :], attended[:, t, :], core.mean[:, bass.ds(t, 1)],
                                                               core.rstd[:, bass.ds(t, 1)], ALU.subtract, ALU.mult)
                            mine.step(last)
                            nc.vector.tensor_tensor(z[s][:], z[s][:], scale[:].unsqueeze(1).to_broadcast([P, GROUP, D]), ALU.mult).then_inc(z_ready, 1)
                        mine.end()
                        for s in range(SLOTS):
                            n = i * SLOTS + s
                            dve.wait_ge(gelu_ready, done(n))
                            part = core.x[:, bass.ds(n * GROUP, GROUP), :]
                            nc.vector.tensor_tensor(part, part, z[s][:], ALU.add).then_inc(added, 1)


HEADS, HD, SLICES, NS, KC = 8, 64, 64, 64, 3
INNER = HEADS * HD
CHUNKS = INNER // P
CONV = INNER + 2 * NS
FC = CONV // P
PAIRS = B // 2
DT0 = INNER + CONV


def order_masks():
    u, t = np.arange(SLICES)[:, None], np.arange(SLICES)[None, :]
    two = lambda m: np.tile(m, (2, 1)).astype(np.float32)
    block = lambda m: np.kron(np.eye(2), m).astype(np.float32)
    return np.stack([two(u < t), two(u > t)], 1), np.stack([block(u > t), block(u < t)], 1)


def slice_block(nc, core, a, result):
    with Stage(nc, "slice") as keep:
        core.u_t = keep.sb("u_t", [P, CHUNKS, B * SLICES])
        make_slices(nc, core, a)
        mix_slices(nc, core, a)
        spread_slices(nc, core, a, result)


def make_slices(nc, core, a):
    SLOTS = 4
    ok = lambda n: n + 1 + SLOTS
    TWO = 2 * (D + 1)
    with Stage(nc, "make") as st:
        wx = st.sb("w_x", [P, CHUNKS, D])
        bx = st.sb("b_x", [P, CHUNKS])
        ws2 = st.sb("w_slice2", [P, P])
        bs = st.sb("b_slice", [P, SLICES])
        temp = st.sb("temperature", [P, HEADS])
        wl = st.sb("w_logits", [P, INNER])
        bl = st.sb("b_logits", [P, INNER])
        wf = st.sb("w_fx", [P, INNER])
        bf = st.sb("b_fx", [CHUNKS, CHUNKS, P])
        y = [st.sb(f"y{s}", [P, HALVES, D + 1]) for s in range(SLOTS)]
        y_t = [st.sb(f"y_t{s}", [P, N]) for s in range(2)]
        sw = [st.sb(f"sw{s}", [P, HALVES * HEADS, SLICES]) for s in range(SLOTS)]
        top = [st.sb(f"max{s}", [P, HALVES * HEADS]) for s in range(2)]
        rinv = st.sb("rinv", [P, CHUNKS, 1])
        ratio = [st.sb(f"ratio{s}", [P, CHUNKS, 1]) for s in range(2)]
        means = [st.sb(f"means{s}", [P, CHUNKS, D]) for s in range(2)]
        means_t = [st.sb(f"means_t{s}", [P, CHUNKS, P]) for s in range(2)]
        ratio_t = [st.sb(f"ratio_t{s}", [CHUNKS, P]) for s in range(2)]
        ps_l = [st.ps(f"ps_logits{h}", [P, 512]) for h in range(2)]
        ps_m = [st.ps(f"ps_sums{h}", [P, 512]) for h in range(2)]
        ps_y = st.ps("ps_y", [P, 512])
        ps_mt = st.ps("ps_means_t", [P, 512])
        ps_rt = st.ps("ps_ratio_t", [P, 512])
        ps_u = st.ps("ps_slices", [P, 512])
        cleared, loaded, pre, w_ps, b_ps, w_ready, passed = [st.sem(n) for n in (
            "cleared", "loaded", "vector_first_steps", "w_product", "b_product", "w_ready", "scalar_passed")]
        total_steps, scale_steps = st.sem("total_steps"), st.sem("scale_steps")
        y_ready, y_ps, y_t_ready, logits_ps, added, top_ready, low_ready, exp_ready, total_ready, sw_ready, sums_ps, scaled, t_ps, t_ready, u_ps, u_ready = [
            st.sem(n, SLOTS) for n in ("y_ready", "y_transposed", "y_t_ready", "logits_product", "logits_taken", "max_ready", "shifted", "exp_ready",
                                       "total_ready", "sw_ready", "sums_product", "means_ready", "means_transposed", "means_t_ready",
                                       "slices_product", "slices_ready")]
        stored = [st.sem(f"sw_stored{s}", 16) for s in range(SLOTS)]

        def turns(eng, turn):
            for n in range(-3, SLOTS):
                turn(n, n // SLOTS, n % SLOTS, lambda d: n + d >= 0)
            with eng.Fori(1, B // SLOTS - 1) as i:
                for s in range(SLOTS):
                    turn(i * SLOTS + s, i, s, lambda d: True)
            for n in range(B - SLOTS, B + 1):
                turn(n, n // SLOTS, n % SLOTS, lambda d: n + d < B)

        with st.block() as block:
            @block.sync
            def _(sp):
                def row(v, n):
                    return v.rearrange("(a n) -> a n", a=1).to_broadcast([P, n])
                sp.dma_start(wx[:], a["L3_ffn_W_x"].rearrange("(c p) d -> p c d", p=P)).then_inc(loaded, 16)
                sp.dma_start(wf[:], a["L3_ffn_W_fx_t"]).then_inc(loaded, 16)
                sp.dma_start(bs[:], row(a["L3_ffn_b_slice"], SLICES)).then_inc(loaded, 16)
                sp.dma_start(temp[:], row(a["L3_ffn_temperature"].rearrange("a h b c -> (a h b c)"), HEADS)).then_inc(loaded, 16)
                with nc.allow_non_contiguous_dma("bias columns"):
                    sp.dma_start(bx[:], a["L3_ffn_b_x"].rearrange("(c p) -> p c", p=P)).then_inc(loaded, 16)
                sp.wait_ge(cleared, 2 + SLOTS)
                for c in range(CHUNKS):
                    sp.dma_start(bf[c:c + 1, c, :], a["L3_ffn_b_fx"].rearrange("(c p) -> c p", p=P)[c:c + 1, :]).then_inc(loaded, 16)
                for k in range(2):
                    sp.dma_start(ws2[k * HD:(k + 1) * HD, k * SLICES:(k + 1) * SLICES], a["L3_ffn_W_slice_t"]).then_inc(loaded, 16)

                def turn(n, i, s, inside):
                    if inside(1):
                        i1, s1 = i + (s + 1) // SLOTS, (s + 1) % SLOTS
                        sp.wait_ge(sw_ready, ok(n + 1))
                        sp.dma_start(core.sw[n + 1, :, :], sw[s1][:].rearrange("p a b -> p (a b)")).then_inc(stored[s1], 16)

                turns(sp, turn)
                for s in range(SLOTS):
                    sp.wait_ge(stored[s], 16 * (B // SLOTS + 1))

            @block.gpsimd
            def _(pool):
                nc.gpsimd.memset(ws2[:], 0.0).then_inc(cleared, 1)
                nc.gpsimd.memset(bf[:], 0.0).then_inc(cleared, 1)
                for s in range(SLOTS):
                    nc.gpsimd.memset(y[s][:], 1.0).then_inc(cleared, 1)

                def each(s):
                    return top[s % 2][:].unsqueeze(2).to_broadcast([P, HALVES * HEADS, SLICES])

                def turn(n, i, s, inside):
                    if inside(2):
                        s2 = (s + 2) % SLOTS
                        pool.wait_ge(top_ready, ok(n + 2))
                        nc.gpsimd.tensor_tensor(sw[s2][:], sw[s2][:], each(s2), ALU.subtract).then_inc(low_ready, 1)
                    if inside(1):
                        s1 = (s + 1) % SLOTS
                        pool.wait_ge(total_ready, ok(n + 1))
                        nc.gpsimd.tensor_tensor(sw[s1][:], sw[s1][:], each(s1), ALU.mult).then_inc(sw_ready, 1)

                turns(pool, turn)

            @block.tensor
            def _(pe):
                mm = nc.tensor.matmul
                pe.wait_ge(loaded, 16 * (7 + CHUNKS))
                for c in range(CHUNKS):
                    last = mm(ps_m[0][:, c * P:(c + 1) * P], wx[:, c, :], ws2[:], start=True, stop=True)
                last.then_inc(w_ps, 1)
                for c in range(CHUNKS):
                    last = mm(ps_m[1][:, c * P:(c + 1) * P], bx[:, c:c + 1].to_broadcast([P, P]), ws2[:], start=True, stop=True)
                last.then_inc(b_ps, 1)
                pe.wait_ge(w_ready, 1)

                def turn(n, i, s, inside):
                    if inside(2):
                        pe.wait_ge(y_t_ready, ok(n + 2))
                        pe.wait_ge(added, ok(n + 1))
                        for h in range(HALVES):
                            last = mm(ps_l[h][:], y_t[s % 2][:, h * P:(h + 1) * P], wl[:], start=True, stop=True)
                        last.then_inc(logits_ps, 1)
                    if inside(-1):
                        pe.wait_ge(scaled, ok(n - 1))
                        pe.wait_ge(t_ready, ok(n - 2))
                        for c in range(CHUNKS):
                            nc.tensor.transpose(ps_mt[:, c * P:(c + 1) * P], means[(s - 1) % 2][:, c, :], core.ident[:])
                        nc.tensor.transpose(ps_rt[0:CHUNKS, 0:P], ratio[(s - 1) % 2][:].rearrange("p c a -> p (c a)"), core.ident[:]).then_inc(t_ps, 1)
                    if inside(3):
                        s3 = (s + 3) % SLOTS
                        pe.wait_ge(y_ready, ok(n + 3))
                        pe.wait_ge(y_t_ready, ok(n + 2))
                        for h in range(HALVES):
                            last = nc.tensor.transpose(ps_y[:, h * P:(h + 1) * P], y[s3][:, h, 0:D], core.ident[:])
                        last.then_inc(y_ps, 1)
                    if inside(0):
                        pe.wait_ge(sw_ready, ok(n))
                        pe.wait_ge(scaled, ok(n - 1))
                        for c in range(CHUNKS):
                            out = ps_m[c // 2][:, (c % 2) * (D + 1):(c % 2 + 1) * (D + 1)]
                            for h in range(HALVES):
                                lhs = sw[s][:, h * HEADS + 2 * c:h * HEADS + 2 * c + 2, :].rearrange("p a b -> p (a b)")
                                last = mm(out, lhs, y[s][:, h, :], start=h == 0, stop=h == HALVES - 1)
                        last.then_inc(sums_ps, 1)
                    if inside(-1):
                        pe.wait_ge(t_ready, ok(n - 1))
                        pe.wait_ge(u_ready, ok(n - 2))
                        for c in range(CHUNKS):
                            out = ps_u[:, c * P:(c + 1) * P]
                            mm(out, wf[:, c * P:(c + 1) * P], means_t[(s - 1) % 2][:, c, :], start=True, stop=False)
                            last = mm(out, bf[:, c, :], ratio_t[(s - 1) % 2][:], start=False, stop=True)
                        last.then_inc(u_ps, 1)

                turns(pe, turn)

            @block.scalar
            def _(act):
                a_ = nc.scalar.activation

                def turn(n, i, s, inside):
                    if inside(-1):
                        act.wait_ge(t_ps, ok(n - 1))
                        act.wait_ge(u_ps, ok(n - 3))
                        a_(means_t[(s - 1) % 2][:], ps_mt[:].rearrange("p (c q) -> p c q", c=CHUNKS), ACT.Copy)
                        a_(ratio_t[(s - 1) % 2][:], ps_rt[0:CHUNKS, 0:P], ACT.Copy).then_inc(t_ready, 1)
                    if inside(3):
                        act.wait_ge(y_ps, ok(n + 3))
                        act.wait_ge(logits_ps, ok(n + 1))
                        a_(y_t[(s + 3) % 2][:], ps_y[:, 0:N], ACT.Copy).then_inc(y_t_ready, 1)
                    if inside(2):
                        s2 = (s + 2) % SLOTS
                        act.wait_ge(low_ready, ok(n + 2))
                        a_(sw[s2][:], sw[s2][:], ACT.Exp).then_inc(exp_ready, 1)
                    if inside(-1):
                        act.wait_ge(u_ps, ok(n - 1))
                        hold(act, passed)
                        for k in range(2):
                            part = slice(k * HD, (k + 1) * HD)
                            from_ps = ps_u[part, :].rearrange("p (c q) -> p c q", c=CHUNKS)[:, :, k * SLICES:(k + 1) * SLICES]
                            last = a_(core.u_t[part, :, bass.ds((n - 1) * SLICES, SLICES)], from_ps, ACT.Copy)
                        last.then_inc(u_ready, 1)

                turns(act, turn)

            @block.vector
            def _(dve):
                v = nc.vector
                dve.wait_ge(loaded, 16 * (7 + CHUNKS))
                heads = lambda ap: ap.rearrange("p (h g) -> p h g", h=HEADS)
                first = Own(dve, pre, 0, 0)
                first.step(v.tensor_scalar(temp[:], temp[:], 1e-6, None, ALU.max))
                first.step(v.reciprocal(temp[:], temp[:]))
                each_head = temp[:].unsqueeze(2).to_broadcast([P, HEADS, SLICES])
                dve.wait_ge(w_ps, 1)
                first.step(v.tensor_tensor(heads(wl[:]), heads(ps_m[0][:]), each_head, ALU.mult))
                dve.wait_ge(b_ps, 1)
                first.step(v.tensor_tensor(heads(bl[:]), heads(ps_m[1][:]), bs[:].unsqueeze(1).to_broadcast([P, HEADS, SLICES]), ALU.add))
                v.tensor_tensor(heads(bl[:]), heads(bl[:]), each_head, ALU.mult).then_inc(w_ready, 1)
                dve.wait_ge(w_ready, 1)

                def turn(n, i, s, inside):
                    if inside(-1):
                        sb = (s - 1) % 2
                        mine = Own(dve, scale_steps, n - 1, 2)
                        dve.wait_ge(sums_ps, ok(n - 1))
                        dve.wait_ge(t_ps, ok(n - 3))
                        sums = [ps[:, 0:TWO].rearrange("p (c d) -> p c d", c=2) for ps in ps_m]
                        for k in range(2):
                            last = v.tensor_scalar(rinv[:, 2 * k:2 * k + 2, :], sums[k][:, :, D:D + 1], 1e-5, None, ALU.add)
                        mine.step(last)
                        mine.step(v.reciprocal(rinv[:], rinv[:]))
                        for k in range(2):
                            two = slice(2 * k, 2 * k + 2)
                            v.tensor_tensor(ratio[sb][:, two, :], sums[k][:, :, D:D + 1], rinv[:, two, :], ALU.mult)
                            last = v.tensor_tensor(means[sb][:, two, :], sums[k][:, :, 0:D], rinv[:, two, :].to_broadcast([P, 2, D]), ALU.mult)
                        last.then_inc(scaled, 1)
                        mine.end()
                    if inside(3):
                        s3 = (s + 3) % SLOTS
                        dve.wait_ge(sums_ps, ok(n - 1))
                        for h in range(HALVES):
                            t = (n + 3) * 2 + h
                            last = v.tensor_scalar(y[s3][:, h, 0:D], core.x[:, t, :], core.mean[:, bass.ds(t, 1)],
                                                   core.rstd[:, bass.ds(t, 1)], ALU.subtract, ALU.mult)
                        last.then_inc(y_ready, 1)
                    if inside(2):
                        i2, s2 = i + (s + 2) // SLOTS, (s + 2) % SLOTS
                        dve.wait_ge(logits_ps, ok(n + 2))
                        dve.wait_ge(sums_ps, ok(n - 2))
                        dve.wait_ge(stored[s2], i2 * 16 + 16)
                        dve.wait_ge(sw_ready, ok(n))
                        for h in range(HALVES):
                            last = v.tensor_tensor(sw[s2][:, h * HEADS:(h + 1) * HEADS, :], heads(ps_l[h][:]), heads(bl[:]), ALU.add)
                        last.then_inc(added, 1)
                        dve.wait_ge(added, ok(n + 2))
                        v.tensor_reduce(top[s2 % 2][:], sw[s2][:], AXX, ALU.max).then_inc(top_ready, 1)
                    if inside(1):
                        s1 = (s + 1) % SLOTS
                        mine = Own(dve, total_steps, n + 1, 1)
                        dve.wait_ge(exp_ready, ok(n + 1))
                        mine.step(v.tensor_reduce(top[s1 % 2][:], sw[s1][:], AXX, ALU.add))
                        v.reciprocal(top[s1 % 2][:], top[s1 % 2][:]).then_inc(total_ready, 1)
                        mine.end()

                turns(dve, turn)


def mix_slices(nc, core, a):
    with Stage(nc, "mix") as keep:
        z = keep.sb("z", [P, PAIRS, INNER])
        xc = keep.sb("xbc_t", [P, FC, B * SLICES])
        dt = keep.sb("dt", [P, PAIRS, 2 * HEADS])
        decay = keep.sb("decay", [P, PAIRS, 2 * HEADS])
        project_slices(nc, core, a, z, xc, dt)
        time_steps(nc, core, a, dt, decay)
        scan_slices(nc, core, a, z, xc, dt, decay)


def project_slices(nc, core, a, z, xc, dt):
    BLOCK = 512
    GRAPHS = BLOCK // SLICES
    with Stage(nc, "project") as st:
        w = st.sb("in_w", [P, CHUNKS, DT0 + 2 * HEADS])
        cw = st.sb("conv_w", [P, FC, KC])
        cb = st.sb("conv_b", [P, FC])
        dtb = st.sb("dt_bias", [P, 2 * HEADS])
        ub = [st.sb(f"u{s}", [P, CHUNKS, P]) for s in range(2)]
        xp = [st.sb(f"padded{s}", [P, GRAPHS, KC - 1 + SLICES]) for s in range(2)]
        acc = [st.sb(f"acc{s}", [P, GRAPHS, SLICES]) for s in range(2)]
        ps_x = [st.ps(f"ps_x{s}", [P, 512]) for s in range(2)]
        ps_z = [st.ps(f"ps_z{s}", [P, 512]) for s in range(2)]
        ps_d = [st.ps(f"ps_dt{s}", [P, 512]) for s in range(2)]
        loaded, cleared, own, passed_a, passed_p = [st.sem(n) for n in ("loaded", "pads_cleared", "vector_steps", "scalar_passed", "pool_passed")]
        x_ps, x_ready, conv_ready, x_kept, ub_ready, z_ps, z_kept, d_kept = [st.sem(n, CREDIT) for n in (
            "x_product", "x_padded", "conv_ready", "x_kept", "u_ready", "z_product", "z_kept", "dt_kept")]
        with st.block() as block:
            @block.sync
            def _(sp):
                sp.dma_start(w[:], a["L3_ffn_hy_in_w_t"].rearrange("(c p) f -> p c f", p=P)).then_inc(loaded, 16)
                for k in range(2):
                    sp.dma_start(dtb[:, k * HEADS:(k + 1) * HEADS], a["L3_ffn_hy_dt_bias"].rearrange("(a n) -> a n", a=1).to_broadcast([P, HEADS])).then_inc(loaded, 16)
                with nc.allow_non_contiguous_dma("columns of the convolution"):
                    sp.dma_start(cw[:], a["L3_ffn_hy_conv_w"].rearrange("(c p) k -> p c k", p=P)).then_inc(loaded, 16)
                    sp.dma_start(cb[:], a["L3_ffn_hy_conv_b"].rearrange("(c p) -> p c", p=P)).then_inc(loaded, 16)

            @block.gpsimd
            def _(pool):
                for s in range(2):
                    nc.gpsimd.memset(xp[s][:], 0.0).then_inc(cleared, 1)
                with pool.Fori(0, PAIRS // 2) as i:
                    for s in range(2):
                        m = i * 2 + s
                        pool.wait_ge(z_ps, freed(m))
                        hold(pool, passed_p)
                        nc.gpsimd.tensor_copy(ub[s][:], core.u_t[:, :, bass.ds(m * P, P)]).then_inc(ub_ready, 1)

            @block.tensor
            def _(pe):
                mm = nc.tensor.matmul
                pe.wait_ge(loaded, 80)
                with pe.Fori(0, B * SLICES // BLOCK // 2) as i:
                    for j in range(2):
                        for f in range(FC):
                            s = (j * FC + f) % 2
                            n = i * (2 * FC) + j * FC + f
                            pe.wait_ge(x_ready, freed(n))
                            for c in range(CHUNKS):
                                last = mm(ps_x[s][:], w[:, c, INNER + f * P:INNER + (f + 1) * P],
                                          core.u_t[:, c, bass.ds((i * 2 + j) * BLOCK, BLOCK)], start=c == 0, stop=c == CHUNKS - 1)
                            last.then_inc(x_ps, 1)
                        for q in range(BLOCK // P):
                            s = q % 2
                            m = (i * 2 + j) * (BLOCK // P) + q
                            pe.wait_ge(ub_ready, done(m))
                            pe.wait_ge(z_kept, freed(m))
                            pe.wait_ge(d_kept, freed(m))
                            for c in range(CHUNKS):
                                mm(ps_z[s][:], ub[s][:, c, :], w[:, c, 0:INNER], start=c == 0, stop=c == CHUNKS - 1)
                            for c in range(CHUNKS):
                                last = mm(ps_d[s][:, 0:2 * HEADS], ub[s][:, c, :], w[:, c, DT0:DT0 + 2 * HEADS], start=c == 0, stop=c == CHUNKS - 1)
                            last.then_inc(z_ps, 1)

            @block.scalar
            def _(act):
                act.wait_ge(cleared, 2)
                act.wait_ge(loaded, 80)

                def pad(n, s):
                    act.wait_ge(conv_ready, freed(n))
                    act.wait_ge(x_ps, done(n))
                    nc.scalar.copy(xp[s][:, :, KC - 1:], ps_x[s][:].rearrange("p (b g) -> p b g", b=GRAPHS)).then_inc(x_ready, 1)

                def keep_x(n, s, f, j):
                    act.wait_ge(conv_ready, done(n))
                    hold(act, passed_a)
                    nc.scalar.activation(xc[:, f, bass.ds(j * BLOCK, BLOCK)], acc[s][:].rearrange("p b g -> p (b g)"),
                                         ACT.Silu, bias=cb[:, f:f + 1]).then_inc(x_kept, 1)

                with act.Fori(0, B * SLICES // BLOCK // 2) as i:
                    for j in range(2):
                        first = i * (2 * FC) + j * FC
                        pad(first, j * FC % 2)
                        for f in range(FC):
                            s = (j * FC + f) % 2
                            if f + 1 < FC:
                                pad(first + f + 1, 1 - s)
                            keep_x(first + f, s, f, i * 2 + j)
                        for q in range(BLOCK // P):
                            m = (i * 2 + j) * (BLOCK // P) + q
                            act.wait_ge(z_ps, done(m))
                            hold(act, passed_a)
                            nc.scalar.activation(z[:, m, :], ps_z[q % 2][:], ACT.Silu).then_inc(z_kept, 1)

            @block.vector
            def _(dve):
                v = nc.vector
                dve.wait_ge(loaded, 80)
                with dve.Fori(0, B * SLICES // BLOCK // 2) as i:
                    mine = Own(dve, own, i, 2 * FC * 2)
                    for j in range(2):
                        for f in range(FC):
                            s = (j * FC + f) % 2
                            n = i * (2 * FC) + j * FC + f
                            dve.wait_ge(x_ready, done(n))
                            dve.wait_ge(x_kept, freed(n))
                            mine.step(v.tensor_scalar(acc[s][:], xp[s][:, :, 0:SLICES], cw[:, f, 0:1], None, ALU.mult))
                            mine.step(v.scalar_tensor_tensor(acc[s][:], xp[s][:, :, 1:1 + SLICES], cw[:, f, 1:2], acc[s][:], ALU.mult, ALU.add))
                            v.scalar_tensor_tensor(acc[s][:], xp[s][:, :, 2:2 + SLICES], cw[:, f, 2:3], acc[s][:], ALU.mult, ALU.add).then_inc(conv_ready, 1)
                        for q in range(BLOCK // P):
                            m = (i * 2 + j) * (BLOCK // P) + q
                            dve.wait_ge(z_ps, done(m))
                            v.tensor_tensor(dt[:, m, :], ps_d[q % 2][:, 0:2 * HEADS], dtb[:], ALU.add).then_inc(d_kept, 1)
                    mine.end()


def time_steps(nc, core, a, dt, decay):
    STEEPEST = 69.0
    with Stage(nc, "steps") as st:
        rate = st.sb("rate", [P, 2 * HEADS])
        shape = [P, PAIRS, 2 * HEADS]
        t0, t1, t2, same = [st.sb(f"t{k}", shape) for k in range(4)]
        loaded, rate_in, own, t_ready, e_ready, w_ready, l_ready = [st.sem(n) for n in (
            "loaded", "rate_clamped", "vector_steps", "minus_abs_ready", "exp_ready", "one_plus_ready", "log_ready")]
        with st.block() as block:
            @block.sync
            def _(sp):
                for k in range(2):
                    sp.dma_start(rate[:, k * HEADS:(k + 1) * HEADS], a["L3_ffn_hy_A_log"].rearrange("(a n) -> a n", a=1).to_broadcast([P, HEADS])).then_inc(loaded, 16)

            @block.scalar
            def _(act):
                act.wait_ge(rate_in, 1)
                nc.scalar.activation(rate[:], rate[:], ACT.Exp)
                act.wait_ge(t_ready, 1)
                nc.scalar.activation(t0[:], t0[:], ACT.Exp).then_inc(e_ready, 1)
                act.wait_ge(w_ready, 1)
                nc.scalar.activation(t2[:], t1[:], ACT.Ln).then_inc(l_ready, 1)

            @block.vector
            def _(dve):
                v = nc.vector
                mine = Own(dve, own, 0, 0)
                dve.wait_ge(loaded, 32)
                v.tensor_scalar(rate[:], rate[:], STEEPEST, None, ALU.min).then_inc(rate_in, 1)
                mine.step(v.tensor_scalar(t0[:], dt[:], -1.0, None, ALU.mult))
                v.tensor_tensor(t0[:], t0[:], dt[:], ALU.min).then_inc(t_ready, 1)
                dve.wait_ge(e_ready, 1)
                v.tensor_scalar(t1[:], t0[:], 1.0, None, ALU.add).then_inc(w_ready, 1)
                dve.wait_ge(w_ready, 1)
                mine.step(v.tensor_scalar(same[:], t1[:], 1.0, None, ALU.is_equal))
                dve.wait_ge(l_ready, 1)
                mine.step(v.tensor_scalar(t1[:], t1[:], 1.0, None, ALU.subtract))
                mine.step(v.tensor_tensor(t1[:], t1[:], same[:], ALU.add))
                mine.step(v.tensor_tensor(t2[:], t2[:], same[:], ALU.add))
                mine.step(v.reciprocal(t1[:], t1[:]))
                mine.step(v.tensor_tensor(t2[:], t2[:], t1[:], ALU.mult))
                mine.step(v.tensor_tensor(t2[:], t2[:], t0[:], ALU.mult))
                mine.step(v.tensor_scalar(dt[:], dt[:], 0.0, None, ALU.max))
                mine.step(v.tensor_tensor(dt[:], dt[:], t2[:], ALU.add))
                mine.step(v.tensor_scalar(rate[:], rate[:], -1.0, None, ALU.mult))
                mine.step(v.tensor_tensor(decay[:], dt[:], rate[:].unsqueeze(1).to_broadcast(shape), ALU.mult))


def scan_slices(nc, core, a, z, xc, dt, decay):
    with Stage(nc, "scan") as st:
        col_mask = st.sb("col_mask", [P, 2, SLICES])
        row_mask = st.sb("row_mask", [P, 2, P])
        fc_w = st.sb("fc_w", [P, CHUNKS, HEADS])
        dp = st.sb("d", [P, HEADS])
        nw = st.sb("norm_w", [P, CHUNKS])
        ow = st.sb("out_w", [P, CHUNKS, INNER])
        xb = [st.sb(f"xbc{s}", [P, FC, P]) for s in range(2)]
        ct = [st.sb(f"c_t{s}", [NS, P]) for s in range(2)]
        part = [[st.sb(f"decay_part{s}{k}", [P, HEADS, SLICES]) for k in range(2)] for s in range(2)]
        xs = [st.sb(f"x{s}", [P, INNER]) for s in range(2)]
        fade = [[st.sb(f"fade{s}{k}", [P, HEADS, SLICES]) for k in range(2)] for s in range(2)]
        near = st.sb("cb", [P, 2, SLICES])
        mat = [st.sb(f"matrix{s}", [P, HEADS, P]) for s in range(2)]
        fcd = [st.sb(f"fcd{s}", [P, HEADS]) for s in range(2)]
        yg = [st.sb(f"yg{s}", [P, INNER]) for s in range(2)]
        sq = st.sb("square", [P, INNER])
        ss = [st.sb(f"sum_square{s}", [P, 1]) for s in range(2)]
        yg_t = st.sb("yg_t", [P, CHUNKS, P])
        ps_x, ps_fc, ps_cb, ps_f, ps_b, ps_y, ps_g, ps_o = [st.ps(n, [P, 512]) for n in (
            "ps_x", "ps_fc", "ps_cb", "ps_forward", "ps_backward", "ps_y", "ps_gated", "ps_out")]
        loaded, cleared, matrix_steps, gated_steps, own_pool, own_act, passed_a, passed_p = [st.sem(n) for n in (
            "loaded", "matrix_cleared", "matrix_steps", "gated_steps", "pool_steps", "log_ready", "scalar_passed", "pool_passed")]
        in_ready, x_ps, xs_ready, fade_ready, fcd_ready, mat_ready, y_ps, yg_ready, ss_ready, ms_ready, rms_ready, ygs_ready, g_ps, g_ready, o_ps, o_kept = [
            st.sem(n, CREDIT) for n in ("inputs_ready", "inputs_product", "x_ready", "fade_ready", "fcd_ready", "matrix_ready", "y_product", "gated_ready",
                                        "square_sum_ready", "mean_square_ready", "rms_ready", "normed_ready", "gated_transposed",
                                        "gated_t_ready", "out_product", "out_kept")]
        def turns(eng, turn):
            for m in range(-1, 2):
                turn(m, m % 2, lambda d: m + d >= 0)
            with eng.Fori(1, PAIRS // 2 - 1) as i:
                for s in range(2):
                    turn(i * 2 + s, s, lambda d: True)
            for m in range(PAIRS - 2, PAIRS + 1):
                turn(m, m % 2, lambda d: m + d < PAIRS)

        with st.block() as block:
            @block.sync
            def _(sp):
                sp.dma_start(col_mask[:], a["col_mask"]).then_inc(loaded, 16)
                sp.dma_start(row_mask[:], a["lhs_mask"]).then_inc(loaded, 16)
                sp.dma_start(fc_w[:], a["L3_ffn_hy_fcD_w_t"].rearrange("(c p) h -> p c h", p=P)).then_inc(loaded, 16)
                sp.dma_start(dp[:], a["L3_ffn_hy_D"].rearrange("(a n) -> a n", a=1).to_broadcast([P, HEADS])).then_inc(loaded, 16)
                with nc.allow_non_contiguous_dma("weight columns"):
                    sp.dma_start(nw[:], a["L3_ffn_hy_norm_w"].rearrange("(c p) -> p c", p=P)).then_inc(loaded, 16)
                sp.dma_start(ow[:], a["L3_ffn_hy_out_w_t"].rearrange("(c p) f -> p c f", p=P)).then_inc(loaded, 16)

            @block.gpsimd
            def _(pool):
                g = nc.gpsimd
                for s in range(2):
                    g.memset(mat[s][:], 0.0).then_inc(cleared, 1)
                g.memset(near[:], 0.0).then_inc(cleared, 1)
                pool.wait_ge(loaded, 96)
                with pool.Fori(0, PAIRS // 2) as i:
                    for s in range(2):
                        m = i * 2 + s
                        pool.wait_ge(x_ps, freed(m))
                        hold(pool, passed_p)
                        g.tensor_copy(xb[s][:], xc[:, :, bass.ds(m * P, P)]).then_inc(own_pool, 1)
                        for k in range(2):
                            g.tensor_tensor(part[s][k][:], decay[:, m, k * HEADS:(k + 1) * HEADS].unsqueeze(2).to_broadcast([P, HEADS, SLICES]),
                                            col_mask[:, k, :].unsqueeze(1).to_broadcast([P, HEADS, SLICES]), ALU.mult).then_inc(own_pool, 1)
                        pool.wait_ge(own_pool, m * 3 + 3)
                        hold(pool, passed_p)
                        g.tensor_copy(ct[s][:], xb[s][NS:2 * NS, FC - 1, :]).then_inc(in_ready, 1)
                        pool.wait_ge(in_ready, done(m))
                        hold(pool, passed_p)

            @block.tensor
            def _(pe):
                mm = nc.tensor.matmul

                def inputs(m, s):
                    pe.wait_ge(in_ready, done(m))
                    pe.wait_ge(xs_ready, m + CREDIT)
                    pe.wait_ge(fade_ready, m + CREDIT)
                    pe.wait_ge(fcd_ready, m + CREDIT)
                    mm(ps_cb[:, 0:P], xb[s][0:NS, FC - 1, :], ct[s][:], start=True, stop=True)
                    for c in range(CHUNKS):
                        mm(ps_fc[:, 0:HEADS], xb[s][:, c, :], fc_w[:, c, :], start=c == 0, stop=c == CHUNKS - 1)
                    for k, out in enumerate((ps_f, ps_b)):
                        last = mm(out[:], row_mask[:, k, :], part[s][k][:], start=True, stop=True)
                    for c in range(CHUNKS):
                        last = nc.tensor.transpose(ps_x[:, c * P:(c + 1) * P], xb[s][:, c, :], core.ident[:])
                    last.then_inc(x_ps, 1)

                def turn(m, s, inside):
                    if inside(1):
                        inputs(m + 1, 1 - s)
                    if inside(-1):
                        pe.wait_ge(ygs_ready, done(m - 1))
                        pe.wait_ge(g_ready, m - 1 + CREDIT)
                        for c in range(CHUNKS):
                            last = nc.tensor.transpose(ps_g[:, c * P:(c + 1) * P], yg[1 - s][:, c * P:(c + 1) * P], core.ident[:])
                        last.then_inc(g_ps, 1)
                    if inside(0):
                        pe.wait_ge(mat_ready, done(m))
                        pe.wait_ge(xs_ready, done(m))
                        pe.wait_ge(yg_ready, m + CREDIT)
                        for h in range(HEADS):
                            last = mm(ps_y[:, h * HD:(h + 1) * HD], mat[s][:, h, :], xs[s][:, h * HD:(h + 1) * HD], start=True, stop=True)
                        last.then_inc(y_ps, 1)
                    if inside(-1):
                        pe.wait_ge(g_ready, done(m - 1))
                        pe.wait_ge(o_kept, m - 1 + CREDIT)
                        for f in range(CHUNKS):
                            for c in range(CHUNKS):
                                last = mm(ps_o[:, f * P:(f + 1) * P], ow[:, c, f * P:(f + 1) * P], yg_t[:, c, :], start=c == 0, stop=c == CHUNKS - 1)
                        last.then_inc(o_ps, 1)

                pe.wait_ge(loaded, 96)
                turns(pe, turn)

            @block.scalar
            def _(act):
                def turn(m, s, inside):
                    if inside(1):
                        other = 1 - s
                        act.wait_ge(yg_ready, freed(m + 1))
                        act.wait_ge(mat_ready, freed(m + 1))
                        act.wait_ge(x_ps, done(m + 1))
                        for k, ps in enumerate((ps_f, ps_b)):
                            last = nc.scalar.activation(fade[other][k][:], ps[:].rearrange("p (h t) -> p h t", h=HEADS), ACT.Exp)
                        last.then_inc(fade_ready, 1)
                        nc.scalar.copy(xs[other][:], ps_x[:]).then_inc(xs_ready, 1)
                    if inside(0):
                        act.wait_ge(yg_ready, done(m))
                        nc.scalar.activation(sq[:], yg[s][:], ACT.Square, accum_out=ss[s][:]).then_inc(ss_ready, 1)
                        act.wait_ge(ms_ready, done(m))
                        nc.scalar.activation(ss[s][:], ss[s][:], ACT.Ln).then_inc(own_act, 1)
                        act.wait_ge(own_act, m + 1)
                        nc.scalar.activation(ss[s][:], ss[s][:], ACT.Exp, scale=-0.5).then_inc(rms_ready, 1)
                    if inside(-1):
                        act.wait_ge(o_ps, done(m - 1))
                        hold(act, passed_a)
                        nc.scalar.copy(core.u_t[:, :, bass.ds((m - 1) * P, P)], ps_o[:].rearrange("p (c t) -> p c t", c=CHUNKS)).then_inc(o_kept, 1)

                turns(act, turn)

            @block.vector
            def _(dve):
                v = nc.vector
                per_head = lambda ap: ap.rearrange("p (h t) -> p h t", h=HEADS)

                def gate_t(m, s):
                    dve.wait_ge(g_ps, done(m))
                    dve.wait_ge(o_ps, m + CREDIT)
                    v.tensor_tensor(yg_t[:], ps_g[:].rearrange("p (c t) -> p c t", c=CHUNKS), nw[:].unsqueeze(2).to_broadcast([P, CHUNKS, P]),
                                    ALU.mult).then_inc(g_ready, 1)

                def matrix(m, s, between):
                    mine = Own(dve, matrix_steps, m, 5)
                    dve.wait_ge(x_ps, done(m))
                    for q in range(2):
                        rows = slice(q * SLICES, (q + 1) * SLICES)
                        at = q * SLICES
                        v.tensor_tensor(near[rows, 0, 1:SLICES], ps_cb[rows, at:at + SLICES - 1], col_mask[rows, 0, 1:SLICES], ALU.mult)
                        last = v.tensor_tensor(near[rows, 1, 0:SLICES - 1], ps_cb[rows, at + 1:at + SLICES], col_mask[rows, 1, 0:SLICES - 1], ALU.mult)
                    mine.mark(last)
                    v.tensor_tensor(fcd[s][:], ps_fc[:, 0:HEADS], dp[:], ALU.add).then_inc(fcd_ready, 1)
                    between()
                    mine.join()
                    dve.wait_ge(fade_ready, done(m))
                    for k in range(2):
                        mine.mark(v.tensor_tensor(fade[s][k][:], fade[s][k][:], near[:, k, :].unsqueeze(1).to_broadcast([P, HEADS, SLICES]), ALU.mult))
                    mine.join()
                    for k in range(2):
                        mine.mark(v.tensor_tensor(fade[s][k][:], fade[s][k][:],
                                                  dt[:, m, k * HEADS:(k + 1) * HEADS].unsqueeze(2).to_broadcast([P, HEADS, SLICES]), ALU.mult))
                    mine.join()
                    dve.wait_ge(y_ps, freed(m))
                    for q in range(2):
                        rows = slice(q * SLICES, (q + 1) * SLICES)
                        last = v.tensor_tensor(mat[s][rows, :, q * SLICES:(q + 1) * SLICES], fade[s][0][rows, :, :], fade[s][1][rows, :, :], ALU.add)
                    last.then_inc(mat_ready, 1)
                    mine.end()

                def turn(m, s, inside):
                    if inside(-1):
                        dve.wait_ge(rms_ready, done(m - 1))
                        v.tensor_scalar(yg[1 - s][:], yg[1 - s][:], ss[1 - s][:], None, ALU.mult).then_inc(ygs_ready, 1)
                    between = (lambda: gate_t(m - 1, 1 - s)) if inside(-1) else (lambda: None)
                    if inside(1):
                        matrix(m + 1, 1 - s, between)
                    else:
                        between()
                    if inside(0):
                        mine = Own(dve, gated_steps, m, 2)
                        dve.wait_ge(xs_ready, done(m))
                        dve.wait_ge(fcd_ready, done(m))
                        dve.wait_ge(g_ps, freed(m))
                        mine.step(v.tensor_tensor(per_head(yg[s][:]), per_head(xs[s][:]), fcd[s][:].unsqueeze(2).to_broadcast([P, HEADS, HD]), ALU.mult))
                        dve.wait_ge(y_ps, done(m))
                        mine.step(v.tensor_tensor(yg[s][:], ps_y[:], yg[s][:], ALU.add))
                        v.tensor_tensor(yg[s][:], yg[s][:], z[:, m, :], ALU.mult).then_inc(yg_ready, 1)
                        dve.wait_ge(ss_ready, done(m))
                        v.tensor_scalar(ss[s][:], ss[s][:], 1.0 / INNER, 1e-5, ALU.mult, ALU.add).then_inc(ms_ready, 1)
                        mine.end()

                dve.wait_ge(loaded, 96)
                dve.wait_ge(cleared, 3)
                turns(dve, turn)


def spread_slices(nc, core, a, result):
    with Stage(nc, "spread") as st:
        w = st.sb("out_w", [P, CHUNKS, D])
        bias = st.sb("out_b", [P, D])
        sw = [st.sb(f"sw{s}", [P, HALVES, INNER]) for s in range(2)]
        sw_t = [[st.sb(f"sw_t{s}{h}", [P, CHUNKS, P]) for h in range(2)] for s in range(2)]
        diag = [st.sb(f"diagonal{s}", [P, CHUNKS, P]) for s in range(2)]
        vs = [st.sb(f"v{s}", [P, CHUNKS, D]) for s in range(2)]
        o = [st.sb(f"o{s}", [P, HALVES, D]) for s in range(2)]
        ps_v = [st.ps(f"ps_v{s}", [P, 512]) for s in range(2)]
        ps_s = [[st.ps(f"ps_sw{s}{h}", [P, 512]) for h in range(2)] for s in range(2)]
        ps_o = [st.ps(f"ps_o{s}", [P, 512]) for s in range(2)]
        loaded, cleared, stored = st.sem("loaded"), st.sem("cleared"), st.sem("result_stored")
        sw_loaded = [st.sem(f"sw_loaded{s}") for s in range(2)]
        diag_ready, v_ps, v_ready, sw_ps, sw_t_ready, o_ps, o_ready, added = [st.sem(n, CREDIT) for n in (
            "diagonal_ready", "v_product", "v_ready", "sw_transposed", "sw_t_ready", "out_product", "out_ready", "added")]
        with st.block() as block:
            @block.sync
            def _(sp):
                sp.dma_start(w[:], a["L3_ffn_out_w_t"].rearrange("(c p) f -> p c f", p=P)).then_inc(loaded, 16)
                sp.dma_start(bias[:], a["L3_ffn_out_b"].rearrange("(a n) -> a n", a=1).to_broadcast([P, D])).then_inc(loaded, 16)
                with sp.Fori(0, B // 2) as i:
                    for s in range(2):
                        n = i * 2 + s
                        sp.wait_ge(sw_ps, freed(n))
                        sp.dma_start(sw[s][:].rearrange("p h f -> p (h f)"), core.sw[n, :, :]).then_inc(sw_loaded[s], 16)

            @block.gpsimd
            def _(pool):
                for s in range(2):
                    nc.gpsimd.memset(diag[s][:], 0.0).then_inc(cleared, 1)
                with pool.Fori(0, B // 2) as i:
                    pool.wait_ge(added, done(i * 2 + 1))
                    pool.dma_start(result[bass.ds(i * 2, 2), :, :].rearrange("b (h p) d -> p (b h) d", p=P),
                                   core.x[:, bass.ds(i * (2 * HALVES), 2 * HALVES), :]).then_inc(stored, 16)
                pool.wait_ge(stored, 16 * (B // 2))

            @block.tensor
            def _(pe):
                mm = nc.tensor.matmul
                pe.wait_ge(loaded, 32)
                with pe.Fori(0, B // 2) as i:
                    for s in range(2):
                        n = i * 2 + s
                        pe.wait_ge(sw_loaded[s], i * 16 + 16)
                        pe.wait_ge(sw_t_ready, freed(n))
                        for h in range(HALVES):
                            for c in range(CHUNKS):
                                last = nc.tensor.transpose(ps_s[s][h][:, c * P:(c + 1) * P], sw[s][:, h, c * P:(c + 1) * P], core.ident[:])
                        last.then_inc(sw_ps, 1)
                        pe.wait_ge(diag_ready, done(n))
                        pe.wait_ge(v_ready, freed(n))
                        for c in range(CHUNKS):
                            last = mm(ps_v[s][:, c * D:(c + 1) * D], diag[s][:, c, :], w[:, c, :], start=True, stop=True)
                        last.then_inc(v_ps, 1)
                    for s in range(2):
                        n = i * 2 + s
                        pe.wait_ge(sw_t_ready, done(n))
                        pe.wait_ge(v_ready, done(n))
                        pe.wait_ge(o_ready, freed(n))
                        for h in range(HALVES):
                            for c in range(CHUNKS):
                                last = mm(ps_o[s][:, h * D:(h + 1) * D], sw_t[s][h][:, c, :], vs[s][:, c, :], start=c == 0, stop=c == CHUNKS - 1)
                        last.then_inc(o_ps, 1)

            @block.scalar
            def _(act):
                with act.Fori(0, B // 2) as i:
                    for s in range(2):
                        n = i * 2 + s
                        act.wait_ge(sw_ps, done(n))
                        act.wait_ge(o_ps, freed(n))
                        for h in range(HALVES):
                            last = nc.scalar.copy(sw_t[s][h][:], ps_s[s][h][:].rearrange("p (c n) -> p c n", c=CHUNKS))
                        last.then_inc(sw_t_ready, 1)
                        act.wait_ge(v_ps, done(n))
                        nc.scalar.copy(vs[s][:], ps_v[s][:].rearrange("p (c n) -> p c n", c=CHUNKS)).then_inc(v_ready, 1)

            @block.vector
            def _(dve):
                v = nc.vector
                dve.wait_ge(cleared, 2)
                dve.wait_ge(loaded, 32)
                with dve.Fori(0, B // 2) as i:
                    for s in range(2):
                        n = i * 2 + s
                        dve.wait_ge(v_ps, freed(n))
                        for k in range(2):
                            rows = slice(k * HD, (k + 1) * HD)
                            last = v.tensor_scalar(diag[s][rows, :, k * SLICES:(k + 1) * SLICES], core.u_t[rows, :, bass.ds(n * SLICES, SLICES)],
                                                   1.0, None, ALU.mult)
                        last.then_inc(diag_ready, 1)
                    for s in range(2):
                        n = i * 2 + s
                        dve.wait_ge(o_ps, done(n))
                        v.tensor_tensor(o[s][:], ps_o[s][:, 0:HALVES * D].rearrange("p (h d) -> p h d", h=HALVES),
                                        bias[:].unsqueeze(1).to_broadcast([P, HALVES, D]), ALU.add).then_inc(o_ready, 1)
                        dve.wait_ge(o_ready, done(n))
                        tiles = core.x[:, bass.ds(n * HALVES, HALVES), :]
                        v.tensor_tensor(tiles, tiles, o[s][:], ALU.add).then_inc(added, 1)
                        dve.wait_ge(added, done(n))


def build(nc, a, out):
    core = Core()
    with ExitStack() as ctx:
        core.x = ctx.enter_context(nc.sbuf_tensor("x", [P, TILES, D], F32))
        core.mean = ctx.enter_context(nc.sbuf_tensor("mean", [P, TILES], F32))
        core.rstd = ctx.enter_context(nc.sbuf_tensor("rstd", [P, TILES], F32))
        core.parts = ctx.enter_context(nc.sbuf_tensor("parts", [P, TILES, 6], F32))
        core.ident = ctx.enter_context(nc.sbuf_tensor("ident", [P, P], F32))
        core.ones = ctx.enter_context(nc.sbuf_tensor("ones", [P, P], F32))
        core.sorted_in = nc.dram_tensor("sorted_in", (ROWS_MAX, D), F32, kind="Internal").ap()
        core.sorted_out = nc.dram_tensor("sorted_out", (ROWS_MAX, D), F32, kind="Internal").ap()
        core.adj_rows = nc.dram_tensor("adj_rows", (P * B, P), F32, kind="Internal").ap()
        core.sw = nc.dram_tensor("slice_weights", (B, P, HALVES * INNER), F32, kind="Internal").ap()
        load_inputs(nc, core, a["x"])
        with Stage(nc, "table") as table:
            written = start_tables(nc, core, table)
            layernorm_statistics(nc, core, "norm0")
            power_graph_block(nc, core, a["adj_t"], a["L0_gnn_W_t"], a["L0_gnn_conv_w"], a["L0_gnn_conv_b"])
            finish_tables(nc, table, *written)
        layernorm_statistics(nc, core, "norm1")
        expert_block(nc, core, "glu", a["L0_ffn_w12"], a["L0_ffn_w3"], a["L0_ffn_gate_w"], a["L0_ffn_gate_b"])
        layernorm_statistics(nc, core, "norm2", parts_known=True)
        grouped_graph_block(nc, core, a["adj_t"], a["L1_gnn_W1"], a["L1_gnn_b1"], a["L1_gnn_W2"], a["L1_gnn_b2"],
                            a["L1_gnn_fusion_w"], a["pair_mask"], a["row_mask"])
        with Stage(nc, "recur_adj") as adj_stage:
            adjacency = start_adjacency(nc, adj_stage, a["adj"])
            layernorm_statistics(nc, core, "norm3")
            expert_block(nc, core, "top1", a["L1_ffn_w1"], a["L1_ffn_w2"], a["L1_ffn_gate_w"], a["L1_ffn_gate_b"],
                         a["L1_ffn_b1"], a["L1_ffn_b2"], top=1, capacity=-(-5 * B * N // (4 * 8)), guard=True)
            layernorm_statistics(nc, core, "norm4", parts_known=True)
            recurrent_block(nc, core, *adjacency, a["L2_gnn_W_ioux_t"], a["L2_gnn_W_iouh_t"], a["L2_gnn_b_ioux"], a["L2_gnn_b_iouh"],
                            a["L2_gnn_W_coux_t"], a["L2_gnn_W_couh_t"], a["L2_gnn_b_coux"], a["L2_gnn_b_couh"])
        layernorm_statistics(nc, core, "norm5")
        expert_block(nc, core, "top2", a["L2_ffn_W1_t"], a["L2_ffn_W2_t"], a["L2_ffn_Wg_t"], a["L2_ffn_bg"],
                     a["L2_ffn_b1"], a["L2_ffn_b2"])
        layernorm_statistics(nc, core, "norm6", parts_known=True)
        attention_block(nc, core, a["adj"], a["L3_gnn_W"], a["L3_gnn_W_t"], a["L3_gnn_a2"], a["L3_gnn_gamma"], a["L3_gnn_beta"])
        layernorm_statistics(nc, core, "norm7")
        slice_block(nc, core, a, out)


def _laid_out(inputs):
    a = {k: np.asarray(v) for k, v in inputs.items()}
    a["adj_t"] = a["adj"].transpose(0, 2, 1)
    a["L0_gnn_W_t"] = a["L0_gnn_W"].T
    a["L0_ffn_w12"] = np.concatenate([a["L0_ffn_w1"], a["L0_ffn_w2"]], axis=2)
    a["L2_ffn_W1_t"] = a["L2_ffn_W1"].transpose(0, 2, 1)
    a["L2_ffn_W2_t"] = a["L2_ffn_W2"].transpose(0, 2, 1)
    a["L2_ffn_Wg_t"] = a["L2_ffn_Wg"].T
    a["pair_mask"], a["row_mask"] = group_masks()
    a["L3_gnn_W_t"] = a["L3_gnn_W"].T
    a["L3_gnn_a2"] = a["L3_gnn_a"].reshape(2, D).T
    for k in ("W_ioux", "W_iouh", "W_coux", "W_couh"):
        a["L2_gnn_" + k + "_t"] = a["L2_gnn_" + k].T
    for k in ("W_fx", "W_slice", "hy_in_w", "hy_fcD_w", "hy_out_w", "out_w"):
        a["L3_ffn_" + k + "_t"] = a["L3_ffn_" + k].T
    a["col_mask"], a["lhs_mask"] = order_masks()
    return {k: np.ascontiguousarray(a[k]) for k in USED}


def kernel(**inputs):
    import concourse.bacc as _bacc
    from concourse.bass_utils import run_bass_kernel_spmd as _run

    nc = _bacc.Bacc("TRN2", target_bir_lowering=False, num_devices=1)
    arrays = _laid_out(inputs)
    aps = {k: nc.dram_tensor("in_" + k, v.shape, mybir.dt.from_np(v.dtype), kind="ExternalInput").ap()
           for k, v in arrays.items()}
    out = nc.dram_tensor("out_0", (B, N, D), F32, kind="ExternalOutput").ap()
    build(nc, aps, out)
    r = _run(nc, [{"in_" + k: v for k, v in arrays.items()}], core_ids=[0])
    return r.results[0]["out_0"]
```
